# Optimizing a Trainium2 kernel written in Bass

```python
import numpy as np
import jax
import jax.numpy as jnp

def _softmax(x, axis=-1):
    return jax.nn.softmax(x, axis=axis)

def _gelu(x):
    return jax.nn.gelu(x, approximate=True)

def _silu(x):
    return jax.nn.silu(x)

def _sigmoid(x):
    return jax.nn.sigmoid(x)

def _layernorm(x, axis=-1, eps=1e-05):
    m = jnp.mean(x, axis=axis, keepdims=True)
    v = jnp.var(x, axis=axis, keepdims=True)
    return (x - m) / jnp.sqrt(v + eps)

def _scatter_add(tgt, idx, src, axis=0):
    return tgt.at[idx].add(src)

def _segment_sum(src, seg, n):
    return jax.ops.segment_sum(src, seg, n)
kernel_name = 'mk_decoder_postln_d2_seqx_r8_c8e846'

def setup_inputs(seed: int=0):
    np.random.seed(seed)
    _w = jnp.asarray

    def _rec_inputs():
        import jax
        import jax.numpy as jnp
        _rk = jax.random.key(seed)
        x = 0.0003765 + 1 * jax.random.normal(jax.random.fold_in(_rk, 1), (16, 256, 128), jnp.float32)
        _lenS = 256 - jax.random.randint(jax.random.fold_in(_rk, 7), (16,), 0, max(1, 256 // 4) + 1, jnp.int32)
        _lenS2 = 1601 - jax.random.randint(jax.random.fold_in(_rk, 8), (16,), 0, max(1, 1601 // 4) + 1, jnp.int32)
        _ctx_1024P = jax.random.normal(jax.random.fold_in(_rk, 11), (16, 16, 128), jnp.float32)
        _ctx_1024c = jax.random.dirichlet(jax.random.fold_in(_rk, 511), 0.3 * jnp.ones((16,), jnp.float32), (16, 1601))
        _ctx_1024t = jnp.einsum('bsk,bkd->bsd', _ctx_1024c, _ctx_1024P)
        _ctx_1024t = _ctx_1024t * jax.lax.rsqrt(jnp.mean(jnp.square(_ctx_1024t)) + 1e-12) * 0.953939
        ctx_1024 = -0.000292821 + 1.00034 * (_ctx_1024t + 0.3 * jax.random.normal(jax.random.fold_in(_rk, 611), (16, 1601, 128), jnp.float32))
        _validS = jnp.arange(256)[None, :] < _lenS[:, None]
        _validS2 = jnp.arange(1601)[None, :] < _lenS2[:, None]
        _causal = jnp.tril(jnp.ones((256, 256), dtype=bool))
        mask_BxS2_bf1 = jnp.ones((16, 1601), dtype=bool)
        return (x, ctx_1024, mask_BxS2_bf1)
    x, ctx_1024, mask_BxS2_bf1 = _rec_inputs()

    def _L0_attn_setup():
        import jax, jax.numpy as jnp
        import numpy as np
        from jax import lax
        D_MODEL, D_STATE, D_CONV, EXPAND = (128, 16, 4, 2)
        D_INNER = D_MODEL * EXPAND
        LN_EPS = 1e-05

        def _silu(v):
            return v * jax.nn.sigmoid(v)

        def _forward(x, W_in, conv_w, conv_b, W_x, W_dt, b_dt, A_log, D_param, W_out, ln_g, ln_b):
            B, T, _ = x.shape
            xz = jnp.einsum('btd,ed->bte', x, W_in)
            xp, z = (xz[..., :D_INNER], xz[..., D_INNER:])
            xc = lax.conv_general_dilated(jnp.transpose(xp, (0, 2, 1)), conv_w, window_strides=(1,), padding=[(D_CONV - 1, 0)], feature_group_count=D_INNER, dimension_numbers=('NCH', 'OIH', 'NCH')) + conv_b[None, :, None]
            xc = _silu(jnp.transpose(xc, (0, 2, 1)))
            ssm = jnp.einsum('bti,si->bts', xc, W_x)
            Bp, Cp = (ssm[..., :D_STATE], ssm[..., D_STATE:])
            dt = jax.nn.softplus(jnp.einsum('bti,oi->bto', xc, W_dt) + b_dt)
            A = -jnp.exp(A_log)

            def step(h, inp):
                x_t, b_t, c_t, dt_t = inp
                dA = jnp.exp(dt_t[..., None] * A)
                h = dA * h + dt_t[..., None] * b_t[:, None, :] * x_t[..., None]
                y_t = jnp.einsum('bds,bs->bd', h, c_t)
                return (h, y_t)
            h0 = jnp.zeros((B, D_INNER, D_STATE), dtype=x.dtype)
            tm = lambda a: jnp.moveaxis(a, 1, 0)
            _, ys = lax.scan(step, h0, (tm(xc), tm(Bp), tm(Cp), tm(dt)))
            y = jnp.moveaxis(ys, 0, 1)
            mu = jnp.mean(y, axis=-1, keepdims=True)
            var = jnp.mean((y - mu) ** 2, axis=-1, keepdims=True)
            y = (y - mu) * lax.rsqrt(var + LN_EPS) * ln_g + ln_b
            y = y + xc * D_param
            y = y * _silu(z)
            return jnp.einsum('bti,di->btd', y, W_out)
        key = jax.random.key(seed)
        ks = jax.random.split(key, 12)
        B, T = (4, 256)
        x = jax.random.normal(ks[0], (B, T, D_MODEL), dtype=jnp.float32)
        W_in = jax.random.normal(ks[1], (2 * D_INNER, D_MODEL), dtype=jnp.float32) * D_MODEL ** (-0.5)
        conv_w = jax.random.normal(ks[2], (D_INNER, 1, D_CONV), dtype=jnp.float32) * D_CONV ** (-0.5)
        conv_b = jax.random.normal(ks[3], (D_INNER,), dtype=jnp.float32) * 0.01
        W_x = jax.random.normal(ks[4], (2 * D_STATE, D_INNER), dtype=jnp.float32) * D_INNER ** (-0.5)
        dt_init_std = D_INNER ** (-0.5)
        W_dt = jax.random.uniform(ks[5], (D_INNER, D_INNER), minval=-dt_init_std, maxval=dt_init_std, dtype=jnp.float32)
        dt = jnp.exp(jax.random.uniform(ks[6], (D_INNER,)) * (np.log(0.1) - np.log(0.001)) + np.log(0.001))
        b_dt = dt + jnp.log(-jnp.expm1(-dt))
        A_log = jnp.log(jnp.arange(1, D_STATE + 1, dtype=jnp.float32) * 0.5)
        D_param = jnp.ones((D_INNER,), dtype=jnp.float32)
        W_out = jax.random.normal(ks[7], (D_MODEL, D_INNER), dtype=jnp.float32) * D_MODEL ** (-0.5)
        ln_g = jnp.ones((D_INNER,), dtype=jnp.float32)
        ln_b = jnp.zeros((D_INNER,), dtype=jnp.float32)
        return {'x': x, 'W_in': W_in, 'conv_w': conv_w, 'conv_b': conv_b, 'W_x': W_x, 'W_dt': W_dt, 'b_dt': b_dt, 'A_log': A_log, 'D_param': D_param, 'W_out': W_out, 'ln_g': ln_g, 'ln_b': ln_b}
    _L0_attn_all = _L0_attn_setup()
    _L0_attn_in = {k: v for k, v in _L0_attn_all.items() if k in ('W_in', 'conv_w', 'conv_b', 'W_x', 'W_dt', 'b_dt', 'A_log', 'D_param', 'W_out', 'ln_g', 'ln_b')}
    del _L0_attn_all

    def _L0_xattn_setup():
        import jax, jax.numpy as jnp
        import numpy as np
        EMB = 128
        HEADS = 16
        HEAD_DIM = EMB // HEADS
        SM_SCALE = 1.0
        NEG_INF = -1000000000.0
        key = jax.random.key(seed)
        ks = jax.random.split(key, 9)
        N, L = (2, 256)
        inp = {'values': jax.random.normal(ks[0], (N, L, EMB), dtype=jnp.float32), 'keys': jax.random.normal(ks[1], (N, L, EMB), dtype=jnp.float32), 'queries': jax.random.normal(ks[2], (N, L, EMB), dtype=jnp.float32), 'mask': jnp.ones((N, L), dtype=jnp.bool_), 'Wv': jax.random.normal(ks[3], (HEAD_DIM, HEAD_DIM), dtype=jnp.float32) / np.sqrt(HEAD_DIM), 'Wk': jax.random.normal(ks[4], (HEAD_DIM, HEAD_DIM), dtype=jnp.float32) / np.sqrt(HEAD_DIM), 'Wq': jax.random.normal(ks[5], (HEAD_DIM, HEAD_DIM), dtype=jnp.float32) / np.sqrt(HEAD_DIM), 'Wo': jax.random.normal(ks[6], (EMB, EMB), dtype=jnp.float32) / np.sqrt(EMB), 'bo': jax.random.normal(ks[7], (EMB,), dtype=jnp.float32) * 0.01}
        return inp
    _L0_xattn_all = _L0_xattn_setup()
    _L0_xattn_in = {k: v for k, v in _L0_xattn_all.items() if k in ('Wv', 'Wk', 'Wq', 'Wo', 'bo')}
    del _L0_xattn_all

    def _L0_ffn_setup():
        import jax, jax.numpy as jnp
        import numpy as np
        D_MODEL = 128
        D_FF = 512
        NUM_EXPERTS = 8
        B, N = (16, 128)
        key = jax.random.key(seed)
        ks = jax.random.split(key, 7)
        s_in = 1.0 / np.sqrt(D_MODEL)
        s_ff = 1.0 / np.sqrt(D_FF)
        return {'x': jax.random.normal(ks[0], (B, N, D_MODEL), dtype=jnp.float32), 'Wr': jax.random.uniform(ks[1], (D_MODEL, NUM_EXPERTS), jnp.float32, -s_in, s_in), 'br': jax.random.uniform(ks[2], (NUM_EXPERTS,), jnp.float32, -s_in, s_in), 'W1': jax.random.uniform(ks[3], (NUM_EXPERTS, D_MODEL, D_FF), jnp.float32, -s_in, s_in), 'b1': jax.random.uniform(ks[4], (NUM_EXPERTS, D_FF), jnp.float32, -s_in, s_in), 'W2': jax.random.uniform(ks[5], (NUM_EXPERTS, D_FF, D_MODEL), jnp.float32, -s_ff, s_ff), 'b2': jax.random.uniform(ks[6], (NUM_EXPERTS, D_MODEL), jnp.float32, -s_ff, s_ff)}
    _L0_ffn_all = _L0_ffn_setup()
    _L0_ffn_in = {k: v for k, v in _L0_ffn_all.items() if k in ('Wr', 'br', 'W1', 'b1', 'W2', 'b2')}
    del _L0_ffn_all

    def _L1_attn_setup():
        import jax, jax.numpy as jnp
        from jax import lax
        import numpy as np
        CHUNK = 64

        def short_conv(x, w):
            L = x.shape[1]
            K = w.shape[1]
            xp = jnp.pad(x, ((0, 0), (K - 1, 0), (0, 0)))
            return sum((xp[:, j:j + L, :] * w[:, j] for j in range(K)))

        def o2b_weighted_delta_rule(k, q, v, b):
            B, L, H, D = k.shape
            C = CHUNK
            Nc = L // C

            def to_chunks(t):
                return t.transpose(0, 2, 1, 3).reshape(B, H, Nc, C, D).transpose(2, 0, 1, 3, 4)
            Kc, Qc, Vc, Bc = map(to_chunks, (k, q, v, b))
            eyeC = jnp.eye(C, dtype=jnp.float32)
            W0 = jnp.zeros((B, H, D, D), jnp.float32)
            Cf = float(C)

            def step(carry, xs):
                W_t, W_avg = carry
                i, Ki, Qi, Vi, Bi = xs
                KiT = jnp.swapaxes(Ki, -1, -2)
                T = jnp.tril(Bi @ KiT, k=-1)
                inv = jnp.linalg.inv(eyeC + T)
                Ui = inv @ (Vi - Bi @ W_t)
                W_new = W_t + KiT @ Ui
                ts = (i * C).astype(jnp.float32)
                idx = jnp.arange(1, C + 1, dtype=jnp.float32) + ts
                cs = jnp.cumsum(idx)
                weighted_idx = idx + idx.sum() - cs
                w_i = (weighted_idx / ((1 + ts + Cf) * (ts + Cf) / 2))[:, None]
                coef1 = ts / (ts + Cf) * ((1 + ts) / (1 + ts + Cf))
                coef2 = Cf / (ts + Cf) * ((ts * 2 + 1 + Cf) / (1 + ts + Cf))
                W_avg_new = coef1 * W_avg + coef2 * W_t + KiT @ (Ui * w_i)
                tri0 = (1 + ts) * ts / 2
                a = (tri0 / (tri0 + cs))[:, None]
                c = 1.0 - a
                r = cs[:, None]
                j_idx = (cs - idx)[None, :]
                T_mat = jnp.where(r >= j_idx, (r - j_idx) / (tri0 + r), 0.0)
                O_i = Qi @ W_avg * a + Qi @ W_t * c + T_mat * (Qi @ KiT) @ Ui
                return ((W_new, W_avg_new), O_i)
            (_, _), O = lax.scan(step, (W0, W0), (jnp.arange(Nc), Kc, Qc, Vc, Bc))
            return O.transpose(1, 2, 0, 3, 4).reshape(B, H, L, D).transpose(0, 2, 1, 3)
        key = jax.random.key(seed)
        ks = jax.random.split(key, 9)
        B, L, Dm, H = (4, 256, 128, 16)
        Dh, K = (Dm // H, 4)
        s = 0.02
        return {'x': jax.random.normal(ks[0], (B, L, Dm), jnp.float32), 'Wk': s * jax.random.normal(ks[1], (Dm, Dm), jnp.float32), 'bk': jnp.zeros((Dm,), jnp.float32), 'Wq': s * jax.random.normal(ks[2], (Dm, Dm), jnp.float32), 'bq': jnp.zeros((Dm,), jnp.float32), 'Wv': s * jax.random.normal(ks[3], (Dm, Dm), jnp.float32), 'bv': jnp.zeros((Dm,), jnp.float32), 'Wbeta': s * jax.random.normal(ks[4], (H, Dm), jnp.float32), 'bbeta': jnp.zeros((H,), jnp.float32), 'conv_k': 0.1 * jax.random.normal(ks[5], (Dm, K), jnp.float32), 'conv_q': 0.1 * jax.random.normal(ks[6], (Dm, K), jnp.float32), 'conv_v': 0.1 * jax.random.normal(ks[7], (Dm, K), jnp.float32), 'rms_w': jnp.ones((Dh,), jnp.float32), 'Wout': s * jax.random.normal(ks[8], (Dm, Dm), jnp.float32), 'bout': jnp.zeros((Dm,), jnp.float32)}
    _L1_attn_all = _L1_attn_setup()
    _L1_attn_in = {k: v for k, v in _L1_attn_all.items() if k in ('Wk', 'bk', 'Wq', 'bq', 'Wv', 'bv', 'Wbeta', 'bbeta', 'conv_k', 'conv_q', 'conv_v', 'rms_w', 'Wout', 'bout')}
    del _L1_attn_all

    def _L1_xattn_setup():
        import jax, jax.numpy as jnp
        import numpy as np
        H = 16
        D = 64
        SCALE = D ** (-0.5)
        TEXT = 77
        IMG = 16
        AUD = 32
        MAXREL = 16
        B, NQ, QD = (32, 128, 128)
        INNER = H * D

        def _heads(t):
            return t.reshape(t.shape[0], t.shape[1], H, D)
        key = jax.random.key(seed)
        ks = jax.random.split(key, 14)
        w = lambda k, s: jax.random.normal(k, s, jnp.float32) * 0.02
        return {'x': jax.random.normal(ks[0], (B, NQ, QD), jnp.float32), 'context': jax.random.normal(ks[1], (B, TEXT + IMG + AUD, QD), jnp.float32), 'Wq': w(ks[2], (QD, INNER)), 'Wk': w(ks[3], (QD, INNER)), 'Wv': w(ks[4], (QD, INNER)), 'Wk_ip': w(ks[5], (QD, INNER)), 'Wv_ip': w(ks[6], (QD, INNER)), 'Wk_ap': w(ks[7], (QD, INNER)), 'Wv_ap': w(ks[8], (QD, INNER)), 'Wo': w(ks[9], (INNER, QD)), 'bo': jnp.zeros((QD,), jnp.float32), 'rel_k': w(ks[10], (2 * MAXREL + 1, D)), 'rel_v': w(ks[11], (2 * MAXREL + 1, D)), 'alpha': jnp.zeros((), jnp.float32), 'beta': jnp.zeros((), jnp.float32)}
    _L1_xattn_all = _L1_xattn_setup()
    _L1_xattn_in = {k: v for k, v in _L1_xattn_all.items() if k in ('Wq', 'Wk', 'Wv', 'Wk_ip', 'Wv_ip', 'Wk_ap', 'Wv_ap', 'Wo', 'bo', 'rel_k', 'rel_v', 'alpha', 'beta')}
    del _L1_xattn_all

    def _L1_ffn_setup():
        import jax, jax.numpy as jnp
        import numpy as np
        CAPACITY_FACTOR = 1.0
        key = jax.random.key(seed)
        ks = jax.random.split(key, 5)
        B, S, D, E, F = (2, 256, 128, 8, 512)
        x = jax.random.normal(ks[0], (B, S, D), dtype=jnp.float32)
        Ws = jax.random.normal(ks[1], (D, E), dtype=jnp.float32) * (1.0 / np.sqrt(D))
        bs = jnp.zeros((E,), dtype=jnp.float32)
        W1 = jax.random.normal(ks[2], (E, D, F), dtype=jnp.float32) * (1.0 / np.sqrt(D))
        b1 = jnp.zeros((E, F), dtype=jnp.float32)
        W2 = jax.random.normal(ks[3], (E, F, D), dtype=jnp.float32) * (1.0 / np.sqrt(F))
        b2 = jnp.zeros((E, D), dtype=jnp.float32)
        return {'x': x, 'Ws': Ws, 'bs': bs, 'W1': W1, 'b1': b1, 'W2': W2, 'b2': b2}
    _L1_ffn_all = _L1_ffn_setup()
    _L1_ffn_in = {k: v for k, v in _L1_ffn_all.items() if k in ('Ws', 'bs', 'W1', 'b1', 'W2', 'b2')}
    del _L1_ffn_all
    return {'x': x, 'ctx_1024': ctx_1024, 'mask_BxS2_bf1': mask_BxS2_bf1, 'L0_attn_W_in': _L0_attn_in['W_in'], 'L0_attn_conv_w': _L0_attn_in['conv_w'], 'L0_attn_conv_b': _L0_attn_in['conv_b'], 'L0_attn_W_x': _L0_attn_in['W_x'], 'L0_attn_W_dt': _L0_attn_in['W_dt'], 'L0_attn_b_dt': _L0_attn_in['b_dt'], 'L0_attn_A_log': _L0_attn_in['A_log'], 'L0_attn_D_param': _L0_attn_in['D_param'], 'L0_attn_W_out': _L0_attn_in['W_out'], 'L0_attn_ln_g': _L0_attn_in['ln_g'], 'L0_attn_ln_b': _L0_attn_in['ln_b'], 'L0_xattn_Wv': _L0_xattn_in['Wv'], 'L0_xattn_Wk': _L0_xattn_in['Wk'], 'L0_xattn_Wq': _L0_xattn_in['Wq'], 'L0_xattn_Wo': _L0_xattn_in['Wo'], 'L0_xattn_bo': _L0_xattn_in['bo'], 'L0_ffn_Wr': _L0_ffn_in['Wr'], 'L0_ffn_br': _L0_ffn_in['br'], 'L0_ffn_W1': _L0_ffn_in['W1'], 'L0_ffn_b1': _L0_ffn_in['b1'], 'L0_ffn_W2': _L0_ffn_in['W2'], 'L0_ffn_b2': _L0_ffn_in['b2'], 'L1_attn_Wk': _L1_attn_in['Wk'], 'L1_attn_bk': _L1_attn_in['bk'], 'L1_attn_Wq': _L1_attn_in['Wq'], 'L1_attn_bq': _L1_attn_in['bq'], 'L1_attn_Wv': _L1_attn_in['Wv'], 'L1_attn_bv': _L1_attn_in['bv'], 'L1_attn_Wbeta': _L1_attn_in['Wbeta'], 'L1_attn_bbeta': _L1_attn_in['bbeta'], 'L1_attn_conv_k': _L1_attn_in['conv_k'], 'L1_attn_conv_q': _L1_attn_in['conv_q'], 'L1_attn_conv_v': _L1_attn_in['conv_v'], 'L1_attn_rms_w': _L1_attn_in['rms_w'], 'L1_attn_Wout': _L1_attn_in['Wout'], 'L1_attn_bout': _L1_attn_in['bout'], 'L1_xattn_Wq': _L1_xattn_in['Wq'], 'L1_xattn_Wk': _L1_xattn_in['Wk'], 'L1_xattn_Wv': _L1_xattn_in['Wv'], 'L1_xattn_Wk_ip': _L1_xattn_in['Wk_ip'], 'L1_xattn_Wv_ip': _L1_xattn_in['Wv_ip'], 'L1_xattn_Wk_ap': _L1_xattn_in['Wk_ap'], 'L1_xattn_Wv_ap': _L1_xattn_in['Wv_ap'], 'L1_xattn_Wo': _L1_xattn_in['Wo'], 'L1_xattn_bo': _L1_xattn_in['bo'], 'L1_xattn_rel_k': _L1_xattn_in['rel_k'], 'L1_xattn_rel_v': _L1_xattn_in['rel_v'], 'L1_xattn_alpha': _L1_xattn_in['alpha'], 'L1_xattn_beta': _L1_xattn_in['beta'], 'L1_ffn_Ws': _L1_ffn_in['Ws'], 'L1_ffn_bs': _L1_ffn_in['bs'], 'L1_ffn_W1': _L1_ffn_in['W1'], 'L1_ffn_b1': _L1_ffn_in['b1'], 'L1_ffn_W2': _L1_ffn_in['W2'], 'L1_ffn_b2': _L1_ffn_in['b2']}

def reference(x, ctx_1024, mask_BxS2_bf1, L0_attn_W_in, L0_attn_conv_w, L0_attn_conv_b, L0_attn_W_x, L0_attn_W_dt, L0_attn_b_dt, L0_attn_A_log, L0_attn_D_param, L0_attn_W_out, L0_attn_ln_g, L0_attn_ln_b, L0_xattn_Wv, L0_xattn_Wk, L0_xattn_Wq, L0_xattn_Wo, L0_xattn_bo, L0_ffn_Wr, L0_ffn_br, L0_ffn_W1, L0_ffn_b1, L0_ffn_W2, L0_ffn_b2, L1_attn_Wk, L1_attn_bk, L1_attn_Wq, L1_attn_bq, L1_attn_Wv, L1_attn_bv, L1_attn_Wbeta, L1_attn_bbeta, L1_attn_conv_k, L1_attn_conv_q, L1_attn_conv_v, L1_attn_rms_w, L1_attn_Wout, L1_attn_bout, L1_xattn_Wq, L1_xattn_Wk, L1_xattn_Wv, L1_xattn_Wk_ip, L1_xattn_Wv_ip, L1_xattn_Wk_ap, L1_xattn_Wv_ap, L1_xattn_Wo, L1_xattn_bo, L1_xattn_rel_k, L1_xattn_rel_v, L1_xattn_alpha, L1_xattn_beta, L1_ffn_Ws, L1_ffn_bs, L1_ffn_W1, L1_ffn_b1, L1_ffn_W2, L1_ffn_b2):
    import jax
    import jax.numpy as jnp

    def _L0_attn_ref(x, W_in, conv_w, conv_b, W_x, W_dt, b_dt, A_log, D_param, W_out, ln_g, ln_b):
        import jax, jax.numpy as jnp
        import numpy as np
        from jax import lax
        D_MODEL, D_STATE, D_CONV, EXPAND = (128, 16, 4, 2)
        D_INNER = D_MODEL * EXPAND
        LN_EPS = 1e-05

        def _silu(v):
            return v * jax.nn.sigmoid(v)

        def _forward(x, W_in, conv_w, conv_b, W_x, W_dt, b_dt, A_log, D_param, W_out, ln_g, ln_b):
            B, T, _ = x.shape
            xz = jnp.einsum('btd,ed->bte', x, W_in)
            xp, z = (xz[..., :D_INNER], xz[..., D_INNER:])
            xc = lax.conv_general_dilated(jnp.transpose(xp, (0, 2, 1)), conv_w, window_strides=(1,), padding=[(D_CONV - 1, 0)], feature_group_count=D_INNER, dimension_numbers=('NCH', 'OIH', 'NCH')) + conv_b[None, :, None]
            xc = _silu(jnp.transpose(xc, (0, 2, 1)))
            ssm = jnp.einsum('bti,si->bts', xc, W_x)
            Bp, Cp = (ssm[..., :D_STATE], ssm[..., D_STATE:])
            dt = jax.nn.softplus(jnp.einsum('bti,oi->bto', xc, W_dt) + b_dt)
            A = -jnp.exp(A_log)

            def step(h, inp):
                x_t, b_t, c_t, dt_t = inp
                dA = jnp.exp(dt_t[..., None] * A)
                h = dA * h + dt_t[..., None] * b_t[:, None, :] * x_t[..., None]
                y_t = jnp.einsum('bds,bs->bd', h, c_t)
                return (h, y_t)
            h0 = jnp.zeros((B, D_INNER, D_STATE), dtype=x.dtype)
            tm = lambda a: jnp.moveaxis(a, 1, 0)
            _, ys = lax.scan(step, h0, (tm(xc), tm(Bp), tm(Cp), tm(dt)))
            y = jnp.moveaxis(ys, 0, 1)
            mu = jnp.mean(y, axis=-1, keepdims=True)
            var = jnp.mean((y - mu) ** 2, axis=-1, keepdims=True)
            y = (y - mu) * lax.rsqrt(var + LN_EPS) * ln_g + ln_b
            y = y + xc * D_param
            y = y * _silu(z)
            return jnp.einsum('bti,di->btd', y, W_out)
        return _forward(x, W_in, conv_w, conv_b, W_x, W_dt, b_dt, A_log, D_param, W_out, ln_g, ln_b)

    def _L0_xattn_ref(values, keys, queries, mask, Wv, Wk, Wq, Wo, bo):
        import jax, jax.numpy as jnp
        import numpy as np
        EMB = 128
        HEADS = 16
        HEAD_DIM = EMB // HEADS
        SM_SCALE = 1.0
        NEG_INF = -1000000000.0
        N, Lq, E = queries.shape
        Lk = keys.shape[1]
        v = values.reshape(N, Lk, HEADS, HEAD_DIM)
        k = keys.reshape(N, Lk, HEADS, HEAD_DIM)
        q = queries.reshape(N, Lq, HEADS, HEAD_DIM)
        q = q @ Wq.T
        k = k @ Wk.T
        v = v @ Wv.T
        scores = jnp.einsum('nqhd,nkhd->nhqk', q, k) * SM_SCALE
        causal = jnp.tril(jnp.ones((Lq, Lk), dtype=jnp.bool_))
        scores = jnp.where(causal[None, None, :, :], scores, NEG_INF)
        attn = jax.nn.softmax(scores, axis=-1)
        out = jnp.einsum('nhqk,nkhd->nqhd', attn, v)
        out = out.reshape(N, Lq, E)
        return out @ Wo.T + bo

    def _L0_ffn_ref(x, Wr, br, W1, b1, W2, b2):
        import jax, jax.numpy as jnp
        import numpy as np
        D_MODEL = 128
        D_FF = 512
        NUM_EXPERTS = 8
        B, N = (16, 128)
        scores = jnp.einsum('bh,he->be', x.mean(axis=1), Wr) + br
        top1 = jnp.argmax(scores, axis=-1)
        w1 = W1[top1]
        c1 = b1[top1]
        w2 = W2[top1]
        c2 = b2[top1]
        h = jax.nn.relu(jnp.einsum('bnh,bhf->bnf', x, w1) + c1[:, None, :])
        out = jnp.einsum('bnf,bfh->bnh', h, w2) + c2[:, None, :]
        return out

    def _L1_attn_ref(x, Wk, bk, Wq, bq, Wv, bv, Wbeta, bbeta, conv_k, conv_q, conv_v, rms_w, Wout, bout):
        import jax, jax.numpy as jnp
        from jax import lax
        import numpy as np
        CHUNK = 64

        def short_conv(x, w):
            L = x.shape[1]
            K = w.shape[1]
            xp = jnp.pad(x, ((0, 0), (K - 1, 0), (0, 0)))
            return sum((xp[:, j:j + L, :] * w[:, j] for j in range(K)))

        def o2b_weighted_delta_rule(k, q, v, b):
            B, L, H, D = k.shape
            C = CHUNK
            Nc = L // C

            def to_chunks(t):
                return t.transpose(0, 2, 1, 3).reshape(B, H, Nc, C, D).transpose(2, 0, 1, 3, 4)
            Kc, Qc, Vc, Bc = map(to_chunks, (k, q, v, b))
            eyeC = jnp.eye(C, dtype=jnp.float32)
            W0 = jnp.zeros((B, H, D, D), jnp.float32)
            Cf = float(C)

            def step(carry, xs):
                W_t, W_avg = carry
                i, Ki, Qi, Vi, Bi = xs
                KiT = jnp.swapaxes(Ki, -1, -2)
                T = jnp.tril(Bi @ KiT, k=-1)
                inv = jnp.linalg.inv(eyeC + T)
                Ui = inv @ (Vi - Bi @ W_t)
                W_new = W_t + KiT @ Ui
                ts = (i * C).astype(jnp.float32)
                idx = jnp.arange(1, C + 1, dtype=jnp.float32) + ts
                cs = jnp.cumsum(idx)
                weighted_idx = idx + idx.sum() - cs
                w_i = (weighted_idx / ((1 + ts + Cf) * (ts + Cf) / 2))[:, None]
                coef1 = ts / (ts + Cf) * ((1 + ts) / (1 + ts + Cf))
                coef2 = Cf / (ts + Cf) * ((ts * 2 + 1 + Cf) / (1 + ts + Cf))
                W_avg_new = coef1 * W_avg + coef2 * W_t + KiT @ (Ui * w_i)
                tri0 = (1 + ts) * ts / 2
                a = (tri0 / (tri0 + cs))[:, None]
                c = 1.0 - a
                r = cs[:, None]
                j_idx = (cs - idx)[None, :]
                T_mat = jnp.where(r >= j_idx, (r - j_idx) / (tri0 + r), 0.0)
                O_i = Qi @ W_avg * a + Qi @ W_t * c + T_mat * (Qi @ KiT) @ Ui
                return ((W_new, W_avg_new), O_i)
            (_, _), O = lax.scan(step, (W0, W0), (jnp.arange(Nc), Kc, Qc, Vc, Bc))
            return O.transpose(1, 2, 0, 3, 4).reshape(B, H, L, D).transpose(0, 2, 1, 3)
        B, L, Dm = x.shape
        H = Wbeta.shape[0]
        Dh = Dm // H
        k = short_conv(x @ Wk.T + bk, conv_k)
        q = short_conv(x @ Wq.T + bq, conv_q)
        v = short_conv(x @ Wv.T + bv, conv_v)
        beta = jax.nn.sigmoid(x @ Wbeta.T + bbeta)
        k = k.reshape(B, L, H, Dh)
        q = q.reshape(B, L, H, Dh)
        v = jax.nn.silu(v.reshape(B, L, H, Dh))
        knorm = jnp.linalg.norm(k, axis=-1, keepdims=True)
        qnorm = jnp.linalg.norm(q, axis=-1, keepdims=True)
        k = k / (knorm + 1e-06)
        q = q / (qnorm + 1e-06)
        eta = beta
        b = eta[..., None] * k
        v = eta[..., None] * v
        o = o2b_weighted_delta_rule(k, q, v, b)
        o = o * jax.lax.rsqrt(jnp.mean(o * o, axis=-1, keepdims=True) + 1e-06) * rms_w
        o = o.reshape(B, L, Dm)
        return o @ Wout.T + bout

    def _L1_xattn_ref(x, context, Wq, Wk, Wv, Wk_ip, Wv_ip, Wk_ap, Wv_ap, Wo, bo, rel_k, rel_v, alpha, beta):
        import jax, jax.numpy as jnp
        import numpy as np
        H = 16
        D = 64
        SCALE = D ** (-0.5)
        TEXT = 77
        IMG = 16
        AUD = 32
        MAXREL = 16
        B, NQ, QD = (32, 128, 128)
        INNER = H * D

        def _heads(t):
            return t.reshape(t.shape[0], t.shape[1], H, D)
        b, nq, _ = x.shape
        q = _heads(x @ Wq)
        ctx_t = context[:, :TEXT]
        ctx_i = context[:, TEXT:TEXT + IMG]
        ctx_a = context[:, TEXT + IMG:]
        k = _heads(ctx_t @ Wk)
        v = _heads(ctx_t @ Wv)
        sim = jnp.einsum('bihd,bjhd->bhij', q, k) * SCALE
        dist = jnp.clip(jnp.arange(TEXT)[None, :] - jnp.arange(nq)[:, None], -MAXREL, MAXREL) + MAXREL
        k2 = rel_k[dist]
        sim = sim + jnp.einsum('bihd,ijd->bhij', q, k2) * SCALE
        attn = jax.nn.softmax(sim, axis=-1)
        out = jnp.einsum('bhij,bjhd->bihd', attn, v)
        out = out + jnp.einsum('bhij,ijd->bihd', attn, rel_v[dist])

        def stream(W_k, W_v, ctx):
            kh = _heads(ctx @ W_k)
            vh = _heads(ctx @ W_v)
            a = jax.nn.softmax(jnp.einsum('bihd,bjhd->bhij', q, kh) * SCALE, axis=-1)
            return jnp.einsum('bhij,bjhd->bihd', a, vh)
        out = out + stream(Wk_ip, Wv_ip, ctx_i) * (jnp.tanh(alpha) + 1.0)
        out = out + stream(Wk_ap, Wv_ap, ctx_a) * (jnp.tanh(beta) + 1.0)
        out = out.reshape(b, nq, INNER)
        return out @ Wo + bo

    def _L1_ffn_ref(x, Ws, bs, W1, b1, W2, b2):
        import jax, jax.numpy as jnp
        import numpy as np
        CAPACITY_FACTOR = 1.0
        B, S, D = x.shape
        E = Ws.shape[1]
        N = B * S
        k = int(CAPACITY_FACTOR * N / E)
        xf = x.reshape(N, D)
        route_prob = jax.nn.softmax(xf @ Ws + bs, axis=-1).T
        route_vals, routes = jax.lax.top_k(route_prob, k)
        xin = xf[routes]
        h = jax.nn.gelu(jnp.einsum('ekd,edf->ekf', xin, W1) + b1[:, None, :])
        out = jnp.einsum('ekf,efd->ekd', h, W2) + b2[:, None, :]
        out = out * route_vals[..., None]
        final = jnp.zeros((N, D), dtype=x.dtype).at[routes.reshape(-1)].add(out.reshape(-1, D))
        return final.reshape(B, S, D)
    x = _layernorm(x + _L0_attn_ref(x, L0_attn_W_in, L0_attn_conv_w, L0_attn_conv_b, L0_attn_W_x, L0_attn_W_dt, L0_attn_b_dt, L0_attn_A_log, L0_attn_D_param, L0_attn_W_out, L0_attn_ln_g, L0_attn_ln_b), axis=-1)
    x = _layernorm(x + _L0_xattn_ref(ctx_1024, ctx_1024, x, mask_BxS2_bf1, L0_xattn_Wv, L0_xattn_Wk, L0_xattn_Wq, L0_xattn_Wo, L0_xattn_bo), axis=-1)
    x = _layernorm(x + _L0_ffn_ref(x, L0_ffn_Wr, L0_ffn_br, L0_ffn_W1, L0_ffn_b1, L0_ffn_W2, L0_ffn_b2), axis=-1)
    x = _layernorm(x + _L1_attn_ref(x, L1_attn_Wk, L1_attn_bk, L1_attn_Wq, L1_attn_bq, L1_attn_Wv, L1_attn_bv, L1_attn_Wbeta, L1_attn_bbeta, L1_attn_conv_k, L1_attn_conv_q, L1_attn_conv_v, L1_attn_rms_w, L1_attn_Wout, L1_attn_bout), axis=-1)
    x = _layernorm(x + _L1_xattn_ref(x, ctx_1024, L1_xattn_Wq, L1_xattn_Wk, L1_xattn_Wv, L1_xattn_Wk_ip, L1_xattn_Wv_ip, L1_xattn_Wk_ap, L1_xattn_Wv_ap, L1_xattn_Wo, L1_xattn_bo, L1_xattn_rel_k, L1_xattn_rel_v, L1_xattn_alpha, L1_xattn_beta), axis=-1)
    x = _layernorm(x + _L1_ffn_ref(x, L1_ffn_Ws, L1_ffn_bs, L1_ffn_W1, L1_ffn_b1, L1_ffn_W2, L1_ffn_b2), axis=-1)
    return x

_drawn_inputs = setup_inputs


def setup_inputs(seed=0):
    import zlib

    import numpy as np

    out = dict(_drawn_inputs(seed))
    spreads = {'L0_attn_D_param': (1.0, 0.2),
     'L0_attn_ln_g': (1.0, 0.2),
     'L0_attn_ln_b': (0.0, 0.1),
     'L1_attn_bk': (0.0, 0.1),
     'L1_attn_bq': (0.0, 0.1),
     'L1_attn_bv': (0.0, 0.1),
     'L1_attn_bbeta': (0.0, 0.532),
     'L1_attn_rms_w': (1.0, 0.2),
     'L1_attn_bout': (0.0, 0.1),
     'L1_xattn_bo': (0.0, 0.1),
     'L1_ffn_bs': (0.0, 0.1),
     'L1_ffn_b1': (0.0, 0.32),
     'L1_ffn_b2': (0.0, 0.1)}
    factors = {'L0_xattn_bo': 4.227,
     'L1_xattn_Wq': 6.32,
     'L1_xattn_Wk': 8.0,
     'L1_xattn_Wk_ip': 8.0,
     'L1_xattn_Wk_ap': 8.0,
     'L1_xattn_rel_k': 50.137,
     'L1_xattn_rel_v': 3.251}
    for name, (base, spread) in spreads.items():
        noise = np.random.default_rng([zlib.crc32(name.encode()), seed]).standard_normal(out[name].shape)
        drawn = base * np.exp(spread * noise) if base else spread * noise
        out[name] = jnp.asarray(drawn.astype(out[name].dtype))
    for name, factor in factors.items():
        out[name] = (out[name] * factor).astype(out[name].dtype)
    return out
```

```python
from contextlib import ExitStack

import concourse.bass as bass
from concourse import mybir

F32 = mybir.dt.float32
BF16 = mybir.dt.bfloat16
U32 = mybir.dt.uint32
I32 = mybir.dt.int32
ALU = mybir.AluOpType
ACT = mybir.ActivationFunctionType
AX = mybir.AxisListType.X

P = 128
B = 16
S = 256
D = 128
TT = S // P
CTX = 1601
LN_EPS = 1e-5
NEG = -1e30


class Scope:

    def __init__(self, nc, stack, tag):
        self.nc, self.stack, self.tag, self.sems = nc, stack, tag, []

    def sb(self, name, shape, dt=F32):
        return self.stack.enter_context(self.nc.sbuf_tensor(f"{self.tag}_{name}", shape, dt))

    def ps(self, name, shape, dt=F32):
        return self.stack.enter_context(self.nc.psum_tensor(f"{self.tag}_{name}", shape, dt))

    def sem(self, name):
        sem = self.stack.enter_context(self.nc.semaphore(f"{self.tag}_{name}"))
        self.sems.append(sem)
        return sem

    def block(self):
        self.stack.callback(self.clear)
        return self.stack.enter_context(self.nc.Block())

    def clear(self):
        with self.nc.Block() as block:
            @block.gpsimd
            def _(pool):
                for sem in self.sems:
                    pool.sem_clear(sem)


class Chain:

    def __init__(self, eng, sem):
        self.eng, self.sem, self.n = eng, sem, 0

    def restart(self):
        self.eng.sem_clear(self.sem)
        self.n = 0

    def link(self, ins):
        self.count(ins)
        self.settle()

    def count(self, ins):
        self.n += 1
        ins.then_inc(self.sem, 1)

    def settle(self):
        self.eng.wait_ge(self.sem, self.n)


def hold(eng, sem, value):
    eng.wait_ge(sem, value)
    eng.nop(nofuse=True)


def bc(ap, axis, n):
    v = ap.unsqueeze(axis)
    return v.broadcast_to([*v.shape[:axis], n, *v.shape[axis + 1:]])


def constants(nc, stack):
    c = Scope(nc, stack, "const")
    ident = c.sb("ident", [P, P])
    ident16 = c.sb("ident16", [P, P], BF16)
    causal16 = c.sb("causal16", [P, P], BF16)
    ones = c.sb("ones", [P, P])
    eps = c.sb("eps", [P, 1])
    with ExitStack() as own:
        fill = Scope(nc, own, "fill")
        filled = fill.sem("filled")
        block = fill.block()

        @block.gpsimd
        def _(pool):
            nc.gpsimd.memset(ident[:, :], 0.0).then_inc(filled, 1)
            nc.gpsimd.memset(ident16[:, :], 0.0).then_inc(filled, 1)
            nc.gpsimd.memset(causal16[:, :], 0.0).then_inc(filled, 1)
            nc.gpsimd.memset(ones[:, :], 1.0).then_inc(filled, 1)
            nc.gpsimd.memset(eps[:, :], LN_EPS).then_inc(filled, 1)
            pool.wait_ge(filled, 5)
            for m in (ident, ident16):
                nc.gpsimd.affine_select(out=m[:, :], in_=m[:, :], compare_op=ALU.not_equal, fill=1.0,
                                        base=0, pattern=[[-1, P]], channel_multiplier=1).then_inc(filled, 1)
            nc.gpsimd.affine_select(out=causal16[:, :], in_=causal16[:, :], compare_op=ALU.is_ge, fill=NEG,
                                    base=0, pattern=[[-1, P]], channel_multiplier=1).then_inc(filled, 1)
            pool.wait_ge(filled, 8)

    return ident, ident16, causal16, ones, eps


def layernorm(nc, dve, own, r, stats, mv, rs, out, b, ln_stats, ln_rs, ready, stored, tiles=TT, step=16):
    for t in range(tiles):
        own.count(nc.vector.bn_stats(stats[:, t, :], r[:, t, :]))
    own.settle()
    for t in range(tiles):
        ins = nc.vector.bn_aggr(mv[:, t, :], stats[:, t, :])
        if t < tiles - 1:
            own.count(ins)
    ins.then_inc(ln_stats, 1)
    dve.wait_ge(ln_stats, b + 1)
    dve.wait_ge(stored, step * b)
    dve.wait_ge(ln_rs, b + 1)
    for t in range(tiles):
        ins = nc.vector.tensor_scalar(out[:, t, :], r[:, t, :], mv[:, t, 0:1], rs[:, t:t + 1], ALU.subtract, ALU.mult)
        if t < tiles - 1:
            own.count(ins)
    ins.then_inc(ready, 1)


DI = 256
HALF = DI // P
NS = 16
TAPS = 4
SG = 2
GROUPS = NS // SG


def scan_stage(nc, T, const):
    ident, ident16, causal16, ones, eps = const
    with ExitStack() as stack:
        c = Scope(nc, stack, "scan")
        w_in = c.sb("w_in", [P, 2 * DI])
        w_x = c.sb("w_x", [P, HALF, 2 * NS])
        w_dt = c.sb("w_dt", [P, HALF, DI])
        w_out = c.sb("w_out", [P, HALF, D])
        conv_w = c.sb("conv_w", [P, HALF, TAPS])
        vec = c.sb("vec", [P, 5, HALF])
        a_neg = c.sb("a_neg", [P, NS])
        pick = c.sb("pick", [2 * NS, 2 * NS, P])
        mean_w = c.sb("mean_w", [P, P])
        x = c.sb("x", [P, TT, D])
        xT = c.sb("xT", [P, S])
        xp = c.sb("xp", [P, HALF, TAPS - 1 + S])
        conv = c.sb("conv", [P, HALF, S])
        sig = c.sb("sig", [P, HALF, S])
        gate = c.sb("gate", [P, HALF, S])
        gsig = c.sb("gsig", [P, HALF, S])
        xc = c.sb("xc", [P, HALF, S])
        bcT = c.sb("bcT", [2 * NS, S])
        dt = c.sb("dt", [P, HALF, S])
        dabs = c.sb("dabs", [P, HALF, S])
        u = c.sb("u", [P, HALF, S])
        decay = c.sb("decay", [P, 2, SG, HALF, S])
        drive = c.sb("drive", [P, 2, SG, HALF, S])
        h = c.sb("h", [P, 2, SG, HALF, S])
        hc = c.sb("hc", [P, 2, SG, HALF, S])
        y2 = c.sb("y2", [P, SG, HALF, S])
        y = c.sb("y", [P, HALF, S])
        sq = c.sb("sq", [P, HALF, S])
        rstd = c.sb("rstd", [P, S])
        r = c.sb("r", [P, TT, D])
        stats = c.sb("stats", [P, TT, 6])
        mv = c.sb("mv", [P, TT, 2])
        rs = c.sb("rs", [P, TT])
        x1 = c.sb("x1", [P, TT, D])
        ps_t = c.ps("ps_t", [P, 512])
        ps_x = c.ps("ps_x", [P, HALF, S])
        ps_z = c.ps("ps_z", [P, HALF, S])
        ps_v = c.ps("ps_v", [P, HALF, S])
        ps_b = [c.ps(f"ps_b{i}", [P, SG, S]) for i in range(2)]
        ps_c = [c.ps(f"ps_c{i}", [P, SG, S]) for i in range(2)]

        weights_in = c.sem("weights_in")
        consts_ready = c.sem("consts_ready")
        a_ready = c.sem("a_ready")
        x_in = c.sem("x_in")
        xT_ps = c.sem("xT_ps")
        xT_sb = c.sem("xT_sb")
        xz_ps = c.sem("xz_ps")
        xp_sb = c.sem("xp_sb")
        z_exp = c.sem("z_exp")
        conv_ready = c.sem("conv_ready")
        conv_exp = c.sem("conv_exp")
        xc_ready = c.sem("xc_ready")
        ssm_ps = c.sem("ssm_ps")
        v_ps = c.sem("v_ps")
        bc_sb = c.sem("bc_sb")
        dlog = c.sem("dlog")
        dt_ready = c.sem("dt_ready")
        u_ready = c.sem("u_ready")
        decay_exp = c.sem("decay_exp")
        decay_cut = c.sem("decay_cut")
        b_ps = c.sem("b_ps")
        c_ps = c.sem("c_ps")
        driven = c.sem("driven")
        scanned = c.sem("scanned")
        hc_ready = c.sem("hc_ready")
        summed = c.sem("summed")
        y_ready = c.sem("y_ready")
        mean_ps = c.sem("mean_ps")
        centred = c.sem("centred")
        squared = c.sem("squared")
        var_ps = c.sem("var_ps")
        rstd_ready = c.sem("rstd_ready")
        gated = c.sem("gated")
        gate_ready = c.sem("gate_ready")
        out_ps = c.sem("out_ps")
        out_read = c.sem("out_read")
        ln_stats = c.sem("ln_stats")
        ln_rs = c.sem("ln_rs")
        x1_ready = c.sem("x1_ready")
        stored = c.sem("stored")
        dve_own = c.sem("dve_own")
        act_own = c.sem("act_own")
        block = c.block()

        @block.sync
        def _(sp):
            loads = [(w_in[:, :], T["w_in"]), (w_x[:, :, :], T["w_x"]), (w_dt[:, :, :], T["w_dt"]),
                     (w_out[:, :, :], T["w_out"]), (conv_w[:, :, :], T["conv_w"]), (vec[:, :, :], T["scan_vec"]),
                     (a_neg[:, :], T["a_log"])]
            for dst, src in loads:
                sp.dma_start(dst, src).then_inc(weights_in, 16)
            with sp.Fori(0, B) as b:
                sp.wait_ge(out_read, b)
                sp.dma_start(x[:, :, :], T["x"][b].rearrange("(t p) d -> p t d", p=P)).then_inc(x_in, 16)
                sp.wait_ge(x1_ready, b + 1)
                sp.dma_start(T["x1"][b].rearrange("(t p) d -> p t d", p=P), x1[:, :, :]).then_inc(stored, 16)
            sp.wait_ge(stored, 16 * B)

        @block.gpsimd
        def _(pool):
            nc.gpsimd.memset(pick[:, :, :], 0.0).then_inc(consts_ready, 1)
            nc.gpsimd.memset(xp[:, :, :], 0.0).then_inc(consts_ready, 1)
            nc.gpsimd.memset(mean_w[:, :], 1.0 / DI).then_inc(consts_ready, 1)
            pool.wait_ge(consts_ready, 3)
            nc.gpsimd.affine_select(out=pick[:, :, :], in_=pick[:, :, :], compare_op=ALU.not_equal, fill=1.0,
                                    base=0, pattern=[[-1, 2 * NS], [0, P]], channel_multiplier=1)\
                .then_inc(consts_ready, 1)
            with pool.Fori(0, B) as b:
                pool.wait_ge(dt_ready, b + 1)
                nc.gpsimd.tensor_tensor(u[:, :, :], dt[:, :, :], xc[:, :, :], ALU.mult).then_inc(u_ready, 1)

                def add_states(g):
                    pool.wait_ge(y_ready, b) if g == 0 else pool.wait_ge(summed, b * GROUPS + g)
                    hold(pool, hc_ready, b * GROUPS + g + 1)
                    if g == 0:
                        nc.gpsimd.tensor_copy(y2[:, :, :, :], hc[:, 0, :, :, :]).then_inc(summed, 1)
                    else:
                        nc.gpsimd.tensor_tensor(y2[:, :, :, :], y2[:, :, :, :], hc[:, g % 2, :, :, :], ALU.add)\
                            .then_inc(summed, 1)

                for g in range(GROUPS):
                    hold(pool, decay_exp, b * NS + SG * (g + 1))
                    nc.gpsimd.memset(decay[:, g % 2, :, :, 0:1], 0.0).then_inc(decay_cut, 1)
                    if g >= 1:
                        add_states(g - 1)
                add_states(GROUPS - 1)
                pool.wait_ge(summed, (b + 1) * GROUPS)
                nc.gpsimd.tensor_tensor(y[:, :, :], y2[:, 0, :, :], y2[:, 1, :, :], ALU.add).then_inc(y_ready, 1)

        @block.scalar
        def _(act):
            own = Chain(act, act_own)
            act.wait_ge(weights_in, 16 * 7)
            own.link(nc.scalar.activation(a_neg[:, :], a_neg[:, :], ACT.Exp))
            nc.scalar.activation(a_neg[:, :], a_neg[:, :], ACT.Copy, scale=-1.0).then_inc(a_ready, 1)
            act.wait_ge(a_ready, 1)
            with act.Fori(0, B) as b:
                own.restart()
                act.wait_ge(xz_ps, 2 * b)
                act.wait_ge(xT_ps, b + 1)
                nc.scalar.activation(xT[:, :], ps_t[:, 0:S], ACT.Copy).then_inc(xT_sb, 1)
                act.wait_ge(conv_ready, b)
                act.wait_ge(xz_ps, 2 * b + 1)
                nc.scalar.activation(xp[:, :, TAPS - 1:], ps_x[:, :, :], ACT.Copy).then_inc(xp_sb, 1)
                act.wait_ge(gate_ready, b)
                act.wait_ge(xz_ps, 2 * b + 2)
                nc.scalar.activation(gsig[:, :, :], ps_z[:, :, :], ACT.Exp, scale=-1.0).then_inc(z_exp, 1)
                act.wait_ge(conv_ready, b + 1)
                nc.scalar.activation(sig[:, :, :], conv[:, :, :], ACT.Exp, scale=-1.0).then_inc(conv_exp, 1)
                act.wait_ge(ssm_ps, b + 1)
                nc.scalar.activation(bcT[:, :], ps_t[0:2 * NS, S:2 * S], ACT.Copy).then_inc(bc_sb, 1)
                act.wait_ge(dt_ready, b)
                act.wait_ge(v_ps, b + 1)
                for m in range(HALF):
                    own.count(nc.scalar.activation(dabs[:, m, :], ps_v[:, m, :], ACT.Abs, bias=vec[:, 1, m:m + 1]))
                own.settle()
                own.link(nc.scalar.activation(dabs[:, :, :], dabs[:, :, :], ACT.Exp, scale=-1.0))
                nc.scalar.activation(dabs[:, :, :], dabs[:, :, :], ACT.Ln, bias=ones[:, 0:1]).then_inc(dlog, 1)
                act.wait_ge(dt_ready, b + 1)
                for g in range(GROUPS):
                    act.wait_ge(scanned, b * GROUPS + max(g - 1, 0))
                    for i in range(SG):
                        s = g * SG + i
                        nc.scalar.activation(decay[:, g % 2, i, :, :], dt[:, :, :], ACT.Exp,
                                             scale=a_neg[:, s:s + 1]).then_inc(decay_exp, 1)
                act.wait_ge(centred, b + 1)
                nc.scalar.activation(sq[:, :, :], y[:, :, :], ACT.Square).then_inc(squared, 1)
                act.wait_ge(var_ps, b + 1)
                own.link(nc.scalar.activation(rstd[:, :], ps_t[:, S:2 * S], ACT.Ln, bias=eps[:, 0:1]))
                nc.scalar.activation(rstd[:, :], rstd[:, :], ACT.Exp, scale=-0.5).then_inc(rstd_ready, 1)
                act.wait_ge(ln_stats, b + 1)
                own.link(nc.scalar.activation(rs[:, :], mv[:, :, 1], ACT.Ln, bias=eps[:, 0:1]))
                nc.scalar.activation(rs[:, :], rs[:, :], ACT.Exp, scale=-0.5).then_inc(ln_rs, 1)
                own.settle()

        @block.tensor
        def _(pe):
            pe.wait_ge(weights_in, 16 * 7)
            pe.wait_ge(consts_ready, 4)
            with pe.Fori(0, B) as b:
                pe.wait_ge(out_read, b)
                pe.wait_ge(x_in, 16 * (b + 1))
                for t in range(TT):
                    mm = nc.tensor.transpose(ps_t[:, t * P:(t + 1) * P], x[:, t, :], ident[:, :])
                mm.then_inc(xT_ps, 1)
                pe.wait_ge(xT_sb, b + 1)
                pe.wait_ge(xp_sb, b)
                for m in range(HALF):
                    mm = nc.tensor.matmul(ps_x[:, m, :], w_in[:, m * P:(m + 1) * P], xT[:, :], start=True, stop=True)
                mm.then_inc(xz_ps, 1)
                pe.wait_ge(gate_ready, b)
                for m in range(HALF):
                    mm = nc.tensor.matmul(ps_z[:, m, :], w_in[:, DI + m * P:DI + (m + 1) * P], xT[:, :],
                                          start=True, stop=True)
                mm.then_inc(xz_ps, 1)
                pe.wait_ge(xc_ready, b + 1)
                for m in range(HALF):
                    mm = nc.tensor.matmul(ps_t[0:2 * NS, S:2 * S], w_x[:, m, :], xc[:, m, :],
                                          start=(m == 0), stop=(m == HALF - 1))
                mm.then_inc(ssm_ps, 1)
                pe.wait_ge(dt_ready, b)
                for o in range(HALF):
                    for m in range(HALF):
                        mm = nc.tensor.matmul(ps_v[:, o, :], w_dt[:, m, o * P:(o + 1) * P], xc[:, m, :],
                                              start=(m == 0), stop=(m == HALF - 1))
                mm.then_inc(v_ps, 1)
                pe.wait_ge(bc_sb, b + 1)
                for g in range(GROUPS):
                    pe.wait_ge(driven, b * GROUPS + max(g - 1, 0))
                    for i in range(SG):
                        mm = nc.tensor.matmul(ps_b[g % 2][:, i, :], pick[:, g * SG + i, :], bcT[:, :],
                                              start=True, stop=True)
                    mm.then_inc(b_ps, 1)
                    pe.wait_ge(hc_ready, b * GROUPS + max(g - 1, 0))
                    for i in range(SG):
                        mm = nc.tensor.matmul(ps_c[g % 2][:, i, :], pick[:, NS + g * SG + i, :], bcT[:, :],
                                              start=True, stop=True)
                    mm.then_inc(c_ps, 1)
                pe.wait_ge(y_ready, b + 1)
                for m in range(HALF):
                    mm = nc.tensor.matmul(ps_t[:, 0:S], mean_w[:, :], y[:, m, :], start=(m == 0), stop=(m == HALF - 1))
                mm.then_inc(mean_ps, 1)
                pe.wait_ge(squared, b + 1)
                for m in range(HALF):
                    mm = nc.tensor.matmul(ps_t[:, S:2 * S], mean_w[:, :], sq[:, m, :], start=(m == 0), stop=(m == HALF - 1))
                mm.then_inc(var_ps, 1)
                pe.wait_ge(gated, b + 1)
                for t in range(TT):
                    for m in range(HALF):
                        mm = nc.tensor.matmul(ps_t[:, t * P:(t + 1) * P], y[:, m, t * P:(t + 1) * P], w_out[:, m, :],
                                              start=(m == 0), stop=(m == HALF - 1))
                mm.then_inc(out_ps, 1)

        @block.vector
        def _(dve):
            own = Chain(dve, dve_own)
            dve.wait_ge(weights_in, 16 * 7)
            with dve.Fori(0, B) as b:
                own.restart()
                dve.wait_ge(xp_sb, b + 1)
                for k in range(TAPS):
                    for m in range(HALF):
                        if k == 0:
                            own.count(nc.vector.tensor_scalar(conv[:, m, :], xp[:, m, 0:S], conv_w[:, m, 0:1],
                                                              vec[:, 0, m:m + 1], ALU.mult, ALU.add))
                        else:
                            ins = nc.vector.scalar_tensor_tensor(
                                out=conv[:, m, :], in0=xp[:, m, k:k + S], scalar=conv_w[:, m, k:k + 1],
                                in1=conv[:, m, :], op0=ALU.mult, op1=ALU.add)
                            if (k, m) == (TAPS - 1, HALF - 1):
                                ins.then_inc(conv_ready, 1)
                            else:
                                own.count(ins)
                    own.settle()
                dve.wait_ge(z_exp, b + 1)
                own.link(nc.vector.tensor_scalar(gsig[:, :, :], gsig[:, :, :], 1.0, None, ALU.add))
                own.link(nc.vector.reciprocal(gsig[:, :, :], gsig[:, :, :]))
                nc.vector.tensor_tensor(gate[:, :, :], ps_z[:, :, :], gsig[:, :, :], ALU.mult).then_inc(gate_ready, 1)
                dve.wait_ge(conv_exp, b + 1)
                own.link(nc.vector.tensor_scalar(sig[:, :, :], sig[:, :, :], 1.0, None, ALU.add))
                own.link(nc.vector.reciprocal(sig[:, :, :], sig[:, :, :]))
                dve.wait_ge(conv_ready, b + 1)
                nc.vector.tensor_tensor(xc[:, :, :], conv[:, :, :], sig[:, :, :], ALU.mult).then_inc(xc_ready, 1)
                dve.wait_ge(dlog, b + 1)
                for m in range(HALF):
                    own.count(nc.vector.tensor_scalar(dt[:, m, :], ps_v[:, m, :], vec[:, 1, m:m + 1], 0.0, ALU.add, ALU.max))
                own.settle()
                nc.vector.tensor_tensor(dt[:, :, :], dt[:, :, :], dabs[:, :, :], ALU.add).then_inc(dt_ready, 1)
                dve.wait_ge(u_ready, b + 1)
                for g in range(GROUPS):
                    q = g % 2
                    dve.wait_ge(b_ps, b * GROUPS + g + 1)
                    nc.vector.tensor_tensor(drive[:, q, :, :, :], bc(u[:, :, :], 1, SG), bc(ps_b[q][:, :, :], 2, HALF),
                                            ALU.mult).then_inc(driven, 1)
                    dve.wait_ge(decay_cut, b * GROUPS + g + 1)
                    dve.wait_ge(driven, b * GROUPS + g + 1)
                    nc.vector.tensor_tensor_scan(h[:, q, :, :, :].rearrange("p a m t -> p (a m t)"),
                                                 decay[:, q, :, :, :].rearrange("p a m t -> p (a m t)"),
                                                 drive[:, q, :, :, :].rearrange("p a m t -> p (a m t)"),
                                                 0.0, ALU.mult, ALU.add).then_inc(scanned, 1)
                    dve.wait_ge(c_ps, b * GROUPS + g + 1)
                    dve.wait_ge(summed, b * GROUPS + max(g - 1, 0))
                    dve.wait_ge(scanned, b * GROUPS + g + 1)
                    nc.vector.tensor_tensor(hc[:, q, :, :, :], h[:, q, :, :, :], bc(ps_c[q][:, :, :], 2, HALF),
                                            ALU.mult).then_inc(hc_ready, 1)
                dve.wait_ge(mean_ps, b + 1)
                nc.vector.tensor_tensor(y[:, :, :], y[:, :, :], bc(ps_t[:, 0:S], 1, HALF), ALU.subtract)\
                    .then_inc(centred, 1)
                dve.wait_ge(squared, b + 1)
                dve.wait_ge(rstd_ready, b + 1)
                own.link(nc.vector.tensor_tensor(y[:, :, :], y[:, :, :], bc(rstd[:, :], 1, HALF), ALU.mult))
                for m in range(HALF):
                    own.count(nc.vector.tensor_scalar(y[:, m, :], y[:, m, :], vec[:, 3, m:m + 1], vec[:, 4, m:m + 1],
                                                      ALU.mult, ALU.add))
                own.settle()
                for m in range(HALF):
                    own.count(nc.vector.scalar_tensor_tensor(out=y[:, m, :], in0=xc[:, m, :], scalar=vec[:, 2, m:m + 1],
                                                             in1=y[:, m, :], op0=ALU.mult, op1=ALU.add))
                own.settle()
                nc.vector.tensor_tensor(y[:, :, :], y[:, :, :], gate[:, :, :], ALU.mult).then_inc(gated, 1)
                dve.wait_ge(out_ps, b + 1)
                nc.vector.tensor_tensor(r[:, :, :], x[:, :, :], ps_t[:, 0:S].rearrange("p (t d) -> p t d", t=TT),
                                        ALU.add).then_inc(out_read, 1)
                dve.wait_ge(out_read, b + 1)
                layernorm(nc, dve, own, r, stats, mv, rs, x1, b, ln_stats, ln_rs, x1_ready, stored)
                own.settle()


AH = 16
AD = 8
JH = 4
GH = AH // JH
PASSES = ((0, (0, 1, 2, 3)), (1, (0, 1)), (1, (2, 3)))
FILLS = 4


def self_stage(nc, T, const):
    ident, ident16, causal16, ones, eps = const
    with ExitStack() as stack:
        c = Scope(nc, stack, "self")
        wq = c.sb("wq", [P, GH, P])
        wk = c.sb("wk", [P, GH, P])
        wv = c.sb("wv", [P, D])
        wo = c.sb("wo", [P, D])
        bo = c.sb("bo", [P, D])
        x = c.sb("x", [P, TT, D])
        cx = c.sb("cx", [P, TT, D])
        xcT = c.sb("xcT", [P, 2, S])
        qT = c.sb("qT", [P, GH, S])
        kT = c.sb("kT", [P, GH, S])
        v = c.sb("v", [P, TT, D])
        negmax = c.sb("negmax", [P, AH])
        sums = c.sb("sums", [P, TT, JH, GH])
        prob = c.sb("prob", [P, 16, P])
        probT = c.sb("probT", [P, 16, P])
        rsum = c.sb("rsum", [P, TT, JH, GH])
        o = c.sb("o", [P, TT, D])
        oT = c.sb("oT", [P, S])
        r = c.sb("r", [P, TT, D])
        stats = c.sb("stats", [P, TT, 6])
        mv = c.sb("mv", [P, TT, 2])
        rs = c.sb("rs", [P, TT])
        x2 = c.sb("x2", [P, TT, D])
        ps_s = c.ps("ps_s", [P, JH, 512])
        ps_t = [c.ps(f"ps_t{i}", [P, 4, P]) for i in range(2)]
        ps_o = c.ps("ps_o", [P, TT, D])
        ps_m = c.ps("ps_m", [P, 4, P])

        weights_in = c.sem("weights_in")
        x_in = c.sem("x_in")
        xcT_ps = c.sem("xcT_ps")
        xcT_sb = c.sem("xcT_sb")
        proj_ps = c.sem("proj_ps")
        q_sb = c.sem("q_sb")
        k_sb = c.sem("k_sb")
        v_sb = c.sem("v_sb")
        scores = c.sem("scores")
        maxed = c.sem("maxed")
        exps = c.sem("exps")
        blocks_ps = c.sem("blocks_ps")
        blocks_sb = c.sem("blocks_sb")
        pv = c.sem("pv")
        normed = c.sem("normed")
        oT_ps = c.sem("oT_ps")
        oT_sb = c.sem("oT_sb")
        out_ps = c.sem("out_ps")
        out_read = c.sem("out_read")
        ln_stats = c.sem("ln_stats")
        ln_rs = c.sem("ln_rs")
        x2_ready = c.sem("x2_ready")
        stored = c.sem("stored")
        dve_own = c.sem("dve_own")
        act_own = c.sem("act_own")
        block = c.block()
        NP = len(PASSES)
        last = {0: 1, 1: 3}

        @block.sync
        def _(sp):
            for dst, src in ((wq[:, :, :], T["wq_pad"]), (wk[:, :, :], T["wk_pad"]), (wv[:, :], T["wv_bd"]),
                             (wo[:, :], T["wo"]), (bo[:, :], T["bo"])):
                sp.dma_start(dst, src).then_inc(weights_in, 16)
            with sp.Fori(0, B) as b:
                sp.wait_ge(out_read, b)
                sp.dma_start(x[:, :, :], T["x1"][b].rearrange("(t p) d -> p t d", p=P)).then_inc(x_in, 16)
                sp.dma_start(cx[:, :, :], T["ctx"][b, 0:S].rearrange("(t p) d -> p t d", p=P)).then_inc(x_in, 16)
                sp.wait_ge(x2_ready, b + 1)
                sp.dma_start(T["x2"][b].rearrange("(t p) d -> p t d", p=P), x2[:, :, :]).then_inc(stored, 16)
            sp.wait_ge(stored, 16 * B)

        @block.tensor
        def _(pe):
            pe.wait_ge(weights_in, 16 * 5)
            with pe.Fori(0, B) as b:
                pe.wait_ge(out_read, b)
                pe.wait_ge(x_in, 32 * (b + 1))
                for i, src in enumerate((x, cx)):
                    for t in range(TT):
                        mm = nc.tensor.transpose(ps_m[:, 2 * i + t, :], src[:, t, :], ident[:, :])
                mm.then_inc(xcT_ps, 1)
                pe.wait_ge(xcT_sb, b + 1)
                for i, w in enumerate((wq, wk)):
                    for g in range(GH):
                        mm = nc.tensor.matmul(ps_s[:, 2 * i + g // 2, (g % 2) * S:(g % 2 + 1) * S], w[:, g, :],
                                              xcT[:, i, :], start=True, stop=True)
                for t in range(TT):
                    mm = nc.tensor.matmul(ps_m[:, t, :], xcT[:, 1, t * P:(t + 1) * P], wv[:, :], start=True, stop=True)
                mm.then_inc(proj_ps, 1)
                pe.wait_ge(q_sb, b + 1)
                pe.wait_ge(k_sb, b + 1)
                pe.wait_ge(v_sb, b + 1)
                for n, (qt, groups) in enumerate(PASSES):
                    nk = (qt + 1) * P
                    if n:
                        pe.wait_ge(exps, b * NP + n)
                    for j in range(JH):
                        rows = slice(32 * j, 32 * j + AD)
                        for i, g in enumerate(groups):
                            nc.tensor.matmul(ps_s[:, j, i * nk:(i + 1) * nk], qT[rows, g, qt * P:(qt + 1) * P],
                                             kT[rows, g, 0:nk], start=True, stop=False)
                            mm = nc.tensor.matmul(ps_s[:, j, (i + 1) * nk - P:(i + 1) * nk], ident16[:, :], causal16[:, :],
                                                  start=False, stop=True)
                    mm.then_inc(scores, 1)
                    pe.wait_ge(exps, b * NP + n + 1)
                    for f in range(FILLS):
                        k = n * FILLS + f
                        pe.wait_ge(blocks_sb, b * NP * FILLS + max(k - 1, 0))
                        for i in range(4):
                            mm = nc.tensor.transpose(ps_t[k % 2][:, i, :], prob[:, 4 * f + i, :], ident[:, :])
                        mm.then_inc(blocks_ps, 1)
                    if n == 0:
                        pe.wait_ge(normed, b * TT)
                    pe.wait_ge(blocks_sb, b * NP * FILLS + (n + 1) * FILLS)
                    for j in range(JH):
                        for i, g in enumerate(groups):
                            head = JH * g + j
                            for kb in range(qt + 1):
                                mm = nc.tensor.matmul(ps_o[:, qt, head * AD:(head + 1) * AD],
                                                      probT[:, (j * len(groups) + i) * (qt + 1) + kb, :],
                                                      v[:, kb, head * AD:(head + 1) * AD],
                                                      start=(kb == 0), stop=(kb == qt))
                    mm.then_inc(pv, 1)
                for t in range(TT):
                    pe.wait_ge(normed, b * TT + t + 1)
                    mm = nc.tensor.transpose(ps_m[:, t, :], o[:, t, :], ident[:, :])
                mm.then_inc(oT_ps, 1)
                pe.wait_ge(oT_sb, b + 1)
                for t in range(TT):
                    mm = nc.tensor.matmul(ps_m[:, 2 + t, :], oT[:, t * P:(t + 1) * P], wo[:, :], start=True, stop=True)
                mm.then_inc(out_ps, 1)

        @block.scalar
        def _(act):
            own = Chain(act, act_own)
            with act.Fori(0, B) as b:
                own.restart()
                act.wait_ge(proj_ps, b)
                act.wait_ge(xcT_ps, b + 1)
                nc.scalar.activation(xcT[:, :, :], ps_m[:, :, :].rearrange("p (a t) n -> p a (t n)", a=2), ACT.Copy)\
                    .then_inc(xcT_sb, 1)
                act.wait_ge(scores, b * NP)
                act.wait_ge(proj_ps, b + 1)
                nc.scalar.activation(qT[:, :, :], ps_s[:, 0:2, :].rearrange("p a (g n) -> p (a g) n", g=2), ACT.Copy)\
                    .then_inc(q_sb, 1)
                for n, (qt, groups) in enumerate(PASSES):
                    nk = (qt + 1) * P
                    act.wait_ge(maxed, b * NP + n + 1)
                    act.wait_ge(blocks_ps, (b * NP + n) * FILLS)
                    for j in range(JH):
                        for i, g in enumerate(groups):
                            a = j * len(groups) + i
                            ins = nc.scalar.activation(
                                prob[:, a * (qt + 1):(a + 1) * (qt + 1), :].rearrange("p a n -> p (a n)"),
                                ps_s[:, j, i * nk:(i + 1) * nk], ACT.Exp, bias=negmax[:, a:a + 1],
                                accum_out=sums[:, qt, j, g:g + 1])
                    ins.then_inc(exps, 1)
                act.wait_ge(oT_ps, b + 1)
                nc.scalar.activation(oT[:, :], ps_m[:, 0:TT, :].rearrange("p t n -> p (t n)"), ACT.Copy).then_inc(oT_sb, 1)
                act.wait_ge(ln_stats, b + 1)
                own.link(nc.scalar.activation(rs[:, :], mv[:, :, 1], ACT.Ln, bias=eps[:, 0:1]))
                nc.scalar.activation(rs[:, :], rs[:, :], ACT.Exp, scale=-0.5).then_inc(ln_rs, 1)
                own.settle()

        @block.vector
        def _(dve):
            own = Chain(dve, dve_own)
            dve.wait_ge(weights_in, 16 * 5)
            with dve.Fori(0, B) as b:
                own.restart()
                dve.wait_ge(proj_ps, b + 1)
                nc.vector.tensor_copy(kT[:, :, :], ps_s[:, 2:4, :].rearrange("p a (g n) -> p (a g) n", g=2)).then_inc(k_sb, 1)
                nc.vector.tensor_copy(v[:, :, :], ps_m[:, 0:TT, :]).then_inc(v_sb, 1)
                for n, (qt, groups) in enumerate(PASSES):
                    nk = (qt + 1) * P
                    heads = JH * len(groups)
                    dve.wait_ge(exps, b * NP + n)
                    dve.wait_ge(scores, b * NP + n + 1)
                    nc.vector.tensor_reduce(negmax[:, 0:heads].rearrange("p (j i) -> p j i", j=JH),
                                            ps_s[:, :, :].rearrange("p j (i n) -> p j i n", n=nk), AX, ALU.max,
                                            negate=True).then_inc(maxed, 1)
                    for f in range(FILLS):
                        k = n * FILLS + f
                        if f == 0:
                            dve.wait_ge(pv, b * NP + n)
                        dve.wait_ge(blocks_ps, b * NP * FILLS + k + 1)
                        nc.vector.tensor_copy(probT[:, 4 * f:4 * f + 4, :], ps_t[k % 2][:, :, :]).then_inc(blocks_sb, 1)
                    if n + 1 in last.values():
                        own.link(nc.vector.reciprocal(rsum[:, qt, :, :], sums[:, qt, :, :]))
                        dve.wait_ge(pv, b * NP + n + 1)
                        nc.vector.tensor_tensor(
                            o[:, qt, :].rearrange("p (g j d) -> p g j d", g=GH, j=JH),
                            ps_o[:, qt, :].rearrange("p (g j d) -> p g j d", g=GH, j=JH),
                            bc(rsum[:, qt, :, :].rearrange("p j g -> p g j"), 3, AD), ALU.mult).then_inc(normed, 1)
                own.link(nc.vector.tensor_tensor(r[:, :, :], x[:, :, :], bc(bo[:, :], 1, TT), ALU.add))
                dve.wait_ge(out_ps, b + 1)
                nc.vector.tensor_tensor(r[:, :, :], r[:, :, :], ps_m[:, 2:4, :], ALU.add).then_inc(out_read, 1)
                dve.wait_ge(out_read, b + 1)
                layernorm(nc, dve, own, r, stats, mv, rs, x2, b, ln_stats, ln_rs, x2_ready, stored)
                own.settle()


NE = 8
DF = 512
FC = DF // P


def ffn_stage(nc, T, const):
    ident, ident16, causal16, ones, eps = const
    with ExitStack() as stack:
        c = Scope(nc, stack, "ffn")
        wr = c.sb("wr", [P, NE])
        br = c.sb("br", [1, NE])
        x = c.sb("x", [P, TT, D])
        xT = c.sb("xT", [P, S])
        mean = c.sb("mean", [P, 1])
        score = c.sb("score", [1, NE])
        top = c.sb("top", [1, 8])
        pick = c.sb("pick", [1, 8], U32)
        w1 = c.sb("w1", [P, DF])
        w2 = c.sb("w2", [P, FC, D])
        b1 = c.sb("b1", [P, FC])
        b2 = c.sb("b2", [P, D])
        hT = c.sb("hT", [P, FC, S])
        r = c.sb("r", [P, TT, D])
        stats = c.sb("stats", [P, TT, 6])
        mv = c.sb("mv", [P, TT, 2])
        rs = c.sb("rs", [P, TT])
        x3 = c.sb("x3", [P, TT, D])
        ps_x = c.ps("ps_x", [P, S])
        ps_r = c.ps("ps_r", [1, NE])
        ps_h = [c.ps(f"ps_h{i}", [P, 2, S]) for i in range(FC // 2)]
        ps_y = c.ps("ps_y", [P, TT, D])

        weights_in = c.sem("weights_in")
        x_in = c.sem("x_in")
        xT_ps = c.sem("xT_ps")
        xT_sb = c.sem("xT_sb")
        mean_ready = c.sem("mean_ready")
        score_ps = c.sem("score_ps")
        picked = c.sem("picked")
        expert_in = c.sem("expert_in")
        h_ps = c.sem("h_ps")
        h_sb = c.sem("h_sb")
        y_ps = c.sem("y_ps")
        y_read = c.sem("y_read")
        ln_stats = c.sem("ln_stats")
        ln_rs = c.sem("ln_rs")
        x3_ready = c.sem("x3_ready")
        stored = c.sem("stored")
        dve_own = c.sem("dve_own")
        act_own = c.sem("act_own")
        block = c.block()

        @block.sync
        def _(sp):
            for dst, src in ((wr[:, :], T["wr"]), (br[:, :], T["br"])):
                sp.dma_start(dst, src).then_inc(weights_in, 16)
            with sp.Fori(0, B) as b:
                sp.wait_ge(y_read, b)
                sp.dma_start(x[:, :, :], T["x2"][b].rearrange("(t p) d -> p t d", p=P)).then_inc(x_in, 16)
                hold(sp, picked, b + 1)
                e = sp.value_load(pick[0:1, 0:1], min_val=0, max_val=NE - 1)
                sp.dma_start(w1[:, :], T["ffn_w1"][bass.ds(e, 1)].rearrange("e p f -> p (e f)")).then_inc(expert_in, 16)
                sp.dma_start(b1[:, :], T["ffn_b1"][bass.ds(e, 1)].rearrange("e p f -> p (e f)")).then_inc(expert_in, 16)
                sp.dma_start(w2[:, :, :], T["ffn_w2"][bass.ds(e, 1)].rearrange("e (c p) d -> p (e c) d", p=P))\
                    .then_inc(expert_in, 16)
                sp.dma_start(b2[:, :], T["ffn_b2"][bass.ds(e, 1)].rearrange("e p d -> p (e d)")).then_inc(expert_in, 16)
                sp.wait_ge(x3_ready, b + 1)
                sp.dma_start(T["x3"][b].rearrange("(t p) d -> p t d", p=P), x3[:, :, :]).then_inc(stored, 16)
            sp.wait_ge(stored, 16 * B)

        @block.tensor
        def _(pe):
            pe.wait_ge(weights_in, 32)
            with pe.Fori(0, B) as b:
                pe.wait_ge(x_in, 16 * (b + 1))
                for t in range(TT):
                    mm = nc.tensor.transpose(ps_x[:, t * P:(t + 1) * P], x[:, t, :], ident[:, :])
                mm.then_inc(xT_ps, 1)
                pe.wait_ge(mean_ready, b + 1)
                nc.tensor.matmul(ps_r[:, :], mean[:, :], wr[:, :], start=True, stop=True).then_inc(score_ps, 1)
                pe.wait_ge(expert_in, 64 * (b + 1))
                for f in range(FC):
                    mm = nc.tensor.matmul(ps_h[f // 2][:, f % 2, :], w1[:, f * P:(f + 1) * P], xT[:, :], start=True, stop=True)
                    if f % 2:
                        mm.then_inc(h_ps, 1)
                for f in range(FC):
                    if f % 2 == 0:
                        pe.wait_ge(h_sb, b * FC + f + 2)
                    for t in range(TT):
                        mm = nc.tensor.matmul(ps_y[:, t, :], hT[:, f, t * P:(t + 1) * P], w2[:, f, :],
                                              start=(f == 0 and t == 0), stop=(f == FC - 1), skip_group_check=True)
                mm.then_inc(y_ps, 1)

        @block.scalar
        def _(act):
            own = Chain(act, act_own)
            with act.Fori(0, B) as b:
                own.restart()
                act.wait_ge(xT_ps, b + 1)
                nc.scalar.activation(xT[:, :], ps_x[:, :], ACT.Copy, accum_out=mean[:, :]).then_inc(xT_sb, 1)
                act.wait_ge(xT_sb, b + 1)
                nc.scalar.activation(mean[:, :], mean[:, :], ACT.Copy, scale=1.0 / S).then_inc(mean_ready, 1)
                act.wait_ge(ln_stats, b + 1)
                own.link(nc.scalar.activation(rs[:, :], mv[:, :, 1], ACT.Ln, bias=eps[:, 0:1]))
                nc.scalar.activation(rs[:, :], rs[:, :], ACT.Exp, scale=-0.5).then_inc(ln_rs, 1)
                own.settle()

        @block.vector
        def _(dve):
            own = Chain(dve, dve_own)
            dve.wait_ge(weights_in, 32)
            with dve.Fori(0, B) as b:
                own.restart()
                dve.wait_ge(score_ps, b + 1)
                own.link(nc.vector.tensor_tensor(score[:, :], ps_r[:, :], br[:, :], ALU.add))
                own.link(nc.vector.max(top[:, :], score[:, :]))
                nc.vector.max_index(pick[:, :], top[:, :], score[:, :]).then_inc(picked, 1)
                dve.wait_ge(expert_in, 64 * (b + 1))
                own.link(nc.vector.tensor_tensor(r[:, :, :], x[:, :, :], bc(b2[:, :], 1, TT), ALU.add))
                for f in range(FC):
                    dve.wait_ge(h_ps, b * (FC // 2) + f // 2 + 1)
                    nc.vector.tensor_scalar(hT[:, f, :], ps_h[f // 2][:, f % 2, :], b1[:, f:f + 1], 0.0, ALU.add, ALU.max)\
                        .then_inc(h_sb, 1)
                dve.wait_ge(y_ps, b + 1)
                nc.vector.tensor_tensor(r[:, :, :], r[:, :, :], ps_y[:, :, :], ALU.add).then_inc(y_read, 1)
                dve.wait_ge(y_read, b + 1)
                layernorm(nc, dve, own, r, stats, mv, rs, x3, b, ln_stats, ln_rs, x3_ready, stored)
                own.settle()


DH = 16
DW = 8
GB = 8
NG = B // GB
PLANES = 3 * DW + 1
GT = NG * S
WIN = P - DH
NORM_EPS = 1e-6


def delta_stage(nc, T, const):
    ident, ident16, causal16, ones, eps = const
    with ExitStack() as stack:
        c = Scope(nc, stack, "delta")
        planes = c.sb("planes", [P, 3 * DW, GT])
        eta = c.sb("eta", [P, GT])
        kb = c.sb("kb", [P, DW, GT])
        own_sem = c.sem("own")
        with ExitStack() as inner:
            project_and_convolve(nc, T, const, Scope(nc, inner, "dproj"), inner, planes, eta)
        k, q, v = (planes[:, i * DW:(i + 1) * DW, :] for i in range(3))
        with ExitStack() as inner:
            normalise(nc, Scope(nc, inner, "dnorm"), inner, const, k, q, v, kb, eta)
        u = c.sb("u", [P, DW, GT])
        with ExitStack() as inner:
            recurrence(nc, Scope(nc, inner, "drec"), inner, k, v, kb, u)
        o = c.sb("o", [P, DW, GT])
        with ExitStack() as inner:
            average(nc, T, const, Scope(nc, inner, "davg"), inner, k, q, u, o)
        with ExitStack() as inner:
            project_out(nc, T, const, Scope(nc, inner, "dout"), inner, o)


def project_and_convolve(nc, T, const, c, stack, planes, eta):
    ident, ident16, causal16, ones, eps = const
    wpad = c.sb("wpad", [P, PLANES, 2 * WIN + DH])
    bias = c.sb("bias", [P, PLANES])
    taps = c.sb("taps", [P, 3 * DW, TAPS])
    x = c.sb("x", [P, B * TT, D])
    xT = c.sb("xT", [P, B, S])
    raw = c.sb("raw", [P, PLANES, NG, TAPS - 1 + S])
    ps = [c.ps(f"ps{i}", [P, 512]) for i in range(4)]
    weights_in = c.sem("weights_in")
    x_in = c.sem("x_in")
    turned = c.sem("turned")
    turned_sb = c.sem("turned_sb")
    plane_ps = c.sem("plane_ps")
    plane_sb = c.sem("plane_sb")
    cleared = c.sem("cleared")
    dve_own = c.sem("dve_own")
    block = c.block()

    @block.sync
    def _(sp):
        for b in range(0, B, 2):
            sp.dma_start(x[:, b * TT:(b + 2) * TT, :], T["x3"][b:b + 2].rearrange("b (t p) d -> p (b t) d", p=P))\
                .then_inc(x_in, 16)
        for dst, src in ((wpad[:, :, :], T["delta_w"]), (bias[:, :], T["delta_bias"]), (taps[:, :, :], T["delta_taps"])):
            sp.dma_start(dst, src).then_inc(weights_in, 16)

    @block.gpsimd
    def _(pool):
        nc.gpsimd.memset(raw[:, :, :, 0:TAPS - 1], 0.0).then_inc(cleared, 1)

    @block.tensor
    def _(pe):
        pe.wait_ge(x_in, 16 * (B // 2))
        for f in range(B * TT // 4):
            if f >= 4:
                pe.wait_ge(turned_sb, f - 3)
            for i in range(4):
                mm = nc.tensor.transpose(ps[f % 4][:, i * P:(i + 1) * P], x[:, 4 * f + i, :], ident[:, :])
            mm.then_inc(turned, 1)
        pe.wait_ge(turned_sb, B * TT // 4)
        pe.wait_ge(weights_in, 48)
        with pe.Fori(0, NG) as g:
            for n in range(PLANES):
                if n >= 4:
                    pe.wait_ge(plane_sb, g * PLANES + n - 3)
                else:
                    pe.wait_ge(plane_sb, g * PLANES)
                for s in range(GB):
                    mm = nc.tensor.matmul(ps[n % 4][:, 0:S], wpad[:, n, WIN - DH * s:WIN - DH * s + P],
                                          xT[:, bass.ds(g * GB + s, 1), :].rearrange("p a t -> p (a t)"),
                                          start=(s == 0), stop=(s == GB - 1))
                mm.then_inc(plane_ps, 1)

    @block.scalar
    def _(act):
        for f in range(B * TT // 4):
            act.wait_ge(turned, f + 1)
            nc.scalar.activation(xT[:, 2 * f:2 * f + 2, :], ps[f % 4][:, :].rearrange("p (b t) -> p b t", b=2), ACT.Copy)\
                .then_inc(turned_sb, 1)
        act.wait_ge(weights_in, 48)
        with act.Fori(0, NG) as g:
            for n in range(PLANES):
                act.wait_ge(plane_ps, g * PLANES + n + 1)
                nc.scalar.activation(raw[:, n, bass.ds(g, 1), TAPS - 1:].rearrange("p a t -> p (a t)"), ps[n % 4][:, 0:S],
                                     ACT.Identity, bias=bias[:, n:n + 1]).then_inc(plane_sb, 1)

    @block.vector
    def _(dve):
        own = Chain(dve, dve_own)
        dve.wait_ge(cleared, 1)
        dve.wait_ge(weights_in, 48)
        dve.wait_ge(plane_sb, NG * PLANES)
        with dve.Fori(0, 3 * DW) as n:
            own.restart()
            out = planes[:, bass.ds(n, 1), :].rearrange("p a (g t) -> p (a g) t", g=NG)
            for j in range(TAPS):
                tap = taps[:, bass.ds(n, 1), j]
                src = raw[:, bass.ds(n, 1), :, j:j + S].rearrange("p a g t -> p (a g) t")
                if j == 0:
                    own.link(nc.vector.tensor_scalar(out, src, tap, None, ALU.mult))
                else:
                    own.link(nc.vector.scalar_tensor_tensor(out=out, in0=src, scalar=tap, in1=out, op0=ALU.mult, op1=ALU.add))
        own.restart()
        own.link(nc.vector.tensor_copy(eta[:, :].rearrange("p (g t) -> p g t", g=NG), raw[:, 3 * DW, :, TAPS - 1:]))


def normalise(nc, c, stack, const, k, q, v, kb, eta):
    ident, ident16, causal16, ones, eps = const
    sq = c.sb("sq", [P, 2, DW, GT])
    ev = c.sb("ev", [P, DW, GT])
    ee = c.sb("ee", [P, GT])
    norm = c.sb("norm", [P, 2, GT])
    squared = c.sem("squared")
    lengths = c.sem("lengths")
    rooted = c.sem("rooted")
    expd = c.sem("expd")
    dve_own = c.sem("dve_own")
    block = c.block()

    @block.scalar
    def _(act):
        nc.scalar.activation(sq[:, 0, :, :], k, ACT.Square).then_inc(squared, 1)
        nc.scalar.activation(sq[:, 1, :, :], q, ACT.Square).then_inc(squared, 1)
        nc.scalar.activation(ev[:, :, :], v, ACT.Exp, scale=-1.0).then_inc(expd, 1)
        nc.scalar.activation(ee[:, :], eta[:, :], ACT.Exp, scale=-1.0).then_inc(expd, 1)
        act.wait_ge(lengths, 2)
        nc.scalar.activation(norm[:, :, :], norm[:, :, :], ACT.Sqrt).then_inc(rooted, 1)

    @block.vector
    def _(dve):
        own = Chain(dve, dve_own)
        for i in range(2):
            dve.wait_ge(squared, i + 1)
            nc.vector.tensor_reduce(norm[:, i, :], sq[:, i, :, :].rearrange("p d n -> p n d"), AX, ALU.add).then_inc(lengths, 1)
        dve.wait_ge(expd, 2)
        own.link(nc.vector.tensor_scalar(ee[:, :], ee[:, :], 1.0, None, ALU.add))
        own.link(nc.vector.reciprocal(eta[:, :], ee[:, :]))
        own.link(nc.vector.tensor_scalar(ev[:, :, :], ev[:, :, :], 1.0, None, ALU.add))
        own.link(nc.vector.reciprocal(ev[:, :, :], ev[:, :, :]))
        own.link(nc.vector.tensor_tensor(v, v, ev[:, :, :], ALU.mult))
        own.link(nc.vector.tensor_tensor(v, v, bc(eta[:, :], 1, DW), ALU.mult))
        dve.wait_ge(rooted, 1)
        own.link(nc.vector.tensor_scalar(norm[:, :, :], norm[:, :, :], NORM_EPS, None, ALU.add))
        own.link(nc.vector.reciprocal(norm[:, :, :], norm[:, :, :]))
        for i, w in enumerate((k, q)):
            own.link(nc.vector.tensor_tensor(w, w, bc(norm[:, i, :], 1, DW), ALU.mult))
        own.link(nc.vector.tensor_tensor(kb[:, :, :], k, bc(eta[:, :], 1, DW), ALU.mult))


STEP = 4


def recurrence(nc, c, stack, k, v, kb, u):
    w = c.sb("w", [P, NG, DW, DW])
    t1 = c.sb("t1", [P, NG, DW, DW])
    t2 = c.sb("t2", [P, NG, DW, DW])
    p = c.sb("p", [P, NG, DW])
    dve_own = c.sem("dve_own")
    block = c.block()

    def token(plane, t):
        return plane.rearrange("p d (g t) -> p g d t", g=NG)[:, :, :, bass.ds(t, 1)].rearrange("p g d a -> p g (d a)")

    @block.vector
    def _(dve):
        own = Chain(dve, dve_own)
        own.link(nc.vector.memset(w[:, :, :, :], 0.0))
        with dve.Fori(0, S // STEP) as turn:
            own.restart()
            for i in range(STEP):
                t = turn * STEP + i
                own.link(nc.vector.tensor_tensor(t1[:, :, :, :], w[:, :, :, :], bc(token(kb[:, :, :], t), 2, DW), ALU.mult))
                own.link(nc.vector.tensor_reduce(p[:, :, :], t1[:, :, :, :], AX, ALU.add))
                own.link(nc.vector.tensor_tensor(token(u[:, :, :], t), token(v, t), p[:, :, :], ALU.subtract))
                own.link(nc.vector.tensor_tensor(t2[:, :, :, :], bc(token(u[:, :, :], t), 3, DW), bc(token(k, t), 2, DW),
                                                 ALU.mult))
                own.link(nc.vector.tensor_tensor(w[:, :, :, :], w[:, :, :, :], t2[:, :, :, :], ALU.add))


def average(nc, T, const, c, stack, k, q, u, o):
    ident, ident16, causal16, ones, eps = const
    coef = c.sb("coef", [P, 3, S])
    fade = c.sb("fade", [P, 2, DW * NG, S])
    a = c.sb("a", [P, DW, GT])
    a2 = c.sb("a2", [P, DW, GT])
    rms = c.sb("rms", [P, DW])
    tiny = c.sb("tiny", [P, 1])
    ms = c.sb("ms", [P, GT])
    coef_in = c.sem("coef_in")
    faded = c.sem("faded")
    squares = c.sem("squares")
    summed = c.sem("summed")
    rooted = c.sem("rooted")
    dve_own = c.sem("dve_own")
    act_own = c.sem("act_own")
    block = c.block()

    @block.sync
    def _(sp):
        sp.dma_start(coef[:, :, :], T["coef"]).then_inc(coef_in, 16)
        sp.dma_start(rms[:, :], T["rms"]).then_inc(coef_in, 16)

    @block.scalar
    def _(act):
        act.wait_ge(coef_in, 32)
        for i in range(2):
            nc.scalar.activation(fade[:, i, :, :], bc(coef[:, i, :], 1, DW * NG), ACT.Copy).then_inc(faded, 1)
        act.wait_ge(squares, 1)
        nc.scalar.activation(a[:, :, :], o[:, :, :], ACT.Square).then_inc(squares, 1)
        act.wait_ge(summed, 1)
        nc.scalar.activation(ms[:, :], ms[:, :], ACT.Ln, scale=1.0 / DW, bias=tiny[:, 0:1]).then_inc(act_own, 1)
        act.wait_ge(act_own, 1)
        nc.scalar.activation(ms[:, :], ms[:, :], ACT.Exp, scale=-0.5).then_inc(rooted, 1)

    @block.vector
    def _(dve):
        own = Chain(dve, dve_own)
        own.link(nc.vector.memset(tiny[:, :], NORM_EPS))
        dve.wait_ge(coef_in, 32)
        own.link(nc.vector.tensor_tensor(u[:, :, :].rearrange("p d (g t) -> p (d g) t", g=NG),
                                         u[:, :, :].rearrange("p d (g t) -> p (d g) t", g=NG),
                                         bc(coef[:, 2, :], 1, DW * NG), ALU.mult))
        dve.wait_ge(faded, 2)
        flat = "p d n -> p (d n)"
        for d in range(DW):
            own.link(nc.vector.tensor_tensor(a[:, :, :], u[:, :, :], bc(k[:, d, :], 1, DW), ALU.mult))
            own.link(nc.vector.tensor_tensor_scan(a2[:, :, :].rearrange(flat), fade[:, 0, :, :].rearrange(flat),
                                                  a[:, :, :].rearrange(flat), 0.0, ALU.mult, ALU.add))
            own.link(nc.vector.tensor_tensor_scan(a[:, :, :].rearrange(flat), fade[:, 1, :, :].rearrange(flat),
                                                  a2[:, :, :].rearrange(flat), 0.0, ALU.mult, ALU.add))
            if d == 0:
                own.link(nc.vector.tensor_tensor(o[:, :, :], a[:, :, :], bc(q[:, d, :], 1, DW), ALU.mult))
            else:
                own.link(nc.vector.tensor_tensor(a2[:, :, :], a[:, :, :], bc(q[:, d, :], 1, DW), ALU.mult))
                own.link(nc.vector.tensor_tensor(o[:, :, :], o[:, :, :], a2[:, :, :], ALU.add))
        nc.vector.tensor_copy(ms[:, 0:1], o[:, 0, 0:1]).then_inc(squares, 1)
        dve.wait_ge(squares, 2)
        nc.vector.tensor_reduce(ms[:, :], a[:, :, :].rearrange("p e n -> p n e"), AX, ALU.add).then_inc(summed, 1)
        dve.wait_ge(rooted, 1)
        own.link(nc.vector.tensor_tensor(o[:, :, :], o[:, :, :], bc(ms[:, :], 1, DW), ALU.mult))
        own.link(nc.vector.tensor_tensor(o[:, :, :], o[:, :, :], bc(rms[:, :], 2, GT), ALU.mult))


def project_out(nc, T, const, c, stack, o):
    ident, ident16, causal16, ones, eps = const
    NT = NG * TT
    w = c.sb("w", [P, GB, DW, D])
    bout = c.sb("bout", [P, D])
    x = c.sb("x", [P, 2, NT, D])
    r = c.sb("r", [P, NT, D])
    stats = c.sb("stats", [P, NT, 6])
    mv = c.sb("mv", [P, NT, 2])
    rs = c.sb("rs", [P, NT])
    x4 = c.sb("x4", [P, NT, D])
    ps = [c.ps(f"ps{i}", [P, NT, D]) for i in range(2)]
    cleared = c.sem("cleared")
    weights_in = c.sem("weights_in")
    x_in = c.sem("x_in")
    out_ps = c.sem("out_ps")
    out_read = c.sem("out_read")
    ln_stats = c.sem("ln_stats")
    ln_rs = c.sem("ln_rs")
    ready = c.sem("x4_ready")
    stored = c.sem("stored")
    dve_own = c.sem("dve_own")
    act_own = c.sem("act_own")
    block = c.block()

    @block.gpsimd
    def _(pool):
        nc.gpsimd.memset(w[:, :, :, :], 0.0).then_inc(cleared, 1)

    @block.sync
    def _(sp):
        sp.dma_start(bout[:, :], T["bout"]).then_inc(weights_in, 16)
        sp.wait_ge(cleared, 1)
        for s in range(GB):
            sp.dma_start(w[DH * s:DH * (s + 1), s, :, :], T["delta_out"]).then_inc(weights_in, 16)
        with sp.Fori(0, GB) as s:
            sp.wait_ge(out_read, s)
            for g in range(NG):
                sp.dma_start(x[:, 0, g * TT:(g + 1) * TT, :],
                             T["x3"][bass.ds(s + g * GB, 1)].rearrange("b (t p) d -> p (b t) d", p=P)).then_inc(x_in, 16)
            sp.wait_ge(ready, s + 1)
            for g in range(NG):
                sp.dma_start(T["x4"][bass.ds(s + g * GB, 1)].rearrange("b (t p) d -> p (b t) d", p=P),
                             x4[:, g * TT:(g + 1) * TT, :]).then_inc(stored, 16)
        sp.wait_ge(stored, 16 * NG * GB)

    @block.tensor
    def _(pe):
        pe.wait_ge(weights_in, 16 * (GB + 1))
        with pe.Fori(0, GB) as s:
            pe.wait_ge(out_read, s)
            for n in range(NT):
                for e in range(DW):
                    mm = nc.tensor.matmul(ps[0][:, n, :], o[:, e, n * P:(n + 1) * P],
                                          w[:, bass.ds(s, 1), e, :].rearrange("p a n -> p (a n)"),
                                          start=(e == 0), stop=(e == DW - 1))
            mm.then_inc(out_ps, 1)

    @block.scalar
    def _(act):
        own = Chain(act, act_own)
        with act.Fori(0, GB) as s:
            own.restart()
            act.wait_ge(ln_stats, s + 1)
            own.link(nc.scalar.activation(rs[:, :], mv[:, :, 1], ACT.Ln, bias=eps[:, 0:1]))
            nc.scalar.activation(rs[:, :], rs[:, :], ACT.Exp, scale=-0.5).then_inc(ln_rs, 1)
            own.settle()

    @block.vector
    def _(dve):
        own = Chain(dve, dve_own)
        dve.wait_ge(weights_in, 16 * (GB + 1))
        with dve.Fori(0, GB) as s:
            own.restart()
            dve.wait_ge(x_in, 16 * NG * (s + 1))
            own.link(nc.vector.tensor_tensor(r[:, :, :], x[:, 0, :, :], bc(bout[:, :], 1, NT), ALU.add))
            dve.wait_ge(out_ps, s + 1)
            nc.vector.tensor_tensor(r[:, :, :], r[:, :, :], ps[0][:, :, :], ALU.add).then_inc(out_read, 1)
            dve.wait_ge(out_read, s + 1)
            layernorm(nc, dve, own, r, stats, mv, rs, x4, s, ln_stats, ln_rs, ready, stored, NT, 16 * NG)
            own.settle()


CH = 16
CD = 64
HP = CH // 2
INNER = CH * CD
TEXT, IMG = 77, 16
TI = TEXT + IMG
AUD = CTX - TI
REL = 16
NREL = 2 * REL + 1
SCALE = CD ** -0.5
AT = -(-AUD // P)
CHUNKS = 3
CHUNK = [min(512, AUD - 512 * i) for i in range(CHUNKS)]
UNITS = 4 * HP
RING = 5
OGRP = 8
R1, R2 = 19, NREL - 19
COL_R1, COL_I, COL_R2 = TEXT, TEXT + R1, TEXT + R1 + IMG
CAT = COL_R2 + R2
FROW = P - 1 + NREL
STEP_SCORES, STEP_EXP, STEP_SUM, STEP_FAR = 2, 8, 9, 18
SCRATCH = {"skew_rel": (P, CH, P + TEXT - 1), "skew_prob": (P, CH, FROW)}


def fills_of():
    todo = []
    for i in range(2 * CHUNKS):
        todo.append(("k" if i < CHUNKS else "v", (0, i % CHUNKS), "act" if i % 2 else "dve"))
    for n in range(UNITS):
        pair, place = divmod(n, 4)
        for f in range(CHUNKS):
            todo.append(("t", (n, f), "act" if f == 2 else "dve"))
            if f < 2 and place < 3 and pair + 1 < HP:
                i = 2 * place + f
                todo.append(("k" if i < CHUNKS else "v", (pair + 1, i % CHUNKS), "act" if i < CHUNKS else "dve"))
    for i in range(2 * CH // 4):
        todo.append(("c", i, "dve" if i % 2 else "act"))
    return todo


FILL_LIST = fills_of()
FILL_AT = {(w, a): i for i, (w, a, _) in enumerate(FILL_LIST)}


def emptied(i):
    eng = FILL_LIST[i][2]
    return eng, sum(1 for f in FILL_LIST[:i + 1] if f[2] == eng)


PER_TURN = {e: sum(1 for f in FILL_LIST if f[2] == e) for e in ("act", "dve")}


def cross_stage(nc, T, const):
    ident, ident16, causal16, ones, eps = const
    with ExitStack() as stack:
        c = Scope(nc, stack, "cross")
        w = {n: c.sb(f"w_{n}", [P, INNER]) for n in ("q", "k", "v", "ki", "vi", "ka", "va")}
        wo = c.sb("wo", [P, HP, D])
        bo = c.sb("bo", [P, D])
        relk = c.sb("relk", [P, NREL])
        gains = c.sb("gains", [P, 2])
        far = c.sb("far", [P, 2, TEXT])
        x = c.sb("x", [P, TT, D])
        cx = c.sb("cx", [P, AT + 1, D])
        xT = c.sb("xT", [P, S])
        cT = c.sb("cT", [P, CTX])
        qT = c.sb("qT", [P, HP, S])
        kti = c.sb("kti", [P, HP, TI])
        vcat = c.sb("vcat", [P, INNER])
        sti = c.sb("sti", [P, TT, CH, TI])
        ext = c.sb("ext", [P, CH, P + TEXT - 1])
        rel = c.sb("rel", [P, TT, CH, TEXT])
        near = c.sb("near", [P, CH])
        pcat = c.sb("pcat", [P, TT, CH, CAT])
        pcT = c.sb("pcT", [P, 2, 4, P])
        small = c.sb("small", [P, 2, TT, CH])
        kT = c.sb("kT", [P, 2, AUD])
        va = c.sb("va", [P, 2, AT, P])
        prob = c.sb("prob", [P, AT * P])
        pT = c.sb("pT", [P, CHUNKS, 4, P])
        max3 = c.sb("max3", [P, 2, CHUNKS])
        negmax = c.sb("negmax", [P, 2])
        sums = c.sb("sums", [P, UNITS, CHUNKS])
        rsum = c.sb("rsum", [P, UNITS])
        oall = c.sb("oall", [P, TT, CH, CD])
        oT = c.sb("oT", [P, HP, S])
        r = c.sb("r", [P, TT, D])
        stats = c.sb("stats", [P, TT, 6])
        mv = c.sb("mv", [P, TT, 2])
        rs = c.sb("rs", [P, TT])
        x5 = c.sb("x5", [P, TT, D])
        ring = [c.ps(f"ring{i}", [P, 512]) for i in range(RING)]
        fill = [c.ps(f"fill{i}", [P, 512]) for i in range(2)]
        ps_o = c.ps("ps_o", [P, 512])

        weights_in = c.sem("weights_in")
        rel_in = c.sem("rel_in")
        cleared = c.sem("cleared")
        far_ready = c.sem("far_ready")
        gains_ready = c.sem("gains_ready")
        zeroed = c.sem("zeroed")
        x_in = c.sem("x_in")
        turned = c.sem("turned")
        turned_act = c.sem("turned_act")
        turned_dve = c.sem("turned_dve")
        q_ps = c.sem("q_ps")
        q_sb = c.sem("q_sb")
        kti_ps = c.sem("kti_ps")
        kti_sb = c.sem("kti_sb")
        vcat_ps = c.sem("vcat_ps")
        vcat_sb = c.sem("vcat_sb")
        ti_ps = c.sem("ti_ps")
        rel_ps = c.sem("rel_ps")
        ti_sb = c.sem("ti_sb")
        rel_sb = c.sem("rel_sb")
        skewed_out = c.sem("skewed_out")
        skewed_in = c.sem("skewed_in")
        ti_max = c.sem("ti_max")
        ti_sub = c.sem("ti_sub")
        ti_exp = c.sem("ti_exp")
        ti_sum = c.sem("ti_sum")
        ti_prob = c.sem("ti_prob")
        band_out = c.sem("band_out")
        band_in = c.sem("band_in")
        far_prob = c.sem("far_prob")
        cat_ready = c.sem("cat_ready")
        scores = c.sem("scores")
        maxed = c.sem("maxed")
        exps = c.sem("exps")
        fill_ps = c.sem("fill_ps")
        fill_sb = {"act": c.sem("fill_act"), "dve": c.sem("fill_dve")}
        pv = c.sem("pv")
        o_sb = c.sem("o_sb")
        cat_ps = c.sem("cat_ps")
        o_ready = c.sem("o_ready")
        oT_ps = c.sem("oT_ps")
        oT_sb = c.sem("oT_sb")
        out_ps = c.sem("out_ps")
        out_read = c.sem("out_read")
        ln_stats = c.sem("ln_stats")
        ln_rs = c.sem("ln_rs")
        x5_ready = c.sem("x5_ready")
        stored = c.sem("stored")
        dve_own = c.sem("dve_own")
        act_own = c.sem("act_own")
        pool_own = c.sem("pool_own")
        block = c.block()
        e_w, f_w = P + TEXT - 1, FROW

        @block.sync
        def _(sp):
            n_w = 0
            for dst, src in [(w[n][:, :], T[f"cross_{n}"]) for n in w] + [
                    (wo[:, :, :], T["cross_o"]), (bo[:, :], T["cross_bo"]), (relk[:, :], T["relk"]),
                    (gains[:, :], T["gains"])]:
                sp.dma_start(dst, src).then_inc(weights_in, 16)
            for lo, n, col in ((0, R1, COL_R1), (R1, R2, COL_R2)):
                sp.dma_start(vcat[col:col + n, :].rearrange("r (h d) -> r h d", h=CH),
                             bc(T["relv"][lo:lo + n], 1, CH)).then_inc(rel_in, 16)
            sp.wait_ge(cleared, 3)
            sp.dma_start(T["skew_prob"], ext[:, :, 0:f_w]).then_inc(zeroed, 16)
            sp.wait_ge(zeroed, 16)
            with sp.Fori(0, B) as b:
                sp.wait_ge(out_read, b)
                sp.dma_start(x[:, :, :], T["x4"][b].rearrange("(t p) d -> p t d", p=P)).then_inc(x_in, 16)
                sp.dma_start(cx[0:TI, 0, :], T["ctx"][b, 0:TI]).then_inc(x_in, 16)
                full = (AT - 1) * P
                sp.dma_start(cx[:, 1:AT, :], T["ctx"][b, TI:TI + full].rearrange("(t p) d -> p t d", p=P)).then_inc(x_in, 16)
                sp.dma_start(cx[0:AUD - full, AT, :], T["ctx"][b, TI + full:CTX]).then_inc(x_in, 16)
                sp.wait_ge(rel_sb, 2 * b + 1)
                sp.dma_start(T["skew_rel"], ext[:, :, :]).then_inc(skewed_out, 16)
                sp.wait_ge(skewed_out, 16 * (b + 1))
                sp.wait_ge(ti_sub, b)
                sp.dma_start(rel[:, 0, :, :], bass.AP(T["skew_rel"].tensor, P - 1, [[CH * e_w - 1, P], [e_w, CH], [1, TEXT]]))\
                    .then_inc(skewed_in, 16)
                sp.wait_ge(ti_prob, b + 1)
                sp.dma_start(T["skew_prob"][:, :, REL:REL + TEXT], pcat[:, 0, :, 0:TEXT]).then_inc(band_out, 16)
                sp.wait_ge(band_out, 16 * (b + 1))
                for lo, n, col in ((0, R1, COL_R1), (R1, R2, COL_R2)):
                    sp.dma_start(pcat[:, 0, :, col:col + n],
                                 bass.AP(T["skew_prob"].tensor, lo, [[CH * f_w + 1, P], [f_w, CH], [1, n]])).then_inc(band_in, 16)
                sp.wait_ge(x5_ready, b + 1)
                sp.dma_start(T["x5"][b].rearrange("(t p) d -> p t d", p=P), x5[:, :, :]).then_inc(stored, 16)
            sp.wait_ge(stored, 16 * B)

        @block.tensor
        def _(pe):
            pe.wait_ge(weights_in, 16 * 11)
            pe.wait_ge(rel_in, 32)
            with pe.Fori(0, B) as b:

                waited = {"act": 0, "dve": 0}

                def wait_fill(*which):
                    need = {"act": -1, "dve": -1}
                    for i in which:
                        if i < 0:
                            need = {e: max(n, 0) for e, n in need.items()}
                        else:
                            e, n = emptied(i)
                            need[e] = max(need[e], n)
                    for e, n in need.items():
                        if n > waited[e] or n == waited[e] == 0:
                            pe.wait_ge(fill_sb[e], b * PER_TURN[e] + n)
                            waited[e] = n

                def project(what, pair, i):
                    n = FILL_AT[(what, (pair, i))]
                    wait_fill(n - 2)
                    bank = fill[n % 2]
                    if what == "k":
                        mm = nc.tensor.matmul(bank[:, 0:CHUNK[i]], w["ka"][:, pair * P:(pair + 1) * P],
                                              cT[:, TI + 512 * i:TI + 512 * i + CHUNK[i]], start=True, stop=True)
                    else:
                        for t in range(4 * i, 4 * i + 4):
                            m = min(P, AUD - t * P)
                            mm = nc.tensor.matmul(bank[0:m, (t % 4) * P:(t % 4 + 1) * P], cT[:, TI + t * P:TI + t * P + m],
                                                  w["va"][:, pair * P:(pair + 1) * P], start=True, stop=True)
                    mm.then_inc(fill_ps, 1)

                def score(n, i):
                    k = n * CHUNKS + i
                    pair, odd, t = n // 4, n // 2 % 2, n % 2
                    if n % 4 == 0 and i == 0:
                        wait_fill(*[FILL_AT[("k", (pair, j))] for j in range(CHUNKS)])
                    if k >= RING:
                        pe.wait_ge(exps, b * UNITS * CHUNKS + k - RING + 1)
                    rows = slice(CD * odd, CD * odd + CD)
                    nc.tensor.matmul(ring[k % RING][:, 0:CHUNK[i]], qT[rows, pair, t * P:(t + 1) * P],
                                     kT[rows, pair % 2, 512 * i:512 * i + CHUNK[i]], start=True, stop=True)\
                        .then_inc(scores, 1)

                def turn(n, i):
                    k = FILL_AT[("t", (n, i))]
                    wait_fill(k - 2)
                    pe.wait_ge(exps, b * UNITS * CHUNKS + n * CHUNKS + i + 1)
                    for t in range(4):
                        m = min(P, AUD - (4 * i + t) * P)
                        mm = nc.tensor.transpose(fill[k % 2][0:m, t * P:(t + 1) * P],
                                                 prob[:, (4 * i + t) * P:(4 * i + t) * P + m], ident[:, :])
                    mm.then_inc(fill_ps, 1)

                pe.wait_ge(out_read, b)
                pe.wait_ge(x_in, 64 * (b + 1))
                blocks = [(x[:, t, :], P) for t in range(TT)] + [(cx[0:TI, 0, :], TI)] + [
                    (cx[0:min(P, AUD - t * P), t + 1, :], min(P, AUD - t * P)) for t in range(AT)]
                at = 0
                for n, (src, m) in enumerate(blocks):
                    mm = nc.tensor.transpose(ring[n // 4][:, (n % 4) * P:(n % 4) * P + m], src, ident[0:m, 0:m])
                    if n % 4 == 3 or n == len(blocks) - 1:
                        mm.then_inc(turned, 1)
                pe.wait_ge(turned_act, 4 * (b + 1))
                pe.wait_ge(turned_dve, 2 * (b + 1))
                for p in range(HP):
                    mm = nc.tensor.matmul(ring[p // 2][:, (p % 2) * S:(p % 2 + 1) * S], w["q"][:, p * P:(p + 1) * P], xT[:, :],
                                          start=True, stop=True)
                    if p % 2:
                        mm.then_inc(q_ps, 1)
                for p in range(HP):
                    bank = (ring[4], ps_o)[p // 4]
                    off = (p % 4) * TI
                    nc.tensor.matmul(bank[:, off:off + TEXT], w["k"][:, p * P:(p + 1) * P], cT[:, 0:TEXT], start=True, stop=True)
                    mm = nc.tensor.matmul(bank[:, off + TEXT:off + TI], w["ki"][:, p * P:(p + 1) * P], cT[:, TEXT:TI],
                                          start=True, stop=True)
                mm.then_inc(kti_ps, 1)
                pe.wait_ge(q_sb, 4 * (b + 1))
                for i in range(2):
                    nc.tensor.matmul(ring[i][0:TEXT, :], cT[:, 0:TEXT], w["v"][:, 512 * i:512 * i + 512], start=True, stop=True)
                    mm = nc.tensor.matmul(ring[i][COL_I:COL_I + IMG, :], cT[:, TEXT:TI], w["vi"][:, 512 * i:512 * i + 512],
                                          start=True, stop=True)
                mm.then_inc(vcat_ps, 1)
                pe.wait_ge(vcat_sb, b + 1)
                pe.wait_ge(kti_sb, b + 1)
                for t in range(TT):
                    if t:
                        pe.wait_ge(ti_sb, TT * b + t)
                        pe.wait_ge(rel_sb, TT * b + t)
                    for h in range(CH):
                        p, odd = h // 2, h % 2
                        rows = slice(CD * odd, CD * odd + CD)
                        mm = nc.tensor.matmul(ring[2 * odd + p // 4][:, (p % 4) * TI:(p % 4 + 1) * TI],
                                              qT[rows, p, t * P:(t + 1) * P], kti[rows, p, :], start=True, stop=True)
                    mm.then_inc(ti_ps, 1)
                    for h in range(CH):
                        p, odd = h // 2, h % 2
                        rows = slice(CD * odd, CD * odd + CD)
                        mm = nc.tensor.matmul((ring[4], ps_o)[odd][:, p * NREL:(p + 1) * NREL],
                                              qT[rows, p, t * P:(t + 1) * P], relk[rows, :], start=True, stop=True)
                    mm.then_inc(rel_ps, 1)
                for i in range(CHUNKS):
                    project("k", 0, i)
                for i in range(CHUNKS):
                    project("v", 0, i)
                pe.wait_ge(ti_sb, TT * (b + 1))
                pe.wait_ge(rel_sb, TT * (b + 1))
                for i in range(CHUNKS):
                    score(0, i)
                for n in range(UNITS):
                    pair, odd, t = n // 4, n // 2 % 2, n % 2
                    for i in range(CHUNKS):
                        turn(n, i)
                        if n + 1 < UNITS:
                            score(n + 1, i)
                        if i < 2 and n % 4 < 3 and pair + 1 < HP:
                            j = 2 * (n % 4) + i
                            project("k" if j < CHUNKS else "v", pair + 1, j % CHUNKS)
                    wait_fill(FILL_AT[("t", (n, 0))], *[FILL_AT[("v", (pair, j))] for j in range(CHUNKS)])
                    if n % OGRP == 0:
                        pe.wait_ge(o_sb, b * (UNITS // OGRP) + n // OGRP)
                    for i in range(CHUNKS):
                        wait_fill(FILL_AT[("t", (n, i))])
                        for j in range(4):
                            kt = 4 * i + j
                            m = min(P, AUD - kt * P)
                            mm = nc.tensor.matmul(ps_o[:, (n % OGRP) * CD:(n % OGRP + 1) * CD], pT[0:m, i, j, :],
                                                  va[0:m, pair % 2, kt, odd * CD:(odd + 1) * CD],
                                                  start=(kt == 0), stop=(kt == AT - 1))
                    mm.then_inc(pv, 1)
                pe.wait_ge(cat_ready, b + 1)
                pe.wait_ge(exps, (b + 1) * UNITS * CHUNKS)

                def cat_products(i):
                    wait_fill(FILL_AT[("c", i)])
                    t, g = divmod(i, CH // 4)
                    for j in range(4):
                        h = 4 * g + j
                        mm = nc.tensor.matmul(ring[2 * t + h // 8][:, (h % 8) * CD:(h % 8 + 1) * CD], pcT[0:CAT, i % 2, j, :],
                                              vcat[0:CAT, h * CD:(h + 1) * CD], start=True, stop=True)
                    return mm

                for i in range(TT * CH // 4):
                    k = FILL_AT[("c", i)]
                    t, g = divmod(i, CH // 4)
                    wait_fill(k - 2)
                    for j in range(4):
                        mm = nc.tensor.transpose(fill[k % 2][0:CAT, j * P:(j + 1) * P], pcat[:, t, 4 * g + j, :], ident[:, :])
                    mm.then_inc(fill_ps, 1)
                    if i:
                        cat_products(i - 1)
                cat_products(TT * CH // 4 - 1).then_inc(cat_ps, 1)
                pe.wait_ge(o_ready, b + 1)
                for p in range(HP):
                    for t in range(TT):
                        mm = nc.tensor.transpose(ring[p // 2][:, (p % 2 * TT + t) * P:(p % 2 * TT + t + 1) * P],
                                                 oall[:, t, 2 * p:2 * p + 2, :].rearrange("p a d -> p (a d)"), ident[:, :])
                    if p % 2:
                        mm.then_inc(oT_ps, 1)
                pe.wait_ge(oT_sb, 4 * (b + 1))
                for t in range(TT):
                    for p in range(HP):
                        mm = nc.tensor.matmul(ps_o[:, t * D:(t + 1) * D], oT[:, p, t * P:(t + 1) * P], wo[:, p, :],
                                              start=(p == 0), stop=(p == HP - 1))
                mm.then_inc(out_ps, 1)

        def empty(eng, copy, name, b, i):
            what, arg, _ = FILL_LIST[i]
            bank = fill[i % 2]
            eng.wait_ge(fill_ps, b * len(FILL_LIST) + i + 1)
            if what == "k":
                pair, j = arg
                dst, src = kT[:, pair % 2, 512 * j:512 * j + CHUNK[j]], bank[:, 0:CHUNK[j]]
            elif what == "v":
                pair, j = arg
                dst, src = va[:, pair % 2, 4 * j:4 * j + 4, :].rearrange("p t d -> p (t d)"), bank[:, :]
                m = AUD - (AT - 1) * P
                if j == CHUNKS - 1:
                    copy(va[:, pair % 2, 4 * j:4 * j + 3, :].rearrange("p t d -> p (t d)"), bank[:, 0:3 * P])
                    dst, src = va[0:m, pair % 2, AT - 1, :], bank[0:m, 3 * P:]
            elif what == "t":
                n, j = arg
                dst, src = pT[:, j, :, :].rearrange("p t d -> p (t d)"), bank[:, :]
                if j == CHUNKS - 1:
                    m = AUD - (AT - 1) * P
                    copy(pT[:, j, 0:3, :].rearrange("p t d -> p (t d)"), bank[:, 0:3 * P])
                    dst, src = pT[0:m, j, 3, :], bank[0:m, 3 * P:]
            else:
                dst, src = pcT[0:CAT, arg % 2, :, :].rearrange("p t d -> p (t d)"), bank[0:CAT, :]
            copy(dst, src).then_inc(fill_sb[name], 1)

        @block.scalar
        def _(act):
            own = Chain(act, act_own)

            def copy(dst, src):
                return nc.scalar.activation(dst, src, ACT.Copy)

            act.wait_ge(weights_in, 16 * 11)
            own.link(nc.scalar.activation(gains[:, :], gains[:, :], ACT.Tanh))
            nc.scalar.activation(gains[:, :], gains[:, :], ACT.Identity, bias=ones[:, 0:1]).then_inc(gains_ready, 1)
            with act.Fori(0, B) as b:
                own.restart()
                act.wait_ge(turned, 4 * b + 1)
                for dst, src in ((xT[:, :], ring[0][:, 0:S]), (cT[:, 0:TI], ring[0][:, S:S + TI]),
                                 (cT[:, TI:TI + P], ring[0][:, 3 * P:])):
                    copy(dst, src).then_inc(turned_act, 1)
                act.wait_ge(turned, 4 * b + 2)
                copy(cT[:, TI + P:TI + 5 * P], ring[1][:, :]).then_inc(turned_act, 1)
                for i in range(4):
                    act.wait_ge(q_ps, 4 * b + i + 1)
                    nc.scalar.activation(qT[:, 2 * i:2 * i + 2, :], ring[i][:, :].rearrange("p (a n) -> p a n", a=2), ACT.Copy,
                                         scale=SCALE).then_inc(q_sb, 1)
                act.wait_ge(vcat_ps, b + 1)
                for i in range(2):
                    for lo, n in ((0, TEXT), (COL_I, IMG)):
                        ins = copy(vcat[lo:lo + n, 512 * i:512 * i + 512], ring[i][lo:lo + n, :])
                ins.then_inc(vcat_sb, 1)
                for t in range(TT):
                    act.wait_ge(ti_ps, TT * b + t + 1)
                    for i in range(4):
                        h = 8 * (i % 2) + i // 2
                        ins = copy(sti[:, t, h:h + 7:2, :], ring[i][:, 0:4 * TI].rearrange("p (a n) -> p a n", a=4))
                    ins.then_inc(ti_sb, 1)
                i = 0
                order = [k for k, f in enumerate(FILL_LIST) if f[2] == "act"]

                def empty_until(k):
                    while order and order[0] <= k:
                        empty(act, copy, "act", b, order.pop(0))

                empty_until(2 * CHUNKS - 1)
                for n in range(UNITS):
                    if n == STEP_EXP:
                        act.wait_ge(ti_sub, b + 1)
                        nc.scalar.activation(sti[:, :, :, :], sti[:, :, :, :], ACT.Exp).then_inc(ti_exp, 1)
                    act.wait_ge(maxed, b * UNITS + n + 1)
                    for i in range(CHUNKS):
                        nc.scalar.activation(prob[:, 512 * i:512 * i + CHUNK[i]],
                                             ring[(n * CHUNKS + i) % RING][:, 0:CHUNK[i]], ACT.Exp,
                                             bias=negmax[:, n % 2:n % 2 + 1], accum_out=sums[:, n, i:i + 1]).then_inc(exps, 1)
                    empty_until(FILL_AT[("t", (n, CHUNKS - 1))])
                empty_until(len(FILL_LIST))
                for i in range(4):
                    act.wait_ge(oT_ps, 4 * b + i + 1)
                    copy(oT[:, 2 * i:2 * i + 2, :], ring[i][:, :].rearrange("p (a n) -> p a n", a=2)).then_inc(oT_sb, 1)
                act.wait_ge(ln_stats, b + 1)
                own.link(nc.scalar.activation(rs[:, :], mv[:, :, 1], ACT.Ln, bias=eps[:, 0:1]))
                nc.scalar.activation(rs[:, :], rs[:, :], ACT.Exp, scale=-0.5).then_inc(ln_rs, 1)
                own.settle()

        @block.gpsimd
        def _(pool):
            own = Chain(pool, pool_own)
            nc.gpsimd.memset(pcat[:, :, :, :], 0.0).then_inc(cleared, 1)
            nc.gpsimd.memset(ext[:, :, :], 0.0).then_inc(cleared, 1)
            nc.gpsimd.memset(far[:, :, :], 0.0).then_inc(cleared, 1)
            pool.wait_ge(cleared, 3)
            nc.gpsimd.affine_select(out=far[:, 0, :], in_=far[:, 0, :], compare_op=ALU.is_gt, fill=1.0,
                                    base=REL, pattern=[[1, TEXT]], channel_multiplier=-1).then_inc(far_ready, 1)
            nc.gpsimd.affine_select(out=far[:, 1, :], in_=far[:, 1, :], compare_op=ALU.is_gt, fill=1.0,
                                    base=REL, pattern=[[-1, TEXT]], channel_multiplier=1).then_inc(far_ready, 1)
            pool.wait_ge(far_ready, 2)
            with pool.Fori(0, B) as b:
                own.restart()
                pool.wait_ge(ti_max, 2 * (b + 1))
                nc.gpsimd.tensor_tensor(sti[:, :, :, 0:TEXT], sti[:, :, :, 0:TEXT], bc(small[:, 0, :, :], 3, TEXT),
                                        ALU.subtract).then_inc(pool_own, 1)
                nc.gpsimd.tensor_tensor(sti[:, :, :, TEXT:], sti[:, :, :, TEXT:], bc(small[:, 1, :, :], 3, IMG),
                                        ALU.subtract).then_inc(ti_sub, 1)
                pool.wait_ge(ti_sum, b + 1)
                nc.gpsimd.tensor_tensor(pcat[:, :, :, COL_I:COL_I + IMG], sti[:, :, :, TEXT:], bc(small[:, 1, :, :], 3, IMG),
                                        ALU.mult).then_inc(pool_own, 1)
                nc.gpsimd.tensor_tensor(pcat[:, :, :, 0:TEXT], sti[:, :, :, 0:TEXT], bc(small[:, 0, :, :], 3, TEXT),
                                        ALU.mult).then_inc(ti_prob, 1)
                pool.wait_ge(pool_own, 2)
                pool.wait_ge(ti_prob, b + 1)
                for i in range(2):
                    nc.gpsimd.tensor_tensor(rel[:, i, :, :], pcat[:, 0, :, 0:TEXT], bc(far[:, i, :], 1, CH), ALU.mult)\
                        .then_inc(far_prob, 1)

        @block.vector
        def _(dve):
            own = Chain(dve, dve_own)

            def copy(dst, src):
                return nc.vector.tensor_copy(dst, src)

            dve.wait_ge(weights_in, 16 * 11)
            dve.wait_ge(gains_ready, 1)
            dve.wait_ge(zeroed, 16)
            with dve.Fori(0, B) as b:
                own.restart()
                for i in range(2, 4):
                    dve.wait_ge(turned, 4 * b + i + 1)
                    lo = TI + P + 512 * (i - 1)
                    copy(cT[:, lo:min(lo + 512, CTX)], ring[i][:, 0:min(512, CTX - lo)]).then_inc(turned_dve, 1)
                dve.wait_ge(kti_ps, b + 1)
                for i in range(2):
                    ins = copy(kti[:, 4 * i:4 * i + 4, :], (ring[4], ps_o)[i][:, 0:4 * TI].rearrange("p (a n) -> p a n", a=4))
                ins.then_inc(kti_sb, 1)
                dve.wait_ge(rel_ps, TT * b + 1)
                dve.wait_ge(skewed_out, 16 * b)
                lo = P - 1 - REL
                for odd in range(2):
                    src = (ring[4], ps_o)[odd][:, 0:HP * NREL].rearrange("p (a n) -> p a n", a=HP)
                    nc.vector.tensor_copy(ext[:, odd::2, lo:lo + NREL], src)
                    nc.vector.tensor_copy(ext[:, odd::2, 0:lo], src[:, :, 0:1].broadcast_to([P, HP, lo]))
                    ins = nc.vector.tensor_copy(ext[:, odd::2, lo + NREL:],
                                                src[:, :, NREL - 1:].broadcast_to([P, HP, e_w - lo - NREL]))
                ins.then_inc(rel_sb, 1)
                dve.wait_ge(rel_ps, TT * b + 2)
                for odd in range(2):
                    src = (ring[4], ps_o)[odd][:, 0:HP * NREL].rearrange("p (a n) -> p a n", a=HP)
                    ins = nc.vector.tensor_copy(near[:, odd::2], src[:, :, 0])
                ins.then_inc(rel_sb, 1)
                order = [k for k, f in enumerate(FILL_LIST) if f[2] == "dve"]

                def empty_next():
                    empty(dve, copy, "dve", b, order.pop(0))

                def chunk_max(n, i):
                    k = n * CHUNKS + i
                    dve.wait_ge(scores, b * UNITS * CHUNKS + k + 1)
                    own.count(nc.vector.tensor_reduce(max3[:, n % 2, i:i + 1], ring[k % RING][:, 0:CHUNK[i]], AX, ALU.max))
                    if i == CHUNKS - 1:
                        own.settle()
                        nc.vector.tensor_reduce(negmax[:, n % 2:n % 2 + 1], max3[:, n % 2, :], AX, ALU.max, negate=True)\
                            .then_inc(maxed, 1)

                def text_scores():
                    dve.wait_ge(skewed_in, 16 * (b + 1))
                    dve.wait_ge(ti_sb, TT * (b + 1))
                    own.count(nc.vector.tensor_tensor(sti[:, 0, :, 0:TEXT], sti[:, 0, :, 0:TEXT], rel[:, 0, :, :], ALU.add))
                    dve.wait_ge(rel_sb, TT * (b + 1))
                    own.link(nc.vector.tensor_tensor(sti[:, 1, :, 0:TEXT], sti[:, 1, :, 0:TEXT], bc(near[:, :], 2, TEXT), ALU.add))

                def text_max():
                    nc.vector.tensor_reduce(small[:, 0, :, :], sti[:, :, :, 0:TEXT], AX, ALU.max).then_inc(ti_max, 1)
                    nc.vector.tensor_reduce(small[:, 1, :, :], sti[:, :, :, TEXT:], AX, ALU.max).then_inc(ti_max, 1)

                def text_sum():
                    dve.wait_ge(ti_exp, b + 1)
                    own.count(nc.vector.tensor_reduce(small[:, 0, :, :], sti[:, :, :, 0:TEXT], AX, ALU.add))
                    own.link(nc.vector.tensor_reduce(small[:, 1, :, :], sti[:, :, :, TEXT:], AX, ALU.add))
                    own.link(nc.vector.reciprocal(small[:, :, :, :], small[:, :, :, :]))
                    nc.vector.tensor_scalar(small[:, 1, :, :], small[:, 1, :, :], gains[:, 0:1], None, ALU.mult)\
                        .then_inc(ti_sum, 1)

                def far_sums():
                    dve.wait_ge(far_prob, 2 * (b + 1))
                    dve.wait_ge(band_in, 32 * (b + 1))
                    nc.vector.tensor_reduce(pcat[:, 0, :, COL_R1], rel[:, 0, :, :], AX, ALU.add)
                    own.count(nc.vector.tensor_reduce(pcat[:, 0, :, CAT - 1], rel[:, 1, :, :], AX, ALU.add))
                    nc.vector.tensor_reduce(pcat[:, 1, :, COL_R1], pcat[:, 1, :, 0:TEXT], AX, ALU.add).then_inc(cat_ready, 1)

                steps = {STEP_SCORES: text_scores, STEP_SCORES + 1: text_max, STEP_SUM: text_sum, STEP_FAR: far_sums}
                while order and order[0] < 2 * CHUNKS:
                    empty_next()
                for i in range(CHUNKS):
                    chunk_max(0, i)
                for n in range(UNITS):
                    for i in range(CHUNKS):
                        if order and order[0] == FILL_AT[("t", (n, i))]:
                            empty_next()
                        if n + 1 < UNITS:
                            chunk_max(n + 1, i)
                        stop = FILL_AT[("t", (n, i + 1))] if i + 1 < CHUNKS else FILL_AT[("t", (n, i))] + 1
                        while order and order[0] < stop:
                            empty_next()
                    if n % OGRP == OGRP - 1:
                        dve.wait_ge(pv, b * UNITS + n + 1)
                        h = (n + 1 - OGRP) // TT
                        copy(oall[:, :, h:h + OGRP // TT, :].rearrange("p t h d -> p h t d"),
                             ps_o[:, :].rearrange("p (h t d) -> p h t d", t=TT, d=CD)).then_inc(o_sb, 1)
                    if n in steps:
                        steps[n]()
                dve.wait_ge(exps, (b + 1) * UNITS * CHUNKS)
                own.link(nc.vector.tensor_reduce(rsum[:, :], sums[:, :, :], AX, ALU.add))
                own.link(nc.vector.reciprocal(rsum[:, :], rsum[:, :]))
                own.link(nc.vector.tensor_scalar(rsum[:, :], rsum[:, :], gains[:, 1:2], None, ALU.mult))
                dve.wait_ge(o_sb, (b + 1) * (UNITS // OGRP))
                every = oall[:, :, :, :].rearrange("p t h d -> p h t d")
                own.link(nc.vector.tensor_tensor(every, every, bc(rsum[:, :].rearrange("p (h t) -> p h t", t=TT), 3, CD),
                                                 ALU.mult))
                while order:
                    empty_next()
                dve.wait_ge(cat_ps, b + 1)
                for i in range(4):
                    t, half = divmod(i, 2)
                    dst = oall[:, t, 8 * half:8 * half + 8, :]
                    ins = nc.vector.tensor_tensor(dst, dst, ring[i][:, :].rearrange("p (a d) -> p a d", d=CD), ALU.add)
                ins.then_inc(o_ready, 1)
                own.link(nc.vector.tensor_tensor(r[:, :, :], x[:, :, :], bc(bo[:, :], 1, TT), ALU.add))
                dve.wait_ge(out_ps, b + 1)
                nc.vector.tensor_tensor(r[:, :, :], r[:, :, :], ps_o[:, 0:TT * D].rearrange("p (t d) -> p t d", t=TT), ALU.add)\
                    .then_inc(out_read, 1)
                dve.wait_ge(out_read, b + 1)
                layernorm(nc, dve, own, r, stats, mv, rs, x5, b, ln_stats, ln_rs, x5_ready, stored)
                own.settle()


TOK = B * S
NT = TOK // P
MT = 4
GW = MT * P
MG = NT // MT
CAP = TOK // NE
BITS = 30


def moe_route(nc, T, const, m):
    ident, ident16, causal16, ones, eps = const
    with ExitStack() as stack:
        c = Scope(nc, stack, "route")
        ws = c.sb("ws", [P, NE])
        bs = c.sb("bs", [P, NE])
        x = [c.sb(f"x{i}", [P, MT, D]) for i in range(2)]
        xs = [c.sb(f"xs{i}", [P, GW]) for i in range(2)]
        logit = c.sb("logit", [P, NT, NE])
        top = c.sb("top", [P, NT])
        ps_x = [c.ps(f"ps_x{i}", [P, GW]) for i in range(2)]
        ps_l = [c.ps(f"ps_l{i}", [P, MT, NE]) for i in range(2)]
        weights_in = c.sem("weights_in")
        x_in = [c.sem(f"x_in{i}") for i in range(2)]
        x_ps = c.sem("x_ps")
        xs_ready = c.sem("xs_ready")
        kept = c.sem("kept")
        l_ps = c.sem("l_ps")
        l_sb = c.sem("l_sb")
        shifted = c.sem("shifted")
        powers = c.sem("powers")
        dve_own = c.sem("dve_own")
        block = c.block()

        @block.sync
        def _(sp):
            sp.dma_start(ws[:, :], T["moe_ws"]).then_inc(weights_in, 16)
            sp.dma_start(bs[:, :], T["moe_bs"]).then_inc(weights_in, 16)
            tiles = T["x5"].rearrange("b (t p) d -> p (b t) d", p=P)
            with sp.Fori(0, MG // 2) as i:
                for h in range(2):
                    sp.wait_ge(x_ps, i * 2)
                    sp.wait_ge(kept, i * 2)
                    sp.dma_start(x[h][:, :, :], tiles[:, bass.ds(i * (2 * MT) + h * MT, MT), :]).then_inc(x_in[h], 16)

        @block.tensor
        def _(pe):
            pe.wait_ge(weights_in, 32)
            with pe.Fori(0, MG // 2) as i:
                for h in range(2):
                    pe.wait_ge(x_in[h], i * 16 + 16)
                    for t in range(MT):
                        mm = nc.tensor.transpose(ps_x[h][:, t * P:(t + 1) * P], x[h][:, t, :], ident[:, :])
                    mm.then_inc(x_ps, 1)
                    pe.wait_ge(xs_ready, i * 2 + h + 1)
                    pe.wait_ge(l_sb, i * 2)
                    for t in range(MT):
                        mm = nc.tensor.matmul(ps_l[h][:, t, :], xs[h][:, t * P:(t + 1) * P], ws[:, :],
                                              start=(t == 0), stop=True, skip_group_check=True)
                    mm.then_inc(l_ps, 1)

        @block.scalar
        def _(act):
            with act.Fori(0, MG // 2) as i:
                for h in range(2):
                    act.wait_ge(x_ps, i * 2 + h + 1)
                    act.wait_ge(m["xT_kept"], i * 2)
                    nc.scalar.activation(xs[h][:, :], ps_x[h][:, :], ACT.Copy).then_inc(xs_ready, 1)
            act.wait_ge(shifted, 1)
            nc.scalar.activation(logit[:, :, :], logit[:, :, :], ACT.Exp).then_inc(powers, 1)

        @block.gpsimd
        def _(pool):
            with pool.Fori(0, MG // 2) as i:
                for h in range(2):
                    hold(pool, x_in[h], i * 16 + 16)
                    nc.gpsimd.tensor_copy(m["x"][:, bass.ds(i * (2 * MT) + h * MT, MT), :], x[h][:, :, :]).then_inc(kept, 1)

        @block.vector
        def _(dve):
            own = Chain(dve, dve_own)
            dve.wait_ge(weights_in, 32)
            with dve.Fori(0, MG // 2) as i:
                for h in range(2):
                    dve.wait_ge(xs_ready, i * 2 + h + 1)
                    nc.vector.tensor_copy(m["xT"][:, bass.ds(i * (2 * GW) + h * GW, GW)], xs[h][:, :]).then_inc(m["xT_kept"], 1)
                    dve.wait_ge(l_ps, i * 2 + h + 1)
                    nc.vector.tensor_tensor(logit[:, bass.ds(i * (2 * MT) + h * MT, MT), :], ps_l[h][:, :, :],
                                            bc(bs[:, :], 1, MT), ALU.add).then_inc(l_sb, 1)
            dve.wait_ge(l_sb, MG)
            own.link(nc.vector.tensor_reduce(top[:, :], logit[:, :, :], axis=AX, op=ALU.max))
            nc.vector.tensor_tensor(logit[:, :, :], logit[:, :, :], bc(top[:, :], 2, NE), ALU.subtract).then_inc(shifted, 1)
            dve.wait_ge(powers, 1)
            own.link(nc.vector.tensor_reduce(top[:, :], logit[:, :, :], axis=AX, op=ALU.add))
            own.link(nc.vector.reciprocal(top[:, :], top[:, :]))
            own.link(nc.vector.tensor_tensor(m["prob"].rearrange("p e t -> p t e"), logit[:, :, :], bc(top[:, :], 2, NE), ALU.mult))


def moe_choose(nc, T, const, m):
    ident, ident16, causal16, ones, eps = const
    with ExitStack() as stack:
        c = Scope(nc, stack, "choose")
        bit = c.sb("bit", [P, NE])
        thr = c.sb("thr", [P, NE])
        cand = c.sb("cand", [P, NE])
        passed = c.sb("passed", [P, NE])
        count = c.sb("count", [P, NE])
        over = c.sb("over", [P, NE, NT])
        equal = c.sb("equal", [P, NE, NT])
        later = c.sb("later", [P, NE, NT])
        total = c.sb("total", [P, NE, NT])
        rank = c.sb("rank", [P, NE, NT])
        below = c.sb("below", [P, P])
        ps_c = c.ps("ps_c", [P, NE])
        ps_b = c.ps("ps_b", [P, NE, NT])
        ps_t = c.ps("ps_t", [P, NE, NT])
        filled = c.sem("filled")
        counted = c.sem("counted")
        summed = c.sem("summed")
        tied = c.sem("tied")
        ranked = c.sem("ranked")
        dve_own = c.sem("dve_own")
        block = c.block()
        prob = m["prob"]

        @block.gpsimd
        def _(pool):
            nc.gpsimd.memset(bit[:, :], 2.0).then_inc(filled, 1)
            nc.gpsimd.memset(thr[:, :], 0.0).then_inc(filled, 1)
            nc.gpsimd.memset(later[:, :, :], 1.0).then_inc(filled, 1)
            nc.gpsimd.memset(below[:, :], 1.0).then_inc(filled, 1)
            pool.wait_ge(filled, 4)
            nc.gpsimd.memset(later[:, :, 0:1], 0.0).then_inc(filled, 1)
            nc.gpsimd.affine_select(out=below[:, :], in_=below[:, :], compare_op=ALU.is_gt, fill=0.0,
                                    base=0, pattern=[[1, P]], channel_multiplier=-1).then_inc(filled, 1)
            pool.wait_ge(filled, 6)

        @block.tensor
        def _(pe):
            with pe.Fori(0, BITS + 1) as i:
                pe.wait_ge(counted, i + 1)
                nc.tensor.matmul(ps_c[:, :], ones[:, :], count[:, :], start=True, stop=True).then_inc(summed, 1)
            pe.wait_ge(filled, 6)
            pe.wait_ge(tied, 1)
            nc.tensor.matmul(ps_b[:, :, :], below[:, :], equal[:, :, :], start=True, stop=True).then_inc(ranked, 1)
            nc.tensor.matmul(ps_t[:, :, :], ones[:, :], equal[:, :, :], start=True, stop=True).then_inc(ranked, 1)

        @block.vector
        def _(dve):
            own = Chain(dve, dve_own)
            dve.wait_ge(filled, 6)
            with dve.Fori(0, BITS) as i:
                own.restart()
                own.link(nc.vector.tensor_scalar(bit.bitcast(U32)[:, :], bit.bitcast(U32)[:, :], 1, None, ALU.logical_shift_right))
                own.link(nc.vector.tensor_tensor(cand.bitcast(U32)[:, :], thr.bitcast(U32)[:, :], bit.bitcast(U32)[:, :], ALU.bitwise_or))
                own.link(nc.vector.tensor_tensor(over[:, :, :], prob[:, :, :], bc(cand[:, :], 2, NT), ALU.is_ge))
                nc.vector.tensor_reduce(count[:, :], over[:, :, :], axis=AX, op=ALU.add).then_inc(counted, 1)
                dve.wait_ge(summed, i + 1)
                own.link(nc.vector.scalar_tensor_tensor(passed[:, :], ps_c[:, :], CAP - 0.5, cand[:, :], ALU.is_ge, ALU.mult))
                own.link(nc.vector.tensor_tensor(thr[:, :], thr[:, :], passed[:, :], ALU.max))
            own.restart()
            own.link(nc.vector.tensor_tensor(equal[:, :, :], prob[:, :, :], bc(thr[:, :], 2, NT), ALU.is_equal))
            nc.vector.tensor_tensor(over[:, :, :], prob[:, :, :], bc(thr[:, :], 2, NT), ALU.is_gt).then_inc(tied, 1)
            dve.wait_ge(tied, 1)
            nc.vector.tensor_reduce(count[:, :], over[:, :, :], axis=AX, op=ALU.add).then_inc(counted, 1)
            dve.wait_ge(ranked, 2)
            own.link(nc.vector.tensor_copy(total[:, :, :], ps_t[:, :, :]))
            own.link(nc.vector.tensor_tensor_scan(rank.rearrange("p e t -> p (e t)"), later.rearrange("p e t -> p (e t)"),
                                                  total.rearrange("p e t -> p (e t)"), 0.0, ALU.mult, ALU.add))
            own.link(nc.vector.tensor_tensor(rank[:, :, :], rank[:, :, :], total[:, :, :], ALU.subtract))
            own.link(nc.vector.tensor_tensor(rank[:, :, :], rank[:, :, :], ps_b[:, :, :], ALU.add))
            dve.wait_ge(summed, BITS + 1)
            own.link(nc.vector.tensor_scalar(count[:, :], ps_c[:, :], -1.0, float(CAP), ALU.mult, ALU.add))
            own.link(nc.vector.tensor_tensor(rank[:, :, :], rank[:, :, :], bc(count[:, :], 2, NT), ALU.is_lt))
            own.link(nc.vector.tensor_tensor(rank[:, :, :], rank[:, :, :], equal[:, :, :], ALU.mult))
            own.link(nc.vector.tensor_tensor(rank[:, :, :], rank[:, :, :], over[:, :, :], ALU.add))
            own.link(nc.vector.tensor_tensor(prob[:, :, :], prob[:, :, :], rank[:, :, :], ALU.mult))


def moe_experts(nc, T, const, m):
    with ExitStack() as stack:
        c = Scope(nc, stack, "experts")
        w1 = [c.sb(f"w1{i}", [P, DF]) for i in range(2)]
        w2 = [c.sb(f"w2{i}", [P, FC, D]) for i in range(2)]
        b1 = [c.sb(f"b1{i}", [P, FC]) for i in range(2)]
        hT = c.sb("hT", [P, FC, GW])
        ps_h = [c.ps(f"ps_h{i}", [P, GW]) for i in range(FC)]
        ps_y = [c.ps(f"ps_y{i}", [P, MT, D]) for i in range(2)]
        expert_in = [c.sem(f"expert_in{i}") for i in range(2)]
        used = c.sem("used")
        h_ps = c.sem("h_ps")
        h_sb = c.sem("h_sb")
        y_ps = c.sem("y_ps")
        y_free = c.sem("y_free")
        block = c.block()

        @block.sync
        def _(sp):
            with sp.Fori(0, NE // 2) as e2:
                for k in range(2):
                    e = e2 * 2 + k
                    sp.wait_ge(used, e2 * 2 + (k + 1))
                    sp.dma_start(w1[k][:, :], T["moe_w1"][bass.ds(e, 1)].rearrange("e p f -> p (e f)")).then_inc(expert_in[k], 16)
                    sp.dma_start(w2[k][:, :, :], T["moe_w2"][bass.ds(e, 1)].rearrange("e (c p) d -> p (e c) d", p=P))\
                        .then_inc(expert_in[k], 16)
                    sp.dma_start(b1[k][:, :], T["moe_b1"][bass.ds(e, 1)].rearrange("e p f -> p (e f)")).then_inc(expert_in[k], 16)

        @block.tensor
        def _(pe):
            with pe.Fori(0, NE // 2) as e2:
                for k in range(2):
                    hold(pe, expert_in[k], e2 * 48 + 48)
                    with pe.Fori(0, MG // 2) as i:
                        for g in range(2):
                            step = e2 * (2 * MG) + i * 2 + (k * MG + g)
                            for f in range(FC):
                                nc.tensor.matmul(ps_h[f][:, :], w1[k][:, f * P:(f + 1) * P],
                                                 m["xT"][:, bass.ds(i * (2 * GW) + g * GW, GW)], start=True, stop=True)\
                                    .then_inc(h_ps, 1)
                            pe.wait_ge(y_free, (step + 1) * MT)
                            for f in range(FC):
                                pe.wait_ge(h_sb, step * FC + f + 1)
                                for t in range(MT):
                                    mm = nc.tensor.matmul(ps_y[g][:, t, :], hT[:, f, t * P:(t + 1) * P], w2[k][:, f, :],
                                                          start=(f == 0 and t == 0), stop=(f == FC - 1), skip_group_check=True)
                            mm.then_inc(y_ps, 1)

        @block.scalar
        def _(act):
            with act.Fori(0, NE // 2) as e2:
                for k in range(2):
                    act.wait_ge(expert_in[k], e2 * 48 + 48)
                    with act.Fori(0, MG) as g:
                        step = e2 * (2 * MG) + g + k * MG
                        for f in range(FC):
                            act.wait_ge(h_ps, step * FC + f + 1)
                            nc.scalar.activation(hT[:, f, :], ps_h[f][:, :], ACT.Gelu_apprx_tanh, bias=b1[k][:, f:f + 1])\
                                .then_inc(h_sb, 1)

        @block.vector
        def _(dve):
            dve.sem_inc(y_free, 2 * MT)
            dve.sem_inc(used, 2)
            with dve.Fori(0, NE) as e:
                with dve.Fori(0, MG // 2) as i:
                    for g in range(2):
                        step = e * MG + i * 2 + g
                        dve.wait_ge(y_ps, step + 1)
                        dve.wait_ge(y_free, (step + 2) * MT)
                        for t in range(MT):
                            xt = m["x"][:, bass.ds(i * (2 * MT) + g * MT + t, 1), :].rearrange("p o d -> p (o d)")
                            nc.vector.scalar_tensor_tensor(
                                xt, ps_y[g][:, t, :],
                                m["prob"].rearrange("p e t -> p (e t)")[:, bass.ds(e * NT + i * (2 * MT) + (g * MT + t), 1)],
                                xt, ALU.mult, ALU.add).then_inc(y_free, 1)
                dve.sem_inc(used, 1)


def moe_finish(nc, T, const, m):
    ident, ident16, causal16, ones, eps = const
    with ExitStack() as stack:
        c = Scope(nc, stack, "finish")
        b2 = c.sb("b2", [NE, D])
        w = c.sb("w", [P, MT, NE])
        wT = c.sb("wT", [NE, GW])
        r = c.sb("r", [P, MT, D])
        stats = c.sb("stats", [P, MT, 6])
        mv = c.sb("mv", [P, MT, 2])
        rs = c.sb("rs", [P, MT])
        out = c.sb("out", [P, MT, D])
        ps_w = c.ps("ps_w", [NE, GW])
        ps_b = c.ps("ps_b", [P, MT, D])
        b2_in = c.sem("b2_in")
        w_ready = c.sem("w_ready")
        w_ps = c.sem("w_ps")
        wT_ready = c.sem("wT_ready")
        b_ps = c.sem("b_ps")
        ln_stats = c.sem("ln_stats")
        ln_rs = c.sem("ln_rs")
        out_ready = c.sem("out_ready")
        stored = c.sem("stored")
        dve_own = c.sem("dve_own")
        act_own = c.sem("act_own")
        block = c.block()

        @block.sync
        def _(sp):
            sp.dma_start(b2[:, :], T["moe_b2"]).then_inc(b2_in, 16)
            tiles = T["out"].rearrange("b (t p) d -> p (b t) d", p=P)
            with sp.Fori(0, MG) as g:
                sp.wait_ge(out_ready, g + 1)
                sp.dma_start(tiles[:, bass.ds(g * MT, MT), :], out[:, :, :]).then_inc(stored, 16)
            sp.wait_ge(stored, 16 * MG)

        @block.tensor
        def _(pe):
            pe.wait_ge(b2_in, 16)
            with pe.Fori(0, MG) as g:
                pe.wait_ge(w_ready, g + 1)
                for t in range(MT):
                    mm = nc.tensor.transpose(ps_w[:, t * P:(t + 1) * P], w[:, t, :], ident[:, :])
                mm.then_inc(w_ps, 1)
                pe.wait_ge(wT_ready, g + 1)
                for t in range(MT):
                    mm = nc.tensor.matmul(ps_b[:, t, :], wT[:, t * P:(t + 1) * P], b2[:, :], start=(t == 0), stop=True,
                                          skip_group_check=True)
                mm.then_inc(b_ps, 1)

        @block.scalar
        def _(act):
            own = Chain(act, act_own)
            with act.Fori(0, MG) as g:
                own.restart()
                act.wait_ge(w_ps, g + 1)
                nc.scalar.activation(wT[:, :], ps_w[:, :], ACT.Copy).then_inc(wT_ready, 1)
                act.wait_ge(ln_stats, g + 1)
                own.link(nc.scalar.activation(rs[:, :], mv[:, :, 1], ACT.Ln, bias=eps[:, 0:1]))
                nc.scalar.activation(rs[:, :], rs[:, :], ACT.Exp, scale=-0.5).then_inc(ln_rs, 1)
                own.settle()

        @block.vector
        def _(dve):
            own = Chain(dve, dve_own)
            with dve.Fori(0, MG) as g:
                own.restart()
                nc.vector.tensor_copy(w[:, :, :], m["prob"].rearrange("p e t -> p t e")[:, bass.ds(g * MT, MT), :])\
                    .then_inc(w_ready, 1)
                dve.wait_ge(b_ps, g + 1)
                own.link(nc.vector.tensor_tensor(r[:, :, :], m["x"][:, bass.ds(g * MT, MT), :], ps_b[:, :, :], ALU.add))
                layernorm(nc, dve, own, r, stats, mv, rs, out, g, ln_stats, ln_rs, out_ready, stored, MT)
                own.settle()


def moe_stage(nc, T, const):
    with ExitStack() as stack:
        c = Scope(nc, stack, "moe")
        m = {"x": c.sb("x", [P, NT, D]), "xT": c.sb("xT", [P, TOK]), "prob": c.sb("prob", [P, NE, NT]),
             "xT_kept": c.sem("xT_kept")}
        moe_route(nc, T, const, m)
        moe_choose(nc, T, const, m)
        moe_experts(nc, T, const, m)
        moe_finish(nc, T, const, m)


def layout(a):
    import numpy as np

    def t(w):
        return np.ascontiguousarray(np.asarray(w).T)

    def rows(w):
        return np.ascontiguousarray(w.reshape(-1, P, w.shape[-1]).transpose(1, 0, 2))

    def every(v):
        return np.ascontiguousarray(np.broadcast_to(np.asarray(v).reshape(1, -1), (P, np.asarray(v).size)))

    def halves(v):
        return np.asarray(v).reshape(HALF, P).T

    L = {"x": np.asarray(a["x"]), "ctx": np.asarray(a["ctx_1024"])}
    L["w_in"] = t(a["L0_attn_W_in"])
    L["w_x"] = rows(t(a["L0_attn_W_x"]))
    L["w_dt"] = rows(t(a["L0_attn_W_dt"]))
    L["w_out"] = rows(t(a["L0_attn_W_out"]))
    L["conv_w"] = np.ascontiguousarray(np.asarray(a["L0_attn_conv_w"]).reshape(HALF, P, TAPS).transpose(1, 0, 2))
    L["scan_vec"] = np.ascontiguousarray(np.stack(
        [halves(a[f"L0_attn_{n}"]) for n in ("conv_b", "b_dt", "D_param", "ln_g", "ln_b")], axis=1))
    L["a_log"] = every(a["L0_attn_A_log"])
    for name in ("q", "k"):
        w = np.asarray(a[f"L0_xattn_W{name}"])
        pad = np.zeros((P, GH, P), w.dtype)
        for h in range(AH):
            pad[h * AD:(h + 1) * AD, h // JH, 32 * (h % JH):32 * (h % JH) + AD] = w.T
        L[f"w{name}_pad"] = pad
    w = np.asarray(a["L0_xattn_Wv"])
    pad = np.zeros((P, P), w.dtype)
    for h in range(AH):
        pad[h * AD:(h + 1) * AD, h * AD:(h + 1) * AD] = w.T
    L["wv_bd"] = pad
    L["wo"] = t(a["L0_xattn_Wo"])
    L["bo"] = every(a["L0_xattn_bo"])
    L["wr"] = np.asarray(a["L0_ffn_Wr"])
    L["br"] = np.asarray(a["L0_ffn_br"]).reshape(1, NE)
    L["ffn_w1"] = np.asarray(a["L0_ffn_W1"])
    L["ffn_b1"] = np.ascontiguousarray(np.asarray(a["L0_ffn_b1"]).reshape(NE, FC, P).transpose(0, 2, 1))
    L["ffn_w2"] = np.asarray(a["L0_ffn_W2"])
    L["ffn_b2"] = np.ascontiguousarray(np.broadcast_to(np.asarray(a["L0_ffn_b2"])[:, None, :], (NE, P, D)))
    names = ("k", "q", "v")
    pad = np.zeros((P, PLANES, 2 * WIN + DH), np.float32)
    bias = np.zeros((P, PLANES), np.float32)
    taps = np.zeros((P, 3 * DW, TAPS), np.float32)
    for i, n in enumerate(names):
        w, wb, wc = (np.asarray(a[f"L1_attn_{x}{n}"]) for x in ("W", "b", "conv_"))
        for d in range(DW):
            pad[:, i * DW + d, WIN:WIN + DH] = w[d::DW].T
            for s in range(GB):
                bias[s * DH:(s + 1) * DH, i * DW + d] = wb[d::DW]
                taps[s * DH:(s + 1) * DH, i * DW + d] = wc[d::DW]
    pad[:, 3 * DW, WIN:WIN + DH] = np.asarray(a["L1_attn_Wbeta"]).T
    for s in range(GB):
        bias[s * DH:(s + 1) * DH, 3 * DW] = np.asarray(a["L1_attn_bbeta"])
    L["delta_w"], L["delta_bias"], L["delta_taps"] = pad, bias, taps
    time = np.arange(1, S + 1, dtype=np.float64)
    coef = np.stack([time / (time + 1), (time - 1) / (time + 1), 2 / (time + 1)])
    coef[0, 0] = 0
    L["coef"] = np.ascontiguousarray(np.broadcast_to(coef.astype(np.float32), (P, 3, S)))
    L["rms"] = every(a["L1_attn_rms_w"])
    L["delta_out"] = np.ascontiguousarray(np.asarray(a["L1_attn_Wout"]).T.reshape(DH, DW, D))
    L["bout"] = every(a["L1_attn_bout"])
    for n, ref in (("q", "q"), ("k", "k"), ("v", "v"), ("ki", "k_ip"), ("vi", "v_ip"), ("ka", "k_ap"), ("va", "v_ap")):
        L[f"cross_{n}"] = np.asarray(a[f"L1_xattn_W{ref}"])
    L["cross_o"] = rows(np.asarray(a["L1_xattn_Wo"]))
    L["cross_bo"] = every(a["L1_xattn_bo"])
    relk = np.asarray(a["L1_xattn_rel_k"]).T
    L["relk"] = np.concatenate([relk, relk])
    L["relv"] = np.asarray(a["L1_xattn_rel_v"])
    L["gains"] = np.ascontiguousarray(np.broadcast_to(np.stack([a["L1_xattn_alpha"], a["L1_xattn_beta"]]), (P, 2)))
    L["moe_ws"] = np.asarray(a["L1_ffn_Ws"])
    L["moe_bs"] = every(a["L1_ffn_bs"])
    L["moe_w1"] = np.asarray(a["L1_ffn_W1"])
    L["moe_b1"] = np.ascontiguousarray(np.asarray(a["L1_ffn_b1"]).reshape(NE, FC, P).transpose(0, 2, 1))
    L["moe_w2"] = np.asarray(a["L1_ffn_W2"])
    L["moe_b2"] = np.asarray(a["L1_ffn_b2"])
    return L


def program(nc, T):
    with ExitStack() as stack:
        const = constants(nc, stack)
        scan_stage(nc, T, const)
        self_stage(nc, T, const)
        ffn_stage(nc, T, const)
        delta_stage(nc, T, const)
        cross_stage(nc, T, const)
        moe_stage(nc, T, const)


def kernel(**inputs):
    import numpy as np
    import concourse.bacc as bacc
    from concourse.bass_utils import run_bass_kernel_spmd

    nc = bacc.Bacc("TRN2", target_bir_lowering=False, num_devices=1)
    arrays, T = {}, {}
    for name, a in layout(inputs).items():
        arrays[f"in_{name}_dram"] = np.ascontiguousarray(a)
        T[name] = nc.dram_tensor(f"in_{name}_dram", a.shape, mybir.dt.from_np(a.dtype), kind="ExternalInput").ap()
    for name in ("x1", "x2", "x3", "x4", "x5"):
        T[name] = nc.dram_tensor(f"{name}_dram", (B, S, D), F32, kind="Internal").ap()
    for name, shape in SCRATCH.items():
        T[name] = nc.dram_tensor(f"{name}_dram", shape, F32, kind="Internal").ap()
    T["out"] = nc.dram_tensor("out_0_dram", (B, S, D), F32, kind="ExternalOutput").ap()
    program(nc, T)
    r = run_bass_kernel_spmd(nc, [arrays], core_ids=[0])
    return r.results[0]["out_0_dram"]
```

```python
from contextlib import ExitStack

import concourse.bass as bass
from concourse import mybir

F32 = mybir.dt.float32
F32R = mybir.dt.float32r
BF16 = mybir.dt.bfloat16
U32 = mybir.dt.uint32
I32 = mybir.dt.int32
ALU = mybir.AluOpType
ACT = mybir.ActivationFunctionType
AX = mybir.AxisListType.X

P = 128
B = 16
S = 256
D = 128
TT = S // P
CTX = 1601
LN_EPS = 1e-5
NEG = -1e30


class Scope:

    def __init__(self, nc, stack, tag):
        self.nc, self.stack, self.tag, self.sems = nc, stack, tag, []

    def sb(self, name, shape, dt=F32):
        return self.stack.enter_context(self.nc.sbuf_tensor(f"{self.tag}_{name}", shape, dt))

    def ps(self, name, shape, dt=F32):
        return self.stack.enter_context(self.nc.psum_tensor(f"{self.tag}_{name}", shape, dt))

    def sem(self, name):
        sem = self.stack.enter_context(self.nc.semaphore(f"{self.tag}_{name}"))
        self.sems.append(sem)
        return sem

    def block(self):
        self.stack.callback(self.clear)
        return self.stack.enter_context(self.nc.Block())

    def clear(self):
        with self.nc.Block() as block:
            @block.gpsimd
            def _(pool):
                for sem in self.sems:
                    pool.sem_clear(sem)


class Chain:

    def __init__(self, eng, sem):
        self.eng, self.sem, self.n = eng, sem, 0

    def restart(self):
        self.eng.sem_clear(self.sem)
        self.n = 0

    def link(self, ins):
        self.count(ins)
        self.settle()

    def count(self, ins):
        self.n += 1
        ins.then_inc(self.sem, 1)

    def settle(self):
        self.eng.wait_ge(self.sem, self.n)


def hold(eng, sem, value):
    eng.wait_ge(sem, value)
    eng.nop(nofuse=True)


def bc(ap, axis, n):
    v = ap.unsqueeze(axis)
    return v.broadcast_to([*v.shape[:axis], n, *v.shape[axis + 1:]])


def constants(nc, stack):
    c = Scope(nc, stack, "const")
    ident = c.sb("ident", [P, P])
    ident16 = c.sb("ident16", [P, P], BF16)
    causal16 = c.sb("causal16", [P, P], BF16)
    ones = c.sb("ones", [P, P])
    eps = c.sb("eps", [P, 1])
    with ExitStack() as own:
        fill = Scope(nc, own, "fill")
        filled = fill.sem("filled")
        block = fill.block()

        @block.gpsimd
        def _(pool):
            nc.gpsimd.memset(ident[:, :], 0.0).then_inc(filled, 1)
            nc.gpsimd.memset(ident16[:, :], 0.0).then_inc(filled, 1)
            nc.gpsimd.memset(causal16[:, :], 0.0).then_inc(filled, 1)
            nc.gpsimd.memset(ones[:, :], 1.0).then_inc(filled, 1)
            nc.gpsimd.memset(eps[:, :], LN_EPS).then_inc(filled, 1)
            pool.wait_ge(filled, 5)
            for m in (ident, ident16):
                nc.gpsimd.affine_select(out=m[:, :], in_=m[:, :], compare_op=ALU.not_equal, fill=1.0,
                                        base=0, pattern=[[-1, P]], channel_multiplier=1).then_inc(filled, 1)
            nc.gpsimd.affine_select(out=causal16[:, :], in_=causal16[:, :], compare_op=ALU.is_ge, fill=NEG,
                                    base=0, pattern=[[-1, P]], channel_multiplier=1).then_inc(filled, 1)
            pool.wait_ge(filled, 8)

    return ident, ident16, causal16, ones, eps


def wait_past(eng, sem, value):
    if not (isinstance(value, int) and value <= 0):
        eng.wait_ge(sem, value)


def hold_past(eng, sem, value):
    if not (isinstance(value, int) and value <= 0):
        hold(eng, sem, value)


def ln_statistics(nc, own, r, stats, mv, ready, tiles=TT):
    for t in range(tiles):
        own.count(nc.vector.bn_stats(stats[:, t, :], r[:, t, :]))
    own.settle()
    for t in range(tiles):
        ins = nc.vector.bn_aggr(mv[:, t, :], stats[:, t, :])
        if t < tiles - 1:
            own.count(ins)
    ins.then_inc(ready, 1)


def ln_apply(nc, own, r, mv, rs, out, ready, tiles=TT):
    for t in range(tiles):
        ins = nc.vector.tensor_scalar(out[:, t, :], r[:, t, :], mv[:, t, 0:1], rs[:, t:t + 1], ALU.subtract, ALU.mult)
        if t < tiles - 1:
            own.count(ins)
    ins.then_inc(ready, 1)


def layernorm(nc, dve, own, r, stats, mv, rs, out, b, ln_stats, ln_rs, ready, stored, tiles=TT, step=16):
    ln_statistics(nc, own, r, stats, mv, ln_stats, tiles)
    dve.wait_ge(ln_stats, b + 1)
    dve.wait_ge(stored, step * b)
    dve.wait_ge(ln_rs, b + 1)
    ln_apply(nc, own, r, mv, rs, out, ready, tiles)


DI = 256
HALF = DI // P
NS = 16
TAPS = 4
SG = 2
GROUPS = NS // SG


def turns(eng, turn):
    turn(0, 0, True, True)
    with eng.Fori(0, B // 2 - 1) as j:
        turn(j * 2 + 1, 1, False, True)
        turn(j * 2 + 2, 0, False, True)
    turn(B - 1, 1, False, False)


def scan_stage(nc, T, const):
    ident, ident16, causal16, ones, eps = const
    with ExitStack() as stack:
        c = Scope(nc, stack, "scan")
        w_in = c.sb("w_in", [P, 2 * DI])
        w_x = c.sb("w_x", [P, HALF, 2 * NS])
        w_dt = c.sb("w_dt", [P, HALF, DI])
        w_out = c.sb("w_out", [P, HALF, D])
        conv_w = c.sb("conv_w", [P, HALF, TAPS])
        vec = c.sb("vec", [P, 5, HALF])
        a_neg = c.sb("a_neg", [P, NS])
        pick = c.sb("pick", [2 * NS, 2 * NS, P])
        mean_w = c.sb("mean_w", [P, P])
        xa = c.sb("xa", [P, TT, D])
        xr = c.sb("xr", [P, TT, D])
        xT = c.sb("xT", [P, S])
        xp = c.sb("xp", [P, HALF, TAPS - 1 + S])
        conv = c.sb("conv", [P, HALF, S])
        sig = c.sb("sig", [P, HALF, S])
        gate = [c.sb(f"gate{i}", [P, HALF, S]) for i in range(2)]
        gsig = c.sb("gsig", [P, HALF, S])
        xc = [c.sb(f"xc{i}", [P, HALF, S]) for i in range(2)]
        bcT = [c.sb(f"bcT{i}", [2 * NS, S]) for i in range(2)]
        dt = [c.sb(f"dt{i}", [P, HALF, S]) for i in range(2)]
        dabs = c.sb("dabs", [P, HALF, S])
        u = [c.sb(f"u{i}", [P, HALF, S]) for i in range(2)]
        decay = c.sb("decay", [P, 2, SG, HALF, S])
        drive = c.sb("drive", [P, 2, SG, HALF, S])
        h = c.sb("h", [P, 2, SG, HALF, S])
        hc = c.sb("hc", [P, 2, SG, HALF, S])
        y2 = c.sb("y2", [P, SG, HALF, S])
        y = c.sb("y", [P, HALF, S])
        sq = c.sb("sq", [P, HALF, S])
        rstd = c.sb("rstd", [P, S])
        r = c.sb("r", [P, TT, D])
        stats = c.sb("stats", [P, TT, 6])
        mv = c.sb("mv", [P, TT, 2])
        rs = c.sb("rs", [P, TT])
        x1 = c.sb("x1", [P, TT, D])
        ps_t = c.ps("ps_t", [P, 512])
        ps_x = c.ps("ps_x", [P, HALF, S])
        ps_z = c.ps("ps_z", [P, HALF, S])
        ps_v = c.ps("ps_v", [P, HALF, S])
        ps_b = [c.ps(f"ps_b{i}", [P, SG, S]) for i in range(2)]
        ps_c = [c.ps(f"ps_c{i}", [P, SG, S]) for i in range(2)]

        weights_in = c.sem("weights_in")
        consts_ready = c.sem("consts_ready")
        a_ready = c.sem("a_ready")
        xa_in = c.sem("xa_in")
        xr_in = c.sem("xr_in")
        xT_ps = c.sem("xT_ps")
        xT_sb = c.sem("xT_sb")
        xz_ps = c.sem("xz_ps")
        xp_sb = c.sem("xp_sb")
        z_exp = c.sem("z_exp")
        conv_ready = c.sem("conv_ready")
        conv_exp = c.sem("conv_exp")
        xc_ready = c.sem("xc_ready")
        ssm_ps = c.sem("ssm_ps")
        v_ps = c.sem("v_ps")
        bc_sb = c.sem("bc_sb")
        dlog = c.sem("dlog")
        dt_ready = c.sem("dt_ready")
        u_ready = c.sem("u_ready")
        decay_exp = c.sem("decay_exp")
        decay_cut = c.sem("decay_cut")
        b_ps = c.sem("b_ps")
        c_ps = c.sem("c_ps")
        driven = c.sem("driven")
        scanned = c.sem("scanned")
        hc_ready = c.sem("hc_ready")
        summed = c.sem("summed")
        y_ready = c.sem("y_ready")
        mean_ps = c.sem("mean_ps")
        centred = c.sem("centred")
        squared = c.sem("squared")
        var_ps = c.sem("var_ps")
        rstd_ready = c.sem("rstd_ready")
        gated = c.sem("gated")
        gate_ready = c.sem("gate_ready")
        out_ps = c.sem("out_ps")
        out_read = c.sem("out_read")
        ln_stats = c.sem("ln_stats")
        ln_rs = c.sem("ln_rs")
        x1_ready = c.sem("x1_ready")
        stored = c.sem("stored")
        dve_own = c.sem("dve_own")
        act_own = c.sem("act_own")
        block = c.block()

        @block.sync
        def _(sp):
            loads = [(w_in[:, :], T["w_in"]), (w_x[:, :, :], T["w_x"]), (w_dt[:, :, :], T["w_dt"]),
                     (w_out[:, :, :], T["w_out"]), (conv_w[:, :, :], T["conv_w"]), (vec[:, :, :], T["scan_vec"]),
                     (a_neg[:, :], T["a_log"])]
            for dst, src in loads:
                sp.dma_start(dst, src).then_inc(weights_in, 16)

            def load_a(b):
                sp.dma_start(xa[:, :, :], T["x"][b].rearrange("(t p) d -> p t d", p=P)).then_inc(xa_in, 16)

            def load_r(b):
                sp.dma_start(xr[:, :, :], T["x"][b].rearrange("(t p) d -> p t d", p=P)).then_inc(xr_in, 16)

            def store(b):
                sp.wait_ge(x1_ready, b + 1)
                sp.dma_start(T["x1"][b].rearrange("(t p) d -> p t d", p=P), x1[:, :, :]).then_inc(stored, 16)

            load_a(0)
            load_r(0)
            sp.wait_ge(xT_ps, 1)
            load_a(1)
            with sp.Fori(0, B - 2) as j:
                hold(sp, xT_ps, j + 2)
                load_a(j + 2)
                hold(sp, out_read, j + 1)
                load_r(j + 1)
                store(j)
            sp.wait_ge(out_read, B - 1)
            load_r(B - 1)
            store(B - 2)
            store(B - 1)
            sp.wait_ge(stored, 16 * B)

        @block.gpsimd
        def _(pool):
            nc.gpsimd.memset(pick[:, :, :], 0.0).then_inc(consts_ready, 1)
            nc.gpsimd.memset(xp[:, :, :], 0.0).then_inc(consts_ready, 1)
            nc.gpsimd.memset(mean_w[:, :], 1.0 / DI).then_inc(consts_ready, 1)
            pool.wait_ge(consts_ready, 3)
            nc.gpsimd.affine_select(out=pick[:, :, :], in_=pick[:, :, :], compare_op=ALU.not_equal, fill=1.0,
                                    base=0, pattern=[[-1, 2 * NS], [0, P]], channel_multiplier=1)\
                .then_inc(consts_ready, 1)

            def drive_input(b, p):
                hold(pool, dt_ready, b + 1)
                nc.gpsimd.tensor_tensor(u[p][:, :, :], dt[p][:, :, :], xc[p][:, :, :], ALU.mult)\
                    .then_inc(u_ready, 1)

            def add_states(b, g):
                if g == 0:
                    hold_past(pool, y_ready, b)
                else:
                    hold(pool, summed, b * GROUPS + g)
                hold(pool, hc_ready, b * GROUPS + g + 1)
                if g == 0:
                    nc.gpsimd.tensor_copy(y2[:, :, :, :], hc[:, 0, :, :, :]).then_inc(summed, 1)
                else:
                    nc.gpsimd.tensor_tensor(y2[:, :, :, :], y2[:, :, :, :], hc[:, g % 2, :, :, :], ALU.add)\
                        .then_inc(summed, 1)

            def turn(b, p, first, more):
                for g in range(GROUPS):
                    hold(pool, decay_exp, b * NS + SG * (g + 1))
                    nc.gpsimd.memset(decay[:, g % 2, :, :, 0:1], 0.0).then_inc(decay_cut, 1)
                    if g >= 1:
                        add_states(b, g - 1)
                if more:
                    drive_input(b + 1, 1 - p)
                add_states(b, GROUPS - 1)
                hold(pool, summed, (b + 1) * GROUPS)
                hold_past(pool, out_ps, b)
                nc.gpsimd.tensor_tensor(y[:, :, :], y2[:, 0, :, :], y2[:, 1, :, :], ALU.add).then_inc(y_ready, 1)

            drive_input(0, 0)
            turns(pool, turn)

        @block.scalar
        def _(act):
            own = Chain(act, act_own)
            act.wait_ge(weights_in, 16 * 7)
            own.link(nc.scalar.activation(a_neg[:, :], a_neg[:, :], ACT.Exp))
            nc.scalar.activation(a_neg[:, :], a_neg[:, :], ACT.Copy, scale=-1.0).then_inc(a_ready, 1)
            act.wait_ge(a_ready, 1)
            nc.scalar.preload_act_table_set("natural_log_exp_and_others")

            def keep_x(b):
                wait_past(act, xz_ps, 2 * b)
                act.wait_ge(xT_ps, b + 1)
                nc.scalar.activation(xT[:, :], ps_v[:, 0, :], ACT.Copy).then_inc(xT_sb, 1)

            def sigmoid(dst, ready):
                own.link(nc.scalar.activation(dst, dst, ACT.Ln, bias=ones[:, 0:1]))
                nc.scalar.activation(dst, dst, ACT.Exp, scale=-1.0).then_inc(ready, 1)

            def keep_xz(b):
                wait_past(act, conv_ready, b)
                act.wait_ge(xz_ps, 2 * b + 1)
                nc.scalar.activation(xp[:, :, TAPS - 1:], ps_x[:, :, :], ACT.Copy).then_inc(xp_sb, 1)
                wait_past(act, gate_ready, b)
                act.wait_ge(xz_ps, 2 * b + 2)
                own.link(nc.scalar.activation(gsig[:, :, :], ps_z[:, :, :], ACT.Exp, scale=-1.0))
                sigmoid(gsig[:, :, :], z_exp)

            def conv_sigmoid(b):
                wait_past(act, xc_ready, b)
                act.wait_ge(conv_ready, b + 1)
                own.link(nc.scalar.activation(sig[:, :, :], conv[:, :, :], ACT.Exp, scale=-1.0))
                sigmoid(sig[:, :, :], conv_exp)

            def keep_bc(b, p):
                act.wait_ge(ssm_ps, b + 1)
                nc.scalar.activation(bcT[p][:, :], ps_x[0:2 * NS, 0, :], ACT.Copy).then_inc(bc_sb, 1)

            def softplus(b):
                wait_past(act, dt_ready, b)
                act.wait_ge(v_ps, b + 1)
                for m in range(HALF):
                    own.count(nc.scalar.activation(dabs[:, m, :], ps_v[:, m, :], ACT.Abs, bias=vec[:, 1, m:m + 1]))
                own.settle()
                own.link(nc.scalar.activation(dabs[:, :, :], dabs[:, :, :], ACT.Exp, scale=-1.0))
                nc.scalar.activation(dabs[:, :, :], dabs[:, :, :], ACT.Ln, bias=ones[:, 0:1]).then_inc(dlog, 1)

            def decays(b, p, g):
                if g < 2:
                    wait_past(act, scanned, b * GROUPS + (g - 1))
                else:
                    act.wait_ge(scanned, b * GROUPS + g - 1)
                for i in range(SG):
                    s = g * SG + i
                    nc.scalar.activation(decay[:, g % 2, i, :, :], dt[p][:, :, :], ACT.Exp,
                                         scale=a_neg[:, s:s + 1]).then_inc(decay_exp, 1)

            def square(b):
                act.wait_ge(centred, b + 1)
                nc.scalar.activation(sq[:, :, :], y[:, :, :], ACT.Square).then_inc(squared, 1)

            def inverse_std(b):
                act.wait_ge(var_ps, b + 1)
                own.link(nc.scalar.activation(rstd[:, :], ps_t[:, S:2 * S], ACT.Ln, bias=eps[:, 0:1]))
                nc.scalar.activation(rstd[:, :], rstd[:, :], ACT.Exp, scale=-0.5).then_inc(rstd_ready, 1)

            def ln_inverse_std(b):
                act.wait_ge(ln_stats, b + 1)
                own.link(nc.scalar.activation(rs[:, :], mv[:, :, 1], ACT.Ln, bias=eps[:, 0:1]))
                nc.scalar.activation(rs[:, :], rs[:, :], ACT.Exp, scale=-0.5).then_inc(ln_rs, 1)

            def turn(b, p, first, more):
                own.restart()
                act.wait_ge(dt_ready, b + 1)
                for g in range(GROUPS):
                    decays(b, p, g)
                    if not first:
                        if g == 2:
                            square(b - 1)
                        if g == 3:
                            inverse_std(b - 1)
                        if g == 5:
                            ln_inverse_std(b - 1)
                    if more:
                        if g == 0:
                            keep_x(b + 1)
                        if g == 1:
                            keep_xz(b + 1)
                        if g == 3:
                            conv_sigmoid(b + 1)
                        if g == 5:
                            keep_bc(b + 1, 1 - p)
                        if g == 6:
                            softplus(b + 1)
                own.settle()

            own.restart()
            keep_x(0)
            keep_xz(0)
            conv_sigmoid(0)
            keep_bc(0, 0)
            softplus(0)
            turns(act, turn)
            square(B - 1)
            inverse_std(B - 1)
            ln_inverse_std(B - 1)

        @block.tensor
        def _(pe):
            pe.wait_ge(weights_in, 16 * 7)
            pe.wait_ge(consts_ready, 4)

            def turn_x(b):
                wait_past(pe, dt_ready, b)
                pe.wait_ge(xa_in, 16 * (b + 1))
                for t in range(TT):
                    mm = nc.tensor.transpose(ps_v[:, 0, t * P:(t + 1) * P], xa[:, t, :], ident[:, :])
                mm.then_inc(xT_ps, 1)

            def project(b):
                pe.wait_ge(xT_sb, b + 1)
                wait_past(pe, bc_sb, b)
                for m in range(HALF):
                    mm = nc.tensor.matmul(ps_x[:, m, :], w_in[:, m * P:(m + 1) * P], xT[:, :], start=True, stop=True)
                mm.then_inc(xz_ps, 1)
                wait_past(pe, gate_ready, b)
                for m in range(HALF):
                    mm = nc.tensor.matmul(ps_z[:, m, :], w_in[:, DI + m * P:DI + (m + 1) * P], xT[:, :],
                                          start=True, stop=True)
                mm.then_inc(xz_ps, 1)

            def project_inner(b, p):
                pe.wait_ge(xc_ready, b + 1)
                for m in range(HALF):
                    mm = nc.tensor.matmul(ps_x[0:2 * NS, 0, :], w_x[:, m, :], xc[p][:, m, :],
                                          start=(m == 0), stop=(m == HALF - 1))
                mm.then_inc(ssm_ps, 1)
                for o in range(HALF):
                    for m in range(HALF):
                        mm = nc.tensor.matmul(ps_v[:, o, :], w_dt[:, m, o * P:(o + 1) * P], xc[p][:, m, :],
                                              start=(m == 0), stop=(m == HALF - 1))
                mm.then_inc(v_ps, 1)

            def spread(b, p, g):
                wait_past(pe, driven, b * GROUPS + (g - 1))
                for i in range(SG):
                    mm = nc.tensor.matmul(ps_b[g % 2][:, i, :], pick[:, g * SG + i, :], bcT[p][:, :],
                                          start=True, stop=True)
                mm.then_inc(b_ps, 1)
                wait_past(pe, hc_ready, b * GROUPS + (g - 1))
                for i in range(SG):
                    mm = nc.tensor.matmul(ps_c[g % 2][:, i, :], pick[:, NS + g * SG + i, :], bcT[p][:, :],
                                          start=True, stop=True)
                mm.then_inc(c_ps, 1)

            def mean(b):
                wait_past(pe, out_read, b)
                pe.wait_ge(y_ready, b + 1)
                for m in range(HALF):
                    mm = nc.tensor.matmul(ps_t[:, 0:S], mean_w[:, :], y[:, m, :], start=(m == 0), stop=(m == HALF - 1))
                mm.then_inc(mean_ps, 1)

            def variance(b):
                pe.wait_ge(squared, b + 1)
                for m in range(HALF):
                    mm = nc.tensor.matmul(ps_t[:, S:2 * S], mean_w[:, :], sq[:, m, :], start=(m == 0), stop=(m == HALF - 1))
                mm.then_inc(var_ps, 1)

            def project_out(b):
                pe.wait_ge(gated, b + 1)
                for t in range(TT):
                    for m in range(HALF):
                        mm = nc.tensor.matmul(ps_t[:, t * P:(t + 1) * P], y[:, m, t * P:(t + 1) * P], w_out[:, m, :],
                                              start=(m == 0), stop=(m == HALF - 1))
                mm.then_inc(out_ps, 1)

            def turn(b, p, first, more):
                pe.wait_ge(bc_sb, b + 1)
                for g in range(GROUPS):
                    spread(b, p, g)
                    if not first:
                        if g == 1:
                            mean(b - 1)
                        if g == 2:
                            variance(b - 1)
                        if g == 4:
                            project_out(b - 1)
                    if more:
                        if g == 0:
                            turn_x(b + 1)
                        if g == 1:
                            project(b + 1)
                        if g == 5:
                            project_inner(b + 1, 1 - p)

            turn_x(0)
            project(0)
            project_inner(0, 0)
            turns(pe, turn)
            mean(B - 1)
            variance(B - 1)
            project_out(B - 1)

        @block.vector
        def _(dve):
            own = Chain(dve, dve_own)
            dve.wait_ge(weights_in, 16 * 7)

            def convolve(b):
                wait_past(dve, conv_exp, b)
                dve.wait_ge(xp_sb, b + 1)
                for k in range(TAPS):
                    for m in range(HALF):
                        if k == 0:
                            own.count(nc.vector.tensor_scalar(conv[:, m, :], xp[:, m, 0:S], conv_w[:, m, 0:1],
                                                              vec[:, 0, m:m + 1], ALU.mult, ALU.add))
                        else:
                            ins = nc.vector.scalar_tensor_tensor(
                                out=conv[:, m, :], in0=xp[:, m, k:k + S], scalar=conv_w[:, m, k:k + 1],
                                in1=conv[:, m, :], op0=ALU.mult, op1=ALU.add)
                            if (k, m) == (TAPS - 1, HALF - 1):
                                ins.then_inc(conv_ready, 1)
                            else:
                                own.count(ins)
                    own.settle()

            def make_gate(b, p):
                dve.wait_ge(z_exp, b + 1)
                nc.vector.tensor_tensor(gate[p][:, :, :], ps_z[:, :, :], gsig[:, :, :], ALU.mult).then_inc(gate_ready, 1)

            def make_xc(b, p):
                dve.wait_ge(conv_exp, b + 1)
                dve.wait_ge(conv_ready, b + 1)
                nc.vector.tensor_tensor(xc[p][:, :, :], conv[:, :, :], sig[:, :, :], ALU.mult).then_inc(xc_ready, 1)

            def make_dt(b, p):
                dve.wait_ge(dlog, b + 1)
                for m in range(HALF):
                    own.count(nc.vector.tensor_scalar(dt[p][:, m, :], ps_v[:, m, :], vec[:, 1, m:m + 1], 0.0,
                                                      ALU.add, ALU.max))
                own.settle()
                nc.vector.tensor_tensor(dt[p][:, :, :], dt[p][:, :, :], dabs[:, :, :], ALU.add).then_inc(dt_ready, 1)

            def group(b, p, g):
                q = g % 2
                dve.wait_ge(b_ps, b * GROUPS + g + 1)
                nc.vector.tensor_tensor(drive[:, q, :, :, :], bc(u[p][:, :, :], 1, SG), bc(ps_b[q][:, :, :], 2, HALF),
                                        ALU.mult).then_inc(driven, 1)
                dve.wait_ge(decay_cut, b * GROUPS + g + 1)
                dve.wait_ge(driven, b * GROUPS + g + 1)
                nc.vector.tensor_tensor_scan(h[:, q, :, :, :].rearrange("p a m t -> p (a m t)"),
                                             decay[:, q, :, :, :].rearrange("p a m t -> p (a m t)"),
                                             drive[:, q, :, :, :].rearrange("p a m t -> p (a m t)"),
                                             0.0, ALU.mult, ALU.add).then_inc(scanned, 1)
                dve.wait_ge(c_ps, b * GROUPS + g + 1)
                wait_past(dve, summed, b * GROUPS + (g - 1))
                dve.wait_ge(scanned, b * GROUPS + g + 1)
                nc.vector.tensor_tensor(hc[:, q, :, :, :], h[:, q, :, :, :], bc(ps_c[q][:, :, :], 2, HALF),
                                        ALU.mult).then_inc(hc_ready, 1)

            def centre(b):
                dve.wait_ge(mean_ps, b + 1)
                nc.vector.tensor_tensor(y[:, :, :], y[:, :, :], bc(ps_t[:, 0:S], 1, HALF), ALU.subtract)\
                    .then_inc(centred, 1)

            def normalise(b, p):
                dve.wait_ge(squared, b + 1)
                dve.wait_ge(rstd_ready, b + 1)
                own.link(nc.vector.tensor_tensor(y[:, :, :], y[:, :, :], bc(rstd[:, :], 1, HALF), ALU.mult))
                for m in range(HALF):
                    own.count(nc.vector.tensor_scalar(y[:, m, :], y[:, m, :], vec[:, 3, m:m + 1], vec[:, 4, m:m + 1],
                                                      ALU.mult, ALU.add))
                own.settle()
                for m in range(HALF):
                    own.count(nc.vector.scalar_tensor_tensor(out=y[:, m, :], in0=xc[p][:, m, :],
                                                             scalar=vec[:, 2, m:m + 1], in1=y[:, m, :], op0=ALU.mult, op1=ALU.add))
                own.settle()
                nc.vector.tensor_tensor(y[:, :, :], y[:, :, :], gate[p][:, :, :], ALU.mult).then_inc(gated, 1)

            def residual(b):
                dve.wait_ge(xr_in, 16 * (b + 1))
                dve.wait_ge(out_ps, b + 1)
                nc.vector.tensor_tensor(r[:, :, :], xr[:, :, :], ps_t[:, 0:S].rearrange("p (t d) -> p t d", t=TT),
                                        ALU.add).then_inc(out_read, 1)
                dve.wait_ge(out_read, b + 1)
                ln_statistics(nc, own, r, stats, mv, ln_stats)

            def finish(b):
                dve.wait_ge(ln_stats, b + 1)
                wait_past(dve, stored, 16 * b)
                dve.wait_ge(ln_rs, b + 1)
                ln_apply(nc, own, r, mv, rs, x1, x1_ready)
                own.settle()

            def turn(b, p, first, more):
                own.restart()
                dve.wait_ge(u_ready, b + 1)
                for g in range(GROUPS):
                    group(b, p, g)
                    if not first:
                        if g == 1:
                            centre(b - 1)
                        if g == 3:
                            normalise(b - 1, 1 - p)
                        if g == 4:
                            residual(b - 1)
                        if g == 5:
                            finish(b - 1)
                    if more:
                        if g == 2:
                            convolve(b + 1)
                        if g == 4:
                            make_gate(b + 1, 1 - p)
                            make_xc(b + 1, 1 - p)
                        if g == 6:
                            make_dt(b + 1, 1 - p)
                own.settle()

            own.restart()
            convolve(0)
            make_gate(0, 0)
            make_xc(0, 0)
            make_dt(0, 0)
            turns(dve, turn)
            centre(B - 1)
            normalise(B - 1, 1)
            residual(B - 1)
            finish(B - 1)


AH = 16
AD = 8
SCORE_CHUNKS = [(0, h) for h in range(0, AH, 4)] + [(1, h) for h in range(0, AH, 2)]
NSC = len(SCORE_CHUNKS)
QP = AH // 2
ITEMS = QP + NSC
SRING = 4
LAG_T, LAG_V = 2, 3


def chunk_heads(k):
    qt, first = SCORE_CHUNKS[k]
    return qt, (qt + 1) * P, range(first, first + 4 // (qt + 1))


def self_stage(nc, T, const):
    ident, ident16, causal16, ones, eps = const
    with ExitStack() as stack:
        c = Scope(nc, stack, "self")
        wq = c.sb("wq", [P, AH, P])
        wk = c.sb("wk", [P, P])
        wv = c.sb("wv", [P, D])
        wo = c.sb("wo", [P, D])
        bo = c.sb("bo", [P, D])
        xs = c.sb("xs", [P, TT, D])
        cs = c.sb("cs", [P, TT, D])
        x = c.sb("x", [P, TT, D])
        xcT = c.sb("xcT", [P, 2, S])
        qT = c.sb("qT", [P, AH, S])
        kT = c.sb("kT", [P, S])
        v = c.sb("v", [P, TT, D])
        negmax = c.sb("negmax", [P, NSC, 4])
        sums = c.sb("sums", [P, TT, AH])
        prob = c.sb("prob", [P, 2, 4 * P])
        probT = c.sb("probT", [P, 2, 4, P])
        o = c.sb("o", [P, TT, D])
        oT = c.sb("oT", [P, S])
        r = c.sb("r", [P, TT, D])
        stats = c.sb("stats", [P, TT, 6])
        mv = c.sb("mv", [P, TT, 2])
        rs = c.sb("rs", [P, TT])
        x2 = c.sb("x2", [P, TT, D])
        ring = [c.ps(f"ring{i}", [P, 512]) for i in range(SRING)]
        ps_t = [c.ps(f"ps_t{i}", [P, 4, P]) for i in range(2)]
        ps_o = c.ps("ps_o", [P, TT, D])
        ps_m = c.ps("ps_m", [P, 4, P])

        weights_in = c.sem("weights_in")
        x_in = c.sem("x_in")
        x_kept = c.sem("x_kept")
        xcT_ps = c.sem("xcT_ps")
        xcT_sb = c.sem("xcT_sb")
        q_ps = c.sem("q_ps")
        kv_ps = c.sem("kv_ps")
        kv_sb = c.sem("kv_sb")
        scores = c.sem("scores")
        maxed = c.sem("maxed")
        emptied_ring = c.sem("emptied_ring")
        t_ps = c.sem("t_ps")
        t_sb = c.sem("t_sb")
        pv = c.sem("pv")
        normed = c.sem("normed")
        oT_ps = c.sem("oT_ps")
        oT_sb = c.sem("oT_sb")
        out_ps = c.sem("out_ps")
        out_read = c.sem("out_read")
        ln_stats = c.sem("ln_stats")
        ln_rs = c.sem("ln_rs")
        x2_ready = c.sem("x2_ready")
        stored = c.sem("stored")
        dve_own = c.sem("dve_own")
        act_own = c.sem("act_own")
        block = c.block()

        @block.sync
        def _(sp):
            for dst, src in ((wq[:, :, :], T["wq_pad"]), (wk[:, :], T["wk_bd"]), (wv[:, :], T["wv_bd"]),
                             (wo[:, :], T["wo"]), (bo[:, :], T["bo"])):
                sp.dma_start(dst, src).then_inc(weights_in, 16)

            def load(b):
                sp.dma_start(xs[:, :, :], T["x1"][b].rearrange("(t p) d -> p t d", p=P)).then_inc(x_in, 16)
                sp.dma_start(cs[:, :, :], T["ctx"][b, 0:S].rearrange("(t p) d -> p t d", p=P)).then_inc(x_in, 16)

            def store(b):
                sp.wait_ge(x2_ready, b + 1)
                sp.dma_start(T["x2"][b].rearrange("(t p) d -> p t d", p=P), x2[:, :, :]).then_inc(stored, 16)

            load(0)
            with sp.Fori(0, B - 1) as b:
                hold(sp, xcT_ps, b + 1)
                hold(sp, x_kept, b + 1)
                load(b + 1)
                store(b)
            store(B - 1)
            sp.wait_ge(stored, 16 * B)

        @block.tensor
        def _(pe):
            pe.wait_ge(weights_in, 16 * 5)

            def take_bank(b, item):
                if not (isinstance(b, int) and ITEMS * b + item < SRING):
                    pe.wait_ge(emptied_ring, b * ITEMS + (item - SRING + 1))
                return ring[item % SRING]

            def transpose_inputs(b):
                pe.wait_ge(x_in, 32 * (b + 1))
                for i, src in enumerate((xs, cs)):
                    for t in range(TT):
                        mm = nc.tensor.transpose(ps_m[:, 2 * i + t, :], src[:, t, :], ident[:, :])
                mm.then_inc(xcT_ps, 1)

            def project_queries(b, banks):
                for i in banks:
                    bank = take_bank(b, i)
                    for h in (2 * i, 2 * i + 1):
                        mm = nc.tensor.matmul(bank[:, (h % 2) * S:(h % 2 + 1) * S], wq[:, h, :], xcT[:, 0, :], start=True, stop=True)
                    mm.then_inc(q_ps, 1)

            def project_keys(b):
                nc.tensor.matmul(ps_m[:, 0:2, :], wk[:, :], xcT[:, 1, :], start=True, stop=True)
                for t in range(TT):
                    mm = nc.tensor.matmul(ps_m[:, 2 + t, :], xcT[:, 1, t * P:(t + 1) * P], wv[:, :], start=True, stop=True)
                mm.then_inc(kv_ps, 1)

            def score(b, k):
                qt, nk, heads = chunk_heads(k)
                bank = take_bank(b, QP + k)
                for i, h in enumerate(heads):
                    nc.tensor.matmul(bank[:, i * nk:(i + 1) * nk], qT[:, h, qt * P:(qt + 1) * P], kT[:, 0:nk],
                                     start=True, stop=False)
                    mm = nc.tensor.matmul(bank[:, (i + 1) * nk - P:(i + 1) * nk], ident16[:, :], causal16[:, :],
                                          start=False, stop=True)
                mm.then_inc(scores, 1)

            def turn(b, k):
                pe.wait_ge(emptied_ring, b * ITEMS + QP + k + 1)
                pe.wait_ge(t_sb, b * NSC + max(k - 1, 0))
                for i in range(4):
                    mm = nc.tensor.transpose(ps_t[k % 2][:, i, :], prob[:, k % 2, i * P:(i + 1) * P], ident[:, :])
                mm.then_inc(t_ps, 1)

            def weigh(b, k):
                qt, nk, heads = chunk_heads(k)
                pe.wait_ge(t_sb, b * NSC + k + 1)
                if k == 0:
                    pe.wait_ge(normed, b)
                for i, h in enumerate(heads):
                    for kb in range(qt + 1):
                        mm = nc.tensor.matmul(ps_o[:, qt, h * AD:(h + 1) * AD], probT[:, k % 2, i * (qt + 1) + kb, :],
                                              v[:, kb, h * AD:(h + 1) * AD], start=(kb == 0), stop=(kb == qt))
                mm.then_inc(pv, 1)

            def sequence(b, more):
                pe.wait_ge(kv_sb, 2 * (b + 1))
                pe.wait_ge(emptied_ring, b * ITEMS + QP)
                for s in range(NSC):
                    score(b, s)
                    if s >= LAG_T:
                        turn(b, s - LAG_T)
                    if s >= LAG_V:
                        weigh(b, s - LAG_V)
                if more:
                    transpose_inputs(b + 1)
                turn(b, NSC - 2)
                weigh(b, NSC - 3)
                if more:
                    pe.wait_ge(xcT_sb, b + 2)
                    project_queries(b + 1, range(0, 2))
                turn(b, NSC - 1)
                weigh(b, NSC - 2)
                if more:
                    project_keys(b + 1)
                    project_queries(b + 1, range(2, 5))
                weigh(b, NSC - 1)
                if more:
                    project_queries(b + 1, range(5, QP))
                    pe.wait_ge(kv_sb, 2 * (b + 2))
                pe.wait_ge(normed, b + 1)
                for t in range(TT):
                    mm = nc.tensor.transpose(ps_m[:, t, :], o[:, t, :], ident[:, :])
                mm.then_inc(oT_ps, 1)
                pe.wait_ge(oT_sb, b + 1)
                for t in range(TT):
                    mm = nc.tensor.matmul(ps_m[:, 2 + t, :], oT[:, t * P:(t + 1) * P], wo[:, :], start=True, stop=True)
                mm.then_inc(out_ps, 1)
                pe.wait_ge(out_read, b + 1)

            transpose_inputs(0)
            pe.wait_ge(xcT_sb, 1)
            project_keys(0)
            project_queries(0, range(QP))
            with pe.Fori(0, B - 1) as b:
                sequence(b, True)
            sequence(B - 1, False)

        @block.scalar
        def _(act):
            own = Chain(act, act_own)

            def keep_inputs(b):
                act.wait_ge(xcT_ps, b + 1)
                nc.scalar.activation(xcT[:, :, :], ps_m[:, :, :].rearrange("p (a t) n -> p a (t n)", a=2), ACT.Copy)\
                    .then_inc(xcT_sb, 1)

            def keep_queries(b):
                for i in range(QP):
                    act.wait_ge(q_ps, b * QP + i + 1)
                    nc.scalar.activation(qT[:, 2 * i:2 * i + 2, :], ring[i % SRING][:, :].rearrange("p (a n) -> p a n", a=2),
                                         ACT.Copy).then_inc(emptied_ring, 1)

            def sequence(b, more):
                own.restart()
                for k in range(NSC):
                    qt, nk, heads = chunk_heads(k)
                    act.wait_ge(maxed, b * NSC + k + 1)
                    act.wait_ge(t_ps, b * NSC + max(k - 1, 0))
                    for i, h in enumerate(heads):
                        ins = nc.scalar.activation(prob[:, k % 2, i * nk:(i + 1) * nk],
                                                   ring[(QP + k) % SRING][:, i * nk:(i + 1) * nk], ACT.Exp,
                                                   bias=negmax[:, k, i:i + 1], accum_out=sums[:, qt, h:h + 1])
                    ins.then_inc(emptied_ring, 1)
                if more:
                    keep_inputs(b + 1)
                    act.wait_ge(scores, (b + 1) * NSC)
                    keep_queries(b + 1)
                act.wait_ge(oT_ps, b + 1)
                nc.scalar.activation(oT[:, :], ps_m[:, 0:TT, :].rearrange("p t n -> p (t n)"), ACT.Copy).then_inc(oT_sb, 1)
                act.wait_ge(ln_stats, b + 1)
                own.link(nc.scalar.activation(rs[:, :], mv[:, :, 1], ACT.Ln, bias=eps[:, 0:1]))
                nc.scalar.activation(rs[:, :], rs[:, :], ACT.Exp, scale=-0.5).then_inc(ln_rs, 1)
                own.settle()

            nc.scalar.preload_act_table_set("natural_log_exp_and_others")
            keep_inputs(0)
            keep_queries(0)
            with act.Fori(0, B - 1) as b:
                sequence(b, True)
            sequence(B - 1, False)

        @block.gpsimd
        def _(pool):
            with pool.Fori(0, B) as b:
                hold(pool, out_read, b)
                hold(pool, x_in, 32 * (b + 1))
                nc.gpsimd.tensor_copy(x[:, :, :], xs[:, :, :]).then_inc(x_kept, 1)

        @block.vector
        def _(dve):
            own = Chain(dve, dve_own)
            dve.wait_ge(weights_in, 16 * 5)

            def keep_keys(b):
                dve.wait_ge(kv_ps, b + 1)
                nc.vector.tensor_copy(kT[:, :], ps_m[:, 0:2, :].rearrange("p a n -> p (a n)")).then_inc(kv_sb, 1)
                dve.wait_ge(pv, b * NSC)
                nc.vector.tensor_copy(v[:, :, :], ps_m[:, 2:4, :]).then_inc(kv_sb, 1)

            def keep_block(b, k):
                dve.wait_ge(pv, b * NSC + max(k - 1, 0))
                dve.wait_ge(t_ps, b * NSC + k + 1)
                nc.vector.tensor_copy(probT[:, k % 2, :, :], ps_t[k % 2][:, :, :]).then_inc(t_sb, 1)

            def sequence(b, more):
                own.restart()
                for s in range(NSC + LAG_T):
                    if s < NSC:
                        qt, nk, heads = chunk_heads(s)
                        dve.wait_ge(scores, b * NSC + s + 1)
                        nc.vector.tensor_reduce(negmax[:, s, 0:len(heads)],
                                                ring[(QP + s) % SRING][:, :].rearrange("p (i n) -> p i n", n=nk), AX, ALU.max,
                                                negate=True).then_inc(maxed, 1)
                    if s >= LAG_T:
                        keep_block(b, s - LAG_T)
                dve.wait_ge(emptied_ring, (b + 1) * ITEMS)
                own.link(nc.vector.reciprocal(sums[:, :, :], sums[:, :, :]))
                dve.wait_ge(x_kept, b + 1)
                own.link(nc.vector.tensor_tensor(r[:, :, :], x[:, :, :], bc(bo[:, :], 1, TT), ALU.add))
                if more:
                    keep_keys(b + 1)
                dve.wait_ge(pv, (b + 1) * NSC)
                nc.vector.tensor_tensor(o[:, :, :].rearrange("p t (h d) -> p t h d", h=AH),
                                        ps_o[:, :, :].rearrange("p t (h d) -> p t h d", h=AH), bc(sums[:, :, :], 3, AD),
                                        ALU.mult).then_inc(normed, 1)
                dve.wait_ge(out_ps, b + 1)
                nc.vector.tensor_tensor(r[:, :, :], r[:, :, :], ps_m[:, 2:4, :], ALU.add).then_inc(out_read, 1)
                dve.wait_ge(out_read, b + 1)
                layernorm(nc, dve, own, r, stats, mv, rs, x2, b, ln_stats, ln_rs, x2_ready, stored)
                own.settle()

            dve.wait_ge(kv_ps, 1)
            nc.vector.tensor_copy(kT[:, :], ps_m[:, 0:2, :].rearrange("p a n -> p (a n)")).then_inc(kv_sb, 1)
            nc.vector.tensor_copy(v[:, :, :], ps_m[:, 2:4, :]).then_inc(kv_sb, 1)
            with dve.Fori(0, B - 1) as b:
                sequence(b, True)
            sequence(B - 1, False)


NE = 8
DF = 512
FC = DF // P


def ffn_stage(nc, T, const):
    ident, ident16, causal16, ones, eps = const
    with ExitStack() as stack:
        c = Scope(nc, stack, "ffn")
        wr = c.sb("wr", [P, NE])
        br = c.sb("br", [1, NE])
        x = c.sb("x", [P, TT, D])
        xT = c.sb("xT", [P, S])
        mean = c.sb("mean", [P, 1])
        score = c.sb("score", [1, NE])
        top = c.sb("top", [1, 8])
        pick = c.sb("pick", [1, 8], U32)
        w1 = c.sb("w1", [P, DF])
        w2 = c.sb("w2", [P, FC, D])
        b1 = c.sb("b1", [P, FC])
        b2 = c.sb("b2", [P, D])
        hT = c.sb("hT", [P, FC, S])
        r = c.sb("r", [P, TT, D])
        stats = c.sb("stats", [P, TT, 6])
        mv = c.sb("mv", [P, TT, 2])
        rs = c.sb("rs", [P, TT])
        x3 = c.sb("x3", [P, TT, D])
        ps_x = c.ps("ps_x", [P, S])
        ps_r = c.ps("ps_r", [1, NE])
        ps_h = [c.ps(f"ps_h{i}", [P, 2, S]) for i in range(FC // 2)]
        ps_y = c.ps("ps_y", [P, TT, D])

        weights_in = c.sem("weights_in")
        x_in = c.sem("x_in")
        xT_ps = c.sem("xT_ps")
        xT_sb = c.sem("xT_sb")
        mean_ready = c.sem("mean_ready")
        score_ps = c.sem("score_ps")
        picked = c.sem("picked")
        expert_in = c.sem("expert_in")
        h_ps = c.sem("h_ps")
        h_sb = c.sem("h_sb")
        y_ps = c.sem("y_ps")
        y_read = c.sem("y_read")
        ln_stats = c.sem("ln_stats")
        ln_rs = c.sem("ln_rs")
        x3_ready = c.sem("x3_ready")
        stored = c.sem("stored")
        dve_own = c.sem("dve_own")
        act_own = c.sem("act_own")
        block = c.block()

        @block.sync
        def _(sp):
            for dst, src in ((wr[:, :], T["wr"]), (br[:, :], T["br"])):
                sp.dma_start(dst, src).then_inc(weights_in, 16)
            with sp.Fori(0, B) as b:
                sp.wait_ge(y_read, b)
                sp.dma_start(x[:, :, :], T["x2"][b].rearrange("(t p) d -> p t d", p=P)).then_inc(x_in, 16)
                hold(sp, picked, b + 1)
                e = sp.value_load(pick[0:1, 0:1], min_val=0, max_val=NE - 1)
                sp.dma_start(w1[:, :], T["ffn_w1"][bass.ds(e, 1)].rearrange("e p f -> p (e f)")).then_inc(expert_in, 16)
                sp.dma_start(b1[:, :], T["ffn_b1"][bass.ds(e, 1)].rearrange("e p f -> p (e f)")).then_inc(expert_in, 16)
                sp.dma_start(w2[:, :, :], T["ffn_w2"][bass.ds(e, 1)].rearrange("e (c p) d -> p (e c) d", p=P))\
                    .then_inc(expert_in, 16)
                sp.dma_start(b2[:, :], T["ffn_b2"][bass.ds(e, 1)].rearrange("e p d -> p (e d)")).then_inc(expert_in, 16)
                sp.wait_ge(x3_ready, b + 1)
                sp.dma_start(T["x3"][b].rearrange("(t p) d -> p t d", p=P), x3[:, :, :]).then_inc(stored, 16)
            sp.wait_ge(stored, 16 * B)

        @block.tensor
        def _(pe):
            pe.wait_ge(weights_in, 32)
            with pe.Fori(0, B) as b:
                pe.wait_ge(x_in, 16 * (b + 1))
                for t in range(TT):
                    mm = nc.tensor.transpose(ps_x[:, t * P:(t + 1) * P], x[:, t, :], ident[:, :])
                mm.then_inc(xT_ps, 1)
                pe.wait_ge(mean_ready, b + 1)
                nc.tensor.matmul(ps_r[:, :], mean[:, :], wr[:, :], start=True, stop=True).then_inc(score_ps, 1)
                pe.wait_ge(expert_in, 64 * (b + 1))
                for f in range(FC):
                    mm = nc.tensor.matmul(ps_h[f // 2][:, f % 2, :], w1[:, f * P:(f + 1) * P], xT[:, :], start=True, stop=True)
                    if f % 2:
                        mm.then_inc(h_ps, 1)
                for f in range(FC):
                    if f % 2 == 0:
                        pe.wait_ge(h_sb, b * FC + f + 2)
                    for t in range(TT):
                        mm = nc.tensor.matmul(ps_y[:, t, :], hT[:, f, t * P:(t + 1) * P], w2[:, f, :],
                                              start=(f == 0 and t == 0), stop=(f == FC - 1), skip_group_check=True)
                mm.then_inc(y_ps, 1)

        @block.scalar
        def _(act):
            own = Chain(act, act_own)
            nc.scalar.preload_act_table_set("natural_log_exp_and_others")
            with act.Fori(0, B) as b:
                own.restart()
                act.wait_ge(xT_ps, b + 1)
                nc.scalar.activation(xT[:, :], ps_x[:, :], ACT.Copy, accum_out=mean[:, :]).then_inc(xT_sb, 1)
                act.wait_ge(xT_sb, b + 1)
                nc.scalar.activation(mean[:, :], mean[:, :], ACT.Copy, scale=1.0 / S).then_inc(mean_ready, 1)
                act.wait_ge(ln_stats, b + 1)
                own.link(nc.scalar.activation(rs[:, :], mv[:, :, 1], ACT.Ln, bias=eps[:, 0:1]))
                nc.scalar.activation(rs[:, :], rs[:, :], ACT.Exp, scale=-0.5).then_inc(ln_rs, 1)
                own.settle()

        @block.vector
        def _(dve):
            own = Chain(dve, dve_own)
            dve.wait_ge(weights_in, 32)
            with dve.Fori(0, B) as b:
                own.restart()
                dve.wait_ge(score_ps, b + 1)
                own.link(nc.vector.tensor_tensor(score[:, :], ps_r[:, :], br[:, :], ALU.add))
                own.link(nc.vector.max(top[:, :], score[:, :]))
                nc.vector.max_index(pick[:, :], top[:, :], score[:, :]).then_inc(picked, 1)
                dve.wait_ge(expert_in, 64 * (b + 1))
                own.link(nc.vector.tensor_tensor(r[:, :, :], x[:, :, :], bc(b2[:, :], 1, TT), ALU.add))
                for f in range(FC):
                    dve.wait_ge(h_ps, b * (FC // 2) + f // 2 + 1)
                    nc.vector.tensor_scalar(hT[:, f, :], ps_h[f // 2][:, f % 2, :], b1[:, f:f + 1], 0.0, ALU.add, ALU.max)\
                        .then_inc(h_sb, 1)
                dve.wait_ge(y_ps, b + 1)
                nc.vector.tensor_tensor(r[:, :, :], r[:, :, :], ps_y[:, :, :], ALU.add).then_inc(y_read, 1)
                dve.wait_ge(y_read, b + 1)
                layernorm(nc, dve, own, r, stats, mv, rs, x3, b, ln_stats, ln_rs, x3_ready, stored)
                own.settle()


DH = 16
DW = 8
GB = 8
NG = B // GB
PLANES = 3 * DW + 1
GT = NG * S
WIN = P - DH
NORM_EPS = 1e-6


def delta_stage(nc, T, const):
    ident, ident16, causal16, ones, eps = const
    with ExitStack() as stack:
        c = Scope(nc, stack, "delta")
        planes = c.sb("planes", [P, 3 * DW, GT])
        eta = c.sb("eta", [P, GT])
        kb = c.sb("kb", [P, DW, GT])
        own_sem = c.sem("own")
        with ExitStack() as inner:
            project_and_convolve(nc, T, const, Scope(nc, inner, "dproj"), inner, planes, eta)
        k, q, v = (planes[:, i * DW:(i + 1) * DW, :] for i in range(3))
        with ExitStack() as inner:
            normalise(nc, Scope(nc, inner, "dnorm"), inner, const, k, q, v, kb, eta)
        u = c.sb("u", [P, DW, GT])
        with ExitStack() as inner:
            recurrence(nc, Scope(nc, inner, "drec"), inner, k, v, kb, u)
        o = c.sb("o", [P, DW, GT])
        with ExitStack() as inner:
            average(nc, T, const, Scope(nc, inner, "davg"), inner, k, q, u, o)
        with ExitStack() as inner:
            project_out(nc, T, const, Scope(nc, inner, "dout"), inner, o)


def project_and_convolve(nc, T, const, c, stack, planes, eta):
    ident, ident16, causal16, ones, eps = const
    wpad = c.sb("wpad", [P, PLANES, 2 * WIN + DH])
    bias = c.sb("bias", [P, PLANES])
    taps = c.sb("taps", [P, 3 * DW, TAPS])
    x = c.sb("x", [P, B * TT, D])
    xT = c.sb("xT", [P, B, S])
    raw = c.sb("raw", [P, PLANES, NG, TAPS - 1 + S])
    ps = [c.ps(f"ps{i}", [P, 512]) for i in range(4)]
    weights_in = c.sem("weights_in")
    x_in = c.sem("x_in")
    turned = c.sem("turned")
    turned_sb = c.sem("turned_sb")
    plane_ps = c.sem("plane_ps")
    plane_sb = c.sem("plane_sb")
    cleared = c.sem("cleared")
    dve_own = c.sem("dve_own")
    block = c.block()

    @block.sync
    def _(sp):
        for b in range(0, B, 2):
            sp.dma_start(x[:, b * TT:(b + 2) * TT, :], T["x3"][b:b + 2].rearrange("b (t p) d -> p (b t) d", p=P))\
                .then_inc(x_in, 16)
        for dst, src in ((wpad[:, :, :], T["delta_w"]), (bias[:, :], T["delta_bias"]), (taps[:, :, :], T["delta_taps"])):
            sp.dma_start(dst, src).then_inc(weights_in, 16)

    @block.gpsimd
    def _(pool):
        nc.gpsimd.memset(raw[:, :, :, 0:TAPS - 1], 0.0).then_inc(cleared, 1)

    @block.tensor
    def _(pe):
        pe.wait_ge(x_in, 16 * (B // 2))
        for f in range(B * TT // 4):
            if f >= 4:
                pe.wait_ge(turned_sb, f - 3)
            for i in range(4):
                mm = nc.tensor.transpose(ps[f % 4][:, i * P:(i + 1) * P], x[:, 4 * f + i, :], ident[:, :])
            mm.then_inc(turned, 1)
        pe.wait_ge(turned_sb, B * TT // 4)
        pe.wait_ge(weights_in, 48)
        with pe.Fori(0, NG) as g:
            for n in range(PLANES):
                if n >= 4:
                    pe.wait_ge(plane_sb, g * PLANES + n - 3)
                else:
                    pe.wait_ge(plane_sb, g * PLANES)
                for s in range(GB):
                    mm = nc.tensor.matmul(ps[n % 4][:, 0:S], wpad[:, n, WIN - DH * s:WIN - DH * s + P],
                                          xT[:, bass.ds(g * GB + s, 1), :].rearrange("p a t -> p (a t)"),
                                          start=(s == 0), stop=(s == GB - 1))
                mm.then_inc(plane_ps, 1)

    @block.scalar
    def _(act):
        for f in range(B * TT // 4):
            act.wait_ge(turned, f + 1)
            nc.scalar.activation(xT[:, 2 * f:2 * f + 2, :], ps[f % 4][:, :].rearrange("p (b t) -> p b t", b=2), ACT.Copy)\
                .then_inc(turned_sb, 1)
        act.wait_ge(weights_in, 48)
        with act.Fori(0, NG) as g:
            for n in range(PLANES):
                act.wait_ge(plane_ps, g * PLANES + n + 1)
                nc.scalar.activation(raw[:, n, bass.ds(g, 1), TAPS - 1:].rearrange("p a t -> p (a t)"), ps[n % 4][:, 0:S],
                                     ACT.Identity, bias=bias[:, n:n + 1]).then_inc(plane_sb, 1)

    @block.vector
    def _(dve):
        own = Chain(dve, dve_own)
        dve.wait_ge(cleared, 1)
        dve.wait_ge(weights_in, 48)
        dve.wait_ge(plane_sb, NG * PLANES)
        with dve.Fori(0, 3 * DW) as n:
            own.restart()
            out = planes[:, bass.ds(n, 1), :].rearrange("p a (g t) -> p (a g) t", g=NG)
            for j in range(TAPS):
                tap = taps[:, bass.ds(n, 1), j]
                src = raw[:, bass.ds(n, 1), :, j:j + S].rearrange("p a g t -> p (a g) t")
                if j == 0:
                    own.link(nc.vector.tensor_scalar(out, src, tap, None, ALU.mult))
                else:
                    own.link(nc.vector.scalar_tensor_tensor(out=out, in0=src, scalar=tap, in1=out, op0=ALU.mult, op1=ALU.add))
        own.restart()
        own.link(nc.vector.tensor_copy(eta[:, :].rearrange("p (g t) -> p g t", g=NG), raw[:, 3 * DW, :, TAPS - 1:]))


def normalise(nc, c, stack, const, k, q, v, kb, eta):
    ident, ident16, causal16, ones, eps = const
    sq = c.sb("sq", [P, 2, DW, GT])
    ev = c.sb("ev", [P, DW, GT])
    ee = c.sb("ee", [P, GT])
    norm = c.sb("norm", [P, 2, GT])
    squared = c.sem("squared")
    lengths = c.sem("lengths")
    rooted = c.sem("rooted")
    expd = c.sem("expd")
    dve_own = c.sem("dve_own")
    block = c.block()

    @block.scalar
    def _(act):
        nc.scalar.activation(sq[:, 0, :, :], k, ACT.Square).then_inc(squared, 1)
        nc.scalar.activation(sq[:, 1, :, :], q, ACT.Square).then_inc(squared, 1)
        nc.scalar.activation(ev[:, :, :], v, ACT.Exp, scale=-1.0).then_inc(expd, 1)
        nc.scalar.activation(ee[:, :], eta[:, :], ACT.Exp, scale=-1.0).then_inc(expd, 1)
        act.wait_ge(lengths, 2)
        nc.scalar.activation(norm[:, :, :], norm[:, :, :], ACT.Sqrt).then_inc(rooted, 1)

    @block.vector
    def _(dve):
        own = Chain(dve, dve_own)
        for i in range(2):
            dve.wait_ge(squared, i + 1)
            nc.vector.tensor_reduce(norm[:, i, :], sq[:, i, :, :].rearrange("p d n -> p n d"), AX, ALU.add).then_inc(lengths, 1)
        dve.wait_ge(expd, 2)
        own.link(nc.vector.tensor_scalar(ee[:, :], ee[:, :], 1.0, None, ALU.add))
        own.link(nc.vector.reciprocal(eta[:, :], ee[:, :]))
        own.link(nc.vector.tensor_scalar(ev[:, :, :], ev[:, :, :], 1.0, None, ALU.add))
        own.link(nc.vector.reciprocal(ev[:, :, :], ev[:, :, :]))
        own.link(nc.vector.tensor_tensor(v, v, ev[:, :, :], ALU.mult))
        own.link(nc.vector.tensor_tensor(v, v, bc(eta[:, :], 1, DW), ALU.mult))
        dve.wait_ge(rooted, 1)
        own.link(nc.vector.tensor_scalar(norm[:, :, :], norm[:, :, :], NORM_EPS, None, ALU.add))
        own.link(nc.vector.reciprocal(norm[:, :, :], norm[:, :, :]))
        for i, w in enumerate((k, q)):
            own.link(nc.vector.tensor_tensor(w, w, bc(norm[:, i, :], 1, DW), ALU.mult))
        own.link(nc.vector.tensor_tensor(kb[:, :, :], k, bc(eta[:, :], 1, DW), ALU.mult))


STEP = 4


def recurrence(nc, c, stack, k, v, kb, u):
    w = c.sb("w", [P, NG, DW, DW])
    t1 = c.sb("t1", [P, NG, DW, DW])
    t2 = c.sb("t2", [P, NG, DW, DW])
    p = c.sb("p", [P, NG, DW])
    dve_own = c.sem("dve_own")
    block = c.block()

    def token(plane, t):
        return plane.rearrange("p d (g t) -> p g d t", g=NG)[:, :, :, bass.ds(t, 1)].rearrange("p g d a -> p g (d a)")

    @block.vector
    def _(dve):
        own = Chain(dve, dve_own)
        own.link(nc.vector.memset(w[:, :, :, :], 0.0))
        with dve.Fori(0, S // STEP) as turn:
            own.restart()
            for i in range(STEP):
                t = turn * STEP + i
                own.link(nc.vector.tensor_tensor(t1[:, :, :, :], w[:, :, :, :], bc(token(kb[:, :, :], t), 2, DW), ALU.mult))
                own.link(nc.vector.tensor_reduce(p[:, :, :], t1[:, :, :, :], AX, ALU.add))
                own.link(nc.vector.tensor_tensor(token(u[:, :, :], t), token(v, t), p[:, :, :], ALU.subtract))
                own.link(nc.vector.tensor_tensor(t2[:, :, :, :], bc(token(u[:, :, :], t), 3, DW), bc(token(k, t), 2, DW),
                                                 ALU.mult))
                own.link(nc.vector.tensor_tensor(w[:, :, :, :], w[:, :, :, :], t2[:, :, :, :], ALU.add))


def average(nc, T, const, c, stack, k, q, u, o):
    ident, ident16, causal16, ones, eps = const
    coef = c.sb("coef", [P, 3, S])
    fade = c.sb("fade", [P, 2, DW * NG, S])
    a = c.sb("a", [P, DW, GT])
    a2 = c.sb("a2", [P, DW, GT])
    rms = c.sb("rms", [P, DW])
    tiny = c.sb("tiny", [P, 1])
    ms = c.sb("ms", [P, GT])
    coef_in = c.sem("coef_in")
    faded = c.sem("faded")
    squares = c.sem("squares")
    summed = c.sem("summed")
    rooted = c.sem("rooted")
    dve_own = c.sem("dve_own")
    act_own = c.sem("act_own")
    block = c.block()

    @block.sync
    def _(sp):
        sp.dma_start(coef[:, :, :], T["coef"]).then_inc(coef_in, 16)
        sp.dma_start(rms[:, :], T["rms"]).then_inc(coef_in, 16)

    @block.scalar
    def _(act):
        act.wait_ge(coef_in, 32)
        for i in range(2):
            nc.scalar.activation(fade[:, i, :, :], bc(coef[:, i, :], 1, DW * NG), ACT.Copy).then_inc(faded, 1)
        act.wait_ge(squares, 1)
        nc.scalar.activation(a[:, :, :], o[:, :, :], ACT.Square).then_inc(squares, 1)
        act.wait_ge(summed, 1)
        nc.scalar.activation(ms[:, :], ms[:, :], ACT.Ln, scale=1.0 / DW, bias=tiny[:, 0:1]).then_inc(act_own, 1)
        act.wait_ge(act_own, 1)
        nc.scalar.activation(ms[:, :], ms[:, :], ACT.Exp, scale=-0.5).then_inc(rooted, 1)

    @block.vector
    def _(dve):
        own = Chain(dve, dve_own)
        own.link(nc.vector.memset(tiny[:, :], NORM_EPS))
        dve.wait_ge(coef_in, 32)
        own.link(nc.vector.tensor_tensor(u[:, :, :].rearrange("p d (g t) -> p (d g) t", g=NG),
                                         u[:, :, :].rearrange("p d (g t) -> p (d g) t", g=NG),
                                         bc(coef[:, 2, :], 1, DW * NG), ALU.mult))
        dve.wait_ge(faded, 2)
        flat = "p d n -> p (d n)"
        for d in range(DW):
            own.link(nc.vector.tensor_tensor(a[:, :, :], u[:, :, :], bc(k[:, d, :], 1, DW), ALU.mult))
            own.link(nc.vector.tensor_tensor_scan(a2[:, :, :].rearrange(flat), fade[:, 0, :, :].rearrange(flat),
                                                  a[:, :, :].rearrange(flat), 0.0, ALU.mult, ALU.add))
            own.link(nc.vector.tensor_tensor_scan(a[:, :, :].rearrange(flat), fade[:, 1, :, :].rearrange(flat),
                                                  a2[:, :, :].rearrange(flat), 0.0, ALU.mult, ALU.add))
            if d == 0:
                own.link(nc.vector.tensor_tensor(o[:, :, :], a[:, :, :], bc(q[:, d, :], 1, DW), ALU.mult))
            else:
                own.link(nc.vector.tensor_tensor(a2[:, :, :], a[:, :, :], bc(q[:, d, :], 1, DW), ALU.mult))
                own.link(nc.vector.tensor_tensor(o[:, :, :], o[:, :, :], a2[:, :, :], ALU.add))
        nc.vector.tensor_copy(ms[:, 0:1], o[:, 0, 0:1]).then_inc(squares, 1)
        dve.wait_ge(squares, 2)
        nc.vector.tensor_reduce(ms[:, :], a[:, :, :].rearrange("p e n -> p n e"), AX, ALU.add).then_inc(summed, 1)
        dve.wait_ge(rooted, 1)
        own.link(nc.vector.tensor_tensor(o[:, :, :], o[:, :, :], bc(ms[:, :], 1, DW), ALU.mult))
        own.link(nc.vector.tensor_tensor(o[:, :, :], o[:, :, :], bc(rms[:, :], 2, GT), ALU.mult))


def project_out(nc, T, const, c, stack, o):
    ident, ident16, causal16, ones, eps = const
    NT = NG * TT
    w = c.sb("w", [P, GB, DW, D])
    bout = c.sb("bout", [P, D])
    x = c.sb("x", [P, 2, NT, D])
    r = c.sb("r", [P, NT, D])
    stats = c.sb("stats", [P, NT, 6])
    mv = c.sb("mv", [P, NT, 2])
    rs = c.sb("rs", [P, NT])
    x4 = c.sb("x4", [P, NT, D])
    ps = [c.ps(f"ps{i}", [P, NT, D]) for i in range(2)]
    cleared = c.sem("cleared")
    weights_in = c.sem("weights_in")
    x_in = c.sem("x_in")
    out_ps = c.sem("out_ps")
    out_read = c.sem("out_read")
    ln_stats = c.sem("ln_stats")
    ln_rs = c.sem("ln_rs")
    ready = c.sem("x4_ready")
    stored = c.sem("stored")
    dve_own = c.sem("dve_own")
    act_own = c.sem("act_own")
    block = c.block()

    @block.gpsimd
    def _(pool):
        nc.gpsimd.memset(w[:, :, :, :], 0.0).then_inc(cleared, 1)

    @block.sync
    def _(sp):
        sp.dma_start(bout[:, :], T["bout"]).then_inc(weights_in, 16)
        sp.wait_ge(cleared, 1)
        for s in range(GB):
            sp.dma_start(w[DH * s:DH * (s + 1), s, :, :], T["delta_out"]).then_inc(weights_in, 16)
        with sp.Fori(0, GB) as s:
            sp.wait_ge(out_read, s)
            for g in range(NG):
                sp.dma_start(x[:, 0, g * TT:(g + 1) * TT, :],
                             T["x3"][bass.ds(s + g * GB, 1)].rearrange("b (t p) d -> p (b t) d", p=P)).then_inc(x_in, 16)
            sp.wait_ge(ready, s + 1)
            for g in range(NG):
                sp.dma_start(T["x4"][bass.ds(s + g * GB, 1)].rearrange("b (t p) d -> p (b t) d", p=P),
                             x4[:, g * TT:(g + 1) * TT, :]).then_inc(stored, 16)
        sp.wait_ge(stored, 16 * NG * GB)

    @block.tensor
    def _(pe):
        pe.wait_ge(weights_in, 16 * (GB + 1))
        with pe.Fori(0, GB) as s:
            pe.wait_ge(out_read, s)
            for n in range(NT):
                for e in range(DW):
                    mm = nc.tensor.matmul(ps[0][:, n, :], o[:, e, n * P:(n + 1) * P],
                                          w[:, bass.ds(s, 1), e, :].rearrange("p a n -> p (a n)"),
                                          start=(e == 0), stop=(e == DW - 1))
            mm.then_inc(out_ps, 1)

    @block.scalar
    def _(act):
        own = Chain(act, act_own)
        nc.scalar.preload_act_table_set("natural_log_exp_and_others")
        with act.Fori(0, GB) as s:
            own.restart()
            act.wait_ge(ln_stats, s + 1)
            own.link(nc.scalar.activation(rs[:, :], mv[:, :, 1], ACT.Ln, bias=eps[:, 0:1]))
            nc.scalar.activation(rs[:, :], rs[:, :], ACT.Exp, scale=-0.5).then_inc(ln_rs, 1)
            own.settle()

    @block.vector
    def _(dve):
        own = Chain(dve, dve_own)
        dve.wait_ge(weights_in, 16 * (GB + 1))
        with dve.Fori(0, GB) as s:
            own.restart()
            dve.wait_ge(x_in, 16 * NG * (s + 1))
            own.link(nc.vector.tensor_tensor(r[:, :, :], x[:, 0, :, :], bc(bout[:, :], 1, NT), ALU.add))
            dve.wait_ge(out_ps, s + 1)
            nc.vector.tensor_tensor(r[:, :, :], r[:, :, :], ps[0][:, :, :], ALU.add).then_inc(out_read, 1)
            dve.wait_ge(out_read, s + 1)
            layernorm(nc, dve, own, r, stats, mv, rs, x4, s, ln_stats, ln_rs, ready, stored, NT, 16 * NG)
            own.settle()


CH = 16
CD = 64
HP = CH // 2
INNER = CH * CD
TEXT, IMG = 77, 16
TI = TEXT + IMG
AUD = CTX - TI
REL = 16
NREL = 2 * REL + 1
SCALE = CD ** -0.5
AT = -(-AUD // P)
CHUNKS = 3
CHUNK = [min(512, AUD - 512 * i) for i in range(CHUNKS)]
UNITS = 4 * HP
RING = 4
HALVES = ((0, AT // 2), (AT // 2, AT))
R1, R2 = 19, NREL - 19
COL_R1, COL_I, COL_R2 = TEXT, TEXT + R1, TEXT + R1 + IMG
CAT = COL_R2 + R2
FROW = P - 1 + NREL
STEP_SCORES, STEP_EXP, STEP_SUM, STEP_FAR = 2, 8, 9, 18
HIGH = -0x1000
SCRATCH = {"skew_rel": (P, CH, P + TEXT - 1), "skew_prob": (P, CH, FROW)}


def fills_of():
    todo = [("q", 0, "dve")]
    for n in range(UNITS):
        for f in range(CHUNKS):
            todo.append(("t", (n, f), "act" if f == 2 else "dve"))
            if f == 0 and n % 2 == 0 and n // 2 + 1 < CH:
                todo.append(("q", n // 2 + 1, "dve"))
    for i in range(2 * CH // 4):
        todo.append(("c", i, "dve" if i % 2 else "act"))
    return todo


FILL_LIST = fills_of()
FILL_AT = {(w, a): i for i, (w, a, _) in enumerate(FILL_LIST)}


def emptied(i):
    eng = FILL_LIST[i][2]
    return eng, sum(1 for f in FILL_LIST[:i + 1] if f[2] == eng)


PER_TURN = {e: sum(1 for f in FILL_LIST if f[2] == e) for e in ("act", "dve")}


def cross_fold(nc, T, const, wo, fq, fv):
    ident, ident16, causal16, ones, eps = const
    with ExitStack() as stack:
        c = Scope(nc, stack, "fold")
        w = {n: c.sb(f"w_{n}", [P, INNER]) for n in ("q", "ka", "va")}
        wT = {n: c.sb(f"wT_{n}", [P, HP, P]) for n in w}
        ps_t = [c.ps(f"ps_t{i}", [P, 4, P]) for i in range(2)]
        ps_f = [c.ps(f"ps_f{i}", [P, 4, P]) for i in range(4)]
        w_in = c.sem("w_in")
        t_ps = c.sem("t_ps")
        t_sb = c.sem("t_sb")
        f_ps = c.sem("f_ps")
        f_sb = c.sem("f_sb")
        block = c.block()

        @block.sync
        def _(sp):
            for n in w:
                sp.dma_start(w[n][:, :], T[f"cross_{n}"]).then_inc(w_in, 16)
            sp.dma_start(wo[:, :, :], T["cross_o"]).then_inc(w_in, 16)

        @block.tensor
        def _(pe):
            pe.wait_ge(w_in, 64)
            for i, (n, g) in enumerate([(n, g) for n in w for g in range(2)]):
                if i >= 2:
                    pe.wait_ge(t_sb, i - 1)
                for p in range(4):
                    at = (4 * g + p) * P
                    mm = nc.tensor.transpose(ps_t[i % 2][:, p, :], w[n][:, at:at + P], ident[:, :])
                mm.then_inc(t_ps, 1)
            pe.wait_ge(t_sb, 6)
            for i, (left, right) in enumerate([(wT["q"], wT["ka"])] * 2 + [(wT["va"], wo)] * 2):
                if i >= 2:
                    pe.wait_ge(f_sb, 2 * (i - 1))
                for odd in range(2):
                    rows = slice(CD * odd, CD * odd + CD)
                    for p in range(4):
                        pair = 4 * (i % 2) + p
                        mm = nc.tensor.matmul(ps_f[2 * (i % 2) + odd][:, p, :], left[rows, pair, :], right[rows, pair, :],
                                              start=True, stop=True)
                    mm.then_inc(f_ps, 1)

        @block.scalar
        def _(act):
            for i, (n, g) in enumerate([(n, g) for n in w for g in range(2)]):
                act.wait_ge(t_ps, i + 1)
                nc.scalar.activation(wT[n][:, 4 * g:4 * g + 4, :], ps_t[i % 2][:, :, :], ACT.Copy).then_inc(t_sb, 1)

        @block.vector
        def _(dve):
            for i in range(8):
                dst, half, odd = (fq, fv)[i // 4], i // 2 % 2, i % 2
                dve.wait_ge(f_ps, i + 1)
                nc.vector.tensor_scalar(dst[:, 8 * half + odd:8 * half + 8:2, :], ps_f[2 * half + odd][:, :, :],
                                        SCALE if i < 4 else 1.0, None, ALU.mult).then_inc(f_sb, 1)


def cross_stage(nc, T, const):
    ident, ident16, causal16, ones, eps = const
    with ExitStack() as stack:
        c = Scope(nc, stack, "cross")
        wo = c.sb("wo", [P, HP, D])
        fq = c.sb("fq", [P, CH, P])
        fv = c.sb("fv", [P, CH, D])
        cross_fold(nc, T, const, wo, fq, fv)
        w = {n: c.sb(f"w_{n}", [P, INNER]) for n in ("q", "k", "v", "ki", "vi")}
        bo = c.sb("bo", [P, D])
        relk = c.sb("relk", [P, NREL])
        gains = c.sb("gains", [P, 2])
        far = c.sb("far", [P, 2, TEXT])
        x = c.sb("x", [P, TT, D])
        cx = c.sb("cx", [P, AT, D])
        xs = c.sb("xs", [P, TT, D])
        cs = c.sb("cs", [P, AT + 1, D])
        xT = c.sb("xT", [P, S])
        cT = c.sb("cT", [P, TI])
        upper = c.sb("upper", [P, 512])
        q_upper = c.sb("q_upper", [P, S])
        cTh = c.sb("cTh", [P, AUD], F32R)
        cTl = c.sb("cTl", [P, AUD], F32R)
        qT = c.sb("qT", [P, HP, S])
        kti = c.sb("kti", [P, HP, TI])
        vcat = c.sb("vcat", [P, INNER])
        sti = c.sb("sti", [P, TT, CH, TI])
        ext = c.sb("ext", [P, CH, P + TEXT - 1])
        rel = c.sb("rel", [P, TT, CH, TEXT])
        near = c.sb("near", [P, CH])
        pcat = c.sb("pcat", [P, TT, CH, CAT])
        pcT = c.sb("pcT", [P, 2, 4, P])
        small = c.sb("small", [P, 2, TT, CH])
        qh = c.sb("qh", [P, 2, S], F32R)
        ql = c.sb("ql", [P, 2, S], F32R)
        prob = c.sb("prob", [P, AT * P])
        pT = c.sb("pT", [P, 2, AT, S])
        uT = c.sb("uT", [P, S])
        acc = c.sb("acc", [P, TT, D])
        max3 = c.sb("max3", [P, 2, CHUNKS])
        negmax = c.sb("negmax", [P, 2])
        sums = c.sb("sums", [P, UNITS, CHUNKS])
        rsum = c.sb("rsum", [P, CH, TT])
        oall = c.sb("oall", [P, TT, CH, CD])
        oT = c.sb("oT", [P, HP, S])
        r = c.sb("r", [P, TT, D])
        stats = c.sb("stats", [P, TT, 6])
        mv = c.sb("mv", [P, TT, 2])
        rs = c.sb("rs", [P, TT])
        x5 = c.sb("x5", [P, TT, D])
        ring = [c.ps(f"ring{i}", [P, 512]) for i in range(RING)]
        fill = [c.ps(f"fill{i}", [P, 512]) for i in range(2)]
        ps_u = c.ps("ps_u", [P, 512])
        ps_y = c.ps("ps_y", [P, 512])

        weights_in = c.sem("weights_in")
        rel_in = c.sem("rel_in")
        cleared = c.sem("cleared")
        far_ready = c.sem("far_ready")
        gains_ready = c.sem("gains_ready")
        zeroed = c.sem("zeroed")
        x_in = c.sem("x_in")
        turned = c.sem("turned")
        turned_act = c.sem("turned_act")
        turned_dve = c.sem("turned_dve")
        q_ps = c.sem("q_ps")
        q_sb = c.sem("q_sb")
        kti_ps = c.sem("kti_ps")
        kti_sb = c.sem("kti_sb")
        vcat_ps = c.sem("vcat_ps")
        vcat_sb = c.sem("vcat_sb")
        ti_ps = c.sem("ti_ps")
        rel_ps = c.sem("rel_ps")
        ti_sb = c.sem("ti_sb")
        rel_sb = c.sem("rel_sb")
        skewed_out = c.sem("skewed_out")
        skewed_in = c.sem("skewed_in")
        ti_max = c.sem("ti_max")
        ti_sub = c.sem("ti_sub")
        ti_exp = c.sem("ti_exp")
        ti_sum = c.sem("ti_sum")
        ti_prob = c.sem("ti_prob")
        band_out = c.sem("band_out")
        band_in = c.sem("band_in")
        far_prob = c.sem("far_prob")
        cat_ready = c.sem("cat_ready")
        scores = c.sem("scores")
        maxed = c.sem("maxed")
        exps = c.sem("exps")
        fill_ps = c.sem("fill_ps")
        fill_sb = {"act": c.sem("fill_act"), "dve": c.sem("fill_dve")}
        copied = c.sem("copied")
        q_high = c.sem("q_high")
        u_ps = c.sem("u_ps")
        u_sb = c.sem("u_sb")
        y_ps = c.sem("y_ps")
        y_read = c.sem("y_read")
        cat_ps = c.sem("cat_ps")
        o_ready = c.sem("o_ready")
        oT_ps = c.sem("oT_ps")
        oT_sb = c.sem("oT_sb")
        out_ps = c.sem("out_ps")
        out_read = c.sem("out_read")
        ln_stats = c.sem("ln_stats")
        ln_rs = c.sem("ln_rs")
        x5_ready = c.sem("x5_ready")
        stored = c.sem("stored")
        dve_own = c.sem("dve_own")
        act_own = c.sem("act_own")
        pool_own = c.sem("pool_own")
        block = c.block()
        e_w, f_w = P + TEXT - 1, FROW

        @block.sync
        def _(sp):
            for dst, src in [(w[n][:, :], T[f"cross_{n}"]) for n in w] + [
                    (bo[:, :], T["cross_bo"]), (relk[:, :], T["relk"]), (gains[:, :], T["gains"])]:
                sp.dma_start(dst, src).then_inc(weights_in, 16)
            for lo, n, col in ((0, R1, COL_R1), (R1, R2, COL_R2)):
                sp.dma_start(vcat[col:col + n, :].rearrange("r (h d) -> r h d", h=CH),
                             bc(T["relv"][lo:lo + n], 1, CH)).then_inc(rel_in, 16)
            sp.wait_ge(cleared, 3)
            sp.dma_start(T["skew_prob"], ext[:, :, 0:f_w]).then_inc(zeroed, 16)
            sp.wait_ge(zeroed, 16)
            full = (AT - 1) * P

            def load(b):
                sp.dma_start(xs[:, :, :], T["x4"][b].rearrange("(t p) d -> p t d", p=P)).then_inc(x_in, 16)
                sp.dma_start(cs[0:TI, 0, :], T["ctx"][b, 0:TI]).then_inc(x_in, 16)
                sp.dma_start(cs[:, 1:AT, :], T["ctx"][b, TI:TI + full].rearrange("(t p) d -> p t d", p=P)).then_inc(x_in, 16)
                sp.dma_start(cs[0:AUD - full, AT, :], T["ctx"][b, TI + full:CTX]).then_inc(x_in, 16)

            def turn(b):
                sp.wait_ge(rel_sb, 2 * b + 1)
                sp.dma_start(T["skew_rel"], ext[:, :, :]).then_inc(skewed_out, 16)
                sp.wait_ge(skewed_out, 16 * (b + 1))
                sp.wait_ge(ti_sub, b)
                sp.dma_start(rel[:, 0, :, :], bass.AP(T["skew_rel"].tensor, P - 1, [[CH * e_w - 1, P], [e_w, CH], [1, TEXT]]))\
                    .then_inc(skewed_in, 16)
                sp.wait_ge(ti_prob, b + 1)
                sp.dma_start(T["skew_prob"][:, :, REL:REL + TEXT], pcat[:, 0, :, 0:TEXT]).then_inc(band_out, 16)
                sp.wait_ge(band_out, 16 * (b + 1))
                for lo, n, col in ((0, R1, COL_R1), (R1, R2, COL_R2)):
                    sp.dma_start(pcat[:, 0, :, col:col + n],
                                 bass.AP(T["skew_prob"].tensor, lo, [[CH * f_w + 1, P], [f_w, CH], [1, n]])).then_inc(band_in, 16)
                sp.wait_ge(x5_ready, b + 1)
                sp.dma_start(T["x5"][b].rearrange("(t p) d -> p t d", p=P), x5[:, :, :]).then_inc(stored, 16)

            load(0)
            with sp.Fori(0, B - 1) as b:
                hold(sp, turned, 4 * (b + 1))
                hold(sp, copied, 3 * (b + 1))
                load(b + 1)
                turn(b)
            turn(B - 1)
            sp.wait_ge(stored, 16 * B)

        @block.tensor
        def _(pe):
            pe.wait_ge(weights_in, 16 * 8)
            pe.wait_ge(rel_in, 32)
            with pe.Fori(0, B) as b:

                waited = {"act": 0, "dve": 0}

                def wait_fill(*which):
                    need = {"act": -1, "dve": -1}
                    for i in which:
                        if i < 0:
                            need = {e: max(n, 0) for e, n in need.items()}
                        else:
                            e, n = emptied(i)
                            need[e] = max(need[e], n)
                    for e, n in need.items():
                        if n > waited[e] or n == waited[e] == 0:
                            pe.wait_ge(fill_sb[e], b * PER_TURN[e] + n)
                            waited[e] = n

                def project(h):
                    n = FILL_AT[("q", h)]
                    wait_fill(n - 2)
                    nc.tensor.matmul(fill[n % 2][:, 0:S], fq[:, h, :], xT[:, :], start=True, stop=True).then_inc(fill_ps, 1)

                def score(n, i):
                    k = n * CHUNKS + i
                    h, t = divmod(n, TT)
                    if t == 0 and i == 0:
                        wait_fill(FILL_AT[("q", h)])
                    if k >= RING:
                        pe.wait_ge(exps, b * UNITS * CHUNKS + k - RING + 1)
                    tile, keys = slice(t * P, (t + 1) * P), slice(512 * i, 512 * i + CHUNK[i])
                    for j, (q, k_part) in enumerate(((qh, cTh), (qh, cTl), (ql, cTh))):
                        mm = nc.tensor.matmul(ring[k % RING][:, 0:CHUNK[i]], q[:, h % 2, tile],
                                              k_part[:, keys], start=(j == 0), stop=(j == 2))
                    mm.then_inc(scores, 1)

                def turn(n, i):
                    k = FILL_AT[("t", (n, i))]
                    wait_fill(k - 2)
                    pe.wait_ge(exps, b * UNITS * CHUNKS + n * CHUNKS + i + 1)
                    for t in range(4):
                        m = min(P, AUD - (4 * i + t) * P)
                        mm = nc.tensor.transpose(fill[k % 2][0:m, t * P:(t + 1) * P],
                                                 prob[:, (4 * i + t) * P:(4 * i + t) * P + m], ident[:, :])
                    mm.then_inc(fill_ps, 1)

                def attend(h, half):
                    if half == 0:
                        pe.wait_ge(u_sb, b * CH + h)
                        wait_fill(*[FILL_AT[("t", (TT * h + t, i))] for t in range(TT) for i in range(CHUNKS)])
                    for kt in range(*HALVES[half]):
                        m = min(P, AUD - kt * P)
                        mm = nc.tensor.matmul(ps_u[:, 0:S], cx[0:m, kt, :], pT[0:m, h % 2, kt, :],
                                              start=(kt == 0), stop=(kt == AT - 1), skip_group_check=True)
                    if half == 1:
                        mm.then_inc(u_ps, 1)

                def give(h):
                    pe.wait_ge(u_sb, b * CH + h + 1)
                    pe.wait_ge(y_read, b * CH + h)
                    for t in range(TT):
                        mm = nc.tensor.matmul(ps_y[:, t * D:(t + 1) * D], uT[:, t * P:(t + 1) * P], fv[:, h, :],
                                              start=True, stop=True)
                    mm.then_inc(y_ps, 1)

                pe.wait_ge(out_read, b)
                pe.wait_ge(x_in, 64 * (b + 1))
                for t in range(TT):
                    nc.tensor.transpose(ring[0][:, t * P:(t + 1) * P], xs[:, t, :], ident[:, :])
                nc.tensor.transpose(ring[0][:, S:S + TI], cs[0:TI, 0, :], ident[0:TI, 0:TI]).then_inc(turned, 1)
                for i in range(CHUNKS):
                    for t in range(4 * i, 4 * i + 4):
                        m = min(P, AUD - t * P)
                        mm = nc.tensor.transpose(ring[i + 1][:, (t % 4) * P:(t % 4) * P + m], cs[0:m, t + 1, :],
                                                 ident[0:m, 0:m])
                    mm.then_inc(turned, 1)
                pe.wait_ge(turned_act, 2 * (b + 1))
                pe.wait_ge(turned_dve, 2 * CHUNKS * (b + 1))
                for p in range(HP):
                    mm = nc.tensor.matmul(ring[p // 2][:, (p % 2) * S:(p % 2 + 1) * S], w["q"][:, p * P:(p + 1) * P], xT[:, :],
                                          start=True, stop=True)
                    if p % 2:
                        mm.then_inc(q_ps, 1)
                for p in range(HP):
                    bank = (ps_u, ps_y)[p // 4]
                    off = (p % 4) * TI
                    nc.tensor.matmul(bank[:, off:off + TEXT], w["k"][:, p * P:(p + 1) * P], cT[:, 0:TEXT], start=True, stop=True)
                    mm = nc.tensor.matmul(bank[:, off + TEXT:off + TI], w["ki"][:, p * P:(p + 1) * P], cT[:, TEXT:TI],
                                          start=True, stop=True)
                mm.then_inc(kti_ps, 1)
                pe.wait_ge(q_sb, 4 * (b + 1))
                for i in range(2):
                    nc.tensor.matmul(ring[i][0:TEXT, :], cT[:, 0:TEXT], w["v"][:, 512 * i:512 * i + 512], start=True, stop=True)
                    mm = nc.tensor.matmul(ring[i][COL_I:COL_I + IMG, :], cT[:, TEXT:TI], w["vi"][:, 512 * i:512 * i + 512],
                                          start=True, stop=True)
                mm.then_inc(vcat_ps, 1)
                pe.wait_ge(vcat_sb, b + 1)
                pe.wait_ge(kti_sb, b + 1)
                for t in range(TT):
                    if t:
                        pe.wait_ge(ti_sb, TT * b + t)
                        pe.wait_ge(rel_sb, TT * b + t)
                    for h in range(CH):
                        p, odd = h // 2, h % 2
                        rows = slice(CD * odd, CD * odd + CD)
                        mm = nc.tensor.matmul(ring[2 * odd + p // 4][:, (p % 4) * TI:(p % 4 + 1) * TI],
                                              qT[rows, p, t * P:(t + 1) * P], kti[rows, p, :], start=True, stop=True)
                    mm.then_inc(ti_ps, 1)
                    for h in range(CH):
                        p, odd = h // 2, h % 2
                        rows = slice(CD * odd, CD * odd + CD)
                        mm = nc.tensor.matmul((ps_u, ps_y)[odd][:, p * NREL:(p + 1) * NREL],
                                              qT[rows, p, t * P:(t + 1) * P], relk[rows, :], start=True, stop=True)
                    mm.then_inc(rel_ps, 1)
                project(0)
                pe.wait_ge(copied, 3 * (b + 1))
                pe.wait_ge(ti_sb, TT * (b + 1))
                pe.wait_ge(rel_sb, TT * (b + 1))
                for i in range(CHUNKS):
                    score(0, i)
                for n in range(UNITS):
                    for i in range(CHUNKS):
                        turn(n, i)
                        if n + 1 < UNITS:
                            score(n + 1, i)
                        if i == 0 and n % 2 == 0 and n // 2 + 1 < CH:
                            project(n // 2 + 1)
                    if n % 2 == 0 and n >= 4:
                        give(n // 2 - 2)
                    if n >= 2:
                        attend(n // 2 - 1, n % 2)
                pe.wait_ge(cat_ready, b + 1)

                def cat_products(i):
                    wait_fill(FILL_AT[("c", i)])
                    t, g = divmod(i, CH // 4)
                    for j in range(4):
                        h = 4 * g + j
                        mm = nc.tensor.matmul(ring[2 * t + h // 8][:, (h % 8) * CD:(h % 8 + 1) * CD], pcT[0:CAT, i % 2, j, :],
                                              vcat[0:CAT, h * CD:(h + 1) * CD], start=True, stop=True)
                    return mm

                def cat_turn(i):
                    k = FILL_AT[("c", i)]
                    t, g = divmod(i, CH // 4)
                    wait_fill(k - 2)
                    for j in range(4):
                        mm = nc.tensor.transpose(fill[k % 2][0:CAT, j * P:(j + 1) * P], pcat[:, t, 4 * g + j, :], ident[:, :])
                    mm.then_inc(fill_ps, 1)

                cat_turn(0)
                attend(CH - 1, 0)
                give(CH - 2)
                attend(CH - 1, 1)
                pe.wait_ge(exps, (b + 1) * UNITS * CHUNKS)
                for i in range(1, TT * CH // 4):
                    cat_turn(i)
                    cat_products(i - 1)
                cat_products(TT * CH // 4 - 1).then_inc(cat_ps, 1)
                give(CH - 1)
                pe.wait_ge(o_ready, 4 * (b + 1))
                for p in range(HP):
                    for t in range(TT):
                        mm = nc.tensor.transpose(ring[p // 2][:, (p % 2 * TT + t) * P:(p % 2 * TT + t + 1) * P],
                                                 oall[:, t, 2 * p:2 * p + 2, :].rearrange("p a d -> p (a d)"), ident[:, :])
                    if p % 2:
                        mm.then_inc(oT_ps, 1)
                pe.wait_ge(oT_sb, 4 * (b + 1))
                for t in range(TT):
                    for p in range(HP):
                        mm = nc.tensor.matmul(ps_u[:, t * D:(t + 1) * D], oT[:, p, t * P:(t + 1) * P], wo[:, p, :],
                                              start=(p == 0), stop=(p == HP - 1))
                mm.then_inc(out_ps, 1)

        def empty(eng, copy, name, b, i):
            what, arg, _ = FILL_LIST[i]
            bank = fill[i % 2]
            eng.wait_ge(fill_ps, b * len(FILL_LIST) + i + 1)
            if what == "q":
                nc.vector.tensor_scalar(q_upper[:, :].bitcast(U32), bank[:, 0:S].bitcast(U32), HIGH, None, ALU.bitwise_and)\
                    .then_inc(q_high, 1)
                eng.wait_ge(q_high, 3 * (b * CH + arg) + 1)
                nc.vector.tensor_copy(qh[:, arg % 2, :], q_upper[:, :]).then_inc(q_high, 1)
                nc.vector.tensor_tensor(ql[:, arg % 2, :], bank[:, 0:S], q_upper[:, :], ALU.subtract).then_inc(q_high, 1)
                eng.wait_ge(q_high, 3 * (b * CH + arg) + 3)
                eng.sem_inc(fill_sb[name], 1)
                return
            if what == "t":
                n, j = arg
                h, t = divmod(n, TT)
                tile = slice(t * P, (t + 1) * P)
                dst, src = pT[:, h % 2, 4 * j:4 * j + 4, tile], bank[:, :].rearrange("p (k n) -> p k n", n=P)
                if j == CHUNKS - 1:
                    m = AUD - (AT - 1) * P
                    copy(pT[:, h % 2, 4 * j:AT - 1, tile], src[:, 0:3, :])
                    dst, src = pT[0:m, h % 2, AT - 1, tile], bank[0:m, 3 * P:]
            else:
                dst, src = pcT[0:CAT, arg % 2, :, :].rearrange("p t d -> p (t d)"), bank[0:CAT, :]
            copy(dst, src).then_inc(fill_sb[name], 1)

        @block.scalar
        def _(act):
            own = Chain(act, act_own)

            def copy(dst, src):
                return nc.scalar.activation(dst, src, ACT.Copy)

            act.wait_ge(weights_in, 16 * 8)
            own.link(nc.scalar.activation(gains[:, :], gains[:, :], ACT.Tanh))
            nc.scalar.activation(gains[:, :], gains[:, :], ACT.Identity, bias=ones[:, 0:1]).then_inc(gains_ready, 1)
            nc.scalar.preload_act_table_set("natural_log_exp_and_others")
            with act.Fori(0, B) as b:
                own.restart()
                act.wait_ge(turned, 4 * b + 1)
                for dst, src in ((xT[:, :], ring[0][:, 0:S]), (cT[:, :], ring[0][:, S:S + TI])):
                    copy(dst, src).then_inc(turned_act, 1)
                for i in range(4):
                    act.wait_ge(q_ps, 4 * b + i + 1)
                    nc.scalar.activation(qT[:, 2 * i:2 * i + 2, :], ring[i][:, :].rearrange("p (a n) -> p a n", a=2), ACT.Copy,
                                         scale=SCALE).then_inc(q_sb, 1)
                act.wait_ge(vcat_ps, b + 1)
                for i in range(2):
                    for lo, n in ((0, TEXT), (COL_I, IMG)):
                        ins = copy(vcat[lo:lo + n, 512 * i:512 * i + 512], ring[i][lo:lo + n, :])
                ins.then_inc(vcat_sb, 1)
                for t in range(TT):
                    act.wait_ge(ti_ps, TT * b + t + 1)
                    for i in range(4):
                        h = 8 * (i % 2) + i // 2
                        ins = copy(sti[:, t, h:h + 7:2, :], ring[i][:, 0:4 * TI].rearrange("p (a n) -> p a n", a=4))
                    ins.then_inc(ti_sb, 1)
                order = [k for k, f in enumerate(FILL_LIST) if f[2] == "act"]

                def empty_until(k):
                    while order and order[0] <= k:
                        empty(act, copy, "act", b, order.pop(0))

                def keep(h):
                    act.wait_ge(u_ps, b * CH + h + 1)
                    act.wait_ge(y_ps, b * CH + h)
                    copy(uT[:, :], ps_u[:, 0:S]).then_inc(u_sb, 1)

                for n in range(UNITS):
                    if n == STEP_EXP:
                        act.wait_ge(ti_sub, b + 1)
                        nc.scalar.activation(sti[:, :, :, :], sti[:, :, :, :], ACT.Exp).then_inc(ti_exp, 1)
                    act.wait_ge(maxed, b * UNITS + n + 1)
                    for i in range(CHUNKS):
                        nc.scalar.activation(prob[:, 512 * i:512 * i + CHUNK[i]],
                                             ring[(n * CHUNKS + i) % RING][:, 0:CHUNK[i]], ACT.Exp,
                                             bias=negmax[:, n % 2:n % 2 + 1], accum_out=sums[:, n, i:i + 1]).then_inc(exps, 1)
                    if n % 2 == 0 and n >= 4:
                        keep(n // 2 - 2)
                    empty_until(FILL_AT[("t", (n, CHUNKS - 1))])
                keep(CH - 2)
                empty_until(FILL_AT[("c", 0)])
                keep(CH - 1)
                empty_until(len(FILL_LIST))
                act.wait_ge(cat_ps, b + 1)
                for i in range(2):
                    copy(oall[:, 0, 8 * i:8 * i + 8, :], ring[i][:, :].rearrange("p (a d) -> p a d", d=CD)).then_inc(o_ready, 1)
                for i in range(4):
                    act.wait_ge(oT_ps, 4 * b + i + 1)
                    copy(oT[:, 2 * i:2 * i + 2, :], ring[i][:, :].rearrange("p (a n) -> p a n", a=2)).then_inc(oT_sb, 1)
                act.wait_ge(ln_stats, b + 1)
                own.link(nc.scalar.activation(rs[:, :], mv[:, :, 1], ACT.Ln, bias=eps[:, 0:1]))
                nc.scalar.activation(rs[:, :], rs[:, :], ACT.Exp, scale=-0.5).then_inc(ln_rs, 1)
                own.settle()

        @block.gpsimd
        def _(pool):
            own = Chain(pool, pool_own)
            nc.gpsimd.memset(pcat[:, :, :, :], 0.0).then_inc(cleared, 1)
            nc.gpsimd.memset(ext[:, :, :], 0.0).then_inc(cleared, 1)
            nc.gpsimd.memset(far[:, :, :], 0.0).then_inc(cleared, 1)
            pool.wait_ge(cleared, 3)
            nc.gpsimd.affine_select(out=far[:, 0, :], in_=far[:, 0, :], compare_op=ALU.is_gt, fill=1.0,
                                    base=REL, pattern=[[1, TEXT]], channel_multiplier=-1).then_inc(far_ready, 1)
            nc.gpsimd.affine_select(out=far[:, 1, :], in_=far[:, 1, :], compare_op=ALU.is_gt, fill=1.0,
                                    base=REL, pattern=[[-1, TEXT]], channel_multiplier=1).then_inc(far_ready, 1)
            pool.wait_ge(far_ready, 2)
            with pool.Fori(0, B) as b:
                own.restart()
                pool.wait_ge(out_read, b)
                hold(pool, x_in, 64 * (b + 1))
                m = AUD - (AT - 1) * P
                for dst, src in ((x[:, :, :], xs[:, :, :]), (cx[:, 0:AT - 1, :], cs[:, 1:AT, :]), (cx[0:m, AT - 1, :], cs[0:m, AT, :])):
                    nc.gpsimd.tensor_copy(dst, src).then_inc(copied, 1)
                pool.wait_ge(ti_max, 2 * (b + 1))
                nc.gpsimd.tensor_tensor(sti[:, :, :, 0:TEXT], sti[:, :, :, 0:TEXT], bc(small[:, 0, :, :], 3, TEXT),
                                        ALU.subtract).then_inc(pool_own, 1)
                nc.gpsimd.tensor_tensor(sti[:, :, :, TEXT:], sti[:, :, :, TEXT:], bc(small[:, 1, :, :], 3, IMG),
                                        ALU.subtract).then_inc(ti_sub, 1)
                pool.wait_ge(ti_sum, b + 1)
                nc.gpsimd.tensor_tensor(pcat[:, :, :, COL_I:COL_I + IMG], sti[:, :, :, TEXT:], bc(small[:, 1, :, :], 3, IMG),
                                        ALU.mult).then_inc(pool_own, 1)
                nc.gpsimd.tensor_tensor(pcat[:, :, :, 0:TEXT], sti[:, :, :, 0:TEXT], bc(small[:, 0, :, :], 3, TEXT),
                                        ALU.mult).then_inc(ti_prob, 1)
                pool.wait_ge(pool_own, 2)
                pool.wait_ge(ti_prob, b + 1)
                for i in range(2):
                    nc.gpsimd.tensor_tensor(rel[:, i, :, :], pcat[:, 0, :, 0:TEXT], bc(far[:, i, :], 1, CH), ALU.mult)\
                        .then_inc(far_prob, 1)

        @block.vector
        def _(dve):
            own = Chain(dve, dve_own)

            def copy(dst, src):
                return nc.vector.tensor_copy(dst, src)

            dve.wait_ge(weights_in, 16 * 8)
            dve.wait_ge(gains_ready, 1)
            dve.wait_ge(zeroed, 16)
            with dve.Fori(0, B) as b:
                own.restart()
                for i in range(CHUNKS):
                    dve.wait_ge(turned, 4 * b + i + 2)
                    keys, src = slice(512 * i, 512 * i + CHUNK[i]), ring[i + 1][:, 0:CHUNK[i]]
                    high = upper[:, 0:CHUNK[i]]
                    own.link(nc.vector.tensor_scalar(high.bitcast(U32), src.bitcast(U32), HIGH, None, ALU.bitwise_and))
                    nc.vector.tensor_copy(cTh[:, keys], high).then_inc(turned_dve, 1)
                    nc.vector.tensor_tensor(cTl[:, keys], src, high, ALU.subtract).then_inc(turned_dve, 1)
                    dve.wait_ge(turned_dve, 2 * (CHUNKS * b + i + 1))
                dve.wait_ge(kti_ps, b + 1)
                for i in range(2):
                    ins = copy(kti[:, 4 * i:4 * i + 4, :], (ps_u, ps_y)[i][:, 0:4 * TI].rearrange("p (a n) -> p a n", a=4))
                ins.then_inc(kti_sb, 1)
                dve.wait_ge(rel_ps, TT * b + 1)
                dve.wait_ge(skewed_out, 16 * b)
                lo = P - 1 - REL
                for odd in range(2):
                    src = (ps_u, ps_y)[odd][:, 0:HP * NREL].rearrange("p (a n) -> p a n", a=HP)
                    nc.vector.tensor_copy(ext[:, odd::2, lo:lo + NREL], src)
                    nc.vector.tensor_copy(ext[:, odd::2, 0:lo], src[:, :, 0:1].broadcast_to([P, HP, lo]))
                    ins = nc.vector.tensor_copy(ext[:, odd::2, lo + NREL:],
                                                src[:, :, NREL - 1:].broadcast_to([P, HP, e_w - lo - NREL]))
                ins.then_inc(rel_sb, 1)
                dve.wait_ge(rel_ps, TT * b + 2)
                for odd in range(2):
                    src = (ps_u, ps_y)[odd][:, 0:HP * NREL].rearrange("p (a n) -> p a n", a=HP)
                    ins = nc.vector.tensor_copy(near[:, odd::2], src[:, :, 0])
                ins.then_inc(rel_sb, 1)
                order = [k for k, f in enumerate(FILL_LIST) if f[2] == "dve"]

                def empty_next():
                    empty(dve, copy, "dve", b, order.pop(0))

                def chunk_max(n, i):
                    k = n * CHUNKS + i
                    dve.wait_ge(scores, b * UNITS * CHUNKS + k + 1)
                    own.count(nc.vector.tensor_reduce(max3[:, n % 2, i:i + 1], ring[k % RING][:, 0:CHUNK[i]], AX, ALU.max))
                    if i == CHUNKS - 1:
                        own.settle()
                        nc.vector.tensor_reduce(negmax[:, n % 2:n % 2 + 1], max3[:, n % 2, :], AX, ALU.max, negate=True)\
                            .then_inc(maxed, 1)

                def text_scores():
                    dve.wait_ge(skewed_in, 16 * (b + 1))
                    dve.wait_ge(ti_sb, TT * (b + 1))
                    own.count(nc.vector.tensor_tensor(sti[:, 0, :, 0:TEXT], sti[:, 0, :, 0:TEXT], rel[:, 0, :, :], ALU.add))
                    dve.wait_ge(rel_sb, TT * (b + 1))
                    own.link(nc.vector.tensor_tensor(sti[:, 1, :, 0:TEXT], sti[:, 1, :, 0:TEXT], bc(near[:, :], 2, TEXT), ALU.add))

                def text_max():
                    nc.vector.tensor_reduce(small[:, 0, :, :], sti[:, :, :, 0:TEXT], AX, ALU.max).then_inc(ti_max, 1)
                    nc.vector.tensor_reduce(small[:, 1, :, :], sti[:, :, :, TEXT:], AX, ALU.max).then_inc(ti_max, 1)

                def text_sum():
                    dve.wait_ge(ti_exp, b + 1)
                    own.count(nc.vector.tensor_reduce(small[:, 0, :, :], sti[:, :, :, 0:TEXT], AX, ALU.add))
                    own.link(nc.vector.tensor_reduce(small[:, 1, :, :], sti[:, :, :, TEXT:], AX, ALU.add))
                    own.link(nc.vector.reciprocal(small[:, :, :, :], small[:, :, :, :]))
                    nc.vector.tensor_scalar(small[:, 1, :, :], small[:, 1, :, :], gains[:, 0:1], None, ALU.mult)\
                        .then_inc(ti_sum, 1)

                def far_sums():
                    dve.wait_ge(far_prob, 2 * (b + 1))
                    dve.wait_ge(band_in, 32 * (b + 1))
                    nc.vector.tensor_reduce(pcat[:, 0, :, COL_R1], rel[:, 0, :, :], AX, ALU.add)
                    own.count(nc.vector.tensor_reduce(pcat[:, 0, :, CAT - 1], rel[:, 1, :, :], AX, ALU.add))
                    nc.vector.tensor_reduce(pcat[:, 1, :, COL_R1], pcat[:, 1, :, 0:TEXT], AX, ALU.add).then_inc(cat_ready, 1)

                steps = {STEP_SCORES: text_scores, STEP_SCORES + 1: text_max, STEP_SUM: text_sum, STEP_FAR: far_sums}

                def add_head(h):
                    dve.wait_ge(exps, b * UNITS * CHUNKS + (h + 1) * TT * CHUNKS)
                    own.link(nc.vector.tensor_reduce(rsum[:, h, :], sums[:, TT * h:TT * h + TT, :], AX, ALU.add))
                    own.link(nc.vector.reciprocal(rsum[:, h, :], rsum[:, h, :]))
                    dve.wait_ge(y_ps, b * CH + h + 1)
                    for t in range(TT):
                        y, rt = ps_y[:, t * D:(t + 1) * D], rsum[:, h, t:t + 1]
                        if h == 0:
                            ins = nc.vector.tensor_scalar(acc[:, t, :], y, rt, None, ALU.mult)
                        else:
                            ins = nc.vector.scalar_tensor_tensor(acc[:, t, :], y, rt, acc[:, t, :], ALU.mult, ALU.add)
                        if t == 0:
                            own.count(ins)
                    ins.then_inc(y_read, 1)
                    dve.wait_ge(y_read, b * CH + h + 1)
                    own.settle()

                empty_next()
                for i in range(CHUNKS):
                    chunk_max(0, i)
                for n in range(UNITS):
                    for i in range(CHUNKS):
                        if order and order[0] == FILL_AT[("t", (n, i))]:
                            empty_next()
                        if n + 1 < UNITS:
                            chunk_max(n + 1, i)
                        stop = FILL_AT[("t", (n, i + 1))] if i + 1 < CHUNKS else FILL_AT[("t", (n, i))] + 1
                        while order and order[0] < stop:
                            empty_next()
                    if n % 2 == 0 and n >= 4:
                        add_head(n // 2 - 2)
                    if n in steps:
                        steps[n]()
                add_head(CH - 2)
                while order:
                    empty_next()
                dve.wait_ge(cat_ps, b + 1)
                for i in range(2, 4):
                    copy(oall[:, 1, 8 * (i - 2):8 * (i - 2) + 8, :], ring[i][:, :].rearrange("p (a d) -> p a d", d=CD))\
                        .then_inc(o_ready, 1)
                add_head(CH - 1)
                dve.wait_ge(copied, 3 * (b + 1))
                own.link(nc.vector.tensor_tensor(r[:, :, :], x[:, :, :], bc(bo[:, :], 1, TT), ALU.add))
                own.link(nc.vector.scalar_tensor_tensor(r[:, :, :], acc[:, :, :], gains[:, 1:2], r[:, :, :], ALU.mult, ALU.add))
                dve.wait_ge(out_ps, b + 1)
                nc.vector.tensor_tensor(r[:, :, :], r[:, :, :], ps_u[:, 0:TT * D].rearrange("p (t d) -> p t d", t=TT), ALU.add)\
                    .then_inc(out_read, 1)
                dve.wait_ge(out_read, b + 1)
                layernorm(nc, dve, own, r, stats, mv, rs, x5, b, ln_stats, ln_rs, x5_ready, stored)
                own.settle()


TOK = B * S
NT = TOK // P
MT = 4
GW = MT * P
MG = NT // MT
CAP = TOK // NE
BITS = 30


def moe_route(nc, T, const, m):
    ident, ident16, causal16, ones, eps = const
    with ExitStack() as stack:
        c = Scope(nc, stack, "route")
        ws = c.sb("ws", [P, NE])
        bs = c.sb("bs", [P, NE])
        x = [c.sb(f"x{i}", [P, MT, D]) for i in range(2)]
        xs = [c.sb(f"xs{i}", [P, GW]) for i in range(2)]
        logit = c.sb("logit", [P, NT, NE])
        top = c.sb("top", [P, NT])
        ps_x = [c.ps(f"ps_x{i}", [P, GW]) for i in range(2)]
        ps_l = [c.ps(f"ps_l{i}", [P, MT, NE]) for i in range(2)]
        weights_in = c.sem("weights_in")
        x_in = [c.sem(f"x_in{i}") for i in range(2)]
        x_ps = c.sem("x_ps")
        xs_ready = c.sem("xs_ready")
        kept = c.sem("kept")
        l_ps = c.sem("l_ps")
        l_sb = c.sem("l_sb")
        shifted = c.sem("shifted")
        powers = c.sem("powers")
        dve_own = c.sem("dve_own")
        block = c.block()

        @block.sync
        def _(sp):
            sp.dma_start(ws[:, :], T["moe_ws"]).then_inc(weights_in, 16)
            sp.dma_start(bs[:, :], T["moe_bs"]).then_inc(weights_in, 16)
            tiles = T["x5"].rearrange("b (t p) d -> p (b t) d", p=P)
            with sp.Fori(0, MG // 2) as i:
                for h in range(2):
                    sp.wait_ge(x_ps, i * 2)
                    sp.wait_ge(kept, i * 2)
                    sp.dma_start(x[h][:, :, :], tiles[:, bass.ds(i * (2 * MT) + h * MT, MT), :]).then_inc(x_in[h], 16)

        @block.tensor
        def _(pe):
            pe.wait_ge(weights_in, 32)
            with pe.Fori(0, MG // 2) as i:
                for h in range(2):
                    pe.wait_ge(x_in[h], i * 16 + 16)
                    for t in range(MT):
                        mm = nc.tensor.transpose(ps_x[h][:, t * P:(t + 1) * P], x[h][:, t, :], ident[:, :])
                    mm.then_inc(x_ps, 1)
                    pe.wait_ge(xs_ready, i * 2 + h + 1)
                    pe.wait_ge(l_sb, i * 2)
                    for t in range(MT):
                        mm = nc.tensor.matmul(ps_l[h][:, t, :], xs[h][:, t * P:(t + 1) * P], ws[:, :],
                                              start=(t == 0), stop=True, skip_group_check=True)
                    mm.then_inc(l_ps, 1)

        @block.scalar
        def _(act):
            with act.Fori(0, MG // 2) as i:
                for h in range(2):
                    act.wait_ge(x_ps, i * 2 + h + 1)
                    act.wait_ge(m["xT_kept"], i * 2)
                    nc.scalar.activation(xs[h][:, :], ps_x[h][:, :], ACT.Copy).then_inc(xs_ready, 1)
            act.wait_ge(shifted, 1)
            nc.scalar.activation(logit[:, :, :], logit[:, :, :], ACT.Exp).then_inc(powers, 1)

        @block.gpsimd
        def _(pool):
            with pool.Fori(0, MG // 2) as i:
                for h in range(2):
                    hold(pool, x_in[h], i * 16 + 16)
                    nc.gpsimd.tensor_copy(m["x"][:, bass.ds(i * (2 * MT) + h * MT, MT), :], x[h][:, :, :]).then_inc(kept, 1)

        @block.vector
        def _(dve):
            own = Chain(dve, dve_own)
            dve.wait_ge(weights_in, 32)
            with dve.Fori(0, MG // 2) as i:
                for h in range(2):
                    dve.wait_ge(xs_ready, i * 2 + h + 1)
                    nc.vector.tensor_copy(m["xT"][:, bass.ds(i * (2 * GW) + h * GW, GW)], xs[h][:, :]).then_inc(m["xT_kept"], 1)
                    dve.wait_ge(l_ps, i * 2 + h + 1)
                    nc.vector.tensor_tensor(logit[:, bass.ds(i * (2 * MT) + h * MT, MT), :], ps_l[h][:, :, :],
                                            bc(bs[:, :], 1, MT), ALU.add).then_inc(l_sb, 1)
            dve.wait_ge(l_sb, MG)
            own.link(nc.vector.tensor_reduce(top[:, :], logit[:, :, :], axis=AX, op=ALU.max))
            nc.vector.tensor_tensor(logit[:, :, :], logit[:, :, :], bc(top[:, :], 2, NE), ALU.subtract).then_inc(shifted, 1)
            dve.wait_ge(powers, 1)
            own.link(nc.vector.tensor_reduce(top[:, :], logit[:, :, :], axis=AX, op=ALU.add))
            own.link(nc.vector.reciprocal(top[:, :], top[:, :]))
            own.link(nc.vector.tensor_tensor(m["prob"].rearrange("p e t -> p t e"), logit[:, :, :], bc(top[:, :], 2, NE), ALU.mult))


def moe_choose(nc, T, const, m):
    ident, ident16, causal16, ones, eps = const
    with ExitStack() as stack:
        c = Scope(nc, stack, "choose")
        bits = c.sb("bits", [P, BITS], U32)
        thr = c.sb("thr", [P, NE])
        cand = c.sb("cand", [P, NE])
        passed = c.sb("passed", [P, NE])
        count = c.sb("count", [P, NE])
        over = c.sb("over", [P, NE, NT])
        equal = c.sb("equal", [P, NE, NT])
        later = c.sb("later", [P, NE, NT])
        total = c.sb("total", [P, NE, NT])
        rank = c.sb("rank", [P, NE, NT])
        below = c.sb("below", [P, P])
        ps_c = c.ps("ps_c", [P, NE])
        ps_b = c.ps("ps_b", [P, NE, NT])
        ps_t = c.ps("ps_t", [P, NE, NT])
        bits_in = c.sem("bits_in")
        filled = c.sem("filled")
        counted = c.sem("counted")
        summed = c.sem("summed")
        tied = c.sem("tied")
        ranked = c.sem("ranked")
        dve_own = c.sem("dve_own")
        block = c.block()
        prob = m["prob"]

        @block.sync
        def _(sp):
            sp.dma_start(bits[:, :], T["bits"]).then_inc(bits_in, 16)

        @block.gpsimd
        def _(pool):
            nc.gpsimd.memset(thr[:, :], 0.0).then_inc(filled, 1)
            nc.gpsimd.memset(later[:, :, :], 1.0).then_inc(filled, 1)
            nc.gpsimd.memset(below[:, :], 1.0).then_inc(filled, 1)
            pool.wait_ge(filled, 3)
            nc.gpsimd.memset(later[:, :, 0:1], 0.0).then_inc(filled, 1)
            nc.gpsimd.affine_select(out=below[:, :], in_=below[:, :], compare_op=ALU.is_gt, fill=0.0,
                                    base=0, pattern=[[1, P]], channel_multiplier=-1).then_inc(filled, 1)
            pool.wait_ge(filled, 5)

        @block.tensor
        def _(pe):
            with pe.Fori(0, BITS + 1) as i:
                pe.wait_ge(counted, i + 1)
                nc.tensor.matmul(ps_c[:, :], ones[:, :], count[:, :], start=True, stop=True).then_inc(summed, 1)
            pe.wait_ge(filled, 5)
            pe.wait_ge(tied, 1)
            nc.tensor.matmul(ps_b[:, :, :], below[:, :], equal[:, :, :], start=True, stop=True).then_inc(ranked, 1)
            nc.tensor.matmul(ps_t[:, :, :], ones[:, :], equal[:, :, :], start=True, stop=True).then_inc(ranked, 1)

        @block.vector
        def _(dve):
            own = Chain(dve, dve_own)
            dve.wait_ge(filled, 5)
            dve.wait_ge(bits_in, 16)
            with dve.Fori(0, BITS) as i:
                own.restart()
                own.link(nc.vector.tensor_tensor(cand[:, :].bitcast(U32), thr[:, :].bitcast(U32),
                                                 bits[:, bass.ds(i, 1)].broadcast_to([P, NE]), ALU.bitwise_or))
                own.link(nc.vector.tensor_tensor(over[:, :, :], prob[:, :, :], bc(cand[:, :], 2, NT), ALU.is_ge))
                nc.vector.tensor_reduce(count[:, :], over[:, :, :], axis=AX, op=ALU.add).then_inc(counted, 1)
                dve.wait_ge(summed, i + 1)
                own.link(nc.vector.scalar_tensor_tensor(passed[:, :], ps_c[:, :], CAP - 0.5, cand[:, :], ALU.is_ge, ALU.mult))
                own.link(nc.vector.tensor_tensor(thr[:, :], thr[:, :], passed[:, :], ALU.max))
            own.restart()
            own.link(nc.vector.tensor_tensor(equal[:, :, :], prob[:, :, :], bc(thr[:, :], 2, NT), ALU.is_equal))
            nc.vector.tensor_tensor(over[:, :, :], prob[:, :, :], bc(thr[:, :], 2, NT), ALU.is_gt).then_inc(tied, 1)
            dve.wait_ge(tied, 1)
            nc.vector.tensor_reduce(count[:, :], over[:, :, :], axis=AX, op=ALU.add).then_inc(counted, 1)
            dve.wait_ge(ranked, 2)
            own.link(nc.vector.tensor_copy(total[:, :, :], ps_t[:, :, :]))
            own.link(nc.vector.tensor_tensor_scan(rank.rearrange("p e t -> p (e t)"), later.rearrange("p e t -> p (e t)"),
                                                  total.rearrange("p e t -> p (e t)"), 0.0, ALU.mult, ALU.add))
            own.link(nc.vector.tensor_tensor(rank[:, :, :], rank[:, :, :], total[:, :, :], ALU.subtract))
            own.link(nc.vector.tensor_tensor(rank[:, :, :], rank[:, :, :], ps_b[:, :, :], ALU.add))
            dve.wait_ge(summed, BITS + 1)
            own.link(nc.vector.tensor_scalar(count[:, :], ps_c[:, :], -1.0, float(CAP), ALU.mult, ALU.add))
            own.link(nc.vector.tensor_tensor(rank[:, :, :], rank[:, :, :], bc(count[:, :], 2, NT), ALU.is_lt))
            own.link(nc.vector.tensor_tensor(rank[:, :, :], rank[:, :, :], equal[:, :, :], ALU.mult))
            own.link(nc.vector.tensor_tensor(rank[:, :, :], rank[:, :, :], over[:, :, :], ALU.add))
            own.link(nc.vector.tensor_tensor(prob[:, :, :], prob[:, :, :], rank[:, :, :], ALU.mult))


def moe_experts(nc, T, const, m):
    with ExitStack() as stack:
        c = Scope(nc, stack, "experts")
        w1 = [c.sb(f"w1{i}", [P, DF]) for i in range(2)]
        w2 = [c.sb(f"w2{i}", [P, FC, D]) for i in range(2)]
        b1 = [c.sb(f"b1{i}", [P, FC]) for i in range(2)]
        hT = c.sb("hT", [P, FC, GW])
        ps_h = [c.ps(f"ps_h{i}", [P, GW]) for i in range(FC)]
        ps_y = [c.ps(f"ps_y{i}", [P, MT, D]) for i in range(2)]
        expert_in = [c.sem(f"expert_in{i}") for i in range(2)]
        used = c.sem("used")
        h_ps = c.sem("h_ps")
        h_sb = c.sem("h_sb")
        y_ps = c.sem("y_ps")
        y_free = c.sem("y_free")
        block = c.block()

        @block.sync
        def _(sp):
            with sp.Fori(0, NE // 2) as e2:
                for k in range(2):
                    e = e2 * 2 + k
                    sp.wait_ge(used, e2 * 2 + (k + 1))
                    sp.dma_start(w1[k][:, :], T["moe_w1"][bass.ds(e, 1)].rearrange("e p f -> p (e f)")).then_inc(expert_in[k], 16)
                    sp.dma_start(w2[k][:, :, :], T["moe_w2"][bass.ds(e, 1)].rearrange("e (c p) d -> p (e c) d", p=P))\
                        .then_inc(expert_in[k], 16)
                    sp.dma_start(b1[k][:, :], T["moe_b1"][bass.ds(e, 1)].rearrange("e p f -> p (e f)")).then_inc(expert_in[k], 16)

        @block.tensor
        def _(pe):
            with pe.Fori(0, NE // 2) as e2:
                for k in range(2):
                    hold(pe, expert_in[k], e2 * 48 + 48)
                    with pe.Fori(0, MG // 2) as i:
                        for g in range(2):
                            step = e2 * (2 * MG) + i * 2 + (k * MG + g)
                            for f in range(FC):
                                nc.tensor.matmul(ps_h[f][:, :], w1[k][:, f * P:(f + 1) * P],
                                                 m["xT"][:, bass.ds(i * (2 * GW) + g * GW, GW)], start=True, stop=True)\
                                    .then_inc(h_ps, 1)
                            pe.wait_ge(y_free, (step + 1) * MT)
                            for f in range(FC):
                                pe.wait_ge(h_sb, step * FC + f + 1)
                                for t in range(MT):
                                    mm = nc.tensor.matmul(ps_y[g][:, t, :], hT[:, f, t * P:(t + 1) * P], w2[k][:, f, :],
                                                          start=(f == 0 and t == 0), stop=(f == FC - 1), skip_group_check=True)
                            mm.then_inc(y_ps, 1)

        @block.scalar
        def _(act):
            nc.scalar.preload_act_table_set("gelu_apprx_tanh_and_others")
            with act.Fori(0, NE // 2) as e2:
                for k in range(2):
                    act.wait_ge(expert_in[k], e2 * 48 + 48)
                    with act.Fori(0, MG) as g:
                        step = e2 * (2 * MG) + g + k * MG
                        for f in range(FC):
                            act.wait_ge(h_ps, step * FC + f + 1)
                            nc.scalar.activation(hT[:, f, :], ps_h[f][:, :], ACT.Gelu_apprx_tanh, bias=b1[k][:, f:f + 1])\
                                .then_inc(h_sb, 1)

        @block.vector
        def _(dve):
            dve.sem_inc(y_free, 2 * MT)
            dve.sem_inc(used, 2)
            with dve.Fori(0, NE) as e:
                with dve.Fori(0, MG // 2) as i:
                    for g in range(2):
                        step = e * MG + i * 2 + g
                        dve.wait_ge(y_ps, step + 1)
                        dve.wait_ge(y_free, (step + 2) * MT)
                        for t in range(MT):
                            xt = m["x"][:, bass.ds(i * (2 * MT) + g * MT + t, 1), :].rearrange("p o d -> p (o d)")
                            nc.vector.scalar_tensor_tensor(
                                xt, ps_y[g][:, t, :],
                                m["prob"].rearrange("p e t -> p (e t)")[:, bass.ds(e * NT + i * (2 * MT) + (g * MT + t), 1)],
                                xt, ALU.mult, ALU.add).then_inc(y_free, 1)
                dve.sem_inc(used, 1)


def moe_finish(nc, T, const, m):
    ident, ident16, causal16, ones, eps = const
    with ExitStack() as stack:
        c = Scope(nc, stack, "finish")
        b2 = c.sb("b2", [NE, D])
        w = c.sb("w", [P, MT, NE])
        wT = c.sb("wT", [NE, GW])
        r = c.sb("r", [P, MT, D])
        stats = c.sb("stats", [P, MT, 6])
        mv = c.sb("mv", [P, MT, 2])
        rs = c.sb("rs", [P, MT])
        out = c.sb("out", [P, MT, D])
        ps_w = c.ps("ps_w", [NE, GW])
        ps_b = c.ps("ps_b", [P, MT, D])
        b2_in = c.sem("b2_in")
        w_ready = c.sem("w_ready")
        w_ps = c.sem("w_ps")
        wT_ready = c.sem("wT_ready")
        b_ps = c.sem("b_ps")
        ln_stats = c.sem("ln_stats")
        ln_rs = c.sem("ln_rs")
        out_ready = c.sem("out_ready")
        stored = c.sem("stored")
        dve_own = c.sem("dve_own")
        act_own = c.sem("act_own")
        block = c.block()

        @block.sync
        def _(sp):
            sp.dma_start(b2[:, :], T["moe_b2"]).then_inc(b2_in, 16)
            tiles = T["out"].rearrange("b (t p) d -> p (b t) d", p=P)
            with sp.Fori(0, MG) as g:
                sp.wait_ge(out_ready, g + 1)
                sp.dma_start(tiles[:, bass.ds(g * MT, MT), :], out[:, :, :]).then_inc(stored, 16)
            sp.wait_ge(stored, 16 * MG)

        @block.tensor
        def _(pe):
            pe.wait_ge(b2_in, 16)
            with pe.Fori(0, MG) as g:
                pe.wait_ge(w_ready, g + 1)
                for t in range(MT):
                    mm = nc.tensor.transpose(ps_w[:, t * P:(t + 1) * P], w[:, t, :], ident[:, :])
                mm.then_inc(w_ps, 1)
                pe.wait_ge(wT_ready, g + 1)
                for t in range(MT):
                    mm = nc.tensor.matmul(ps_b[:, t, :], wT[:, t * P:(t + 1) * P], b2[:, :], start=(t == 0), stop=True,
                                          skip_group_check=True)
                mm.then_inc(b_ps, 1)

        @block.scalar
        def _(act):
            own = Chain(act, act_own)
            nc.scalar.preload_act_table_set("natural_log_exp_and_others")
            with act.Fori(0, MG) as g:
                own.restart()
                act.wait_ge(w_ps, g + 1)
                nc.scalar.activation(wT[:, :], ps_w[:, :], ACT.Copy).then_inc(wT_ready, 1)
                act.wait_ge(ln_stats, g + 1)
                own.link(nc.scalar.activation(rs[:, :], mv[:, :, 1], ACT.Ln, bias=eps[:, 0:1]))
                nc.scalar.activation(rs[:, :], rs[:, :], ACT.Exp, scale=-0.5).then_inc(ln_rs, 1)
                own.settle()

        @block.vector
        def _(dve):
            own = Chain(dve, dve_own)
            with dve.Fori(0, MG) as g:
                own.restart()
                nc.vector.tensor_copy(w[:, :, :], m["prob"].rearrange("p e t -> p t e")[:, bass.ds(g * MT, MT), :])\
                    .then_inc(w_ready, 1)
                dve.wait_ge(b_ps, g + 1)
                own.link(nc.vector.tensor_tensor(r[:, :, :], m["x"][:, bass.ds(g * MT, MT), :], ps_b[:, :, :], ALU.add))
                layernorm(nc, dve, own, r, stats, mv, rs, out, g, ln_stats, ln_rs, out_ready, stored, MT)
                own.settle()


def moe_stage(nc, T, const):
    with ExitStack() as stack:
        c = Scope(nc, stack, "moe")
        m = {"x": c.sb("x", [P, NT, D]), "xT": c.sb("xT", [P, TOK]), "prob": c.sb("prob", [P, NE, NT]),
             "xT_kept": c.sem("xT_kept")}
        moe_route(nc, T, const, m)
        moe_choose(nc, T, const, m)
        moe_experts(nc, T, const, m)
        moe_finish(nc, T, const, m)


def layout(a):
    import numpy as np

    def t(w):
        return np.ascontiguousarray(np.asarray(w).T)

    def rows(w):
        return np.ascontiguousarray(w.reshape(-1, P, w.shape[-1]).transpose(1, 0, 2))

    def every(v):
        return np.ascontiguousarray(np.broadcast_to(np.asarray(v).reshape(1, -1), (P, np.asarray(v).size)))

    def halves(v):
        return np.asarray(v).reshape(HALF, P).T

    L = {"x": np.asarray(a["x"]), "ctx": np.asarray(a["ctx_1024"])}
    L["w_in"] = t(a["L0_attn_W_in"])
    L["w_x"] = rows(t(a["L0_attn_W_x"]))
    L["w_dt"] = rows(t(a["L0_attn_W_dt"]))
    L["w_out"] = rows(t(a["L0_attn_W_out"]))
    L["conv_w"] = np.ascontiguousarray(np.asarray(a["L0_attn_conv_w"]).reshape(HALF, P, TAPS).transpose(1, 0, 2))
    L["scan_vec"] = np.ascontiguousarray(np.stack(
        [halves(a[f"L0_attn_{n}"]) for n in ("conv_b", "b_dt", "D_param", "ln_g", "ln_b")], axis=1))
    L["a_log"] = every(a["L0_attn_A_log"])
    for name, dst in (("q", "wq_pad"), ("k", "wk_bd"), ("v", "wv_bd")):
        w = np.asarray(a[f"L0_xattn_W{name}"])
        pad = np.zeros((P, AH, P) if name == "q" else (P, P), w.dtype)
        for h in range(AH):
            own = slice(h * AD, (h + 1) * AD)
            if name == "q":
                pad[own, h, own] = w.T
            else:
                pad[own, own] = w.T
        L[dst] = pad
    L["wo"] = t(a["L0_xattn_Wo"])
    L["bo"] = every(a["L0_xattn_bo"])
    L["wr"] = np.asarray(a["L0_ffn_Wr"])
    L["br"] = np.asarray(a["L0_ffn_br"]).reshape(1, NE)
    L["ffn_w1"] = np.asarray(a["L0_ffn_W1"])
    L["ffn_b1"] = np.ascontiguousarray(np.asarray(a["L0_ffn_b1"]).reshape(NE, FC, P).transpose(0, 2, 1))
    L["ffn_w2"] = np.asarray(a["L0_ffn_W2"])
    L["ffn_b2"] = np.ascontiguousarray(np.broadcast_to(np.asarray(a["L0_ffn_b2"])[:, None, :], (NE, P, D)))
    names = ("k", "q", "v")
    pad = np.zeros((P, PLANES, 2 * WIN + DH), np.float32)
    bias = np.zeros((P, PLANES), np.float32)
    taps = np.zeros((P, 3 * DW, TAPS), np.float32)
    for i, n in enumerate(names):
        w, wb, wc = (np.asarray(a[f"L1_attn_{x}{n}"]) for x in ("W", "b", "conv_"))
        for d in range(DW):
            pad[:, i * DW + d, WIN:WIN + DH] = w[d::DW].T
            for s in range(GB):
                bias[s * DH:(s + 1) * DH, i * DW + d] = wb[d::DW]
                taps[s * DH:(s + 1) * DH, i * DW + d] = wc[d::DW]
    pad[:, 3 * DW, WIN:WIN + DH] = np.asarray(a["L1_attn_Wbeta"]).T
    for s in range(GB):
        bias[s * DH:(s + 1) * DH, 3 * DW] = np.asarray(a["L1_attn_bbeta"])
    L["delta_w"], L["delta_bias"], L["delta_taps"] = pad, bias, taps
    time = np.arange(1, S + 1, dtype=np.float64)
    coef = np.stack([time / (time + 1), (time - 1) / (time + 1), 2 / (time + 1)])
    coef[0, 0] = 0
    L["coef"] = np.ascontiguousarray(np.broadcast_to(coef.astype(np.float32), (P, 3, S)))
    L["rms"] = every(a["L1_attn_rms_w"])
    L["delta_out"] = np.ascontiguousarray(np.asarray(a["L1_attn_Wout"]).T.reshape(DH, DW, D))
    L["bout"] = every(a["L1_attn_bout"])
    for n, ref in (("q", "q"), ("k", "k"), ("v", "v"), ("ki", "k_ip"), ("vi", "v_ip"), ("ka", "k_ap"), ("va", "v_ap")):
        L[f"cross_{n}"] = np.asarray(a[f"L1_xattn_W{ref}"])
    L["cross_o"] = rows(np.asarray(a["L1_xattn_Wo"]))
    L["cross_bo"] = every(a["L1_xattn_bo"])
    relk = np.asarray(a["L1_xattn_rel_k"]).T
    L["relk"] = np.concatenate([relk, relk])
    L["relv"] = np.asarray(a["L1_xattn_rel_v"])
    L["gains"] = np.ascontiguousarray(np.broadcast_to(np.stack([a["L1_xattn_alpha"], a["L1_xattn_beta"]]), (P, 2)))
    L["moe_ws"] = np.asarray(a["L1_ffn_Ws"])
    L["moe_bs"] = every(a["L1_ffn_bs"])
    L["moe_w1"] = np.asarray(a["L1_ffn_W1"])
    L["moe_b1"] = np.ascontiguousarray(np.asarray(a["L1_ffn_b1"]).reshape(NE, FC, P).transpose(0, 2, 1))
    L["moe_w2"] = np.asarray(a["L1_ffn_W2"])
    L["moe_b2"] = np.asarray(a["L1_ffn_b2"])
    L["bits"] = np.ascontiguousarray(np.broadcast_to(np.array([1 << i for i in reversed(range(BITS))], np.uint32), (P, BITS)))
    return L


def program(nc, T):
    with ExitStack() as stack:
        const = constants(nc, stack)
        scan_stage(nc, T, const)
        self_stage(nc, T, const)
        ffn_stage(nc, T, const)
        delta_stage(nc, T, const)
        cross_stage(nc, T, const)
        moe_stage(nc, T, const)


def kernel(**inputs):
    import numpy as np
    import concourse.bacc as bacc
    from concourse.bass_utils import run_bass_kernel_spmd

    nc = bacc.Bacc("TRN2", target_bir_lowering=False, num_devices=1)
    arrays, T = {}, {}
    for name, a in layout(inputs).items():
        arrays[f"in_{name}_dram"] = np.ascontiguousarray(a)
        T[name] = nc.dram_tensor(f"in_{name}_dram", a.shape, mybir.dt.from_np(a.dtype), kind="ExternalInput").ap()
    for name in ("x1", "x2", "x3", "x4", "x5"):
        T[name] = nc.dram_tensor(f"{name}_dram", (B, S, D), F32, kind="Internal").ap()
    for name, shape in SCRATCH.items():
        T[name] = nc.dram_tensor(f"{name}_dram", shape, F32, kind="Internal").ap()
    T["out"] = nc.dram_tensor("out_0_dram", (B, S, D), F32, kind="ExternalOutput").ap()
    program(nc, T)
    r = run_bass_kernel_spmd(nc, [arrays], core_ids=[0])
    return r.results[0]["out_0_dram"]
```

```python
from contextlib import ExitStack

import concourse.bass as bass
from concourse import mybir

F32 = mybir.dt.float32
F32R = mybir.dt.float32r
BF16 = mybir.dt.bfloat16
U32 = mybir.dt.uint32
ALU = mybir.AluOpType
ACT = mybir.ActivationFunctionType
AX = mybir.AxisListType.X

P = 128
B = 16
S = 256
D = 128
TT = S // P
CTX = 1601
LN_EPS = 1e-5
HIGH = -0x1000
NEG = -1e30


class Scope:

    def __init__(self, nc, stack, tag):
        self.nc, self.stack, self.tag, self.sems = nc, stack, tag, []

    def sb(self, name, shape, dt=F32):
        return self.stack.enter_context(self.nc.sbuf_tensor(f"{self.tag}_{name}", shape, dt))

    def ps(self, name, shape, dt=F32):
        return self.stack.enter_context(self.nc.psum_tensor(f"{self.tag}_{name}", shape, dt))

    def sem(self, name):
        sem = self.stack.enter_context(self.nc.semaphore(f"{self.tag}_{name}"))
        self.sems.append(sem)
        return sem

    def block(self):
        self.stack.callback(self.clear)
        return self.stack.enter_context(self.nc.Block())

    def clear(self):
        with self.nc.Block() as block:
            @block.gpsimd
            def _(pool):
                for sem in self.sems:
                    pool.sem_clear(sem)


class Chain:

    def __init__(self, eng, sem):
        self.eng, self.sem, self.n = eng, sem, 0

    def restart(self):
        self.eng.sem_clear(self.sem)
        self.n = 0

    def link(self, ins):
        self.count(ins)
        self.settle()

    def count(self, ins):
        self.n += 1
        ins.then_inc(self.sem, 1)

    def settle(self):
        self.eng.wait_ge(self.sem, self.n)


def hold(eng, sem, value):
    eng.wait_ge(sem, value)
    eng.nop(nofuse=True)


def bc(ap, axis, n):
    v = ap.unsqueeze(axis)
    return v.broadcast_to([*v.shape[:axis], n, *v.shape[axis + 1:]])


def constants(nc, stack):
    c = Scope(nc, stack, "const")
    ident = c.sb("ident", [P, P])
    ident16 = c.sb("ident16", [P, P], BF16)
    causal16 = c.sb("causal16", [P, P], BF16)
    ones = c.sb("ones", [P, P])
    eps = c.sb("eps", [P, 1])
    with ExitStack() as own:
        fill = Scope(nc, own, "fill")
        filled = fill.sem("filled")
        block = fill.block()

        @block.gpsimd
        def _(pool):
            nc.gpsimd.memset(ident[:, :], 0.0).then_inc(filled, 1)
            nc.gpsimd.memset(ident16[:, :], 0.0).then_inc(filled, 1)
            nc.gpsimd.memset(causal16[:, :], 0.0).then_inc(filled, 1)
            nc.gpsimd.memset(ones[:, :], 1.0).then_inc(filled, 1)
            nc.gpsimd.memset(eps[:, :], LN_EPS).then_inc(filled, 1)
            pool.wait_ge(filled, 5)
            for m in (ident, ident16):
                nc.gpsimd.affine_select(out=m[:, :], in_=m[:, :], compare_op=ALU.not_equal, fill=1.0,
                                        base=0, pattern=[[-1, P]], channel_multiplier=1).then_inc(filled, 1)
            nc.gpsimd.affine_select(out=causal16[:, :], in_=causal16[:, :], compare_op=ALU.is_ge, fill=NEG,
                                    base=0, pattern=[[-1, P]], channel_multiplier=1).then_inc(filled, 1)
            pool.wait_ge(filled, 8)

    return ident, ident16, causal16, ones, eps


def turns(eng, turn):
    turn(0, 0, True, True)
    with eng.Fori(0, B // 2 - 1) as j:
        turn(j * 2 + 1, 1, False, True)
        turn(j * 2 + 2, 0, False, True)
    turn(B - 1, 1, False, False)


def wait_past(eng, sem, value):
    if not (isinstance(value, int) and value <= 0):
        eng.wait_ge(sem, value)


def hold_past(eng, sem, value):
    if not (isinstance(value, int) and value <= 0):
        hold(eng, sem, value)


def ln_statistics(nc, own, r, stats, mv, ready, tiles=TT):
    for t in range(tiles):
        own.count(nc.vector.bn_stats(stats[:, t, :], r[:, t, :]))
    own.settle()
    for t in range(tiles):
        ins = nc.vector.bn_aggr(mv[:, t, :], stats[:, t, :])
        if t < tiles - 1:
            own.count(ins)
    ins.then_inc(ready, 1)


def ln_apply(nc, own, r, mv, rs, out, ready, tiles=TT):
    for t in range(tiles):
        ins = nc.vector.tensor_scalar(out[:, t, :], r[:, t, :], mv[:, t, 0:1], rs[:, t:t + 1], ALU.subtract, ALU.mult)
        if t < tiles - 1:
            own.count(ins)
    ins.then_inc(ready, 1)


def layernorm(nc, dve, own, r, stats, mv, rs, out, b, ln_stats, ln_rs, ready, stored, tiles=TT, step=16):
    ln_statistics(nc, own, r, stats, mv, ln_stats, tiles)
    dve.wait_ge(ln_stats, b + 1)
    dve.wait_ge(stored, step * b)
    dve.wait_ge(ln_rs, b + 1)
    ln_apply(nc, own, r, mv, rs, out, ready, tiles)


DI = 256
HALF = DI // P
NS = 16
TAPS = 4
SG = 2
GROUPS = NS // SG


def scan_stage(nc, T, const):
    ident, ident16, causal16, ones, eps = const
    with ExitStack() as stack:
        c = Scope(nc, stack, "scan")
        w_in = c.sb("w_in", [P, 2 * DI])
        w_x = c.sb("w_x", [P, HALF, 2 * NS])
        w_dt = c.sb("w_dt", [P, HALF, DI])
        w_out = c.sb("w_out", [P, HALF, D])
        conv_w = c.sb("conv_w", [P, HALF, TAPS])
        vec = c.sb("vec", [P, 5, HALF])
        a_neg = c.sb("a_neg", [P, NS])
        pick32 = c.sb("pick32", [2 * NS, 2 * NS, P])
        pick = c.sb("pick", [2 * NS, 2 * NS, P], F32R)
        mean_w = c.sb("mean_w", [P, P])
        xa = c.sb("xa", [P, TT, D])
        xr = c.sb("xr", [P, TT, D])
        xT = c.sb("xT", [P, S])
        xp = c.sb("xp", [P, HALF, TAPS - 1 + S])
        conv = c.sb("conv", [P, HALF, S])
        sig = c.sb("sig", [P, HALF, S])
        gate = [c.sb(f"gate{i}", [P, HALF, S]) for i in range(2)]
        gsig = c.sb("gsig", [P, HALF, S])
        xc = [c.sb(f"xc{i}", [P, HALF, S]) for i in range(2)]
        bc_upper = c.sb("bc_upper", [2 * NS, S])
        bcT = [[c.sb(f"bcT{i}{part}", [2 * NS, S], F32R) for part in ("h", "l")] for i in range(2)]
        dt = [c.sb(f"dt{i}", [P, HALF, S]) for i in range(2)]
        dabs = c.sb("dabs", [P, HALF, S])
        u = [c.sb(f"u{i}", [P, HALF, S]) for i in range(2)]
        decay = c.sb("decay", [P, 2, SG, HALF, S])
        drive = c.sb("drive", [P, 2, SG, HALF, S])
        h = c.sb("h", [P, 2, SG, HALF, S])
        hc = c.sb("hc", [P, 2, SG, HALF, S])
        y2 = c.sb("y2", [P, SG, HALF, S])
        y = c.sb("y", [P, HALF, S])
        sq = c.sb("sq", [P, HALF, S])
        rstd = c.sb("rstd", [P, S])
        r = c.sb("r", [P, TT, D])
        stats = c.sb("stats", [P, TT, 6])
        mv = c.sb("mv", [P, TT, 2])
        rs = c.sb("rs", [P, TT])
        x1 = c.sb("x1", [P, TT, D])
        ps_t = c.ps("ps_t", [P, 512])
        ps_x = c.ps("ps_x", [P, HALF, S])
        ps_z = c.ps("ps_z", [P, HALF, S])
        ps_v = c.ps("ps_v", [P, HALF, S])
        ps_b = [c.ps(f"ps_b{i}", [P, SG, S]) for i in range(2)]
        ps_c = [c.ps(f"ps_c{i}", [P, SG, S]) for i in range(2)]

        weights_in = c.sem("weights_in")
        consts_ready = c.sem("consts_ready")
        a_ready = c.sem("a_ready")
        xa_in = c.sem("xa_in")
        xr_in = c.sem("xr_in")
        xT_ps = c.sem("xT_ps")
        xT_sb = c.sem("xT_sb")
        xz_ps = c.sem("xz_ps")
        xp_sb = c.sem("xp_sb")
        z_exp = c.sem("z_exp")
        conv_ready = c.sem("conv_ready")
        conv_exp = c.sem("conv_exp")
        xc_ready = c.sem("xc_ready")
        ssm_ps = c.sem("ssm_ps")
        v_ps = c.sem("v_ps")
        bc_sb = c.sem("bc_sb")
        dlog = c.sem("dlog")
        dt_ready = c.sem("dt_ready")
        u_ready = c.sem("u_ready")
        decay_exp = c.sem("decay_exp")
        decay_cut = c.sem("decay_cut")
        b_ps = c.sem("b_ps")
        c_ps = c.sem("c_ps")
        driven = c.sem("driven")
        scanned = c.sem("scanned")
        hc_ready = c.sem("hc_ready")
        summed = c.sem("summed")
        y_ready = c.sem("y_ready")
        mean_ps = c.sem("mean_ps")
        centred = c.sem("centred")
        squared = c.sem("squared")
        var_ps = c.sem("var_ps")
        rstd_ready = c.sem("rstd_ready")
        gated = c.sem("gated")
        gate_ready = c.sem("gate_ready")
        out_ps = c.sem("out_ps")
        out_read = c.sem("out_read")
        ln_stats = c.sem("ln_stats")
        ln_rs = c.sem("ln_rs")
        x1_ready = c.sem("x1_ready")
        stored = c.sem("stored")
        dve_own = c.sem("dve_own")
        act_own = c.sem("act_own")
        block = c.block()

        @block.sync
        def _(sp):
            loads = [(w_in[:, :], T["w_in"]), (w_x[:, :, :], T["w_x"]), (w_dt[:, :, :], T["w_dt"]),
                     (w_out[:, :, :], T["w_out"]), (conv_w[:, :, :], T["conv_w"]), (vec[:, :, :], T["scan_vec"]),
                     (a_neg[:, :], T["a_log"])]
            for dst, src in loads:
                sp.dma_start(dst, src).then_inc(weights_in, 16)

            def load_a(b):
                sp.dma_start(xa[:, :, :], T["x"][b].rearrange("(t p) d -> p t d", p=P)).then_inc(xa_in, 16)

            def load_r(b):
                sp.dma_start(xr[:, :, :], T["x"][b].rearrange("(t p) d -> p t d", p=P)).then_inc(xr_in, 16)

            def store(b):
                sp.wait_ge(x1_ready, b + 1)
                sp.dma_start(T["x1"][b].rearrange("(t p) d -> p t d", p=P), x1[:, :, :]).then_inc(stored, 16)

            load_a(0)
            load_r(0)
            sp.wait_ge(xT_ps, 1)
            load_a(1)
            with sp.Fori(0, B - 2) as j:
                hold(sp, xT_ps, j + 2)
                load_a(j + 2)
                hold(sp, out_read, j + 1)
                load_r(j + 1)
                store(j)
            sp.wait_ge(out_read, B - 1)
            load_r(B - 1)
            store(B - 2)
            store(B - 1)
            sp.wait_ge(stored, 16 * B)

        @block.gpsimd
        def _(pool):
            nc.gpsimd.memset(pick32[:, :, :], 0.0).then_inc(consts_ready, 1)
            nc.gpsimd.memset(xp[:, :, :], 0.0).then_inc(consts_ready, 1)
            nc.gpsimd.memset(mean_w[:, :], 1.0 / DI).then_inc(consts_ready, 1)
            pool.wait_ge(consts_ready, 3)
            nc.gpsimd.affine_select(out=pick32[:, :, :], in_=pick32[:, :, :], compare_op=ALU.not_equal, fill=1.0,
                                    base=0, pattern=[[-1, 2 * NS], [0, P]], channel_multiplier=1)\
                .then_inc(consts_ready, 1)

            def drive_input(b, p):
                hold(pool, dt_ready, b + 1)
                nc.gpsimd.tensor_tensor(u[p][:, :, :], dt[p][:, :, :], xc[p][:, :, :], ALU.mult)\
                    .then_inc(u_ready, 1)

            def add_states(b, g):
                if g == 0:
                    hold_past(pool, y_ready, b)
                else:
                    hold(pool, summed, b * GROUPS + g)
                hold(pool, hc_ready, b * GROUPS + g + 1)
                if g == 0:
                    nc.gpsimd.tensor_copy(y2[:, :, :, :], hc[:, 0, :, :, :]).then_inc(summed, 1)
                else:
                    nc.gpsimd.tensor_tensor(y2[:, :, :, :], y2[:, :, :, :], hc[:, g % 2, :, :, :], ALU.add)\
                        .then_inc(summed, 1)

            def turn(b, p, first, more):
                for g in range(GROUPS):
                    hold(pool, decay_exp, b * NS + SG * (g + 1))
                    nc.gpsimd.memset(decay[:, g % 2, :, :, 0:1], 0.0).then_inc(decay_cut, 1)
                    if g >= 1:
                        add_states(b, g - 1)
                if more:
                    drive_input(b + 1, 1 - p)
                add_states(b, GROUPS - 1)
                hold(pool, summed, (b + 1) * GROUPS)
                hold_past(pool, out_ps, b)
                nc.gpsimd.tensor_tensor(y[:, :, :], y2[:, 0, :, :], y2[:, 1, :, :], ALU.add).then_inc(y_ready, 1)

            drive_input(0, 0)
            turns(pool, turn)

        @block.scalar
        def _(act):
            own = Chain(act, act_own)
            act.wait_ge(weights_in, 16 * 7)
            own.link(nc.scalar.activation(a_neg[:, :], a_neg[:, :], ACT.Exp))
            nc.scalar.activation(a_neg[:, :], a_neg[:, :], ACT.Copy, scale=-1.0).then_inc(a_ready, 1)
            act.wait_ge(a_ready, 1)
            nc.scalar.preload_act_table_set("natural_log_exp_and_others")

            def keep_x(b):
                wait_past(act, xz_ps, 2 * b)
                act.wait_ge(xT_ps, b + 1)
                nc.scalar.activation(xT[:, :], ps_v[:, 0, :], ACT.Copy).then_inc(xT_sb, 1)

            def sigmoid(dst, ready):
                own.link(nc.scalar.activation(dst, dst, ACT.Ln, bias=ones[:, 0:1]))
                nc.scalar.activation(dst, dst, ACT.Exp, scale=-1.0).then_inc(ready, 1)

            def keep_xz(b):
                wait_past(act, conv_ready, b)
                act.wait_ge(xz_ps, 2 * b + 1)
                nc.scalar.activation(xp[:, :, TAPS - 1:], ps_x[:, :, :], ACT.Copy).then_inc(xp_sb, 1)
                wait_past(act, gate_ready, b)
                act.wait_ge(xz_ps, 2 * b + 2)
                own.link(nc.scalar.activation(gsig[:, :, :], ps_z[:, :, :], ACT.Exp, scale=-1.0))
                sigmoid(gsig[:, :, :], z_exp)

            def conv_sigmoid(b):
                wait_past(act, xc_ready, b)
                act.wait_ge(conv_ready, b + 1)
                own.link(nc.scalar.activation(sig[:, :, :], conv[:, :, :], ACT.Exp, scale=-1.0))
                sigmoid(sig[:, :, :], conv_exp)

            def softplus(b):
                wait_past(act, dt_ready, b)
                act.wait_ge(v_ps, b + 1)
                for m in range(HALF):
                    own.count(nc.scalar.activation(dabs[:, m, :], ps_v[:, m, :], ACT.Abs, bias=vec[:, 1, m:m + 1]))
                own.settle()
                own.link(nc.scalar.activation(dabs[:, :, :], dabs[:, :, :], ACT.Exp, scale=-1.0))
                nc.scalar.activation(dabs[:, :, :], dabs[:, :, :], ACT.Ln, bias=ones[:, 0:1]).then_inc(dlog, 1)

            def decays(b, p, g):
                if g < 2:
                    wait_past(act, scanned, b * GROUPS + (g - 1))
                else:
                    act.wait_ge(scanned, b * GROUPS + g - 1)
                for i in range(SG):
                    s = g * SG + i
                    nc.scalar.activation(decay[:, g % 2, i, :, :], dt[p][:, :, :], ACT.Exp,
                                         scale=a_neg[:, s:s + 1]).then_inc(decay_exp, 1)

            def square(b):
                act.wait_ge(centred, b + 1)
                nc.scalar.activation(sq[:, :, :], y[:, :, :], ACT.Square).then_inc(squared, 1)

            def inverse_std(b):
                act.wait_ge(var_ps, b + 1)
                own.link(nc.scalar.activation(rstd[:, :], ps_t[:, S:2 * S], ACT.Ln, bias=eps[:, 0:1]))
                nc.scalar.activation(rstd[:, :], rstd[:, :], ACT.Exp, scale=-0.5).then_inc(rstd_ready, 1)

            def ln_inverse_std(b):
                act.wait_ge(ln_stats, b + 1)
                own.link(nc.scalar.activation(rs[:, :], mv[:, :, 1], ACT.Ln, bias=eps[:, 0:1]))
                nc.scalar.activation(rs[:, :], rs[:, :], ACT.Exp, scale=-0.5).then_inc(ln_rs, 1)

            def turn(b, p, first, more):
                own.restart()
                act.wait_ge(dt_ready, b + 1)
                for g in range(GROUPS):
                    decays(b, p, g)
                    if not first:
                        if g == 2:
                            square(b - 1)
                        if g == 3:
                            inverse_std(b - 1)
                        if g == 5:
                            ln_inverse_std(b - 1)
                    if more:
                        if g == 0:
                            keep_x(b + 1)
                        if g == 1:
                            keep_xz(b + 1)
                        if g == 3:
                            conv_sigmoid(b + 1)
                        if g == 6:
                            softplus(b + 1)
                own.settle()

            own.restart()
            keep_x(0)
            keep_xz(0)
            conv_sigmoid(0)
            softplus(0)
            turns(act, turn)
            square(B - 1)
            inverse_std(B - 1)
            ln_inverse_std(B - 1)

        @block.tensor
        def _(pe):
            pe.wait_ge(weights_in, 16 * 7)
            pe.wait_ge(consts_ready, 5)

            def turn_x(b):
                wait_past(pe, dt_ready, b)
                pe.wait_ge(xa_in, 16 * (b + 1))
                for t in range(TT):
                    mm = nc.tensor.transpose(ps_v[:, 0, t * P:(t + 1) * P], xa[:, t, :], ident[:, :])
                mm.then_inc(xT_ps, 1)

            def project(b):
                pe.wait_ge(xT_sb, b + 1)
                wait_past(pe, bc_sb, 2 * b)
                for m in range(HALF):
                    mm = nc.tensor.matmul(ps_x[:, m, :], w_in[:, m * P:(m + 1) * P], xT[:, :], start=True, stop=True)
                mm.then_inc(xz_ps, 1)
                wait_past(pe, gate_ready, b)
                for m in range(HALF):
                    mm = nc.tensor.matmul(ps_z[:, m, :], w_in[:, DI + m * P:DI + (m + 1) * P], xT[:, :],
                                          start=True, stop=True)
                mm.then_inc(xz_ps, 1)

            def project_inner(b, p):
                pe.wait_ge(xc_ready, b + 1)
                for m in range(HALF):
                    mm = nc.tensor.matmul(ps_x[0:2 * NS, 0, :], w_x[:, m, :], xc[p][:, m, :],
                                          start=(m == 0), stop=(m == HALF - 1))
                mm.then_inc(ssm_ps, 1)
                for o in range(HALF):
                    for m in range(HALF):
                        mm = nc.tensor.matmul(ps_v[:, o, :], w_dt[:, m, o * P:(o + 1) * P], xc[p][:, m, :],
                                              start=(m == 0), stop=(m == HALF - 1))
                mm.then_inc(v_ps, 1)

            def spread(b, p, g):
                wait_past(pe, driven, b * GROUPS + (g - 1))
                for i in range(SG):
                    for j, part in enumerate(bcT[p]):
                        mm = nc.tensor.matmul(ps_b[g % 2][:, i, :], pick[:, g * SG + i, :], part[:, :], start=(j == 0), stop=(j == 1))
                mm.then_inc(b_ps, 1)
                wait_past(pe, hc_ready, b * GROUPS + (g - 1))
                for i in range(SG):
                    for j, part in enumerate(bcT[p]):
                        mm = nc.tensor.matmul(ps_c[g % 2][:, i, :], pick[:, NS + g * SG + i, :], part[:, :],
                                              start=(j == 0), stop=(j == 1))
                mm.then_inc(c_ps, 1)

            def mean(b):
                wait_past(pe, out_read, b)
                pe.wait_ge(y_ready, b + 1)
                for m in range(HALF):
                    mm = nc.tensor.matmul(ps_t[:, 0:S], mean_w[:, :], y[:, m, :], start=(m == 0), stop=(m == HALF - 1))
                mm.then_inc(mean_ps, 1)

            def variance(b):
                pe.wait_ge(squared, b + 1)
                for m in range(HALF):
                    mm = nc.tensor.matmul(ps_t[:, S:2 * S], mean_w[:, :], sq[:, m, :], start=(m == 0), stop=(m == HALF - 1))
                mm.then_inc(var_ps, 1)

            def project_out(b):
                pe.wait_ge(gated, b + 1)
                for t in range(TT):
                    for m in range(HALF):
                        mm = nc.tensor.matmul(ps_t[:, t * P:(t + 1) * P], y[:, m, t * P:(t + 1) * P], w_out[:, m, :],
                                              start=(m == 0), stop=(m == HALF - 1))
                mm.then_inc(out_ps, 1)

            def turn(b, p, first, more):
                pe.wait_ge(bc_sb, 2 * (b + 1))
                for g in range(GROUPS):
                    spread(b, p, g)
                    if not first:
                        if g == 1:
                            mean(b - 1)
                        if g == 2:
                            variance(b - 1)
                        if g == 4:
                            project_out(b - 1)
                    if more:
                        if g == 0:
                            turn_x(b + 1)
                        if g == 1:
                            project(b + 1)
                        if g == 5:
                            project_inner(b + 1, 1 - p)

            turn_x(0)
            project(0)
            project_inner(0, 0)
            turns(pe, turn)
            mean(B - 1)
            variance(B - 1)
            project_out(B - 1)

        @block.vector
        def _(dve):
            own = Chain(dve, dve_own)
            dve.wait_ge(consts_ready, 4)
            nc.vector.tensor_copy(pick[:, :, :], pick32[:, :, :]).then_inc(consts_ready, 1)
            dve.wait_ge(weights_in, 16 * 7)

            def convolve(b):
                wait_past(dve, conv_exp, b)
                dve.wait_ge(xp_sb, b + 1)
                for k in range(TAPS):
                    for m in range(HALF):
                        if k == 0:
                            own.count(nc.vector.tensor_scalar(conv[:, m, :], xp[:, m, 0:S], conv_w[:, m, 0:1],
                                                              vec[:, 0, m:m + 1], ALU.mult, ALU.add))
                        else:
                            ins = nc.vector.scalar_tensor_tensor(
                                out=conv[:, m, :], in0=xp[:, m, k:k + S], scalar=conv_w[:, m, k:k + 1],
                                in1=conv[:, m, :], op0=ALU.mult, op1=ALU.add)
                            if (k, m) == (TAPS - 1, HALF - 1):
                                ins.then_inc(conv_ready, 1)
                            else:
                                own.count(ins)
                    own.settle()

            def make_gate(b, p):
                dve.wait_ge(z_exp, b + 1)
                nc.vector.tensor_tensor(gate[p][:, :, :], ps_z[:, :, :], gsig[:, :, :], ALU.mult).then_inc(gate_ready, 1)

            def make_xc(b, p):
                dve.wait_ge(conv_exp, b + 1)
                dve.wait_ge(conv_ready, b + 1)
                nc.vector.tensor_tensor(xc[p][:, :, :], conv[:, :, :], sig[:, :, :], ALU.mult).then_inc(xc_ready, 1)

            def split_bc(b, p):
                dve.wait_ge(ssm_ps, b + 1)
                src = ps_x[0:2 * NS, 0, :]
                own.link(nc.vector.tensor_scalar(bc_upper[:, :].bitcast(U32), src.bitcast(U32), HIGH, None, ALU.bitwise_and))
                nc.vector.tensor_copy(bcT[p][0][:, :], bc_upper[:, :]).then_inc(bc_sb, 1)
                nc.vector.tensor_tensor(bcT[p][1][:, :], src, bc_upper[:, :], ALU.subtract).then_inc(bc_sb, 1)
                dve.wait_ge(bc_sb, 2 * (b + 1))

            def make_dt(b, p):
                dve.wait_ge(dlog, b + 1)
                for m in range(HALF):
                    own.count(nc.vector.tensor_scalar(dt[p][:, m, :], ps_v[:, m, :], vec[:, 1, m:m + 1], 0.0,
                                                      ALU.add, ALU.max))
                own.settle()
                nc.vector.tensor_tensor(dt[p][:, :, :], dt[p][:, :, :], dabs[:, :, :], ALU.add).then_inc(dt_ready, 1)

            def group(b, p, g):
                q = g % 2
                dve.wait_ge(b_ps, b * GROUPS + g + 1)
                nc.vector.tensor_tensor(drive[:, q, :, :, :], bc(u[p][:, :, :], 1, SG), bc(ps_b[q][:, :, :], 2, HALF),
                                        ALU.mult).then_inc(driven, 1)
                dve.wait_ge(decay_cut, b * GROUPS + g + 1)
                dve.wait_ge(driven, b * GROUPS + g + 1)
                nc.vector.tensor_tensor_scan(h[:, q, :, :, :].rearrange("p a m t -> p (a m t)"),
                                             decay[:, q, :, :, :].rearrange("p a m t -> p (a m t)"),
                                             drive[:, q, :, :, :].rearrange("p a m t -> p (a m t)"),
                                             0.0, ALU.mult, ALU.add).then_inc(scanned, 1)
                dve.wait_ge(c_ps, b * GROUPS + g + 1)
                wait_past(dve, summed, b * GROUPS + (g - 1))
                dve.wait_ge(scanned, b * GROUPS + g + 1)
                nc.vector.tensor_tensor(hc[:, q, :, :, :], h[:, q, :, :, :], bc(ps_c[q][:, :, :], 2, HALF),
                                        ALU.mult).then_inc(hc_ready, 1)

            def centre(b):
                dve.wait_ge(mean_ps, b + 1)
                nc.vector.tensor_tensor(y[:, :, :], y[:, :, :], bc(ps_t[:, 0:S], 1, HALF), ALU.subtract)\
                    .then_inc(centred, 1)

            def normalise(b, p):
                dve.wait_ge(squared, b + 1)
                dve.wait_ge(rstd_ready, b + 1)
                own.link(nc.vector.tensor_tensor(y[:, :, :], y[:, :, :], bc(rstd[:, :], 1, HALF), ALU.mult))
                for m in range(HALF):
                    own.count(nc.vector.tensor_scalar(y[:, m, :], y[:, m, :], vec[:, 3, m:m + 1], vec[:, 4, m:m + 1],
                                                      ALU.mult, ALU.add))
                own.settle()
                for m in range(HALF):
                    own.count(nc.vector.scalar_tensor_tensor(out=y[:, m, :], in0=xc[p][:, m, :],
                                                             scalar=vec[:, 2, m:m + 1], in1=y[:, m, :], op0=ALU.mult, op1=ALU.add))
                own.settle()
                nc.vector.tensor_tensor(y[:, :, :], y[:, :, :], gate[p][:, :, :], ALU.mult).then_inc(gated, 1)

            def residual(b):
                dve.wait_ge(xr_in, 16 * (b + 1))
                dve.wait_ge(out_ps, b + 1)
                nc.vector.tensor_tensor(r[:, :, :], xr[:, :, :], ps_t[:, 0:S].rearrange("p (t d) -> p t d", t=TT),
                                        ALU.add).then_inc(out_read, 1)
                dve.wait_ge(out_read, b + 1)
                ln_statistics(nc, own, r, stats, mv, ln_stats)

            def finish(b):
                dve.wait_ge(ln_stats, b + 1)
                wait_past(dve, stored, 16 * b)
                dve.wait_ge(ln_rs, b + 1)
                ln_apply(nc, own, r, mv, rs, x1, x1_ready)
                own.settle()

            def turn(b, p, first, more):
                own.restart()
                dve.wait_ge(u_ready, b + 1)
                for g in range(GROUPS):
                    group(b, p, g)
                    if not first:
                        if g == 1:
                            centre(b - 1)
                        if g == 3:
                            normalise(b - 1, 1 - p)
                        if g == 4:
                            residual(b - 1)
                        if g == 5:
                            finish(b - 1)
                    if more:
                        if g == 2:
                            convolve(b + 1)
                        if g == 4:
                            make_gate(b + 1, 1 - p)
                            make_xc(b + 1, 1 - p)
                        if g == 6:
                            split_bc(b + 1, 1 - p)
                            make_dt(b + 1, 1 - p)
                own.settle()

            own.restart()
            convolve(0)
            make_gate(0, 0)
            make_xc(0, 0)
            split_bc(0, 0)
            make_dt(0, 0)
            turns(dve, turn)
            centre(B - 1)
            normalise(B - 1, 1)
            residual(B - 1)
            finish(B - 1)


AH = 16
AD = 8
SCORE_CHUNKS = [(0, h) for h in range(0, AH, 4)] + [(1, h) for h in range(0, AH, 2)]
NSC = len(SCORE_CHUNKS)
QP = AH // 2
ITEMS = QP + NSC
SRING = 4
LAG_T, LAG_V = 2, 3


def chunk_heads(k):
    qt, first = SCORE_CHUNKS[k]
    return qt, (qt + 1) * P, range(first, first + 4 // (qt + 1))


def self_stage(nc, T, const):
    ident, ident16, causal16, ones, eps = const
    with ExitStack() as stack:
        c = Scope(nc, stack, "self")
        wq = c.sb("wq", [P, AH, P])
        wk = c.sb("wk", [P, P])
        wv = c.sb("wv", [P, D])
        wo = c.sb("wo", [P, D])
        bo = c.sb("bo", [P, D])
        xs = c.sb("xs", [P, TT, D])
        cs = c.sb("cs", [P, TT, D])
        x = c.sb("x", [P, TT, D])
        xcT = c.sb("xcT", [P, 2, S])
        qT = c.sb("qT", [P, AH, S])
        kT = c.sb("kT", [P, S])
        v = c.sb("v", [P, TT, D])
        negmax = c.sb("negmax", [P, NSC, 4])
        sums = c.sb("sums", [P, TT, AH])
        prob = c.sb("prob", [P, 2, 4 * P])
        probT = c.sb("probT", [P, 2, 4, P])
        o = c.sb("o", [P, TT, D])
        oT = c.sb("oT", [P, S])
        r = c.sb("r", [P, TT, D])
        stats = c.sb("stats", [P, TT, 6])
        mv = c.sb("mv", [P, TT, 2])
        rs = c.sb("rs", [P, TT])
        x2 = c.sb("x2", [P, TT, D])
        ring = [c.ps(f"ring{i}", [P, 512]) for i in range(SRING)]
        ps_t = [c.ps(f"ps_t{i}", [P, 4, P]) for i in range(2)]
        ps_o = c.ps("ps_o", [P, TT, D])
        ps_m = c.ps("ps_m", [P, 4, P])

        weights_in = c.sem("weights_in")
        x_in = c.sem("x_in")
        x_kept = c.sem("x_kept")
        xcT_ps = c.sem("xcT_ps")
        xcT_sb = c.sem("xcT_sb")
        q_ps = c.sem("q_ps")
        kv_ps = c.sem("kv_ps")
        kv_sb = c.sem("kv_sb")
        scores = c.sem("scores")
        maxed = c.sem("maxed")
        emptied_ring = c.sem("emptied_ring")
        t_ps = c.sem("t_ps")
        t_sb = c.sem("t_sb")
        pv = c.sem("pv")
        normed = c.sem("normed")
        oT_ps = c.sem("oT_ps")
        oT_sb = c.sem("oT_sb")
        out_ps = c.sem("out_ps")
        out_read = c.sem("out_read")
        ln_stats = c.sem("ln_stats")
        ln_rs = c.sem("ln_rs")
        x2_ready = c.sem("x2_ready")
        stored = c.sem("stored")
        dve_own = c.sem("dve_own")
        act_own = c.sem("act_own")
        block = c.block()

        @block.sync
        def _(sp):
            for dst, src in ((wq[:, :, :], T["wq_pad"]), (wk[:, :], T["wk_bd"]), (wv[:, :], T["wv_bd"]),
                             (wo[:, :], T["wo"]), (bo[:, :], T["bo"])):
                sp.dma_start(dst, src).then_inc(weights_in, 16)

            def load(b):
                sp.dma_start(xs[:, :, :], T["x1"][b].rearrange("(t p) d -> p t d", p=P)).then_inc(x_in, 16)
                sp.dma_start(cs[:, :, :], T["ctx"][b, 0:S].rearrange("(t p) d -> p t d", p=P)).then_inc(x_in, 16)

            def store(b):
                sp.wait_ge(x2_ready, b + 1)
                sp.dma_start(T["x2"][b].rearrange("(t p) d -> p t d", p=P), x2[:, :, :]).then_inc(stored, 16)

            load(0)
            with sp.Fori(0, B - 1) as b:
                hold(sp, xcT_ps, b + 1)
                hold(sp, x_kept, b + 1)
                load(b + 1)
                store(b)
            store(B - 1)
            sp.wait_ge(stored, 16 * B)

        @block.tensor
        def _(pe):
            pe.wait_ge(weights_in, 16 * 5)

            def take_bank(b, item):
                if not (isinstance(b, int) and ITEMS * b + item < SRING):
                    pe.wait_ge(emptied_ring, b * ITEMS + (item - SRING + 1))
                return ring[item % SRING]

            def transpose_inputs(b):
                pe.wait_ge(x_in, 32 * (b + 1))
                for i, src in enumerate((xs, cs)):
                    for t in range(TT):
                        mm = nc.tensor.transpose(ps_m[:, 2 * i + t, :], src[:, t, :], ident[:, :])
                mm.then_inc(xcT_ps, 1)

            def project_queries(b, banks):
                for i in banks:
                    bank = take_bank(b, i)
                    for h in (2 * i, 2 * i + 1):
                        mm = nc.tensor.matmul(bank[:, (h % 2) * S:(h % 2 + 1) * S], wq[:, h, :], xcT[:, 0, :], start=True, stop=True)
                    mm.then_inc(q_ps, 1)

            def project_keys(b):
                nc.tensor.matmul(ps_m[:, 0:2, :], wk[:, :], xcT[:, 1, :], start=True, stop=True)
                for t in range(TT):
                    mm = nc.tensor.matmul(ps_m[:, 2 + t, :], xcT[:, 1, t * P:(t + 1) * P], wv[:, :], start=True, stop=True)
                mm.then_inc(kv_ps, 1)

            def score(b, k):
                qt, nk, heads = chunk_heads(k)
                bank = take_bank(b, QP + k)
                for i, h in enumerate(heads):
                    nc.tensor.matmul(bank[:, i * nk:(i + 1) * nk], qT[:, h, qt * P:(qt + 1) * P], kT[:, 0:nk],
                                     start=True, stop=False)
                    mm = nc.tensor.matmul(bank[:, (i + 1) * nk - P:(i + 1) * nk], ident16[:, :], causal16[:, :],
                                          start=False, stop=True)
                mm.then_inc(scores, 1)

            def turn(b, k):
                pe.wait_ge(emptied_ring, b * ITEMS + QP + k + 1)
                pe.wait_ge(t_sb, b * NSC + max(k - 1, 0))
                for i in range(4):
                    mm = nc.tensor.transpose(ps_t[k % 2][:, i, :], prob[:, k % 2, i * P:(i + 1) * P], ident[:, :])
                mm.then_inc(t_ps, 1)

            def weigh(b, k):
                qt, nk, heads = chunk_heads(k)
                pe.wait_ge(t_sb, b * NSC + k + 1)
                if k == 0:
                    pe.wait_ge(normed, b)
                for i, h in enumerate(heads):
                    for kb in range(qt + 1):
                        mm = nc.tensor.matmul(ps_o[:, qt, h * AD:(h + 1) * AD], probT[:, k % 2, i * (qt + 1) + kb, :],
                                              v[:, kb, h * AD:(h + 1) * AD], start=(kb == 0), stop=(kb == qt))
                mm.then_inc(pv, 1)

            def sequence(b, more):
                pe.wait_ge(kv_sb, 2 * (b + 1))
                pe.wait_ge(emptied_ring, b * ITEMS + QP)
                for s in range(NSC):
                    score(b, s)
                    if s >= LAG_T:
                        turn(b, s - LAG_T)
                    if s >= LAG_V:
                        weigh(b, s - LAG_V)
                if more:
                    transpose_inputs(b + 1)
                turn(b, NSC - 2)
                weigh(b, NSC - 3)
                if more:
                    pe.wait_ge(xcT_sb, b + 2)
                    project_queries(b + 1, range(0, 2))
                turn(b, NSC - 1)
                weigh(b, NSC - 2)
                if more:
                    project_keys(b + 1)
                    project_queries(b + 1, range(2, 5))
                weigh(b, NSC - 1)
                if more:
                    project_queries(b + 1, range(5, QP))
                    pe.wait_ge(kv_sb, 2 * (b + 2))
                pe.wait_ge(normed, b + 1)
                for t in range(TT):
                    mm = nc.tensor.transpose(ps_m[:, t, :], o[:, t, :], ident[:, :])
                mm.then_inc(oT_ps, 1)
                pe.wait_ge(oT_sb, b + 1)
                for t in range(TT):
                    mm = nc.tensor.matmul(ps_m[:, 2 + t, :], oT[:, t * P:(t + 1) * P], wo[:, :], start=True, stop=True)
                mm.then_inc(out_ps, 1)
                pe.wait_ge(out_read, b + 1)

            transpose_inputs(0)
            pe.wait_ge(xcT_sb, 1)
            project_keys(0)
            project_queries(0, range(QP))
            with pe.Fori(0, B - 1) as b:
                sequence(b, True)
            sequence(B - 1, False)

        @block.scalar
        def _(act):
            own = Chain(act, act_own)

            def keep_inputs(b):
                act.wait_ge(xcT_ps, b + 1)
                nc.scalar.activation(xcT[:, :, :], ps_m[:, :, :].rearrange("p (a t) n -> p a (t n)", a=2), ACT.Copy)\
                    .then_inc(xcT_sb, 1)

            def keep_queries(b):
                for i in range(QP):
                    act.wait_ge(q_ps, b * QP + i + 1)
                    nc.scalar.activation(qT[:, 2 * i:2 * i + 2, :], ring[i % SRING][:, :].rearrange("p (a n) -> p a n", a=2),
                                         ACT.Copy).then_inc(emptied_ring, 1)

            def sequence(b, more):
                own.restart()
                for k in range(NSC):
                    qt, nk, heads = chunk_heads(k)
                    act.wait_ge(maxed, b * NSC + k + 1)
                    act.wait_ge(t_ps, b * NSC + max(k - 1, 0))
                    for i, h in enumerate(heads):
                        ins = nc.scalar.activation(prob[:, k % 2, i * nk:(i + 1) * nk],
                                                   ring[(QP + k) % SRING][:, i * nk:(i + 1) * nk], ACT.Exp,
                                                   bias=negmax[:, k, i:i + 1], accum_out=sums[:, qt, h:h + 1])
                    ins.then_inc(emptied_ring, 1)
                if more:
                    keep_inputs(b + 1)
                    act.wait_ge(scores, (b + 1) * NSC)
                    keep_queries(b + 1)
                act.wait_ge(oT_ps, b + 1)
                nc.scalar.activation(oT[:, :], ps_m[:, 0:TT, :].rearrange("p t n -> p (t n)"), ACT.Copy).then_inc(oT_sb, 1)
                act.wait_ge(ln_stats, b + 1)
                own.link(nc.scalar.activation(rs[:, :], mv[:, :, 1], ACT.Ln, bias=eps[:, 0:1]))
                nc.scalar.activation(rs[:, :], rs[:, :], ACT.Exp, scale=-0.5).then_inc(ln_rs, 1)
                own.settle()

            nc.scalar.preload_act_table_set("natural_log_exp_and_others")
            keep_inputs(0)
            keep_queries(0)
            with act.Fori(0, B - 1) as b:
                sequence(b, True)
            sequence(B - 1, False)

        @block.gpsimd
        def _(pool):
            with pool.Fori(0, B) as b:
                hold(pool, out_read, b)
                hold(pool, x_in, 32 * (b + 1))
                nc.gpsimd.tensor_copy(x[:, :, :], xs[:, :, :]).then_inc(x_kept, 1)

        @block.vector
        def _(dve):
            own = Chain(dve, dve_own)
            dve.wait_ge(weights_in, 16 * 5)

            def keep_keys(b):
                dve.wait_ge(kv_ps, b + 1)
                nc.vector.tensor_copy(kT[:, :], ps_m[:, 0:2, :].rearrange("p a n -> p (a n)")).then_inc(kv_sb, 1)
                dve.wait_ge(pv, b * NSC)
                nc.vector.tensor_copy(v[:, :, :], ps_m[:, 2:4, :]).then_inc(kv_sb, 1)

            def keep_block(b, k):
                dve.wait_ge(pv, b * NSC + max(k - 1, 0))
                dve.wait_ge(t_ps, b * NSC + k + 1)
                nc.vector.tensor_copy(probT[:, k % 2, :, :], ps_t[k % 2][:, :, :]).then_inc(t_sb, 1)

            def sequence(b, more):
                own.restart()
                for s in range(NSC + LAG_T):
                    if s < NSC:
                        qt, nk, heads = chunk_heads(s)
                        dve.wait_ge(scores, b * NSC + s + 1)
                        nc.vector.tensor_reduce(negmax[:, s, 0:len(heads)],
                                                ring[(QP + s) % SRING][:, :].rearrange("p (i n) -> p i n", n=nk), AX, ALU.max,
                                                negate=True).then_inc(maxed, 1)
                    if s >= LAG_T:
                        keep_block(b, s - LAG_T)
                dve.wait_ge(emptied_ring, (b + 1) * ITEMS)
                own.link(nc.vector.reciprocal(sums[:, :, :], sums[:, :, :]))
                dve.wait_ge(x_kept, b + 1)
                own.link(nc.vector.tensor_tensor(r[:, :, :], x[:, :, :], bc(bo[:, :], 1, TT), ALU.add))
                if more:
                    keep_keys(b + 1)
                dve.wait_ge(pv, (b + 1) * NSC)
                nc.vector.tensor_tensor(o[:, :, :].rearrange("p t (h d) -> p t h d", h=AH),
                                        ps_o[:, :, :].rearrange("p t (h d) -> p t h d", h=AH), bc(sums[:, :, :], 3, AD),
                                        ALU.mult).then_inc(normed, 1)
                dve.wait_ge(out_ps, b + 1)
                nc.vector.tensor_tensor(r[:, :, :], r[:, :, :], ps_m[:, 2:4, :], ALU.add).then_inc(out_read, 1)
                dve.wait_ge(out_read, b + 1)
                layernorm(nc, dve, own, r, stats, mv, rs, x2, b, ln_stats, ln_rs, x2_ready, stored)
                own.settle()

            dve.wait_ge(kv_ps, 1)
            nc.vector.tensor_copy(kT[:, :], ps_m[:, 0:2, :].rearrange("p a n -> p (a n)")).then_inc(kv_sb, 1)
            nc.vector.tensor_copy(v[:, :, :], ps_m[:, 2:4, :]).then_inc(kv_sb, 1)
            with dve.Fori(0, B - 1) as b:
                sequence(b, True)
            sequence(B - 1, False)


NE = 8
DF = 512
FC = DF // P


def ffn_stage(nc, T, const):
    ident, ident16, causal16, ones, eps = const
    with ExitStack() as stack:
        c = Scope(nc, stack, "ffn")
        wr = c.sb("wr", [P, NE])
        br = c.sb("br", [1, NE])
        x = [c.sb(f"x{i}", [P, TT, D]) for i in range(2)]
        xT = [c.sb(f"xT{i}", [P, S]) for i in range(2)]
        mean = c.sb("mean", [P, 1])
        score = c.sb("score", [1, NE])
        top = c.sb("top", [1, 8])
        pick = c.sb("pick", [1, 8], U32)
        w1 = [c.sb(f"w1{i}", [P, DF]) for i in range(2)]
        w2 = [c.sb(f"w2{i}", [P, FC, D]) for i in range(2)]
        b1 = [c.sb(f"b1{i}", [P, FC]) for i in range(2)]
        b2 = [c.sb(f"b2{i}", [P, D]) for i in range(2)]
        hT = c.sb("hT", [P, FC, S])
        r = c.sb("r", [P, TT, D])
        stats = c.sb("stats", [P, TT, 6])
        mv = c.sb("mv", [P, TT, 2])
        rs = c.sb("rs", [P, TT])
        x3 = c.sb("x3", [P, TT, D])
        ps_x = c.ps("ps_x", [P, S])
        ps_r = c.ps("ps_r", [1, NE])
        ps_h = [c.ps(f"ps_h{i}", [P, 2, S]) for i in range(FC // 2)]
        ps_y = c.ps("ps_y", [P, TT, D])

        weights_in = c.sem("weights_in")
        x_in = c.sem("x_in")
        xT_ps = c.sem("xT_ps")
        xT_sb = c.sem("xT_sb")
        mean_ready = c.sem("mean_ready")
        score_ps = c.sem("score_ps")
        picked = c.sem("picked")
        expert_in = c.sem("expert_in")
        x_used = c.sem("x_used")
        h_ps = c.sem("h_ps")
        h_sb = c.sem("h_sb")
        y_ps = c.sem("y_ps")
        y_read = c.sem("y_read")
        ln_stats = c.sem("ln_stats")
        ln_rs = c.sem("ln_rs")
        x3_ready = c.sem("x3_ready")
        stored = c.sem("stored")
        dve_own = c.sem("dve_own")
        act_own = c.sem("act_own")
        block = c.block()

        @block.sync
        def _(sp):
            for dst, src in ((wr[:, :], T["wr"]), (br[:, :], T["br"])):
                sp.dma_start(dst, src).then_inc(weights_in, 16)

            def load_x(b, p):
                sp.dma_start(x[p][:, :, :], T["x2"][b].rearrange("(t p) d -> p t d", p=P)).then_inc(x_in, 16)

            def load_expert(b, p):
                if isinstance(b, int):
                    if b >= 2:
                        sp.wait_ge(y_read, b - 1)
                else:
                    hold(sp, y_read, b - 1)
                hold(sp, picked, b + 1)
                e = sp.value_load(pick[0:1, 0:1], min_val=0, max_val=NE - 1)
                sp.dma_start(w1[p][:, :], T["ffn_w1"][bass.ds(e, 1)].rearrange("e p f -> p (e f)")).then_inc(expert_in, 16)
                sp.dma_start(b1[p][:, :], T["ffn_b1"][bass.ds(e, 1)].rearrange("e p f -> p (e f)")).then_inc(expert_in, 16)
                sp.dma_start(w2[p][:, :, :], T["ffn_w2"][bass.ds(e, 1)].rearrange("e (c p) d -> p (e c) d", p=P))\
                    .then_inc(expert_in, 16)
                sp.dma_start(b2[p][:, :], T["ffn_b2"][bass.ds(e, 1)].rearrange("e p d -> p (e d)")).then_inc(expert_in, 16)

            def store(b):
                sp.wait_ge(x3_ready, b + 1)
                sp.dma_start(T["x3"][b].rearrange("(t p) d -> p t d", p=P), x3[:, :, :]).then_inc(stored, 16)

            def turn(b, p, first, more):
                if more:
                    hold(sp, xT_ps, b + 1)
                    hold_past(sp, x_used, b)
                    load_x(b + 1, 1 - p)
                load_expert(b, p)
                if not first:
                    store(b - 1)

            load_x(0, 0)
            turns(sp, turn)
            store(B - 1)
            sp.wait_ge(stored, 16 * B)

        @block.tensor
        def _(pe):

            def turn_x(b, p):
                wait_past(pe, mean_ready, b)
                pe.wait_ge(x_in, 16 * (b + 1))
                for t in range(TT):
                    mm = nc.tensor.transpose(ps_x[:, t * P:(t + 1) * P], x[p][:, t, :], ident[:, :])
                mm.then_inc(xT_ps, 1)

            def score_experts(b):
                wait_past(pe, picked, b)
                pe.wait_ge(mean_ready, b + 1)
                nc.tensor.matmul(ps_r[:, :], mean[:, :], wr[:, :], start=True, stop=True).then_inc(score_ps, 1)

            def hidden(b, p, half):
                if half == 0:
                    pe.wait_ge(expert_in, 64 * (b + 1))
                wait_past(pe, h_sb, b * FC)
                for f in (2 * half, 2 * half + 1):
                    mm = nc.tensor.matmul(ps_h[half][:, f % 2, :], w1[p][:, f * P:(f + 1) * P], xT[p][:, :], start=True, stop=True)
                mm.then_inc(h_ps, 1)

            def output(b, p):
                wait_past(pe, y_read, b)
                for f in range(FC):
                    if f % 2 == 0:
                        pe.wait_ge(h_sb, b * FC + f + 2)
                    for t in range(TT):
                        mm = nc.tensor.matmul(ps_y[:, t, :], hT[:, f, t * P:(t + 1) * P], w2[p][:, f, :],
                                              start=(f == 0 and t == 0), stop=(f == FC - 1), skip_group_check=True)
                mm.then_inc(y_ps, 1)

            def turn(b, p, first, more):
                if more:
                    turn_x(b + 1, 1 - p)
                hidden(b, p, 0)
                hidden(b, p, 1)
                if more:
                    score_experts(b + 1)
                output(b, p)

            pe.wait_ge(weights_in, 32)
            turn_x(0, 0)
            score_experts(0)
            turns(pe, turn)

        @block.scalar
        def _(act):
            own = Chain(act, act_own)

            def keep_x(b, p):
                wait_past(act, score_ps, b)
                act.wait_ge(xT_ps, b + 1)
                nc.scalar.activation(xT[p][:, :], ps_x[:, :], ACT.Copy, accum_out=mean[:, :]).then_inc(xT_sb, 1)
                act.wait_ge(xT_sb, b + 1)
                nc.scalar.activation(mean[:, :], mean[:, :], ACT.Copy, scale=1.0 / S).then_inc(mean_ready, 1)

            def turn(b, p, first, more):
                own.restart()
                if more:
                    keep_x(b + 1, 1 - p)
                act.wait_ge(ln_stats, b + 1)
                own.link(nc.scalar.activation(rs[:, :], mv[:, :, 1], ACT.Ln, bias=eps[:, 0:1]))
                nc.scalar.activation(rs[:, :], rs[:, :], ACT.Exp, scale=-0.5).then_inc(ln_rs, 1)
                own.settle()

            nc.scalar.preload_act_table_set("natural_log_exp_and_others")
            keep_x(0, 0)
            turns(act, turn)

        @block.vector
        def _(dve):
            own = Chain(dve, dve_own)

            def choose(b):
                dve.wait_ge(score_ps, b + 1)
                own.link(nc.vector.tensor_tensor(score[:, :], ps_r[:, :], br[:, :], ALU.add))
                own.link(nc.vector.max(top[:, :], score[:, :]))
                wait_past(dve, expert_in, 64 * b)
                dve.nop(nofuse=True)
                nc.vector.max_index(pick[:, :], top[:, :], score[:, :]).then_inc(picked, 1)

            def turn(b, p, first, more):
                own.restart()
                wait_past(dve, x3_ready, b)
                dve.wait_ge(expert_in, 64 * (b + 1))
                nc.vector.tensor_tensor(r[:, :, :], x[p][:, :, :], bc(b2[p][:, :], 1, TT), ALU.add).then_inc(x_used, 1)
                for f in range(FC):
                    dve.wait_ge(h_ps, b * (FC // 2) + f // 2 + 1)
                    nc.vector.tensor_scalar(hT[:, f, :], ps_h[f // 2][:, f % 2, :], b1[p][:, f:f + 1], 0.0, ALU.add, ALU.max)\
                        .then_inc(h_sb, 1)
                if more:
                    choose(b + 1)
                dve.wait_ge(x_used, b + 1)
                dve.wait_ge(y_ps, b + 1)
                nc.vector.tensor_tensor(r[:, :, :], r[:, :, :], ps_y[:, :, :], ALU.add).then_inc(y_read, 1)
                dve.wait_ge(y_read, b + 1)
                ln_statistics(nc, own, r, stats, mv, ln_stats)
                dve.wait_ge(ln_stats, b + 1)
                wait_past(dve, stored, 16 * b)
                dve.wait_ge(ln_rs, b + 1)
                ln_apply(nc, own, r, mv, rs, x3, x3_ready)
                own.settle()

            dve.wait_ge(weights_in, 32)
            own.restart()
            choose(0)
            turns(dve, turn)


DH = 16
DW = 8
GB = 8
NG = B // GB
PLANES = 3 * DW + 1
GT = NG * S
WIN = P - DH
NORM_EPS = 1e-6


def delta_stage(nc, T, const):
    ident, ident16, causal16, ones, eps = const
    with ExitStack() as stack:
        c = Scope(nc, stack, "delta")
        planes = c.sb("planes", [P, 3 * DW, GT])
        eta = c.sb("eta", [P, GT])
        kb = c.sb("kb", [P, DW, GT])
        with ExitStack() as inner:
            project_and_convolve(nc, T, const, Scope(nc, inner, "dproj"), inner, planes, eta)
        k, q, v = (planes[:, i * DW:(i + 1) * DW, :] for i in range(3))
        with ExitStack() as inner:
            normalise(nc, Scope(nc, inner, "dnorm"), inner, const, k, q, v, kb, eta)
        u = c.sb("u", [P, DW, GT])
        with ExitStack() as inner:
            solve_blocks(nc, Scope(nc, inner, "dsolve"), inner, k, v, kb)
        with ExitStack() as inner:
            recurrence(nc, Scope(nc, inner, "drec"), inner, k, v, kb, u)
        o = c.sb("o", [P, DW, GT])
        with ExitStack() as inner:
            average(nc, T, const, Scope(nc, inner, "davg"), inner, k, q, u, o)
        with ExitStack() as inner:
            project_out(nc, T, const, Scope(nc, inner, "dout"), inner, o)


def project_and_convolve(nc, T, const, c, stack, planes, eta):
    ident, ident16, causal16, ones, eps = const
    wpad = c.sb("wpad", [P, PLANES, 2 * WIN + DH])
    bias = c.sb("bias", [P, PLANES])
    taps = c.sb("taps", [P, 3 * DW, TAPS])
    x = c.sb("x", [P, B * TT, D])
    xT = c.sb("xT", [P, B, S])
    raw = c.sb("raw", [P, PLANES, NG, TAPS - 1 + S])
    ps = [c.ps(f"ps{i}", [P, 512]) for i in range(4)]
    weights_in = c.sem("weights_in")
    x_in = c.sem("x_in")
    turned = c.sem("turned")
    turned_sb = c.sem("turned_sb")
    plane_ps = c.sem("plane_ps")
    plane_sb = c.sem("plane_sb")
    cleared = c.sem("cleared")
    dve_own = c.sem("dve_own")
    block = c.block()

    @block.sync
    def _(sp):
        for b in range(0, B, 2):
            sp.dma_start(x[:, b * TT:(b + 2) * TT, :], T["x3"][b:b + 2].rearrange("b (t p) d -> p (b t) d", p=P))\
                .then_inc(x_in, 16)
        for dst, src in ((wpad[:, :, :], T["delta_w"]), (bias[:, :], T["delta_bias"]), (taps[:, :, :], T["delta_taps"])):
            sp.dma_start(dst, src).then_inc(weights_in, 16)

    @block.gpsimd
    def _(pool):
        nc.gpsimd.memset(raw[:, :, :, 0:TAPS - 1], 0.0).then_inc(cleared, 1)

    @block.tensor
    def _(pe):
        pe.wait_ge(x_in, 16 * (B // 2))
        for f in range(B * TT // 4):
            if f >= 4:
                pe.wait_ge(turned_sb, f - 3)
            for i in range(4):
                mm = nc.tensor.transpose(ps[f % 4][:, i * P:(i + 1) * P], x[:, 4 * f + i, :], ident[:, :])
            mm.then_inc(turned, 1)
        pe.wait_ge(turned_sb, B * TT // 4)
        pe.wait_ge(weights_in, 48)
        with pe.Fori(0, NG) as g:
            for n in range(PLANES):
                if n >= 4:
                    pe.wait_ge(plane_sb, g * PLANES + n - 3)
                else:
                    pe.wait_ge(plane_sb, g * PLANES)
                for s in range(GB):
                    mm = nc.tensor.matmul(ps[n % 4][:, 0:S], wpad[:, n, WIN - DH * s:WIN - DH * s + P],
                                          xT[:, bass.ds(g * GB + s, 1), :].rearrange("p a t -> p (a t)"),
                                          start=(s == 0), stop=(s == GB - 1))
                mm.then_inc(plane_ps, 1)

    @block.scalar
    def _(act):
        for f in range(B * TT // 4):
            act.wait_ge(turned, f + 1)
            nc.scalar.activation(xT[:, 2 * f:2 * f + 2, :], ps[f % 4][:, :].rearrange("p (b t) -> p b t", b=2), ACT.Copy)\
                .then_inc(turned_sb, 1)
        act.wait_ge(weights_in, 48)
        with act.Fori(0, NG) as g:
            for n in range(PLANES):
                act.wait_ge(plane_ps, g * PLANES + n + 1)
                nc.scalar.activation(raw[:, n, bass.ds(g, 1), TAPS - 1:].rearrange("p a t -> p (a t)"), ps[n % 4][:, 0:S],
                                     ACT.Identity, bias=bias[:, n:n + 1]).then_inc(plane_sb, 1)

    @block.vector
    def _(dve):
        own = Chain(dve, dve_own)
        dve.wait_ge(cleared, 1)
        dve.wait_ge(weights_in, 48)
        with dve.Fori(0, NG) as g:
            for n in range(3 * DW):
                own.restart()
                out = planes[:, n, :].rearrange("p (g t) -> p g t", g=NG)[:, bass.ds(g, 1), :].rearrange("p a t -> p (a t)")
                dve.wait_ge(plane_sb, g * PLANES + n + 1)
                for j in range(TAPS):
                    src = raw[:, n, bass.ds(g, 1), j:j + S].rearrange("p a t -> p (a t)")
                    if j == 0:
                        own.link(nc.vector.tensor_scalar(out, src, taps[:, n, 0:1], None, ALU.mult))
                    else:
                        own.link(nc.vector.scalar_tensor_tensor(out=out, in0=src, scalar=taps[:, n, j:j + 1], in1=out,
                                                                op0=ALU.mult, op1=ALU.add))
        own.restart()
        dve.wait_ge(plane_sb, NG * PLANES)
        own.link(nc.vector.tensor_copy(eta[:, :].rearrange("p (g t) -> p g t", g=NG), raw[:, 3 * DW, :, TAPS - 1:]))


def normalise(nc, c, stack, const, k, q, v, kb, eta):
    ident, ident16, causal16, ones, eps = const
    sq = c.sb("sq", [P, 2, DW, GT])
    ev = c.sb("ev", [P, DW, GT])
    ee = c.sb("ee", [P, GT])
    norm = c.sb("norm", [P, 2, GT])
    squared = c.sem("squared")
    lengths = c.sem("lengths")
    rooted = c.sem("rooted")
    expd = c.sem("expd")
    dve_own = c.sem("dve_own")
    block = c.block()

    @block.scalar
    def _(act):
        nc.scalar.activation(sq[:, 0, :, :], k, ACT.Square).then_inc(squared, 1)
        nc.scalar.activation(sq[:, 1, :, :], q, ACT.Square).then_inc(squared, 1)
        nc.scalar.activation(ev[:, :, :], v, ACT.Exp, scale=-1.0).then_inc(expd, 1)
        nc.scalar.activation(ee[:, :], eta[:, :], ACT.Exp, scale=-1.0).then_inc(expd, 1)
        act.wait_ge(lengths, 2)
        nc.scalar.activation(norm[:, :, :], norm[:, :, :], ACT.Sqrt).then_inc(rooted, 1)

    @block.vector
    def _(dve):
        own = Chain(dve, dve_own)
        for i in range(2):
            dve.wait_ge(squared, i + 1)
            nc.vector.tensor_reduce(norm[:, i, :], sq[:, i, :, :].rearrange("p d n -> p n d"), AX, ALU.add).then_inc(lengths, 1)
        dve.wait_ge(expd, 2)
        own.link(nc.vector.tensor_scalar(ee[:, :], ee[:, :], 1.0, None, ALU.add))
        own.link(nc.vector.reciprocal(eta[:, :], ee[:, :]))
        own.link(nc.vector.tensor_scalar(ev[:, :, :], ev[:, :, :], 1.0, None, ALU.add))
        own.link(nc.vector.reciprocal(ev[:, :, :], ev[:, :, :]))
        own.link(nc.vector.tensor_tensor(v, v, ev[:, :, :], ALU.mult))
        own.link(nc.vector.tensor_tensor(v, v, bc(eta[:, :], 1, DW), ALU.mult))
        dve.wait_ge(rooted, 1)
        own.link(nc.vector.tensor_scalar(norm[:, :, :], norm[:, :, :], NORM_EPS, None, ALU.add))
        own.link(nc.vector.reciprocal(norm[:, :, :], norm[:, :, :]))
        for i, w in enumerate((k, q)):
            own.link(nc.vector.tensor_tensor(w, w, bc(norm[:, i, :], 1, DW), ALU.mult))
        own.link(nc.vector.tensor_tensor(kb[:, :, :], k, bc(eta[:, :], 1, DW), ALU.mult))


LC = 8
BLOCKS = S // LC


def solve_blocks(nc, c, stack, k, v, kb):
    NB = NG * BLOCKS
    dots = c.sb("dots", [P, NB, LC, LC])
    t = c.sb("t", [P, NB, LC, DW])
    t2 = c.sb("t2", [P, DW, NB, LC])
    total = c.sb("total", [P, 2, DW, NB])
    dve_own = c.sem("dve_own")
    block = c.block()

    def blocked(plane):
        return plane.rearrange("p d (n i) -> p d n i", i=LC)

    @block.vector
    def _(dve):
        own = Chain(dve, dve_own)
        for i in range(1, LC):
            b_i = bc(blocked(kb[:, :, :])[:, :, :, i].rearrange("p d n -> p n d"), 2, i)
            own.link(nc.vector.tensor_tensor(t[:, :, 0:i, :], b_i, blocked(k)[:, :, :, 0:i].rearrange("p d n s -> p n s d"),
                                             ALU.mult))
            own.link(nc.vector.tensor_reduce(dots[:, :, i, 0:i], t[:, :, 0:i, :], AX, ALU.add))
        for i in range(1, LC):
            for j, plane in enumerate((v, kb[:, :, :])):
                rows = blocked(plane)
                own.link(nc.vector.tensor_tensor(t2[:, :, :, 0:i], rows[:, :, :, 0:i], bc(dots[:, :, i, 0:i], 1, DW), ALU.mult))
                own.link(nc.vector.tensor_reduce(total[:, j, :, :], t2[:, :, :, 0:i], AX, ALU.add))
                own.link(nc.vector.tensor_tensor(rows[:, :, :, i], rows[:, :, :, i], total[:, j, :, :], ALU.subtract))


def recurrence(nc, c, stack, k, v, kb, u):
    w = c.sb("w", [P, NG, DW, DW])
    t1 = c.sb("t1", [P, NG, LC, DW, DW])
    t2 = c.sb("t2", [P, NG, DW, DW, LC])
    p = c.sb("p", [P, NG, LC, DW])
    dw = c.sb("dw", [P, NG, DW, DW])
    cleared = c.sem("cleared")
    done = [c.sem(f"done{g}") for g in range(NG)]
    block = c.block()

    @block.vector
    def _(dve):
        nc.vector.memset(w[:, :, :, :], 0.0).then_inc(cleared, 1)
        dve.wait_ge(cleared, 1)
        with dve.Fori(0, BLOCKS) as n:
            own = [Chain(dve, done[g]) for g in range(NG)]
            for chain in own:
                chain.restart()

            def tokens(plane, g):
                return plane[:, :, bass.ds(n * LC + g * S, LC)]

            for g in range(NG):
                own[g].count(nc.vector.tensor_tensor(t1[:, g, :, :, :], bc(w[:, g, :, :], 1, LC),
                                                     bc(tokens(kb, g).rearrange("p d i -> p i d"), 2, DW), ALU.mult))
            for g in range(NG):
                own[g].settle()
                own[g].count(nc.vector.tensor_reduce(p[:, g, :, :], t1[:, g, :, :, :], AX, ALU.add))
            for g in range(NG):
                own[g].settle()
                own[g].count(nc.vector.tensor_tensor(tokens(u, g), tokens(v, g), p[:, g, :, :].rearrange("p i e -> p e i"),
                                                     ALU.subtract))
            for g in range(NG):
                own[g].settle()
                own[g].count(nc.vector.tensor_tensor(t2[:, g, :, :, :], bc(tokens(u, g), 2, DW), bc(tokens(k, g), 1, DW), ALU.mult))
            for g in range(NG):
                own[g].settle()
                own[g].count(nc.vector.tensor_reduce(dw[:, g, :, :], t2[:, g, :, :, :], AX, ALU.add))
            for g in range(NG):
                own[g].settle()
                own[g].count(nc.vector.tensor_tensor(w[:, g, :, :], w[:, g, :, :], dw[:, g, :, :], ALU.add))
            for g in range(NG):
                own[g].settle()


def average(nc, T, const, c, stack, k, q, u, o):
    ident, ident16, causal16, ones, eps = const
    coef = c.sb("coef", [P, 3, S])
    fade = c.sb("fade", [P, 2, DW * NG, S])
    a = [c.sb(f"a{i}", [P, DW, GT]) for i in range(3)]
    rms = c.sb("rms", [P, DW])
    tiny = c.sb("tiny", [P, 1])
    ms = c.sb("ms", [P, GT])
    coef_in = c.sem("coef_in")
    faded = c.sem("faded")
    scaled = c.sem("scaled")
    inputs = c.sem("inputs")
    outputs = c.sem("outputs")
    added = c.sem("added")
    squares = c.sem("squares")
    summed = c.sem("summed")
    rooted = c.sem("rooted")
    dve_own = c.sem("dve_own")
    act_own = c.sem("act_own")
    block = c.block()

    @block.sync
    def _(sp):
        sp.dma_start(coef[:, :, :], T["coef"]).then_inc(coef_in, 16)
        sp.dma_start(rms[:, :], T["rms"]).then_inc(coef_in, 16)

    @block.gpsimd
    def _(pool):
        def make_input(d):
            nc.gpsimd.tensor_tensor(a[d % 3][:, :, :], u[:, :, :], bc(k[:, d, :], 1, DW), ALU.mult).then_inc(inputs, 1)

        pool.wait_ge(scaled, 1)
        make_input(0)
        make_input(1)
        for d in range(DW):
            pool.wait_ge(outputs, d + 1)
            if d == 0:
                nc.gpsimd.tensor_copy(o[:, :, :], a[0][:, :, :]).then_inc(added, 1)
            else:
                pool.wait_ge(added, d)
                nc.gpsimd.tensor_tensor(o[:, :, :], o[:, :, :], a[d % 3][:, :, :], ALU.add).then_inc(added, 1)
            if d + 2 < DW:
                if d:
                    pool.wait_ge(added, d)
                make_input(d + 2)

    @block.scalar
    def _(act):
        act.wait_ge(coef_in, 32)
        for i in range(2):
            nc.scalar.activation(fade[:, i, :, :], bc(coef[:, i, :], 1, DW * NG), ACT.Copy).then_inc(faded, 1)
        act.wait_ge(added, DW)
        nc.scalar.activation(a[0][:, :, :], o[:, :, :], ACT.Square).then_inc(squares, 1)
        act.wait_ge(summed, 1)
        nc.scalar.activation(ms[:, :], ms[:, :], ACT.Ln, scale=1.0 / DW, bias=tiny[:, 0:1]).then_inc(act_own, 1)
        act.wait_ge(act_own, 1)
        nc.scalar.activation(ms[:, :], ms[:, :], ACT.Exp, scale=-0.5).then_inc(rooted, 1)

    @block.vector
    def _(dve):
        own = Chain(dve, dve_own)
        own.link(nc.vector.memset(tiny[:, :], NORM_EPS))
        dve.wait_ge(coef_in, 32)
        nc.vector.tensor_tensor(u[:, :, :].rearrange("p d (g t) -> p (d g) t", g=NG),
                                u[:, :, :].rearrange("p d (g t) -> p (d g) t", g=NG),
                                bc(coef[:, 2, :], 1, DW * NG), ALU.mult).then_inc(scaled, 1)
        dve.wait_ge(faded, 2)
        flat = "p d n -> p (d n)"
        for d in range(DW):
            x = a[d % 3]
            dve.wait_ge(inputs, d + 1)
            for i in range(2):
                own.link(nc.vector.tensor_tensor_scan(x[:, :, :].rearrange(flat), fade[:, i, :, :].rearrange(flat),
                                                      x[:, :, :].rearrange(flat), 0.0, ALU.mult, ALU.add))
            nc.vector.tensor_tensor(x[:, :, :], x[:, :, :], bc(q[:, d, :], 1, DW), ALU.mult).then_inc(outputs, 1)
        dve.wait_ge(squares, 1)
        nc.vector.tensor_reduce(ms[:, :], a[0][:, :, :].rearrange("p e n -> p n e"), AX, ALU.add).then_inc(summed, 1)
        dve.wait_ge(rooted, 1)
        own.link(nc.vector.tensor_tensor(o[:, :, :], o[:, :, :], bc(ms[:, :], 1, DW), ALU.mult))
        own.link(nc.vector.tensor_tensor(o[:, :, :], o[:, :, :], bc(rms[:, :], 2, GT), ALU.mult))


def project_out(nc, T, const, c, stack, o):
    ident, ident16, causal16, ones, eps = const
    NT = NG * TT
    w = c.sb("w", [P, GB, DW, D])
    bout = c.sb("bout", [P, D])
    x = c.sb("x", [P, 2, NT, D])
    r = c.sb("r", [P, NT, D])
    stats = c.sb("stats", [P, NT, 6])
    mv = c.sb("mv", [P, NT, 2])
    rs = c.sb("rs", [P, NT])
    x4 = c.sb("x4", [P, NT, D])
    ps = [c.ps(f"ps{i}", [P, NT, D]) for i in range(2)]
    cleared = c.sem("cleared")
    weights_in = c.sem("weights_in")
    x_in = c.sem("x_in")
    out_ps = c.sem("out_ps")
    out_read = c.sem("out_read")
    ln_stats = c.sem("ln_stats")
    ln_rs = c.sem("ln_rs")
    ready = c.sem("x4_ready")
    stored = c.sem("stored")
    dve_own = c.sem("dve_own")
    act_own = c.sem("act_own")
    block = c.block()

    @block.gpsimd
    def _(pool):
        nc.gpsimd.memset(w[:, :, :, :], 0.0).then_inc(cleared, 1)

    @block.sync
    def _(sp):
        sp.dma_start(bout[:, :], T["bout"]).then_inc(weights_in, 16)
        sp.wait_ge(cleared, 1)
        for s in range(GB):
            sp.dma_start(w[DH * s:DH * (s + 1), s, :, :], T["delta_out"]).then_inc(weights_in, 16)
        with sp.Fori(0, GB) as s:
            sp.wait_ge(out_read, s)
            for g in range(NG):
                sp.dma_start(x[:, 0, g * TT:(g + 1) * TT, :],
                             T["x3"][bass.ds(s + g * GB, 1)].rearrange("b (t p) d -> p (b t) d", p=P)).then_inc(x_in, 16)
            sp.wait_ge(ready, s + 1)
            for g in range(NG):
                sp.dma_start(T["x4"][bass.ds(s + g * GB, 1)].rearrange("b (t p) d -> p (b t) d", p=P),
                             x4[:, g * TT:(g + 1) * TT, :]).then_inc(stored, 16)
        sp.wait_ge(stored, 16 * NG * GB)

    @block.tensor
    def _(pe):
        pe.wait_ge(weights_in, 16 * (GB + 1))
        with pe.Fori(0, GB) as s:
            pe.wait_ge(out_read, s)
            for n in range(NT):
                for e in range(DW):
                    mm = nc.tensor.matmul(ps[0][:, n, :], o[:, e, n * P:(n + 1) * P],
                                          w[:, bass.ds(s, 1), e, :].rearrange("p a n -> p (a n)"),
                                          start=(e == 0), stop=(e == DW - 1))
            mm.then_inc(out_ps, 1)

    @block.scalar
    def _(act):
        own = Chain(act, act_own)
        nc.scalar.preload_act_table_set("natural_log_exp_and_others")
        with act.Fori(0, GB) as s:
            own.restart()
            act.wait_ge(ln_stats, s + 1)
            own.link(nc.scalar.activation(rs[:, :], mv[:, :, 1], ACT.Ln, bias=eps[:, 0:1]))
            nc.scalar.activation(rs[:, :], rs[:, :], ACT.Exp, scale=-0.5).then_inc(ln_rs, 1)
            own.settle()

    @block.vector
    def _(dve):
        own = Chain(dve, dve_own)
        dve.wait_ge(weights_in, 16 * (GB + 1))
        with dve.Fori(0, GB) as s:
            own.restart()
            dve.wait_ge(x_in, 16 * NG * (s + 1))
            own.link(nc.vector.tensor_tensor(r[:, :, :], x[:, 0, :, :], bc(bout[:, :], 1, NT), ALU.add))
            dve.wait_ge(out_ps, s + 1)
            nc.vector.tensor_tensor(r[:, :, :], r[:, :, :], ps[0][:, :, :], ALU.add).then_inc(out_read, 1)
            dve.wait_ge(out_read, s + 1)
            layernorm(nc, dve, own, r, stats, mv, rs, x4, s, ln_stats, ln_rs, ready, stored, NT, 16 * NG)
            own.settle()


CH = 16
CD = 64
HP = CH // 2
INNER = CH * CD
TEXT, IMG = 77, 16
TI = TEXT + IMG
AUD = CTX - TI
REL = 16
NREL = 2 * REL + 1
TR = TI + NREL
SCALE = CD ** -0.5
AT = -(-AUD // P)
CHUNKS = 3
CHUNK = [min(512, AUD - 512 * i) for i in range(CHUNKS)]
UNITS = 4 * HP
RING = 4
HALVES = ((0, AT // 2), (AT // 2, AT))
R1, R2 = 19, NREL - 19
COL_R1, COL_I, COL_R2 = TEXT, TEXT + R1, TEXT + R1 + IMG
CAT = COL_R2 + R2
FROW = P - 1 + NREL
STEP_SCORES, STEP_MAX, STEP_EXP, STEP_SUM, STEP_RECIPROCAL, STEP_ALL_FAR, STEP_FAR = 13, 15, 17, 19, 20, 21, 23
SCRATCH = {"skew_rel": (P, CH, P + TEXT - 1), "skew_prob": (P, CH, FROW)}


SMALL = {(0, 0): ("tq", 0), (1, 0): ("tq", 1), (1, 2): ("vc", 0), (2, 0): ("tq", 3), (3, 0): ("kt", 0), (3, 1): ("kt", 1),
         (4, 0): ("tq", 2), (5, 0): ("vc", 1), (5, 2): ("s", (0, 0)), (6, 0): ("s", (1, 0)),
         (7, 0): ("s", (1, 1)), (7, 2): ("s", (0, 1)), (8, 0): ("s", (0, 2)), (9, 0): ("s", (1, 2)),
         (9, 2): ("s", (0, 3)), (10, 0): ("s", (1, 3)),
         (24, 0): ("c", 0), (25, 0): ("c", 1), (25, 1): ("cp", 0), (25, 2): ("c", 2), (26, 0): ("c", 3),
         (27, 0): ("cp", 1), (27, 2): ("c", 4), (28, 0): ("c", 5), (29, 0): ("cp", 2), (29, 1): ("c", 6),
         (29, 2): ("c", 7), (30, 0): ("cp", 3), (31, 0): ("o", 0), (31, 1): ("o", 1)}
TAIL = [("o", 2), ("o", 3), ("out", 0), ("out", 1)]


def by_act(what, arg):
    if what == "t":
        return arg[1] == 2
    if what == "s":
        return arg[0] == 1
    if what == "c":
        return arg % 2 == 0
    return what in ("tq", "kt", "vc", "cp", "o")


def after_scores(n, i):
    if i == CHUNKS - 1 and n % 2 == 0:
        return [("q", n // 2 + 1)] if n // 2 + 1 < CH else []
    return [SMALL[n, i]] if (n, i) in SMALL else []


def fills_of():
    todo = []
    for n in range(UNITS):
        for f in range(CHUNKS):
            todo.append(("t", (n, f)))
            todo += after_scores(n, f)
    todo += TAIL + [("q", 0)]
    return [(what, arg, "act" if by_act(what, arg) else "dve") for what, arg in todo]


FILL_LIST = fills_of()
FILL_AT = {(w, a): i for i, (w, a, _) in enumerate(FILL_LIST)}


def emptied(i):
    eng = FILL_LIST[i][2]
    return eng, sum(1 for f in FILL_LIST[:i + 1] if f[2] == eng)


PER_TURN = {e: sum(1 for f in FILL_LIST if f[2] == e) for e in ("act", "dve")}
BEFORE = {"act": 0, "dve": 1}
FILLS_PER_TURN = len(FILL_LIST)


def bank_of(i):
    return (i + 1) % 2


def cross_fold(nc, T, const, wo, fq, fv):
    ident, ident16, causal16, ones, eps = const
    with ExitStack() as stack:
        c = Scope(nc, stack, "fold")
        w = {n: c.sb(f"w_{n}", [P, INNER]) for n in ("q", "ka", "va")}
        wT = {n: c.sb(f"wT_{n}", [P, HP, P]) for n in w}
        ps_t = [c.ps(f"ps_t{i}", [P, 4, P]) for i in range(2)]
        ps_f = [c.ps(f"ps_f{i}", [P, 4, P]) for i in range(4)]
        w_in = c.sem("w_in")
        t_ps = c.sem("t_ps")
        t_sb = c.sem("t_sb")
        f_ps = c.sem("f_ps")
        f_sb = c.sem("f_sb")
        block = c.block()

        @block.sync
        def _(sp):
            for n in w:
                sp.dma_start(w[n][:, :], T[f"cross_{n}"]).then_inc(w_in, 16)
            sp.dma_start(wo[:, :, :], T["cross_o"]).then_inc(w_in, 16)

        @block.tensor
        def _(pe):
            pe.wait_ge(w_in, 64)
            for i, (n, g) in enumerate([(n, g) for n in w for g in range(2)]):
                if i >= 2:
                    pe.wait_ge(t_sb, i - 1)
                for p in range(4):
                    at = (4 * g + p) * P
                    mm = nc.tensor.transpose(ps_t[i % 2][:, p, :], w[n][:, at:at + P], ident[:, :])
                mm.then_inc(t_ps, 1)
            pe.wait_ge(t_sb, 6)
            for i, (left, right) in enumerate([(wT["q"], wT["ka"])] * 2 + [(wT["va"], wo)] * 2):
                if i >= 2:
                    pe.wait_ge(f_sb, 2 * (i - 1))
                for odd in range(2):
                    rows = slice(CD * odd, CD * odd + CD)
                    for p in range(4):
                        pair = 4 * (i % 2) + p
                        mm = nc.tensor.matmul(ps_f[2 * (i % 2) + odd][:, p, :], left[rows, pair, :], right[rows, pair, :],
                                              start=True, stop=True)
                    mm.then_inc(f_ps, 1)

        @block.scalar
        def _(act):
            for i, (n, g) in enumerate([(n, g) for n in w for g in range(2)]):
                act.wait_ge(t_ps, i + 1)
                nc.scalar.activation(wT[n][:, 4 * g:4 * g + 4, :], ps_t[i % 2][:, :, :], ACT.Copy).then_inc(t_sb, 1)

        @block.vector
        def _(dve):
            for i in range(8):
                dst, half, odd = (fq, fv)[i // 4], i // 2 % 2, i % 2
                dve.wait_ge(f_ps, i + 1)
                nc.vector.tensor_scalar(dst[:, 8 * half + odd:8 * half + 8:2, :], ps_f[2 * half + odd][:, :, :],
                                        SCALE if i < 4 else 1.0, None, ALU.mult).then_inc(f_sb, 1)


def cross_stage(nc, T, const):
    ident, ident16, causal16, ones, eps = const
    with ExitStack() as stack:
        c = Scope(nc, stack, "cross")
        wo = c.sb("wo", [P, HP, D])
        fq = c.sb("fq", [P, CH, P])
        fv = c.sb("fv", [P, CH, D])
        cross_fold(nc, T, const, wo, fq, fv)
        w = {n: c.sb(f"w_{n}", [P, INNER]) for n in ("q", "k", "v", "ki", "vi")}
        bo = c.sb("bo", [P, D])
        relk = c.sb("relk", [P, NREL])
        gains = c.sb("gains", [P, 2])
        far = c.sb("far", [P, 2, TEXT])
        x = c.sb("x", [P, TT, D])
        cx = c.sb("cx", [P, AT, D])
        xs = c.sb("xs", [P, TT, D])
        cs = c.sb("cs", [P, AT + 1, D])
        xT = c.sb("xT", [P, S])
        cT = c.sb("cT", [P, TI])
        upper = c.sb("upper", [P, 512])
        q_upper = c.sb("q_upper", [P, S])
        cTh = c.sb("cTh", [P, AUD], F32R)
        cTl = c.sb("cTl", [P, AUD], F32R)
        qT = c.sb("qT", [P, HP, S])
        kti = c.sb("kti", [P, HP, TR])
        vcat = c.sb("vcat", [P, INNER])
        sti = c.sb("sti", [P, TT, CH, TI])
        ext = c.sb("ext", [P, CH, P + TEXT - 1])
        rel = c.sb("rel", [P, TT, CH, TEXT])
        near = c.sb("near", [P, CH])
        pcat = c.sb("pcat", [P, TT, CH, CAT])
        pcT = c.sb("pcT", [P, 2, 4, P])
        small = c.sb("small", [P, 2, TT, CH])
        qh = c.sb("qh", [P, 2, S], F32R)
        ql = c.sb("ql", [P, 2, S], F32R)
        prob = c.sb("prob", [P, AT * P])
        pT = c.sb("pT", [P, 2, AT, S])
        uT = c.sb("uT", [P, S])
        acc = c.sb("acc", [P, TT, D])
        max3 = c.sb("max3", [P, 2, CHUNKS])
        negmax = c.sb("negmax", [P, 2])
        sums = c.sb("sums", [P, UNITS, CHUNKS])
        rsum = c.sb("rsum", [P, CH, TT])
        oall = c.sb("oall", [P, TT, CH, CD])
        oT = c.sb("oT", [P, HP, S])
        r = c.sb("r", [P, TT, D])
        stats = c.sb("stats", [P, TT, 6])
        mv = c.sb("mv", [P, TT, 2])
        rs = c.sb("rs", [P, TT])
        x5 = c.sb("x5", [P, TT, D])
        ring = [c.ps(f"ring{i}", [P, 512]) for i in range(RING)]
        fill = [c.ps(f"fill{i}", [P, 512]) for i in range(2)]
        ps_u = c.ps("ps_u", [P, 512])
        ps_y = c.ps("ps_y", [P, 512])

        weights_in = c.sem("weights_in")
        rel_in = c.sem("rel_in")
        cleared = c.sem("cleared")
        far_ready = c.sem("far_ready")
        gains_ready = c.sem("gains_ready")
        zeroed = c.sem("zeroed")
        x_used = c.sem("x_used")
        x_in = c.sem("x_in")
        turned = c.sem("turned")
        turned_act = c.sem("turned_act")
        turned_dve = c.sem("turned_dve")
        skewed_out = c.sem("skewed_out")
        skewed_in = c.sem("skewed_in")
        ti_max = c.sem("ti_max")
        ti_sub = c.sem("ti_sub")
        ti_exp = c.sem("ti_exp")
        ti_sum = c.sem("ti_sum")
        ti_prob = c.sem("ti_prob")
        band_out = c.sem("band_out")
        band_in = c.sem("band_in")
        far_prob = c.sem("far_prob")
        cat_ready = c.sem("cat_ready")
        scores = c.sem("scores")
        maxed = c.sem("maxed")
        exps = c.sem("exps")
        fill_ps = c.sem("fill_ps")
        fill_sb = {"act": c.sem("fill_act"), "dve": c.sem("fill_dve")}
        copied = c.sem("copied")
        q_high = c.sem("q_high")
        u_ps = c.sem("u_ps")
        u_sb = c.sem("u_sb")
        y_ps = c.sem("y_ps")
        y_read = c.sem("y_read")
        ln_stats = c.sem("ln_stats")
        ln_rs = c.sem("ln_rs")
        x5_ready = c.sem("x5_ready")
        stored = c.sem("stored")
        dve_own = c.sem("dve_own")
        act_own = c.sem("act_own")
        pool_own = c.sem("pool_own")
        block = c.block()
        e_w, f_w = P + TEXT - 1, FROW

        @block.sync
        def _(sp):
            for dst, src in [(w[n][:, :], T[f"cross_{n}"]) for n in w] + [
                    (bo[:, :], T["cross_bo"]), (relk[:, :], T["relk"]), (gains[:, :], T["gains"])]:
                sp.dma_start(dst, src).then_inc(weights_in, 16)
            for lo, n, col in ((0, R1, COL_R1), (R1, R2, COL_R2)):
                sp.dma_start(vcat[col:col + n, :].rearrange("r (h d) -> r h d", h=CH),
                             bc(T["relv"][lo:lo + n], 1, CH)).then_inc(rel_in, 16)
            sp.wait_ge(cleared, 3)
            sp.dma_start(T["skew_prob"], ext[:, :, 0:f_w]).then_inc(zeroed, 16)
            sp.wait_ge(zeroed, 16)
            full = (AT - 1) * P

            def load(b):
                sp.dma_start(xs[:, :, :], T["x4"][b].rearrange("(t p) d -> p t d", p=P)).then_inc(x_in, 16)
                sp.dma_start(cs[0:TI, 0, :], T["ctx"][b, 0:TI]).then_inc(x_in, 16)
                sp.dma_start(cs[:, 1:AT, :], T["ctx"][b, TI:TI + full].rearrange("(t p) d -> p t d", p=P)).then_inc(x_in, 16)
                sp.dma_start(cs[0:AUD - full, AT, :], T["ctx"][b, TI + full:CTX]).then_inc(x_in, 16)

            def turn(b):
                sp.wait_ge(fill_sb["dve"], b * PER_TURN["dve"] + (BEFORE["dve"] + emptied(FILL_AT[("s", (0, 3))])[1]))
                sp.dma_start(T["skew_rel"], ext[:, :, :]).then_inc(skewed_out, 16)
                sp.wait_ge(skewed_out, 16 * (b + 1))
                sp.wait_ge(ti_sub, b)
                sp.dma_start(rel[:, 0, :, :], bass.AP(T["skew_rel"].tensor, P - 1, [[CH * e_w - 1, P], [e_w, CH], [1, TEXT]]))\
                    .then_inc(skewed_in, 16)
                sp.wait_ge(ti_prob, b + 1)
                sp.dma_start(T["skew_prob"][:, :, REL:REL + TEXT], pcat[:, 0, :, 0:TEXT]).then_inc(band_out, 16)
                sp.wait_ge(band_out, 16 * (b + 1))
                for lo, n, col in ((0, R1, COL_R1), (R1, R2, COL_R2)):
                    sp.dma_start(pcat[:, 0, :, col:col + n],
                                 bass.AP(T["skew_prob"].tensor, lo, [[CH * f_w + 1, P], [f_w, CH], [1, n]])).then_inc(band_in, 16)
                sp.wait_ge(x5_ready, b + 1)
                sp.dma_start(T["x5"][b].rearrange("(t p) d -> p t d", p=P), x5[:, :, :]).then_inc(stored, 16)

            load(0)
            with sp.Fori(0, B - 1) as b:
                hold(sp, turned, 4 * (b + 1))
                hold(sp, copied, 3 * (b + 1))
                load(b + 1)
                turn(b)
            turn(B - 1)
            sp.wait_ge(stored, 16 * B)

        @block.tensor
        def _(pe):
            pe.wait_ge(weights_in, 16 * 8)
            pe.wait_ge(rel_in, 32)
            def transpose_inputs(b):
                if not isinstance(b, int):
                    pe.wait_ge(exps, b * UNITS * CHUNKS)
                pe.wait_ge(x_in, 64 * (b + 1))
                for t in range(TT):
                    nc.tensor.transpose(ring[0][:, t * P:(t + 1) * P], xs[:, t, :], ident[:, :])
                nc.tensor.transpose(ring[0][:, S:S + TI], cs[0:TI, 0, :], ident[0:TI, 0:TI]).then_inc(turned, 1)
                for i in range(CHUNKS):
                    for t in range(4 * i, 4 * i + 4):
                        m = min(P, AUD - t * P)
                        mm = nc.tensor.transpose(ring[i + 1][:, (t % 4) * P:(t % 4) * P + m], cs[0:m, t + 1, :],
                                                 ident[0:m, 0:m])
                    mm.then_inc(turned, 1)

            def sequence(b, more):
                waited = {"act": 0, "dve": 0}

                def wait_fill(*which):
                    need = {"act": -1, "dve": -1}
                    for i in which:
                        if i < 0:
                            need = {e: max(n, 0) for e, n in need.items()}
                        else:
                            e, n = emptied(i)
                            need[e] = max(need[e], n)
                    for e, n in need.items():
                        if n > waited[e] or n == waited[e] == 0:
                            wait_past(pe, fill_sb[e], b * PER_TURN[e] + (BEFORE[e] + n))
                            waited[e] = n

                def score(n, i):
                    k = n * CHUNKS + i
                    h, t = divmod(n, TT)
                    if t == 0 and i == 0:
                        wait_fill(FILL_AT[("q", h)] if h else -1)
                    if k >= RING:
                        pe.wait_ge(exps, b * UNITS * CHUNKS + (k - RING + 1))
                    tile, keys = slice(t * P, (t + 1) * P), slice(512 * i, 512 * i + CHUNK[i])
                    for j, (q, k_part) in enumerate(((qh, cTh), (qh, cTl), (ql, cTh))):
                        mm = nc.tensor.matmul(ring[k % RING][:, 0:CHUNK[i]], q[:, h % 2, tile],
                                              k_part[:, keys], start=(j == 0), stop=(j == 2))
                    mm.then_inc(scores, 1)

                def fill_bank(i):
                    wait_fill(i - 2)
                    return fill[bank_of(i)]

                def turn(n, i):
                    bank = fill_bank(FILL_AT[("t", (n, i))])
                    pe.wait_ge(exps, b * UNITS * CHUNKS + n * CHUNKS + i + 1)
                    for t in range(4):
                        m = min(P, AUD - (4 * i + t) * P)
                        mm = nc.tensor.transpose(bank[0:m, t * P:(t + 1) * P],
                                                 prob[:, (4 * i + t) * P:(4 * i + t) * P + m], ident[:, :])
                    mm.then_inc(fill_ps, 1)

                def use(what, arg):
                    bank = fill_bank(FILL_AT[(what, arg)])
                    if what == "q":
                        mm = nc.tensor.matmul(bank[:, 0:S], fq[:, arg, :], xT[:, :], start=True, stop=True)
                    if what == "tq":
                        for j in range(2):
                            p = 2 * arg + j
                            mm = nc.tensor.matmul(bank[:, j * S:(j + 1) * S], w["q"][:, p * P:(p + 1) * P], xT[:, :],
                                                  start=True, stop=True)
                    if what == "kt":
                        for j in range(4):
                            p = 4 * arg + j
                            nc.tensor.matmul(bank[:, j * TI:j * TI + TEXT], w["k"][:, p * P:(p + 1) * P], cT[:, 0:TEXT],
                                             start=True, stop=True)
                            mm = nc.tensor.matmul(bank[:, j * TI + TEXT:(j + 1) * TI], w["ki"][:, p * P:(p + 1) * P],
                                                  cT[:, TEXT:TI], start=True, stop=True)
                    if what == "vc":
                        cols = slice(512 * arg, 512 * arg + 512)
                        nc.tensor.matmul(bank[0:TEXT, :], cT[:, 0:TEXT], w["v"][:, cols], start=True, stop=True)
                        mm = nc.tensor.matmul(bank[COL_I:COL_I + IMG, :], cT[:, TEXT:TI], w["vi"][:, cols],
                                              start=True, stop=True)
                    if what == "s":
                        wait_fill(*[FILL_AT[("tq", j)] for j in range(4)], *[FILL_AT[("kt", j)] for j in range(2)])
                        t, (quad, odd) = arg[0], divmod(arg[1], 2)
                        rows = slice(CD * odd, CD * odd + CD)
                        for j in range(4):
                            p = 4 * quad + j
                            mm = nc.tensor.matmul(bank[:, j * TR:(j + 1) * TR], qT[rows, p, t * P:(t + 1) * P], kti[rows, p, :],
                                                  start=True, stop=True)
                    if what == "c":
                        if arg == 0:
                            pe.wait_ge(cat_ready, b + 1)
                        t, g = divmod(arg, CH // 4)
                        for j in range(4):
                            mm = nc.tensor.transpose(bank[0:CAT, j * P:(j + 1) * P], pcat[:, t, 4 * g + j, :], ident[:, :])
                    if what == "cp":
                        wait_fill(FILL_AT[("vc", 0)], FILL_AT[("vc", 1)], FILL_AT[("c", 2 * arg)], FILL_AT[("c", 2 * arg + 1)])
                        for j in range(8):
                            h = 8 * (arg % 2) + j
                            mm = nc.tensor.matmul(bank[:, j * CD:(j + 1) * CD], pcT[0:CAT, j // 4, j % 4, :],
                                                  vcat[0:CAT, h * CD:(h + 1) * CD], start=True, stop=True)
                    if what == "o":
                        wait_fill(*[FILL_AT[("cp", j)] for j in range(4)])
                        for j in range(4):
                            p, t = 2 * arg + j // 2, j % 2
                            mm = nc.tensor.transpose(bank[:, j * P:(j + 1) * P],
                                                     oall[:, t, 2 * p:2 * p + 2, :].rearrange("p a d -> p (a d)"), ident[:, :])
                    if what == "out":
                        wait_fill(*[FILL_AT[("o", j)] for j in range(4)])
                        for p in range(HP):
                            mm = nc.tensor.matmul(bank[:, 0:D], oT[:, p, arg * P:(arg + 1) * P], wo[:, p, :],
                                                  start=(p == 0), stop=(p == HP - 1))
                    mm.then_inc(fill_ps, 1)

                def attend(h, half):
                    if half == 0:
                        wait_past(pe, u_sb, b * CH + h)
                        wait_fill(*[FILL_AT[("t", (TT * h + t, i))] for t in range(TT) for i in range(CHUNKS)])
                    for kt in range(*HALVES[half]):
                        m = min(P, AUD - kt * P)
                        mm = nc.tensor.matmul(ps_u[:, 0:S], cx[0:m, kt, :], pT[0:m, h % 2, kt, :],
                                              start=(kt == 0), stop=(kt == AT - 1), skip_group_check=True)
                    if half == 1:
                        mm.then_inc(u_ps, 1)

                def give(h):
                    pe.wait_ge(u_sb, b * CH + h + 1)
                    wait_past(pe, y_read, b * CH + h)
                    for t in range(TT):
                        mm = nc.tensor.matmul(ps_y[:, t * D:(t + 1) * D], uT[:, t * P:(t + 1) * P], fv[:, h, :],
                                              start=True, stop=True)
                    mm.then_inc(y_ps, 1)

                pe.wait_ge(turned_act, 2 * (b + 1))
                pe.wait_ge(turned_dve, 2 * CHUNKS * (b + 1))
                for i in range(CHUNKS):
                    score(0, i)
                pe.wait_ge(copied, 3 * (b + 1))
                for n in range(UNITS):
                    for i in range(CHUNKS):
                        turn(n, i)
                        if n + 1 < UNITS:
                            score(n + 1, i)
                        for what, arg in after_scores(n, i):
                            use(what, arg)
                    if n % 2 == 0 and n >= 4:
                        give(n // 2 - 2)
                    if n >= 2:
                        attend(n // 2 - 1, n % 2)
                if more:
                    transpose_inputs(b + 1)
                attend(CH - 1, 0)
                give(CH - 2)
                attend(CH - 1, 1)
                use("o", 2)
                use("o", 3)
                give(CH - 1)
                use("out", 0)
                use("out", 1)
                if more:
                    pe.wait_ge(turned_act, 2 * (b + 2))
                    use("q", 0)

            transpose_inputs(0)
            pe.wait_ge(turned_act, 2)
            nc.tensor.matmul(fill[bank_of(-1)][:, 0:S], fq[:, 0, :], xT[:, :], start=True, stop=True).then_inc(fill_ps, 1)
            with pe.Fori(0, B - 1) as b:
                sequence(b, True)
            sequence(B - 1, False)

        def empty(eng, copy, name, b, i):
            what, arg, _ = FILL_LIST[i]
            bank = fill[bank_of(i)]
            eng.wait_ge(fill_ps, b * FILLS_PER_TURN + (i + 2))
            if what == "q":
                n = arg if arg else CH
                nc.vector.tensor_scalar(q_upper[:, :].bitcast(U32), bank[:, 0:S].bitcast(U32), HIGH, None, ALU.bitwise_and)\
                    .then_inc(q_high, 1)
                eng.wait_ge(q_high, b * (3 * CH) + (3 * n + 1))
                nc.vector.tensor_copy(qh[:, arg % 2, :], q_upper[:, :]).then_inc(q_high, 1)
                nc.vector.tensor_tensor(ql[:, arg % 2, :], bank[:, 0:S], q_upper[:, :], ALU.subtract).then_inc(q_high, 1)
                eng.wait_ge(q_high, b * (3 * CH) + (3 * n + 3))
                eng.sem_inc(fill_sb[name], 1)
                return
            if what == "s":
                t, (quad, odd) = arg[0], divmod(arg[1], 2)
                heads = slice(8 * quad + odd, 8 * quad + odd + 7, 2)
                small_scores = bank[:, 0:4 * TR].rearrange("p (a n) -> p a n", a=4)
                src = small_scores[:, :, TI:]
                if t == 0:
                    if arg[1] == 0:
                        wait_past(eng, skewed_out, 16 * b)
                    lo = P - 1 - REL
                    copy(ext[:, heads, lo:lo + NREL], src)
                    copy(ext[:, heads, 0:lo], src[:, :, 0:1].broadcast_to([P, 4, lo]))
                    copy(ext[:, heads, lo + NREL:], src[:, :, NREL - 1:].broadcast_to([P, 4, e_w - lo - NREL]))
                else:
                    copy(near[:, heads], src[:, :, 0])
                dst, src = sti[:, t, heads, :], small_scores[:, :, 0:TI]
            if what == "vc":
                cols = slice(512 * arg, 512 * arg + 512)
                copy(vcat[0:TEXT, cols], bank[0:TEXT, :])
                dst, src = vcat[COL_I:COL_I + IMG, cols], bank[COL_I:COL_I + IMG, :]
            if what == "tq":
                nc.scalar.activation(qT[:, 2 * arg:2 * arg + 2, :], bank[:, :].rearrange("p (a n) -> p a n", a=2), ACT.Copy,
                                     scale=SCALE).then_inc(fill_sb[name], 1)
                return
            if what == "kt":
                dst, src = kti[:, 4 * arg:4 * arg + 4, 0:TI], bank[:, 0:4 * TI].rearrange("p (a n) -> p a n", a=4)
            if what == "cp":
                t, half = divmod(arg, 2)
                dst, src = oall[:, t, 8 * half:8 * half + 8, :], bank[:, :].rearrange("p (a d) -> p a d", d=CD)
            if what == "o":
                dst, src = oT[:, 2 * arg:2 * arg + 2, :], bank[:, :].rearrange("p (a n) -> p a n", a=2)
            if what == "out":
                nc.vector.tensor_tensor(r[:, arg, :], r[:, arg, :], bank[:, 0:D], ALU.add).then_inc(fill_sb[name], 1)
                return
            if what == "c":
                dst, src = pcT[0:CAT, arg % 2, :, :].rearrange("p t d -> p (t d)"), bank[0:CAT, :]
            if what == "t":
                n, j = arg
                h, t = divmod(n, TT)
                tile = slice(t * P, (t + 1) * P)
                dst, src = pT[:, h % 2, 4 * j:4 * j + 4, tile], bank[:, :].rearrange("p (k n) -> p k n", n=P)
                if j == CHUNKS - 1:
                    m = AUD - (AT - 1) * P
                    copy(pT[:, h % 2, 4 * j:AT - 1, tile], src[:, 0:3, :])
                    dst, src = pT[0:m, h % 2, AT - 1, tile], bank[0:m, 3 * P:]
            copy(dst, src).then_inc(fill_sb[name], 1)

        @block.scalar
        def _(act):
            own = Chain(act, act_own)

            def copy(dst, src):
                return nc.scalar.activation(dst, src, ACT.Copy)

            act.wait_ge(weights_in, 16 * 8)
            own.link(nc.scalar.activation(gains[:, :], gains[:, :], ACT.Tanh))
            nc.scalar.activation(gains[:, :], gains[:, :], ACT.Identity, bias=ones[:, 0:1]).then_inc(gains_ready, 1)
            nc.scalar.preload_act_table_set("natural_log_exp_and_others")

            def keep_inputs(b):
                act.wait_ge(turned, 4 * b + 1)
                for dst, src in ((xT[:, :], ring[0][:, 0:S]), (cT[:, :], ring[0][:, S:S + TI])):
                    copy(dst, src).then_inc(turned_act, 1)

            def sequence(b, more):
                own.restart()
                order = [k for k, f in enumerate(FILL_LIST) if f[2] == "act"]

                def empty_until(k):
                    while order and order[0] <= k:
                        empty(act, copy, "act", b, order.pop(0))

                def keep(h):
                    act.wait_ge(u_ps, b * CH + h + 1)
                    wait_past(act, y_ps, b * CH + h)
                    copy(uT[:, :], ps_u[:, 0:S]).then_inc(u_sb, 1)

                for n in range(UNITS):
                    act.wait_ge(maxed, b * UNITS + n + 1)
                    for i in range(CHUNKS):
                        nc.scalar.activation(prob[:, 512 * i:512 * i + CHUNK[i]],
                                             ring[(n * CHUNKS + i) % RING][:, 0:CHUNK[i]], ACT.Exp,
                                             bias=negmax[:, n % 2:n % 2 + 1], accum_out=sums[:, n, i:i + 1]).then_inc(exps, 1)
                    if n % 2 == 0 and n >= 4:
                        keep(n // 2 - 2)
                    if n == STEP_EXP:
                        act.wait_ge(ti_sub, b + 1)
                        nc.scalar.activation(sti[:, :, :, :], sti[:, :, :, :], ACT.Exp).then_inc(ti_exp, 1)
                    empty_until(FILL_AT[("t", (n, CHUNKS - 1))] + len(after_scores(n, CHUNKS - 1)))
                if more:
                    keep_inputs(b + 1)
                keep(CH - 2)
                keep(CH - 1)
                empty_until(len(FILL_LIST))
                act.wait_ge(ln_stats, b + 1)
                own.link(nc.scalar.activation(rs[:, :], mv[:, :, 1], ACT.Ln, bias=eps[:, 0:1]))
                nc.scalar.activation(rs[:, :], rs[:, :], ACT.Exp, scale=-0.5).then_inc(ln_rs, 1)
                own.settle()

            keep_inputs(0)
            with act.Fori(0, B - 1) as b:
                sequence(b, True)
            sequence(B - 1, False)

        @block.gpsimd
        def _(pool):
            own = Chain(pool, pool_own)
            nc.gpsimd.memset(pcat[:, :, :, :], 0.0).then_inc(cleared, 1)
            nc.gpsimd.memset(ext[:, :, :], 0.0).then_inc(cleared, 1)
            nc.gpsimd.memset(far[:, :, :], 0.0).then_inc(cleared, 1)
            pool.wait_ge(cleared, 3)
            nc.gpsimd.affine_select(out=far[:, 0, :], in_=far[:, 0, :], compare_op=ALU.is_gt, fill=1.0,
                                    base=REL, pattern=[[1, TEXT]], channel_multiplier=-1).then_inc(far_ready, 1)
            nc.gpsimd.affine_select(out=far[:, 1, :], in_=far[:, 1, :], compare_op=ALU.is_gt, fill=1.0,
                                    base=REL, pattern=[[-1, TEXT]], channel_multiplier=1).then_inc(far_ready, 1)
            pool.wait_ge(far_ready, 2)
            with pool.Fori(0, B) as b:
                own.restart()
                hold(pool, u_ps, b * CH)
                hold(pool, x_used, b)
                hold(pool, x_in, 64 * (b + 1))
                m = AUD - (AT - 1) * P
                for dst, src in ((x[:, :, :], xs[:, :, :]), (cx[:, 0:AT - 1, :], cs[:, 1:AT, :]), (cx[0:m, AT - 1, :], cs[0:m, AT, :])):
                    nc.gpsimd.tensor_copy(dst, src).then_inc(copied, 1)
                pool.wait_ge(ti_max, 2 * (b + 1))
                nc.gpsimd.tensor_tensor(sti[:, :, :, 0:TEXT], sti[:, :, :, 0:TEXT], bc(small[:, 0, :, :], 3, TEXT),
                                        ALU.subtract).then_inc(pool_own, 1)
                nc.gpsimd.tensor_tensor(sti[:, :, :, TEXT:], sti[:, :, :, TEXT:], bc(small[:, 1, :, :], 3, IMG),
                                        ALU.subtract).then_inc(ti_sub, 1)
                pool.wait_ge(ti_sum, b + 1)
                nc.gpsimd.tensor_tensor(pcat[:, :, :, COL_I:COL_I + IMG], sti[:, :, :, TEXT:], bc(small[:, 1, :, :], 3, IMG),
                                        ALU.mult).then_inc(pool_own, 1)
                nc.gpsimd.tensor_tensor(pcat[:, :, :, 0:TEXT], sti[:, :, :, 0:TEXT], bc(small[:, 0, :, :], 3, TEXT),
                                        ALU.mult).then_inc(ti_prob, 1)
                pool.wait_ge(pool_own, 2)
                pool.wait_ge(ti_prob, b + 1)
                for i in range(2):
                    nc.gpsimd.tensor_tensor(rel[:, i, :, :], pcat[:, 0, :, 0:TEXT], bc(far[:, i, :], 1, CH), ALU.mult)\
                        .then_inc(far_prob, 1)

        @block.vector
        def _(dve):
            own = Chain(dve, dve_own)

            def copy(dst, src):
                return nc.vector.tensor_copy(dst, src)

            dve.wait_ge(weights_in, 16 * 8)
            dve.wait_ge(gains_ready, 1)
            dve.wait_ge(zeroed, 16)
            for p in range(HP):
                own.link(nc.vector.tensor_copy(kti[:, p, TI:], relk[:, :]))

            def split_inputs(b):
                wait_past(dve, scores, b * UNITS * CHUNKS)
                for i in range(CHUNKS):
                    dve.wait_ge(turned, 4 * b + i + 2)
                    keys, src = slice(512 * i, 512 * i + CHUNK[i]), ring[i + 1][:, 0:CHUNK[i]]
                    high = upper[:, 0:CHUNK[i]]
                    own.link(nc.vector.tensor_scalar(high.bitcast(U32), src.bitcast(U32), HIGH, None, ALU.bitwise_and))
                    nc.vector.tensor_copy(cTh[:, keys], high).then_inc(turned_dve, 1)
                    nc.vector.tensor_tensor(cTl[:, keys], src, high, ALU.subtract).then_inc(turned_dve, 1)
                    dve.wait_ge(turned_dve, b * (2 * CHUNKS) + 2 * (i + 1))

            def chunk_max(b, n, i):
                k = n * CHUNKS + i
                dve.wait_ge(scores, b * UNITS * CHUNKS + (k + 1))
                own.count(nc.vector.tensor_reduce(max3[:, n % 2, i:i + 1], ring[k % RING][:, 0:CHUNK[i]], AX, ALU.max))
                if i == CHUNKS - 1:
                    own.settle()
                    nc.vector.tensor_reduce(negmax[:, n % 2:n % 2 + 1], max3[:, n % 2, :], AX, ALU.max, negate=True)\
                        .then_inc(maxed, 1)

            def first_maxima(b):
                for i in range(CHUNKS):
                    chunk_max(b, 0, i)

            def sequence(b, more):
                own.restart()
                order = [k for k, f in enumerate(FILL_LIST) if f[2] == "dve"]

                def empty_next():
                    empty(dve, copy, "dve", b, order.pop(0))

                def text_scores():
                    dve.wait_ge(skewed_in, 16 * (b + 1))
                    e, n = emptied(FILL_AT[("s", (1, 3))])
                    dve.wait_ge(fill_sb[e], b * PER_TURN[e] + (BEFORE[e] + n))
                    own.count(nc.vector.tensor_tensor(sti[:, 0, :, 0:TEXT], sti[:, 0, :, 0:TEXT], rel[:, 0, :, :], ALU.add))
                    own.link(nc.vector.tensor_tensor(sti[:, 1, :, 0:TEXT], sti[:, 1, :, 0:TEXT], bc(near[:, :], 2, TEXT), ALU.add))

                def text_max():
                    nc.vector.tensor_reduce(small[:, 0, :, :], sti[:, :, :, 0:TEXT], AX, ALU.max).then_inc(ti_max, 1)
                    nc.vector.tensor_reduce(small[:, 1, :, :], sti[:, :, :, TEXT:], AX, ALU.max).then_inc(ti_max, 1)

                def text_sum():
                    dve.wait_ge(ti_exp, b + 1)
                    own.count(nc.vector.tensor_reduce(small[:, 0, :, :], sti[:, :, :, 0:TEXT], AX, ALU.add))

                def text_reciprocal():
                    own.link(nc.vector.tensor_reduce(small[:, 1, :, :], sti[:, :, :, TEXT:], AX, ALU.add))
                    own.link(nc.vector.reciprocal(small[:, :, :, :], small[:, :, :, :]))
                    nc.vector.tensor_scalar(small[:, 1, :, :], small[:, 1, :, :], gains[:, 0:1], None, ALU.mult)\
                        .then_inc(ti_sum, 1)

                def all_far_sum():
                    dve.wait_ge(ti_prob, b + 1)
                    own.count(nc.vector.tensor_reduce(pcat[:, 1, :, COL_R1], pcat[:, 1, :, 0:TEXT], AX, ALU.add))

                def far_sums():
                    dve.wait_ge(far_prob, 2 * (b + 1))
                    dve.wait_ge(band_in, 32 * (b + 1))
                    nc.vector.tensor_reduce(pcat[:, 0, :, COL_R1], rel[:, 0, :, :], AX, ALU.add)
                    nc.vector.tensor_reduce(pcat[:, 0, :, CAT - 1], rel[:, 1, :, :], AX, ALU.add).then_inc(cat_ready, 1)

                steps = {STEP_SCORES: text_scores, STEP_MAX: text_max, STEP_SUM: text_sum,
                         STEP_RECIPROCAL: text_reciprocal, STEP_ALL_FAR: all_far_sum, STEP_FAR: far_sums}

                def add_head(h):
                    dve.wait_ge(exps, b * UNITS * CHUNKS + (h + 1) * TT * CHUNKS)
                    own.link(nc.vector.tensor_reduce(rsum[:, h, :], sums[:, TT * h:TT * h + TT, :], AX, ALU.add))
                    own.link(nc.vector.reciprocal(rsum[:, h, :], rsum[:, h, :]))
                    dve.wait_ge(y_ps, b * CH + h + 1)
                    for t in range(TT):
                        y, rt = ps_y[:, t * D:(t + 1) * D], rsum[:, h, t:t + 1]
                        if h == 0:
                            ins = nc.vector.tensor_scalar(acc[:, t, :], y, rt, None, ALU.mult)
                        else:
                            ins = nc.vector.scalar_tensor_tensor(acc[:, t, :], y, rt, acc[:, t, :], ALU.mult, ALU.add)
                        if t == 0:
                            own.count(ins)
                    ins.then_inc(y_read, 1)
                    dve.wait_ge(y_read, b * CH + h + 1)
                    own.settle()

                for n in range(UNITS):
                    for i in range(CHUNKS):
                        if order and order[0] == FILL_AT[("t", (n, i))]:
                            empty_next()
                        if n + 1 < UNITS:
                            chunk_max(b, n + 1, i)
                        stop = FILL_AT[("t", (n, i))] + 1 + len(after_scores(n, i))
                        while order and order[0] < stop:
                            empty_next()
                    if n % 2 == 0 and n >= 4:
                        add_head(n // 2 - 2)
                    if n in steps:
                        steps[n]()
                if more:
                    split_inputs(b + 1)
                add_head(CH - 2)
                dve.wait_ge(copied, 3 * (b + 1))
                nc.vector.tensor_tensor(r[:, :, :], x[:, :, :], bc(bo[:, :], 1, TT), ALU.add).then_inc(x_used, 1)
                add_head(CH - 1)
                dve.wait_ge(x_used, b + 1)
                own.link(nc.vector.scalar_tensor_tensor(r[:, :, :], acc[:, :, :], gains[:, 1:2], r[:, :, :], ALU.mult, ALU.add))
                empty_next()
                empty_next()
                if more:
                    empty_next()
                dve.wait_ge(fill_sb["dve"], b * PER_TURN["dve"] + (BEFORE["dve"] + emptied(FILL_AT[("out", 1)])[1]))
                ln_statistics(nc, own, r, stats, mv, ln_stats)
                if more:
                    own.settle()
                    first_maxima(b + 1)
                dve.wait_ge(ln_stats, b + 1)
                dve.wait_ge(stored, 16 * b)
                dve.wait_ge(ln_rs, b + 1)
                ln_apply(nc, own, r, mv, rs, x5, x5_ready)
                own.settle()

            own.restart()
            split_inputs(0)
            empty(dve, copy, "dve", -1, FILLS_PER_TURN - 1)
            first_maxima(0)
            with dve.Fori(0, B - 1) as b:
                sequence(b, True)
            sequence(B - 1, False)


TOK = B * S
NT = TOK // P
MT = 4
GW = MT * P
MG = NT // MT
CAP = TOK // NE
BITS = 30


def moe_route(nc, T, const, m):
    ident, ident16, causal16, ones, eps = const
    with ExitStack() as stack:
        c = Scope(nc, stack, "route")
        ws = c.sb("ws", [P, NE])
        bs = c.sb("bs", [P, NE])
        x = [c.sb(f"x{i}", [P, MT, D]) for i in range(2)]
        xs = [c.sb(f"xs{i}", [P, GW]) for i in range(2)]
        logit = c.sb("logit", [P, NT, NE])
        top = c.sb("top", [P, NT])
        ps_x = [c.ps(f"ps_x{i}", [P, GW]) for i in range(2)]
        ps_l = [c.ps(f"ps_l{i}", [P, MT, NE]) for i in range(2)]
        weights_in = c.sem("weights_in")
        x_in = [c.sem(f"x_in{i}") for i in range(2)]
        x_ps = c.sem("x_ps")
        xs_ready = c.sem("xs_ready")
        kept = c.sem("kept")
        l_ps = c.sem("l_ps")
        l_sb = c.sem("l_sb")
        shifted = c.sem("shifted")
        powers = c.sem("powers")
        dve_own = c.sem("dve_own")
        block = c.block()

        @block.sync
        def _(sp):
            sp.dma_start(ws[:, :], T["moe_ws"]).then_inc(weights_in, 16)
            sp.dma_start(bs[:, :], T["moe_bs"]).then_inc(weights_in, 16)
            tiles = T["x5"].rearrange("b (t p) d -> p (b t) d", p=P)
            with sp.Fori(0, MG // 2) as i:
                for h in range(2):
                    sp.wait_ge(x_ps, i * 2)
                    sp.wait_ge(kept, i * 2)
                    sp.dma_start(x[h][:, :, :], tiles[:, bass.ds(i * (2 * MT) + h * MT, MT), :]).then_inc(x_in[h], 16)

        @block.tensor
        def _(pe):
            pe.wait_ge(weights_in, 32)
            with pe.Fori(0, MG // 2) as i:
                for h in range(2):
                    pe.wait_ge(x_in[h], i * 16 + 16)
                    for t in range(MT):
                        mm = nc.tensor.transpose(ps_x[h][:, t * P:(t + 1) * P], x[h][:, t, :], ident[:, :])
                    mm.then_inc(x_ps, 1)
                    pe.wait_ge(xs_ready, i * 2 + h + 1)
                    pe.wait_ge(l_sb, i * 2)
                    for t in range(MT):
                        mm = nc.tensor.matmul(ps_l[h][:, t, :], xs[h][:, t * P:(t + 1) * P], ws[:, :],
                                              start=(t == 0), stop=True, skip_group_check=True)
                    mm.then_inc(l_ps, 1)

        @block.scalar
        def _(act):
            with act.Fori(0, MG // 2) as i:
                for h in range(2):
                    act.wait_ge(x_ps, i * 2 + h + 1)
                    act.wait_ge(m["xT_kept"], i * 2)
                    nc.scalar.activation(xs[h][:, :], ps_x[h][:, :], ACT.Copy).then_inc(xs_ready, 1)
            act.wait_ge(shifted, 1)
            nc.scalar.activation(logit[:, :, :], logit[:, :, :], ACT.Exp).then_inc(powers, 1)

        @block.gpsimd
        def _(pool):
            with pool.Fori(0, MG // 2) as i:
                for h in range(2):
                    hold(pool, x_in[h], i * 16 + 16)
                    nc.gpsimd.tensor_copy(m["x"][:, bass.ds(i * (2 * MT) + h * MT, MT), :], x[h][:, :, :]).then_inc(kept, 1)

        @block.vector
        def _(dve):
            own = Chain(dve, dve_own)
            dve.wait_ge(weights_in, 32)
            with dve.Fori(0, MG // 2) as i:
                for h in range(2):
                    dve.wait_ge(xs_ready, i * 2 + h + 1)
                    nc.vector.tensor_copy(m["xT"][:, bass.ds(i * (2 * GW) + h * GW, GW)], xs[h][:, :]).then_inc(m["xT_kept"], 1)
                    dve.wait_ge(l_ps, i * 2 + h + 1)
                    nc.vector.tensor_tensor(logit[:, bass.ds(i * (2 * MT) + h * MT, MT), :], ps_l[h][:, :, :],
                                            bc(bs[:, :], 1, MT), ALU.add).then_inc(l_sb, 1)
            dve.wait_ge(l_sb, MG)
            own.link(nc.vector.tensor_reduce(top[:, :], logit[:, :, :], axis=AX, op=ALU.max))
            nc.vector.tensor_tensor(logit[:, :, :], logit[:, :, :], bc(top[:, :], 2, NE), ALU.subtract).then_inc(shifted, 1)
            dve.wait_ge(powers, 1)
            own.link(nc.vector.tensor_reduce(top[:, :], logit[:, :, :], axis=AX, op=ALU.add))
            own.link(nc.vector.reciprocal(top[:, :], top[:, :]))
            own.link(nc.vector.tensor_tensor(m["prob"].rearrange("p e t -> p t e"), logit[:, :, :], bc(top[:, :], 2, NE), ALU.mult))


def moe_choose(nc, T, const, m):
    ident, ident16, causal16, ones, eps = const
    with ExitStack() as stack:
        c = Scope(nc, stack, "choose")
        bits = c.sb("bits", [P, BITS], U32)
        thr = c.sb("thr", [P, NE])
        cand = c.sb("cand", [P, NE])
        passed = c.sb("passed", [P, NE])
        count = c.sb("count", [P, NE])
        over = c.sb("over", [P, NE, NT])
        equal = c.sb("equal", [P, NE, NT])
        later = c.sb("later", [P, NE, NT])
        total = c.sb("total", [P, NE, NT])
        rank = c.sb("rank", [P, NE, NT])
        below = c.sb("below", [P, P])
        ps_c = c.ps("ps_c", [P, NE])
        ps_b = c.ps("ps_b", [P, NE, NT])
        ps_t = c.ps("ps_t", [P, NE, NT])
        bits_in = c.sem("bits_in")
        filled = c.sem("filled")
        counted = c.sem("counted")
        summed = c.sem("summed")
        tied = c.sem("tied")
        ranked = c.sem("ranked")
        dve_own = c.sem("dve_own")
        block = c.block()
        prob = m["prob"]

        @block.sync
        def _(sp):
            sp.dma_start(bits[:, :], T["bits"]).then_inc(bits_in, 16)

        @block.gpsimd
        def _(pool):
            nc.gpsimd.memset(thr[:, :], 0.0).then_inc(filled, 1)
            nc.gpsimd.memset(later[:, :, :], 1.0).then_inc(filled, 1)
            nc.gpsimd.memset(below[:, :], 1.0).then_inc(filled, 1)
            pool.wait_ge(filled, 3)
            nc.gpsimd.memset(later[:, :, 0:1], 0.0).then_inc(filled, 1)
            nc.gpsimd.affine_select(out=below[:, :], in_=below[:, :], compare_op=ALU.is_gt, fill=0.0,
                                    base=0, pattern=[[1, P]], channel_multiplier=-1).then_inc(filled, 1)
            pool.wait_ge(filled, 5)

        @block.tensor
        def _(pe):
            with pe.Fori(0, BITS + 1) as i:
                pe.wait_ge(counted, i + 1)
                nc.tensor.matmul(ps_c[:, :], ones[:, :], count[:, :], start=True, stop=True).then_inc(summed, 1)
            pe.wait_ge(filled, 5)
            pe.wait_ge(tied, 1)
            nc.tensor.matmul(ps_b[:, :, :], below[:, :], equal[:, :, :], start=True, stop=True).then_inc(ranked, 1)
            nc.tensor.matmul(ps_t[:, :, :], ones[:, :], equal[:, :, :], start=True, stop=True).then_inc(ranked, 1)

        @block.vector
        def _(dve):
            own = Chain(dve, dve_own)
            dve.wait_ge(filled, 5)
            dve.wait_ge(bits_in, 16)

            def try_bit(i):
                own.link(nc.vector.tensor_tensor(cand[:, :].bitcast(U32), thr[:, :].bitcast(U32),
                                                 bits[:, bass.ds(i, 1)].broadcast_to([P, NE]), ALU.bitwise_or))
                own.link(nc.vector.tensor_tensor(over[:, :, :], prob[:, :, :], bc(cand[:, :], 2, NT), ALU.is_ge))
                nc.vector.tensor_reduce(count[:, :], over[:, :, :], axis=AX, op=ALU.add).then_inc(counted, 1)
                dve.wait_ge(summed, i + 1)
                own.link(nc.vector.scalar_tensor_tensor(passed[:, :], ps_c[:, :], CAP - 0.5, cand[:, :], ALU.is_ge, ALU.mult))
                own.link(nc.vector.tensor_tensor(thr[:, :], thr[:, :], passed[:, :], ALU.max))

            with dve.Fori(0, BITS // 3) as turn:
                own.restart()
                for i in range(3):
                    try_bit(turn * 3 + i)
            own.restart()
            own.link(nc.vector.tensor_tensor(equal[:, :, :], prob[:, :, :], bc(thr[:, :], 2, NT), ALU.is_equal))
            nc.vector.tensor_tensor(over[:, :, :], prob[:, :, :], bc(thr[:, :], 2, NT), ALU.is_gt).then_inc(tied, 1)
            dve.wait_ge(tied, 1)
            nc.vector.tensor_reduce(count[:, :], over[:, :, :], axis=AX, op=ALU.add).then_inc(counted, 1)
            dve.wait_ge(ranked, 2)
            own.link(nc.vector.tensor_copy(total[:, :, :], ps_t[:, :, :]))
            own.link(nc.vector.tensor_tensor_scan(rank.rearrange("p e t -> p (e t)"), later.rearrange("p e t -> p (e t)"),
                                                  total.rearrange("p e t -> p (e t)"), 0.0, ALU.mult, ALU.add))
            own.link(nc.vector.tensor_tensor(rank[:, :, :], rank[:, :, :], total[:, :, :], ALU.subtract))
            own.link(nc.vector.tensor_tensor(rank[:, :, :], rank[:, :, :], ps_b[:, :, :], ALU.add))
            dve.wait_ge(summed, BITS + 1)
            own.link(nc.vector.tensor_scalar(count[:, :], ps_c[:, :], -1.0, float(CAP), ALU.mult, ALU.add))
            own.link(nc.vector.tensor_tensor(rank[:, :, :], rank[:, :, :], bc(count[:, :], 2, NT), ALU.is_lt))
            own.link(nc.vector.tensor_tensor(rank[:, :, :], rank[:, :, :], equal[:, :, :], ALU.mult))
            own.link(nc.vector.tensor_tensor(rank[:, :, :], rank[:, :, :], over[:, :, :], ALU.add))
            own.link(nc.vector.tensor_tensor(prob[:, :, :], prob[:, :, :], rank[:, :, :], ALU.mult))


def moe_experts(nc, T, const, m):
    ident, ident16, causal16, ones, eps = const
    with ExitStack() as stack:
        c = Scope(nc, stack, "experts")
        w1 = [c.sb(f"w1{i}", [P, DF]) for i in range(2)]
        w2 = [c.sb(f"w2{i}", [P, FC, D]) for i in range(2)]
        b1 = [c.sb(f"b1{i}", [P, FC]) for i in range(2)]
        b2 = c.sb("b2", [NE, D])
        hT = c.sb("hT", [P, FC, GW])
        w = c.sb("w", [P, MT, NE])
        wT = c.sb("wT", [NE, GW])
        r = c.sb("r", [P, MT, D])
        stats = c.sb("stats", [P, MT, 6])
        mv = c.sb("mv", [P, MT, 2])
        rs = c.sb("rs", [P, MT])
        out = c.sb("out", [P, MT, D])
        ps_h = [c.ps(f"ps_h{i}", [P, GW]) for i in range(FC)]
        ps_y = [c.ps(f"ps_y{i}", [P, MT, D]) for i in range(2)]
        ps_w = c.ps("ps_w", [NE, GW])
        ps_b = c.ps("ps_b", [P, MT, D])
        expert_in = [c.sem(f"expert_in{i}") for i in range(2)]
        used = c.sem("used")
        h_ps = c.sem("h_ps")
        h_sb = c.sem("h_sb")
        y_ps = c.sem("y_ps")
        y_free = c.sem("y_free")
        b2_in = c.sem("b2_in")
        w_ready = c.sem("w_ready")
        w_ps = c.sem("w_ps")
        wT_ready = c.sem("wT_ready")
        b_ps = c.sem("b_ps")
        ln_stats = c.sem("ln_stats")
        ln_rs = c.sem("ln_rs")
        out_ready = c.sem("out_ready")
        stored = c.sem("stored")
        dve_own = c.sem("dve_own")
        act_own = c.sem("act_own")
        block = c.block()

        def experts(eng, run):
            with eng.Fori(0, NE // 2 - 1) as e2:
                run(e2, 0, False)
                run(e2, 1, False)
            run(NE // 2 - 1, 0, False)
            run(NE // 2 - 1, 1, True)

        @block.sync
        def _(sp):
            sp.dma_start(b2[:, :], T["moe_b2"]).then_inc(b2_in, 16)

            def load(e2, k, last):
                e = e2 * 2 + k
                sp.wait_ge(used, e2 * 2 + (k + 1))
                sp.dma_start(w1[k][:, :], T["moe_w1"][bass.ds(e, 1)].rearrange("e p f -> p (e f)")).then_inc(expert_in[k], 16)
                sp.dma_start(w2[k][:, :, :], T["moe_w2"][bass.ds(e, 1)].rearrange("e (c p) d -> p (e c) d", p=P))\
                    .then_inc(expert_in[k], 16)
                sp.dma_start(b1[k][:, :], T["moe_b1"][bass.ds(e, 1)].rearrange("e p f -> p (e f)")).then_inc(expert_in[k], 16)

            experts(sp, load)
            tiles = T["out"].rearrange("b (t p) d -> p (b t) d", p=P)
            with sp.Fori(0, MG) as g:
                sp.wait_ge(out_ready, g + 1)
                sp.dma_start(tiles[:, bass.ds(g * MT, MT), :], out[:, :, :]).then_inc(stored, 16)
            sp.wait_ge(stored, 16 * MG)

        @block.tensor
        def _(pe):
            pe.wait_ge(b2_in, 16)

            def run(e2, k, last):
                hold(pe, expert_in[k], e2 * 48 + 48)
                with pe.Fori(0, MG // 2) as i:
                    for g in range(2):
                        step = i * 2 + e2 * (2 * MG) + (k * MG + g)
                        for f in range(FC):
                            nc.tensor.matmul(ps_h[f][:, :], w1[k][:, f * P:(f + 1) * P],
                                             m["xT"][:, bass.ds(i * (2 * GW) + g * GW, GW)], start=True, stop=True)\
                                .then_inc(h_ps, 1)
                        if last:
                            pe.wait_ge(w_ready, i * 2 + g + 1)
                            for t in range(MT):
                                mm = nc.tensor.transpose(ps_w[:, t * P:(t + 1) * P], w[:, t, :], ident[:, :])
                            mm.then_inc(w_ps, 1)
                        pe.wait_ge(y_free, (step + 1) * MT)
                        for f in range(FC):
                            pe.wait_ge(h_sb, step * FC + f + 1)
                            for t in range(MT):
                                mm = nc.tensor.matmul(ps_y[g][:, t, :], hT[:, f, t * P:(t + 1) * P], w2[k][:, f, :],
                                                      start=(f == 0 and t == 0), stop=(f == FC - 1), skip_group_check=True)
                        mm.then_inc(y_ps, 1)
                        if last:
                            pe.wait_ge(ln_stats, i * 2 + g)
                            pe.wait_ge(wT_ready, i * 2 + g + 1)
                            for t in range(MT):
                                mm = nc.tensor.matmul(ps_b[:, t, :], wT[:, t * P:(t + 1) * P], b2[:, :], start=(t == 0), stop=True,
                                                      skip_group_check=True)
                            mm.then_inc(b_ps, 1)

            experts(pe, run)

        @block.scalar
        def _(act):
            own = Chain(act, act_own)

            def run(e2, k, last):
                act.wait_ge(expert_in[k], e2 * 48 + 48)
                with act.Fori(0, MG) as g:
                    step = g + e2 * (2 * MG) + k * MG
                    for f in range(FC):
                        act.wait_ge(h_ps, step * FC + f + 1)
                        nc.scalar.activation(hT[:, f, :], ps_h[f][:, :], ACT.Gelu_apprx_tanh, bias=b1[k][:, f:f + 1])\
                            .then_inc(h_sb, 1)
                    if last:
                        own.restart()
                        act.wait_ge(w_ps, g + 1)
                        nc.scalar.activation(wT[:, :], ps_w[:, :], ACT.Copy).then_inc(wT_ready, 1)
                        act.wait_ge(ln_stats, g + 1)
                        own.link(nc.scalar.activation(rs[:, :], mv[:, :, 1], ACT.Ln, bias=eps[:, 0:1]))
                        nc.scalar.activation(rs[:, :], rs[:, :], ACT.Exp, scale=-0.5).then_inc(ln_rs, 1)
                        own.settle()

            nc.scalar.preload_act_table_set("gelu_apprx_tanh_and_others")
            experts(act, run)

        @block.vector
        def _(dve):
            own = Chain(dve, dve_own)

            def run(e2, k, last):
                with dve.Fori(0, MG // 2) as i:
                    for g in range(2):
                        step = i * 2 + e2 * (2 * MG) + (k * MG + g)
                        group = bass.ds(i * (2 * MT) + g * MT, MT)
                        if last:
                            own.restart()
                            dve.wait_ge(w_ps, i * 2 + g)
                            nc.vector.tensor_copy(w[:, :, :], m["prob"].rearrange("p e t -> p t e")[:, group, :])\
                                .then_inc(w_ready, 1)
                        dve.wait_ge(y_ps, step + 1)
                        dve.wait_ge(y_free, (step + 2) * MT)
                        for t in range(MT):
                            xt = m["x"][:, bass.ds(i * (2 * MT) + (g * MT + t), 1), :].rearrange("p o d -> p (o d)")
                            at = i * (2 * MT) + e2 * (2 * NT) + (k * NT + g * MT + t)
                            nc.vector.scalar_tensor_tensor(xt, ps_y[g][:, t, :],
                                                           m["prob"].rearrange("p e t -> p (e t)")[:, bass.ds(at, 1)],
                                                           xt, ALU.mult, ALU.add).then_inc(y_free, 1)
                        if last:
                            n = i * 2 + g
                            dve.wait_ge(out_ready, n)
                            dve.wait_ge(y_free, (step + 3) * MT)
                            dve.wait_ge(b_ps, n + 1)
                            own.link(nc.vector.tensor_tensor(r[:, :, :], m["x"][:, group, :], ps_b[:, :, :], ALU.add))
                            layernorm(nc, dve, own, r, stats, mv, rs, out, n, ln_stats, ln_rs, out_ready, stored, MT)
                            own.settle()
                dve.sem_inc(used, 1)

            dve.sem_inc(y_free, 2 * MT)
            dve.sem_inc(used, 2)
            experts(dve, run)


def moe_stage(nc, T, const):
    with ExitStack() as stack:
        c = Scope(nc, stack, "moe")
        m = {"x": c.sb("x", [P, NT, D]), "xT": c.sb("xT", [P, TOK]), "prob": c.sb("prob", [P, NE, NT]),
             "xT_kept": c.sem("xT_kept")}
        moe_route(nc, T, const, m)
        moe_choose(nc, T, const, m)
        moe_experts(nc, T, const, m)


def layout(a):
    import numpy as np

    def t(w):
        return np.ascontiguousarray(np.asarray(w).T)

    def rows(w):
        return np.ascontiguousarray(w.reshape(-1, P, w.shape[-1]).transpose(1, 0, 2))

    def every(v):
        return np.ascontiguousarray(np.broadcast_to(np.asarray(v).reshape(1, -1), (P, np.asarray(v).size)))

    def halves(v):
        return np.asarray(v).reshape(HALF, P).T

    L = {"x": np.asarray(a["x"]), "ctx": np.asarray(a["ctx_1024"])}
    L["w_in"] = t(a["L0_attn_W_in"])
    L["w_x"] = rows(t(a["L0_attn_W_x"]))
    L["w_dt"] = rows(t(a["L0_attn_W_dt"]))
    L["w_out"] = rows(t(a["L0_attn_W_out"]))
    L["conv_w"] = np.ascontiguousarray(np.asarray(a["L0_attn_conv_w"]).reshape(HALF, P, TAPS).transpose(1, 0, 2))
    L["scan_vec"] = np.ascontiguousarray(np.stack(
        [halves(a[f"L0_attn_{n}"]) for n in ("conv_b", "b_dt", "D_param", "ln_g", "ln_b")], axis=1))
    L["a_log"] = every(a["L0_attn_A_log"])
    for name, dst in (("q", "wq_pad"), ("k", "wk_bd"), ("v", "wv_bd")):
        w = np.asarray(a[f"L0_xattn_W{name}"])
        pad = np.zeros((P, AH, P) if name == "q" else (P, P), w.dtype)
        for h in range(AH):
            own = slice(h * AD, (h + 1) * AD)
            if name == "q":
                pad[own, h, own] = w.T
            else:
                pad[own, own] = w.T
        L[dst] = pad
    L["wo"] = t(a["L0_xattn_Wo"])
    L["bo"] = every(a["L0_xattn_bo"])
    L["wr"] = np.asarray(a["L0_ffn_Wr"])
    L["br"] = np.asarray(a["L0_ffn_br"]).reshape(1, NE)
    L["ffn_w1"] = np.asarray(a["L0_ffn_W1"])
    L["ffn_b1"] = np.ascontiguousarray(np.asarray(a["L0_ffn_b1"]).reshape(NE, FC, P).transpose(0, 2, 1))
    L["ffn_w2"] = np.asarray(a["L0_ffn_W2"])
    L["ffn_b2"] = np.ascontiguousarray(np.broadcast_to(np.asarray(a["L0_ffn_b2"])[:, None, :], (NE, P, D)))
    names = ("k", "q", "v")
    pad = np.zeros((P, PLANES, 2 * WIN + DH), np.float32)
    bias = np.zeros((P, PLANES), np.float32)
    taps = np.zeros((P, 3 * DW, TAPS), np.float32)
    for i, n in enumerate(names):
        w, wb, wc = (np.asarray(a[f"L1_attn_{x}{n}"]) for x in ("W", "b", "conv_"))
        for d in range(DW):
            pad[:, i * DW + d, WIN:WIN + DH] = w[d::DW].T
            for s in range(GB):
                bias[s * DH:(s + 1) * DH, i * DW + d] = wb[d::DW]
                taps[s * DH:(s + 1) * DH, i * DW + d] = wc[d::DW]
    pad[:, 3 * DW, WIN:WIN + DH] = np.asarray(a["L1_attn_Wbeta"]).T
    for s in range(GB):
        bias[s * DH:(s + 1) * DH, 3 * DW] = np.asarray(a["L1_attn_bbeta"])
    L["delta_w"], L["delta_bias"], L["delta_taps"] = pad, bias, taps
    time = np.arange(1, S + 1, dtype=np.float64)
    coef = np.stack([time / (time + 1), (time - 1) / (time + 1), 2 / (time + 1)])
    coef[0, 0] = 0
    L["coef"] = np.ascontiguousarray(np.broadcast_to(coef.astype(np.float32), (P, 3, S)))
    L["rms"] = every(a["L1_attn_rms_w"])
    L["delta_out"] = np.ascontiguousarray(np.asarray(a["L1_attn_Wout"]).T.reshape(DH, DW, D))
    L["bout"] = every(a["L1_attn_bout"])
    for n, ref in (("q", "q"), ("k", "k"), ("v", "v"), ("ki", "k_ip"), ("vi", "v_ip"), ("ka", "k_ap"), ("va", "v_ap")):
        L[f"cross_{n}"] = np.asarray(a[f"L1_xattn_W{ref}"])
    L["cross_o"] = rows(np.asarray(a["L1_xattn_Wo"]))
    L["cross_bo"] = every(a["L1_xattn_bo"])
    relk = np.asarray(a["L1_xattn_rel_k"]).T
    L["relk"] = np.concatenate([relk, relk])
    L["relv"] = np.asarray(a["L1_xattn_rel_v"])
    L["gains"] = np.ascontiguousarray(np.broadcast_to(np.stack([a["L1_xattn_alpha"], a["L1_xattn_beta"]]), (P, 2)))
    L["moe_ws"] = np.asarray(a["L1_ffn_Ws"])
    L["moe_bs"] = every(a["L1_ffn_bs"])
    L["moe_w1"] = np.asarray(a["L1_ffn_W1"])
    L["moe_b1"] = np.ascontiguousarray(np.asarray(a["L1_ffn_b1"]).reshape(NE, FC, P).transpose(0, 2, 1))
    L["moe_w2"] = np.asarray(a["L1_ffn_W2"])
    L["moe_b2"] = np.asarray(a["L1_ffn_b2"])
    L["bits"] = np.ascontiguousarray(np.broadcast_to(np.array([1 << i for i in reversed(range(BITS))], np.uint32), (P, BITS)))
    return L


def program(nc, T):
    with ExitStack() as stack:
        const = constants(nc, stack)
        scan_stage(nc, T, const)
        self_stage(nc, T, const)
        ffn_stage(nc, T, const)
        delta_stage(nc, T, const)
        cross_stage(nc, T, const)
        moe_stage(nc, T, const)


def kernel(**inputs):
    import numpy as np
    import concourse.bacc as bacc
    from concourse.bass_utils import run_bass_kernel_spmd

    nc = bacc.Bacc("TRN2", target_bir_lowering=False, num_devices=1)
    arrays, T = {}, {}
    for name, a in layout(inputs).items():
        arrays[f"in_{name}_dram"] = np.ascontiguousarray(a)
        T[name] = nc.dram_tensor(f"in_{name}_dram", a.shape, mybir.dt.from_np(a.dtype), kind="ExternalInput").ap()
    for name in ("x1", "x2", "x3", "x4", "x5"):
        T[name] = nc.dram_tensor(f"{name}_dram", (B, S, D), F32, kind="Internal").ap()
    for name, shape in SCRATCH.items():
        T[name] = nc.dram_tensor(f"{name}_dram", shape, F32, kind="Internal").ap()
    T["out"] = nc.dram_tensor("out_0_dram", (B, S, D), F32, kind="ExternalOutput").ap()
    program(nc, T)
    r = run_bass_kernel_spmd(nc, [arrays], core_ids=[0])
    return r.results[0]["out_0_dram"]
```
